# Optimizing a Trainium2 kernel written in Bass

```python
import numpy as np
import jax
import jax.numpy as jnp

def _softmax(x, axis=-1):
    return jax.nn.softmax(x, axis=axis)

def _gelu(x):
    return jax.nn.gelu(x, approximate=True)

def _silu(x):
    return jax.nn.silu(x)

def _sigmoid(x):
    return jax.nn.sigmoid(x)

def _layernorm(x, axis=-1, eps=1e-05):
    m = jnp.mean(x, axis=axis, keepdims=True)
    v = jnp.var(x, axis=axis, keepdims=True)
    return (x - m) / jnp.sqrt(v + eps)

def _scatter_add(tgt, idx, src, axis=0):
    return tgt.at[idx].add(src)

def _segment_sum(src, seg, n):
    return jax.ops.segment_sum(src, seg, n)
kernel_name = 'mk_early_fusion_d4_tok_img512_r4_d7827d'

def setup_inputs(seed: int=0):
    np.random.seed(seed)
    _w = jnp.asarray

    def _rec_inputs():
        import jax
        import jax.numpy as jnp
        _rk = jax.random.key(seed)
        x = -7.10856e-05 + 0.999911 * jax.random.normal(jax.random.fold_in(_rk, 1), (16, 64, 64, 128), jnp.float32)
        txt = 0.000364437 + 0.0219324 * jax.random.normal(jax.random.fold_in(_rk, 2), (16, 128, 128), jnp.float32)
        return (x, txt)
    x, txt = _rec_inputs()

    def _L0_tok_setup():
        import jax, jax.numpy as jnp
        import numpy as np
        from jax import lax
        B, H, W, C = (32, 64, 64, 128)
        POOL = 8
        STRIDE = 8
        key = jax.random.key(seed)
        k1, k2, k3 = jax.random.split(key, 3)
        x = jax.random.normal(k1, (B, H, W, C), dtype=jnp.float32)
        conv_w = jax.random.normal(k2, (3, 3, 1, C), dtype=jnp.float32) * 0.02
        conv_b = jax.random.normal(k3, (C,), dtype=jnp.float32) * 0.02
        return {'x': x, 'conv_w': conv_w, 'conv_b': conv_b}
    _L0_tok_all = _L0_tok_setup()
    _L0_tok_in = {k: v for k, v in _L0_tok_all.items() if k in ('conv_w', 'conv_b')}
    del _L0_tok_all

    def _L0_attn_setup():
        import jax, jax.numpy as jnp
        import numpy as np
        import math
        N_HEAD = 8
        key = jax.random.key(seed)
        k1, k2 = jax.random.split(key)
        B, L, C = (4, 512, 128)
        x = jax.random.normal(k1, (B, L, C), dtype=jnp.float32)
        W_qkv = jax.random.normal(k2, (C, 3 * C), dtype=jnp.float32) * 0.02
        b_qkv = jnp.zeros((3 * C,), dtype=jnp.float32)
        return {'x': x, 'W_qkv': W_qkv, 'b_qkv': b_qkv}
    _L0_attn_all = _L0_attn_setup()
    _L0_attn_in = {k: v for k, v in _L0_attn_all.items() if k in ('W_qkv', 'b_qkv')}
    del _L0_attn_all

    def _L0_ffn_setup():
        import jax, jax.numpy as jnp
        import numpy as np
        import math
        B, T, D, H, E, TOPK = (8, 1024, 128, 512, 8, 2)
        CAP_FRAC = 1.0

        def _expert_ffn(x, w1, w2, w3):
            h = jax.nn.gelu(x @ w2 * (x @ w1), approximate=False)
            return h @ w3
        key = jax.random.key(seed)
        ks = jax.random.split(key, 6)
        x = jax.random.normal(ks[0], (B, T, D), dtype=jnp.float32)
        Wr = jax.random.normal(ks[1], (D, E), dtype=jnp.float32) * 0.02
        br = jnp.zeros((E,), dtype=jnp.float32)
        W1 = jax.random.normal(ks[2], (E, D, H), dtype=jnp.float32) * 0.02
        W2 = jax.random.normal(ks[3], (E, D, H), dtype=jnp.float32) * 0.02
        W3 = jax.random.normal(ks[4], (E, H, D), dtype=jnp.float32) * 0.02
        return {'x': x, 'Wr': Wr, 'br': br, 'W1': W1, 'W2': W2, 'W3': W3}
    _L0_ffn_all = _L0_ffn_setup()
    _L0_ffn_in = {k: v for k, v in _L0_ffn_all.items() if k in ('Wr', 'br', 'W1', 'W2', 'W3')}
    del _L0_ffn_all

    def _L1_attn_setup():
        import jax, jax.numpy as jnp
        import numpy as np
        BUCKET = 32
        HEADS = 8
        LN_EPS = 1e-05
        SELF_ATTN_VALUE = -50000.0

        def _layer_norm(x, g, b):
            m = jnp.mean(x, axis=-1, keepdims=True)
            v = jnp.mean((x - m) ** 2, axis=-1, keepdims=True)
            return (x - m) / jnp.sqrt(v + LN_EPS) * g + b

        def _lsh_attention(qk, v, rot):
            B, T, D = qk.shape
            n_buckets = T // BUCKET
            r = jnp.einsum('btf,fi->bti', qk, rot)
            r = jnp.concatenate([r, -r], axis=-1)
            buckets = jnp.argmax(r, axis=-1)
            t = jnp.arange(T)
            key = buckets * T + t
            sticker = jnp.argsort(key, axis=-1)
            undo = jnp.argsort(sticker, axis=-1)
            sqk = jnp.take_along_axis(qk, sticker[..., None], axis=1)
            sv = jnp.take_along_axis(v, sticker[..., None], axis=1)
            bq_t = sticker.reshape(B, n_buckets, BUCKET)
            bq = sqk.reshape(B, n_buckets, BUCKET, D)
            bv = sv.reshape(B, n_buckets, BUCKET, D)
            nrm = jnp.sqrt(jnp.sum(bq * bq, axis=-1, keepdims=True))
            bk = bq / jnp.maximum(nrm, 1e-12)

            def look_one_back(xx):
                return jnp.concatenate([xx, jnp.roll(xx, 1, axis=1)], axis=2)
            bk = look_one_back(bk)
            bvv = look_one_back(bv)
            bkv_t = look_one_back(bq_t)
            dots = jnp.einsum('bcie,bcje->bcij', bq, bk) * D ** (-0.5)
            self_mask = bq_t[:, :, :, None] == bkv_t[:, :, None, :]
            dots = jnp.where(self_mask, SELF_ATTN_VALUE, dots)
            attn = jax.nn.softmax(dots, axis=-1)
            bo = jnp.einsum('bcij,bcje->bcie', attn, bvv)
            so = bo.reshape(B, T, D)
            return jnp.take_along_axis(so, undo[..., None], axis=1)

        def _lsh_self_attention(h, w_qk, w_v, w_out, b_out, rot):
            b, t, d = h.shape
            dh = d // HEADS
            qk = (h @ w_qk).reshape(b, t, HEADS, dh).transpose(0, 2, 1, 3).reshape(b * HEADS, t, dh)
            vv = (h @ w_v).reshape(b, t, HEADS, dh).transpose(0, 2, 1, 3).reshape(b * HEADS, t, dh)
            o = _lsh_attention(qk, vv, rot)
            o = o.reshape(b, HEADS, t, dh).transpose(0, 2, 1, 3).reshape(b, t, d)
            return o @ w_out + b_out
        key = jax.random.key(seed)
        ks = jax.random.split(key, 8)
        B, T, D, F = (8, 1024, 128, 512)
        dh, nb = (D // HEADS, T // BUCKET)
        s = 0.02
        return {'x': jax.random.normal(ks[0], (B, T, D), jnp.float32), 'w_qk': jax.random.normal(ks[1], (D, D), jnp.float32) * s, 'w_v': jax.random.normal(ks[2], (D, D), jnp.float32) * s, 'w_out': jax.random.normal(ks[3], (D, D), jnp.float32) * s, 'b_out': jnp.zeros((D,), jnp.float32), 'ln1_g': jnp.ones((D,), jnp.float32), 'ln1_b': jnp.zeros((D,), jnp.float32), 'w_ff1': jax.random.normal(ks[4], (D, F), jnp.float32) * s, 'b_ff1': jnp.zeros((F,), jnp.float32), 'w_ff2': jax.random.normal(ks[5], (F, D), jnp.float32) * s, 'b_ff2': jnp.zeros((D,), jnp.float32), 'ln2_g': jnp.ones((D,), jnp.float32), 'ln2_b': jnp.zeros((D,), jnp.float32), 'rotations': jax.random.normal(ks[6], (dh, nb // 2), jnp.float32)}
    _L1_attn_all = _L1_attn_setup()
    _L1_attn_in = {k: v for k, v in _L1_attn_all.items() if k in ('w_qk', 'w_v', 'w_out', 'b_out', 'ln1_g', 'ln1_b', 'w_ff1', 'b_ff1', 'w_ff2', 'b_ff2', 'ln2_g', 'ln2_b', 'rotations')}
    del _L1_attn_all

    def _L1_ffn_setup():
        import jax, jax.numpy as jnp
        import numpy as np
        CAPACITY_FACTOR = 1.25
        TOP_K = 2

        def _moe(x, Wg, W1, b1, W2, b2):
            B, T, D = x.shape
            N = Wg.shape[1]
            K = TOP_K
            BT = B * T
            BTK = BT * K
            C = int(np.ceil(CAPACITY_FACTOR * BTK / N))
            x_flat = x.reshape(BT, D)
            probs = jax.nn.softmax(x_flat @ Wg, axis=-1)
            vals, idx = jax.lax.top_k(probs, K)
            vals = vals / jnp.clip(vals.sum(-1, keepdims=True), 1e-09)
            a = idx.reshape(BTK)
            oh = jax.nn.one_hot(a, N, dtype=jnp.int32)
            rank = jnp.cumsum(oh, axis=0) - oh
            pos = jnp.take_along_axis(rank, a[:, None], axis=1)[:, 0]
            keep = pos < C
            dest = jnp.where(keep, a * C + pos, N * C)
            token = jnp.arange(BTK) // K
            buf = jnp.zeros((N * C, D), x.dtype).at[dest].set(x_flat[token], mode='drop')
            buf = buf.reshape(N, C, D)
            h = jax.nn.relu(jnp.einsum('ncd,ndh->nch', buf, W1) + b1[:, None, :])
            o = (jnp.einsum('nch,nhd->ncd', h, W2) + b2[:, None, :]).reshape(N * C, D)
            gathered = o[jnp.minimum(dest, N * C - 1)]
            w = vals.reshape(BTK) * keep.astype(x.dtype)
            y_flat = jax.ops.segment_sum(gathered * w[:, None], token, num_segments=BT)
            contrib = jax.ops.segment_sum(w, token, num_segments=BT)
            y_flat = jnp.where(contrib[:, None] <= 1e-12, x_flat, y_flat)
            return y_flat.reshape(B, T, D)
        key = jax.random.key(seed)
        ks = jax.random.split(key, 4)
        B, T, D, H, N = (8, 2048, 128, 128, 32)
        x = jax.random.normal(ks[0], (B, T, D), jnp.float32)
        Wg = jax.random.normal(ks[1], (D, N), jnp.float32) * 0.02
        W1 = jax.random.normal(ks[2], (N, D, H), jnp.float32) * 0.02
        b1 = jnp.zeros((N, H), jnp.float32)
        W2 = jax.random.normal(ks[3], (N, H, D), jnp.float32) * 0.02
        b2 = jnp.zeros((N, D), jnp.float32)
        return {'x': x, 'Wg': Wg, 'W1': W1, 'b1': b1, 'W2': W2, 'b2': b2}
    _L1_ffn_all = _L1_ffn_setup()
    _L1_ffn_in = {k: v for k, v in _L1_ffn_all.items() if k in ('Wg', 'W1', 'b1', 'W2', 'b2')}
    del _L1_ffn_all

    def _L2_attn_setup():
        import jax, jax.numpy as jnp
        import numpy as np
        B, S, D = (8, 512, 128)
        HEADS = 8
        DEPTH = D // HEADS
        SCALE = DEPTH ** (-0.5)
        LN_EPS = 0.001
        key = jax.random.key(seed)
        ks = jax.random.split(key, 9)

        def w(k, shape, scale=0.02):
            return jax.random.normal(k, shape, dtype=jnp.float32) * scale
        return {'x': jax.random.normal(ks[0], (B, S, D), dtype=jnp.float32), 'Wq': w(ks[1], (D, D)), 'bq': jnp.zeros((D,), jnp.float32), 'Wk': w(ks[2], (D, D)), 'bk': jnp.zeros((D,), jnp.float32), 'Wv': w(ks[3], (D, D)), 'bv': jnp.zeros((D,), jnp.float32), 'Wo': w(ks[4], (D, D)), 'bo': jnp.zeros((D,), jnp.float32), 'gamma': jnp.ones((D,), jnp.float32), 'beta': jnp.zeros((D,), jnp.float32)}
    _L2_attn_all = _L2_attn_setup()
    _L2_attn_in = {k: v for k, v in _L2_attn_all.items() if k in ('Wq', 'bq', 'Wk', 'bk', 'Wv', 'bv', 'Wo', 'bo', 'gamma', 'beta')}
    del _L2_attn_all

    def _L2_ffn_setup():
        import jax, jax.numpy as jnp
        import numpy as np
        K_INPUT, K_PROCESS, K_OUTPUT = (64, 128, 64)

        def _gelu(x):
            return jax.nn.gelu(x, approximate=False)
        key = jax.random.key(seed)
        ks = jax.random.split(key, 6)
        d_model, n_in, n_proc, n_out, d_pv = (128, 512, 256, 512, 64)
        B, S = (2, 256)

        def xavier(k, shape):
            std = (2.0 / (shape[0] + shape[1])) ** 0.5
            return jax.random.normal(k, shape, dtype=jnp.float32) * std
        return {'x': jax.random.normal(ks[0], (B, S, d_model), dtype=jnp.float32), 'input_patterns': xavier(ks[1], (n_in, d_model)), 'process_input_weights': xavier(ks[2], (n_proc, n_in)), 'process_values': xavier(ks[3], (n_proc, d_pv)), 'output_input_weights': xavier(ks[4], (n_out, d_pv)), 'output_patterns': xavier(ks[5], (n_out, d_model))}
    _L2_ffn_all = _L2_ffn_setup()
    _L2_ffn_in = {k: v for k, v in _L2_ffn_all.items() if k in ('input_patterns', 'process_input_weights', 'process_values', 'output_input_weights', 'output_patterns')}
    del _L2_ffn_all

    def _L3_attn_setup():
        import jax, jax.numpy as jnp
        import numpy as np
        BN_EPS = 1e-05
        B, N, C, H, HID = (16, 256, 128, 8, 512)

        def _bn(x, g, b, m, v):
            return (x - m) * (g * jax.lax.rsqrt(v + BN_EPS)) + b

        def _stage(x, w, bias, g, be, m, v):
            return jax.nn.relu(_bn(x @ w.T + bias, g, be, m, v))
        key = jax.random.key(seed)
        ks = iter(jax.random.split(key, 64))
        d = {'x': jax.random.normal(next(ks), (B, N, C), dtype=jnp.float32)}

        def lin_bn(pref, out_f, in_f):
            d[pref + '_w'] = jax.random.normal(next(ks), (out_f, in_f), dtype=jnp.float32) * 0.02
            d[pref + '_b'] = jax.random.normal(next(ks), (out_f,), dtype=jnp.float32) * 0.02
            d[pref + '_g'] = 1.0 + 0.1 * jax.random.normal(next(ks), (out_f,), dtype=jnp.float32)
            d[pref + '_be'] = 0.1 * jax.random.normal(next(ks), (out_f,), dtype=jnp.float32)
            d[pref + '_m'] = 0.1 * jax.random.normal(next(ks), (out_f,), dtype=jnp.float32)
            d[pref + '_v'] = jax.random.uniform(next(ks), (out_f,), dtype=jnp.float32, minval=0.5, maxval=1.5)
        for p in ('q', 'k', 'v', 'p'):
            lin_bn(p, C, C)
        lin_bn('f1', HID, C)
        lin_bn('f2', C, HID)
        return d
    _L3_attn_all = _L3_attn_setup()
    _L3_attn_in = {k: v for k, v in _L3_attn_all.items() if k in ('q_w', 'q_b', 'q_g', 'q_be', 'q_m', 'q_v', 'k_w', 'k_b', 'k_g', 'k_be', 'k_m', 'k_v', 'v_w', 'v_b', 'v_g', 'v_be', 'v_m', 'v_v', 'p_w', 'p_b', 'p_g', 'p_be', 'p_m', 'p_v', 'f1_w', 'f1_b', 'f1_g', 'f1_be', 'f1_m', 'f1_v', 'f2_w', 'f2_b', 'f2_g', 'f2_be', 'f2_m', 'f2_v')}
    del _L3_attn_all

    def _L3_ffn_setup():
        import jax, jax.numpy as jnp
        import numpy as np
        E = 64
        K = 6
        NS = 2
        D = 128
        F = 128

        def _swiglu_ffn(x, wg, wu, wd):
            return jax.nn.silu(x @ wg) * (x @ wu) @ wd
        key = jax.random.key(seed)
        ks = jax.random.split(key, 8)
        s = 0.02
        return {'hidden_states': jax.random.normal(ks[0], (2, 256, D), dtype=jnp.float32), 'Wr': jax.random.normal(ks[1], (D, E), dtype=jnp.float32) * s, 'sWg': jax.random.normal(ks[2], (NS, D, F), dtype=jnp.float32) * s, 'sWu': jax.random.normal(ks[3], (NS, D, F), dtype=jnp.float32) * s, 'sWd': jax.random.normal(ks[4], (NS, F, D), dtype=jnp.float32) * s, 'Wg': jax.random.normal(ks[5], (E, D, F), dtype=jnp.float32) * s, 'Wu': jax.random.normal(ks[6], (E, D, F), dtype=jnp.float32) * s, 'Wd': jax.random.normal(ks[7], (E, F, D), dtype=jnp.float32) * s}
    _L3_ffn_all = _L3_ffn_setup()
    _L3_ffn_in = {k: v for k, v in _L3_ffn_all.items() if k in ('Wr', 'sWg', 'sWu', 'sWd', 'Wg', 'Wu', 'Wd')}
    del _L3_ffn_all
    return {'x': x, 'txt': txt, 'L0_tok_conv_w': _L0_tok_in['conv_w'], 'L0_tok_conv_b': _L0_tok_in['conv_b'], 'L0_attn_W_qkv': _L0_attn_in['W_qkv'], 'L0_attn_b_qkv': _L0_attn_in['b_qkv'], 'L0_ffn_Wr': _L0_ffn_in['Wr'], 'L0_ffn_br': _L0_ffn_in['br'], 'L0_ffn_W1': _L0_ffn_in['W1'], 'L0_ffn_W2': _L0_ffn_in['W2'], 'L0_ffn_W3': _L0_ffn_in['W3'], 'L1_attn_w_qk': _L1_attn_in['w_qk'], 'L1_attn_w_v': _L1_attn_in['w_v'], 'L1_attn_w_out': _L1_attn_in['w_out'], 'L1_attn_b_out': _L1_attn_in['b_out'], 'L1_attn_ln1_g': _L1_attn_in['ln1_g'], 'L1_attn_ln1_b': _L1_attn_in['ln1_b'], 'L1_attn_w_ff1': _L1_attn_in['w_ff1'], 'L1_attn_b_ff1': _L1_attn_in['b_ff1'], 'L1_attn_w_ff2': _L1_attn_in['w_ff2'], 'L1_attn_b_ff2': _L1_attn_in['b_ff2'], 'L1_attn_ln2_g': _L1_attn_in['ln2_g'], 'L1_attn_ln2_b': _L1_attn_in['ln2_b'], 'L1_attn_rotations': _L1_attn_in['rotations'], 'L1_ffn_Wg': _L1_ffn_in['Wg'], 'L1_ffn_W1': _L1_ffn_in['W1'], 'L1_ffn_b1': _L1_ffn_in['b1'], 'L1_ffn_W2': _L1_ffn_in['W2'], 'L1_ffn_b2': _L1_ffn_in['b2'], 'L2_attn_Wq': _L2_attn_in['Wq'], 'L2_attn_bq': _L2_attn_in['bq'], 'L2_attn_Wk': _L2_attn_in['Wk'], 'L2_attn_bk': _L2_attn_in['bk'], 'L2_attn_Wv': _L2_attn_in['Wv'], 'L2_attn_bv': _L2_attn_in['bv'], 'L2_attn_Wo': _L2_attn_in['Wo'], 'L2_attn_bo': _L2_attn_in['bo'], 'L2_attn_gamma': _L2_attn_in['gamma'], 'L2_attn_beta': _L2_attn_in['beta'], 'L2_ffn_input_patterns': _L2_ffn_in['input_patterns'], 'L2_ffn_process_input_weights': _L2_ffn_in['process_input_weights'], 'L2_ffn_process_values': _L2_ffn_in['process_values'], 'L2_ffn_output_input_weights': _L2_ffn_in['output_input_weights'], 'L2_ffn_output_patterns': _L2_ffn_in['output_patterns'], 'L3_attn_q_w': _L3_attn_in['q_w'], 'L3_attn_q_b': _L3_attn_in['q_b'], 'L3_attn_q_g': _L3_attn_in['q_g'], 'L3_attn_q_be': _L3_attn_in['q_be'], 'L3_attn_q_m': _L3_attn_in['q_m'], 'L3_attn_q_v': _L3_attn_in['q_v'], 'L3_attn_k_w': _L3_attn_in['k_w'], 'L3_attn_k_b': _L3_attn_in['k_b'], 'L3_attn_k_g': _L3_attn_in['k_g'], 'L3_attn_k_be': _L3_attn_in['k_be'], 'L3_attn_k_m': _L3_attn_in['k_m'], 'L3_attn_k_v': _L3_attn_in['k_v'], 'L3_attn_v_w': _L3_attn_in['v_w'], 'L3_attn_v_b': _L3_attn_in['v_b'], 'L3_attn_v_g': _L3_attn_in['v_g'], 'L3_attn_v_be': _L3_attn_in['v_be'], 'L3_attn_v_m': _L3_attn_in['v_m'], 'L3_attn_v_v': _L3_attn_in['v_v'], 'L3_attn_p_w': _L3_attn_in['p_w'], 'L3_attn_p_b': _L3_attn_in['p_b'], 'L3_attn_p_g': _L3_attn_in['p_g'], 'L3_attn_p_be': _L3_attn_in['p_be'], 'L3_attn_p_m': _L3_attn_in['p_m'], 'L3_attn_p_v': _L3_attn_in['p_v'], 'L3_attn_f1_w': _L3_attn_in['f1_w'], 'L3_attn_f1_b': _L3_attn_in['f1_b'], 'L3_attn_f1_g': _L3_attn_in['f1_g'], 'L3_attn_f1_be': _L3_attn_in['f1_be'], 'L3_attn_f1_m': _L3_attn_in['f1_m'], 'L3_attn_f1_v': _L3_attn_in['f1_v'], 'L3_attn_f2_w': _L3_attn_in['f2_w'], 'L3_attn_f2_b': _L3_attn_in['f2_b'], 'L3_attn_f2_g': _L3_attn_in['f2_g'], 'L3_attn_f2_be': _L3_attn_in['f2_be'], 'L3_attn_f2_m': _L3_attn_in['f2_m'], 'L3_attn_f2_v': _L3_attn_in['f2_v'], 'L3_ffn_Wr': _L3_ffn_in['Wr'], 'L3_ffn_sWg': _L3_ffn_in['sWg'], 'L3_ffn_sWu': _L3_ffn_in['sWu'], 'L3_ffn_sWd': _L3_ffn_in['sWd'], 'L3_ffn_Wg': _L3_ffn_in['Wg'], 'L3_ffn_Wu': _L3_ffn_in['Wu'], 'L3_ffn_Wd': _L3_ffn_in['Wd']}

def reference(x, txt, L0_tok_conv_w, L0_tok_conv_b, L0_attn_W_qkv, L0_attn_b_qkv, L0_ffn_Wr, L0_ffn_br, L0_ffn_W1, L0_ffn_W2, L0_ffn_W3, L1_attn_w_qk, L1_attn_w_v, L1_attn_w_out, L1_attn_b_out, L1_attn_ln1_g, L1_attn_ln1_b, L1_attn_w_ff1, L1_attn_b_ff1, L1_attn_w_ff2, L1_attn_b_ff2, L1_attn_ln2_g, L1_attn_ln2_b, L1_attn_rotations, L1_ffn_Wg, L1_ffn_W1, L1_ffn_b1, L1_ffn_W2, L1_ffn_b2, L2_attn_Wq, L2_attn_bq, L2_attn_Wk, L2_attn_bk, L2_attn_Wv, L2_attn_bv, L2_attn_Wo, L2_attn_bo, L2_attn_gamma, L2_attn_beta, L2_ffn_input_patterns, L2_ffn_process_input_weights, L2_ffn_process_values, L2_ffn_output_input_weights, L2_ffn_output_patterns, L3_attn_q_w, L3_attn_q_b, L3_attn_q_g, L3_attn_q_be, L3_attn_q_m, L3_attn_q_v, L3_attn_k_w, L3_attn_k_b, L3_attn_k_g, L3_attn_k_be, L3_attn_k_m, L3_attn_k_v, L3_attn_v_w, L3_attn_v_b, L3_attn_v_g, L3_attn_v_be, L3_attn_v_m, L3_attn_v_v, L3_attn_p_w, L3_attn_p_b, L3_attn_p_g, L3_attn_p_be, L3_attn_p_m, L3_attn_p_v, L3_attn_f1_w, L3_attn_f1_b, L3_attn_f1_g, L3_attn_f1_be, L3_attn_f1_m, L3_attn_f1_v, L3_attn_f2_w, L3_attn_f2_b, L3_attn_f2_g, L3_attn_f2_be, L3_attn_f2_m, L3_attn_f2_v, L3_ffn_Wr, L3_ffn_sWg, L3_ffn_sWu, L3_ffn_sWd, L3_ffn_Wg, L3_ffn_Wu, L3_ffn_Wd):
    import jax
    import jax.numpy as jnp

    def _L0_tok_ref(x, conv_w, conv_b):
        import jax, jax.numpy as jnp
        import numpy as np
        from jax import lax
        B, H, W, C = (32, 64, 64, 128)
        POOL = 8
        STRIDE = 8
        y = lax.conv_general_dilated(x, conv_w, window_strides=(1, 1), padding=[(1, 1), (1, 1)], dimension_numbers=('NHWC', 'HWIO', 'NHWC'), feature_group_count=C) + conv_b
        y = lax.reduce_window(y, jnp.float32(0.0), lax.add, (1, POOL, POOL, 1), (1, STRIDE, STRIDE, 1), 'VALID') / jnp.float32(POOL * POOL)
        b = y.shape[0]
        ct = y.reshape(b, -1, C)
        return ct

    def _L0_attn_ref(x, W_qkv, b_qkv):
        import jax, jax.numpy as jnp
        import numpy as np
        import math
        N_HEAD = 8
        B, L, C = x.shape
        H = N_HEAD
        ch = C // H
        qkv = x @ W_qkv + b_qkv
        q, k, v = jnp.split(qkv, 3, axis=-1)
        scale = 1.0 / math.sqrt(math.sqrt(ch))
        qh = (q * scale).reshape(B * H, L, ch)
        kh = (k * scale).reshape(B * H, L, ch)
        vh = v.reshape(B * H, L, ch)
        w = jnp.einsum('btc,bsc->bts', qh, kh)
        w = jax.nn.softmax(w.astype(jnp.float32), axis=-1).astype(qh.dtype)
        a = jnp.einsum('bts,bsc->btc', w, vh)
        return a.reshape(B, L, -1)

    def _L0_ffn_ref(x, Wr, br, W1, W2, W3):
        import jax, jax.numpy as jnp
        import numpy as np
        import math
        B, T, D, H, E, TOPK = (8, 1024, 128, 512, 8, 2)
        CAP_FRAC = 1.0

        def _expert_ffn(x, w1, w2, w3):
            h = jax.nn.gelu(x @ w2 * (x @ w1), approximate=False)
            return h @ w3
        b, t, d = x.shape
        Bt = b * t
        x_flat = x.reshape(Bt, d)
        logits = x_flat.astype(jnp.float32) @ Wr + br
        vals, idx = jax.lax.top_k(logits, TOPK)
        scores = jax.nn.softmax(vals, axis=-1).astype(x.dtype).reshape(b, t, TOPK)
        onehot = jax.nn.one_hot(idx, E, dtype=jnp.float32)
        pos = jnp.cumsum(jnp.cumsum(onehot, axis=0), axis=1).astype(jnp.int32)
        capacity = math.floor(Bt * CAP_FRAC)
        mask3 = onehot * (pos < capacity)
        token_mask = mask3.sum(-1).reshape(b, t, TOPK)
        assign = jnp.einsum('tke,e->tk', mask3, jnp.arange(E, dtype=jnp.float32)).astype(jnp.int32)
        i_max = assign.reshape(b, t, TOPK).max(axis=-1)
        y = jnp.zeros_like(x)
        for i in range(E):
            yi = _expert_ffn(x, W1[i], W2[i], W3[i])
            y = jnp.where((i_max == i)[..., None], yi, y)
        expert_outputs = jnp.where(token_mask[..., None] > 0, y[:, :, None, :], x[:, :, None, :])
        return jnp.einsum('btkD,btk->btD', expert_outputs, scores)

    def _L1_attn_ref(x, w_qk, w_v, w_out, b_out, ln1_g, ln1_b, w_ff1, b_ff1, w_ff2, b_ff2, ln2_g, ln2_b, rotations):
        import jax, jax.numpy as jnp
        import numpy as np
        BUCKET = 32
        HEADS = 8
        LN_EPS = 1e-05
        SELF_ATTN_VALUE = -50000.0

        def _layer_norm(x, g, b):
            m = jnp.mean(x, axis=-1, keepdims=True)
            v = jnp.mean((x - m) ** 2, axis=-1, keepdims=True)
            return (x - m) / jnp.sqrt(v + LN_EPS) * g + b

        def _lsh_attention(qk, v, rot):
            B, T, D = qk.shape
            n_buckets = T // BUCKET
            r = jnp.einsum('btf,fi->bti', qk, rot)
            r = jnp.concatenate([r, -r], axis=-1)
            buckets = jnp.argmax(r, axis=-1)
            t = jnp.arange(T)
            key = buckets * T + t
            sticker = jnp.argsort(key, axis=-1)
            undo = jnp.argsort(sticker, axis=-1)
            sqk = jnp.take_along_axis(qk, sticker[..., None], axis=1)
            sv = jnp.take_along_axis(v, sticker[..., None], axis=1)
            bq_t = sticker.reshape(B, n_buckets, BUCKET)
            bq = sqk.reshape(B, n_buckets, BUCKET, D)
            bv = sv.reshape(B, n_buckets, BUCKET, D)
            nrm = jnp.sqrt(jnp.sum(bq * bq, axis=-1, keepdims=True))
            bk = bq / jnp.maximum(nrm, 1e-12)

            def look_one_back(xx):
                return jnp.concatenate([xx, jnp.roll(xx, 1, axis=1)], axis=2)
            bk = look_one_back(bk)
            bvv = look_one_back(bv)
            bkv_t = look_one_back(bq_t)
            dots = jnp.einsum('bcie,bcje->bcij', bq, bk) * D ** (-0.5)
            self_mask = bq_t[:, :, :, None] == bkv_t[:, :, None, :]
            dots = jnp.where(self_mask, SELF_ATTN_VALUE, dots)
            attn = jax.nn.softmax(dots, axis=-1)
            bo = jnp.einsum('bcij,bcje->bcie', attn, bvv)
            so = bo.reshape(B, T, D)
            return jnp.take_along_axis(so, undo[..., None], axis=1)

        def _lsh_self_attention(h, w_qk, w_v, w_out, b_out, rot):
            b, t, d = h.shape
            dh = d // HEADS
            qk = (h @ w_qk).reshape(b, t, HEADS, dh).transpose(0, 2, 1, 3).reshape(b * HEADS, t, dh)
            vv = (h @ w_v).reshape(b, t, HEADS, dh).transpose(0, 2, 1, 3).reshape(b * HEADS, t, dh)
            o = _lsh_attention(qk, vv, rot)
            o = o.reshape(b, HEADS, t, dh).transpose(0, 2, 1, 3).reshape(b, t, d)
            return o @ w_out + b_out
        h1 = _layer_norm(x, ln1_g, ln1_b)
        y1 = x + _lsh_self_attention(h1, w_qk, w_v, w_out, b_out, rotations)
        h2 = _layer_norm(y1, ln2_g, ln2_b)
        ffn = jax.nn.relu(h2 @ w_ff1 + b_ff1) @ w_ff2 + b_ff2
        y2 = x + ffn
        return 0.5 * (y1 + y2)

    def _L1_ffn_ref(x, Wg, W1, b1, W2, b2):
        import jax, jax.numpy as jnp
        import numpy as np
        CAPACITY_FACTOR = 1.25
        TOP_K = 2

        def _moe(x, Wg, W1, b1, W2, b2):
            B, T, D = x.shape
            N = Wg.shape[1]
            K = TOP_K
            BT = B * T
            BTK = BT * K
            C = int(np.ceil(CAPACITY_FACTOR * BTK / N))
            x_flat = x.reshape(BT, D)
            probs = jax.nn.softmax(x_flat @ Wg, axis=-1)
            vals, idx = jax.lax.top_k(probs, K)
            vals = vals / jnp.clip(vals.sum(-1, keepdims=True), 1e-09)
            a = idx.reshape(BTK)
            oh = jax.nn.one_hot(a, N, dtype=jnp.int32)
            rank = jnp.cumsum(oh, axis=0) - oh
            pos = jnp.take_along_axis(rank, a[:, None], axis=1)[:, 0]
            keep = pos < C
            dest = jnp.where(keep, a * C + pos, N * C)
            token = jnp.arange(BTK) // K
            buf = jnp.zeros((N * C, D), x.dtype).at[dest].set(x_flat[token], mode='drop')
            buf = buf.reshape(N, C, D)
            h = jax.nn.relu(jnp.einsum('ncd,ndh->nch', buf, W1) + b1[:, None, :])
            o = (jnp.einsum('nch,nhd->ncd', h, W2) + b2[:, None, :]).reshape(N * C, D)
            gathered = o[jnp.minimum(dest, N * C - 1)]
            w = vals.reshape(BTK) * keep.astype(x.dtype)
            y_flat = jax.ops.segment_sum(gathered * w[:, None], token, num_segments=BT)
            contrib = jax.ops.segment_sum(w, token, num_segments=BT)
            y_flat = jnp.where(contrib[:, None] <= 1e-12, x_flat, y_flat)
            return y_flat.reshape(B, T, D)
        return _moe(x, Wg, W1, b1, W2, b2)

    def _L2_attn_ref(x, Wq, bq, Wk, bk, Wv, bv, Wo, bo, gamma, beta):
        import jax, jax.numpy as jnp
        import numpy as np
        B, S, D = (8, 512, 128)
        HEADS = 8
        DEPTH = D // HEADS
        SCALE = DEPTH ** (-0.5)
        LN_EPS = 0.001
        q = jax.nn.relu(x @ Wq + bq) * SCALE
        k = jax.nn.relu(x @ Wk + bk)
        v = jax.nn.relu(x @ Wv + bv)
        scores = jnp.einsum('bsd,btd->bst', q, k)
        attn = jax.nn.softmax(scores, axis=-1)
        ctx = jnp.einsum('bst,btd->bsd', attn, v)
        out = jax.nn.relu(ctx @ Wo + bo)
        mu = jnp.mean(out, axis=-1, keepdims=True)
        var = jnp.var(out, axis=-1, keepdims=True)
        return (out - mu) * jax.lax.rsqrt(var + LN_EPS) * gamma + beta

    def _L2_ffn_ref(x, input_patterns, process_input_weights, process_values, output_input_weights, output_patterns):
        import jax, jax.numpy as jnp
        import numpy as np
        K_INPUT, K_PROCESS, K_OUTPUT = (64, 128, 64)

        def _gelu(x):
            return jax.nn.gelu(x, approximate=False)
        B, S, d_model = x.shape
        n_in = input_patterns.shape[0]
        input_acts = _gelu(jnp.einsum('bsd,nd->bsn', x, input_patterns))
        top_in_acts, top_in_idx = jax.lax.top_k(input_acts, K_INPUT)
        bi = jnp.arange(B)[:, None, None]
        si = jnp.arange(S)[None, :, None]
        input_repr = jnp.zeros((B, S, n_in), dtype=x.dtype).at[bi, si, top_in_idx].set(top_in_acts)
        process_acts = _gelu(jnp.einsum('bsn,pn->bsp', input_repr, process_input_weights))
        top_p_acts, top_p_idx = jax.lax.top_k(process_acts, K_PROCESS)
        sel_values = process_values[top_p_idx]
        p_weights = jax.nn.softmax(top_p_acts, axis=-1)
        agg_value = jnp.einsum('bsk,bskd->bsd', p_weights, sel_values)
        output_acts = _gelu(jnp.einsum('bsd,od->bso', agg_value, output_input_weights))
        top_o_acts, top_o_idx = jax.lax.top_k(output_acts, K_OUTPUT)
        sel_patterns = output_patterns[top_o_idx]
        out = jnp.einsum('bsk,bskm->bsm', top_o_acts, sel_patterns)
        return out

    def _L3_attn_ref(x, q_w, q_b, q_g, q_be, q_m, q_v, k_w, k_b, k_g, k_be, k_m, k_v, v_w, v_b, v_g, v_be, v_m, v_v, p_w, p_b, p_g, p_be, p_m, p_v, f1_w, f1_b, f1_g, f1_be, f1_m, f1_v, f2_w, f2_b, f2_g, f2_be, f2_m, f2_v):
        import jax, jax.numpy as jnp
        import numpy as np
        BN_EPS = 1e-05
        B, N, C, H, HID = (16, 256, 128, 8, 512)

        def _bn(x, g, b, m, v):
            return (x - m) * (g * jax.lax.rsqrt(v + BN_EPS)) + b

        def _stage(x, w, bias, g, be, m, v):
            return jax.nn.relu(_bn(x @ w.T + bias, g, be, m, v))
        b, n, c = x.shape
        hd = c // H

        def heads(t):
            return t.reshape(b, n, H, hd).transpose(0, 2, 1, 3)
        q = heads(_stage(x, q_w, q_b, q_g, q_be, q_m, q_v))
        k = heads(_stage(x, k_w, k_b, k_g, k_be, k_m, k_v))
        v = heads(_stage(x, v_w, v_b, v_g, v_be, v_m, v_v))
        attn = jnp.einsum('bhqd,bhkd->bhqk', q, k) * 0.125
        o = jnp.einsum('bhqk,bhkd->bhqd', attn, v)
        o = o.transpose(0, 2, 1, 3).reshape(b, n, c)
        o = jax.nn.relu(o)
        x1 = x + _stage(o, p_w, p_b, p_g, p_be, p_m, p_v)
        h = _stage(x1, f1_w, f1_b, f1_g, f1_be, f1_m, f1_v)
        y = _stage(h, f2_w, f2_b, f2_g, f2_be, f2_m, f2_v)
        return x1 + y

    def _L3_ffn_ref(hidden_states, Wr, sWg, sWu, sWd, Wg, Wu, Wd):
        import jax, jax.numpy as jnp
        import numpy as np
        E = 64
        K = 6
        NS = 2
        D = 128
        F = 128

        def _swiglu_ffn(x, wg, wu, wd):
            return jax.nn.silu(x @ wg) * (x @ wu) @ wd
        B, S, d = hidden_states.shape
        x = hidden_states.reshape(-1, d)
        N = x.shape[0]
        shared = jnp.zeros_like(x)
        for e in range(NS):
            shared = shared + _swiglu_ffn(x, sWg[e], sWu[e], sWd[e])
        logits = x @ Wr
        probs = jax.nn.softmax(logits, axis=-1)
        top_w, top_i = jax.lax.top_k(probs, K)
        top_w = top_w / jnp.sum(top_w, axis=-1, keepdims=True)
        gate = jnp.zeros((N, E), dtype=x.dtype).at[jnp.arange(N)[:, None], top_i].set(top_w)
        routed = jnp.zeros_like(x)
        for e in range(E):
            routed = routed + _swiglu_ffn(x, Wg[e], Wu[e], Wd[e]) * gate[:, e:e + 1]
        out = (shared + routed + x).reshape(B, S, d)
        return out
    h = _L0_tok_ref(x, L0_tok_conv_w, L0_tok_conv_b)
    h = jnp.concatenate([h, txt], axis=1)
    h = h + _L0_attn_ref(_layernorm(h, axis=-1), L0_attn_W_qkv, L0_attn_b_qkv)
    h = h + _L0_ffn_ref(_layernorm(h, axis=-1), L0_ffn_Wr, L0_ffn_br, L0_ffn_W1, L0_ffn_W2, L0_ffn_W3)
    h = h + _L1_attn_ref(_layernorm(h, axis=-1), L1_attn_w_qk, L1_attn_w_v, L1_attn_w_out, L1_attn_b_out, L1_attn_ln1_g, L1_attn_ln1_b, L1_attn_w_ff1, L1_attn_b_ff1, L1_attn_w_ff2, L1_attn_b_ff2, L1_attn_ln2_g, L1_attn_ln2_b, L1_attn_rotations)
    h = h + _L1_ffn_ref(_layernorm(h, axis=-1), L1_ffn_Wg, L1_ffn_W1, L1_ffn_b1, L1_ffn_W2, L1_ffn_b2)
    h = h + _L2_attn_ref(_layernorm(h, axis=-1), L2_attn_Wq, L2_attn_bq, L2_attn_Wk, L2_attn_bk, L2_attn_Wv, L2_attn_bv, L2_attn_Wo, L2_attn_bo, L2_attn_gamma, L2_attn_beta)
    h = h + _L2_ffn_ref(_layernorm(h, axis=-1), L2_ffn_input_patterns, L2_ffn_process_input_weights, L2_ffn_process_values, L2_ffn_output_input_weights, L2_ffn_output_patterns)
    h = h + _L3_attn_ref(_layernorm(h, axis=-1), L3_attn_q_w, L3_attn_q_b, L3_attn_q_g, L3_attn_q_be, L3_attn_q_m, L3_attn_q_v, L3_attn_k_w, L3_attn_k_b, L3_attn_k_g, L3_attn_k_be, L3_attn_k_m, L3_attn_k_v, L3_attn_v_w, L3_attn_v_b, L3_attn_v_g, L3_attn_v_be, L3_attn_v_m, L3_attn_v_v, L3_attn_p_w, L3_attn_p_b, L3_attn_p_g, L3_attn_p_be, L3_attn_p_m, L3_attn_p_v, L3_attn_f1_w, L3_attn_f1_b, L3_attn_f1_g, L3_attn_f1_be, L3_attn_f1_m, L3_attn_f1_v, L3_attn_f2_w, L3_attn_f2_b, L3_attn_f2_g, L3_attn_f2_be, L3_attn_f2_m, L3_attn_f2_v)
    h = h + _L3_ffn_ref(_layernorm(h, axis=-1), L3_ffn_Wr, L3_ffn_sWg, L3_ffn_sWu, L3_ffn_sWd, L3_ffn_Wg, L3_ffn_Wu, L3_ffn_Wd)
    return h

_drawn_inputs = setup_inputs


def setup_inputs(seed=0):
    import zlib

    import numpy as np

    out = dict(_drawn_inputs(seed))
    spreads = {'L0_attn_b_qkv': (0.0, 0.1),
     'L0_ffn_br': (0.0, 0.1),
     'L1_attn_b_out': (0.0, 0.1),
     'L1_attn_ln1_g': (1.0, 0.2),
     'L1_attn_ln1_b': (0.0, 0.324),
     'L1_attn_b_ff1': (0.0, 0.1),
     'L1_attn_b_ff2': (0.0, 0.1),
     'L1_attn_ln2_g': (1.0, 0.2),
     'L1_attn_ln2_b': (0.0, 0.1),
     'L1_ffn_b1': (0.0, 0.8),
     'L1_ffn_b2': (0.0, 0.276),
     'L2_attn_bq': (0.0, 0.8),
     'L2_attn_bk': (0.0, 0.8),
     'L2_attn_bv': (0.0, 0.1),
     'L2_attn_bo': (0.0, 0.1),
     'L2_attn_gamma': (1.0, 0.2),
     'L2_attn_beta': (0.0, 0.1)}
    factors = {'L1_attn_rotations': 2.872,
     'L1_ffn_W1': 6.322,
     'L1_ffn_W2': 5.086,
     'L2_attn_Wq': 8.0,
     'L2_attn_Wk': 8.0,
     'L2_ffn_input_patterns': 8.0,
     'L2_ffn_process_input_weights': 8.0,
     'L2_ffn_process_values': 8.0,
     'L2_ffn_output_input_weights': 8.0,
     'L2_ffn_output_patterns': 8.0,
     'L3_attn_q_b': 8.0,
     'L3_attn_q_g': 8.0,
     'L3_attn_q_be': 8.0,
     'L3_attn_q_m': 5.639,
     'L3_attn_q_v': 8.0,
     'L3_attn_k_w': 3.207,
     'L3_attn_k_b': 8.0,
     'L3_attn_k_g': 8.0,
     'L3_attn_k_be': 5.079,
     'L3_attn_k_m': 4.735,
     'L3_attn_k_v': 8.0,
     'L3_attn_v_b': 8.0,
     'L3_attn_v_g': 8.0,
     'L3_attn_v_be': 3.584,
     'L3_attn_v_m': 2.923,
     'L3_attn_v_v': 8.0,
     'L3_attn_p_b': 64.0,
     'L3_attn_p_g': 8.0,
     'L3_attn_p_be': 64.272,
     'L3_attn_p_v': 8.0,
     'L3_attn_f1_w': 3.172,
     'L3_attn_f1_b': 64.0,
     'L3_attn_f1_g': 8.0,
     'L3_attn_f1_be': 57.0,
     'L3_attn_f1_m': 57.784,
     'L3_attn_f1_v': 8.0,
     'L3_attn_f2_b': 64.0,
     'L3_attn_f2_g': 8.0,
     'L3_attn_f2_be': 90.798,
     'L3_attn_f2_v': 8.0,
     'L3_ffn_Wr': 64.0,
     'L3_ffn_sWg': 32.989,
     'L3_ffn_sWu': 30.079,
     'L3_ffn_sWd': 24.679,
     'L3_ffn_Wg': 64.0,
     'L3_ffn_Wu': 64.0,
     'L3_ffn_Wd': 64.0,
     'L3_attn_p_m': 8.0,
     'L3_attn_f2_m': 30.362}
    for name, (base, spread) in spreads.items():
        noise = np.random.default_rng([zlib.crc32(name.encode()), seed]).standard_normal(out[name].shape)
        drawn = base * np.exp(spread * noise) if base else spread * noise
        out[name] = jnp.asarray(drawn.astype(out[name].dtype))
    for name, factor in factors.items():
        out[name] = (out[name] * factor).astype(out[name].dtype)
    return out
```

```python
from contextlib import ExitStack

import numpy as np

import concourse.bass as bass
from concourse import mybir

ALU = mybir.AluOpType
ACT = mybir.ActivationFunctionType
AX = mybir.AxisListType.X
F32 = mybir.dt.float32
BF16 = mybir.dt.bfloat16

P = 128
C = 128
B = 16
GRID = 8
IMG_TOKENS = GRID * GRID
TXT_TOKENS = 128
T = IMG_TOKENS + TXT_TOKENS
N = B * T
HALF = T // 2
HEADS = 8
HD = C // HEADS
TILES = N // P
CH = 512
CHUNKS = N // CH
BIG = 2.0 ** 100
PAD = GRID + 2
SLOTS = 2


def shape_constants():
    parts, at = {}, 0
    out = []

    def put(name, a):
        nonlocal at
        full = np.zeros((P, a.shape[1]), np.float32)
        full[:a.shape[0]] = a
        out.append(full)
        parts[name] = (at, at + a.shape[1])
        at += a.shape[1]

    eye = np.eye(P, dtype=np.float32)
    put("ident", eye)
    put("centre", eye - np.float32(1.0 / C))
    put("mean", np.full((P, P), 1.0 / C, np.float32))
    put("ones", np.ones((P, P), np.float32))
    rows = np.zeros((P, 3, PAD, 2), np.float32)
    for p in range(P):
        row, side = p // 2, p % 2
        kind = {0: 1, 7: 2}.get(row % 8, 0)
        rows[p, kind, row // 8 + 1, side] = 1.0
    put("rows", rows.reshape(P, -1))
    block = np.kron(np.eye(HEADS, dtype=np.float32), np.ones((HD, HD), np.float32))
    put("head_block", block)
    put("before", np.triu(np.ones((P, P), np.float32), 1))
    put("neg_diag", (-BIG * eye[:, :HALF]).astype(np.float32))
    put("rev32", np.tile(32.0 - np.arange(32, dtype=np.float32), (P, 1)))
    put("rev8", np.tile(8.0 - np.arange(8, dtype=np.float32), (P, 1)))
    put("iota8", np.tile(np.arange(8, dtype=np.float32), (P, 1)))
    put("chunk_edge", np.tile(32.0 * np.arange(8, dtype=np.float32), (P, 1)))
    last = np.zeros((P, 1), np.float32)
    last[P - 1] = 1.0
    put("last_row", last)
    spread = np.zeros((2 * HEADS, 2, HEADS, HD), np.float32)
    for h in range(HEADS):
        for s in range(2):
            spread[HEADS * s + h, s, h] = 1.0
    put("spread", spread.reshape(2 * HEADS, -1))
    return np.concatenate(out, 1), parts


CONSTS, WHERE = shape_constants()

VECTORS = [
    ("L0_tok_conv_b", 1), ("L0_attn_b_qkv", 3),
    ("L1_attn_b_out", 1), ("L1_attn_ln1_g", 1), ("L1_attn_ln1_b", 1), ("L1_attn_b_ff1", 4), ("L1_attn_b_ff2", 1),
    ("L1_attn_ln2_g", 1), ("L1_attn_ln2_b", 1),
    ("L2_attn_bq", 1), ("L2_attn_bk", 1), ("L2_attn_bv", 1), ("L2_attn_bo", 1), ("L2_attn_gamma", 1),
    ("L2_attn_beta", 1),
]
for _s in ("q", "k", "v", "p", "f1", "f2"):
    for _v in ("b", "g", "be", "m", "v"):
        VECTORS.append((f"L3_attn_{_s}_{_v}", 4 if _s == "f1" else 1))
VECTORS.append(("L0_tok_conv_w", 9))
COLUMN, _at = {}, 0
for _n, _k in VECTORS:
    COLUMN[_n] = _at
    _at += _k
NCOL = _at

WEIGHTS = [
    ("L0_attn_W_qkv", 3 * C), ("L1_attn_w_qk", C), ("L1_attn_w_v", C), ("L1_attn_w_out", C), ("L1_attn_w_ff1", 4 * C),
    ("L2_attn_Wq", C), ("L2_attn_Wk", C), ("L2_attn_Wv", C), ("L2_attn_Wo", C), ("L1_ffn_Wg", 32), ("L0_ffn_Wr", 8),
    ("L3_ffn_Wr", 64),
]


class Chain:

    def __init__(self, eng, sem):
        self.eng, self.sem, self.base, self.n = eng, sem, 0, 0

    def __call__(self, ins):
        ins.then_inc(self.sem, 1)
        self.n += 1
        self.eng.wait_ge(self.sem, self.base + self.n)

    def turn(self, i, per, before=0):
        self.base, self.n = i * per + before, 0
        self.per = per

    def restart(self):
        self.eng.sem_clear(self.sem)
        self.n = 0

    def close(self):
        assert self.n == self.per, (self.n, self.per)

    def after(self, total):
        self.base, self.n = total, 0


class Resident:

    def __init__(self, nc, ctx, ins, out):
        self.ins, self.out = ins, out

        def sb(name, shape, dt=F32):
            return ctx.enter_context(nc.sbuf_tensor(name, shape, dt))

        self.hT = sb("hT", [P, N])
        self.xT = sb("xT", [P, N])
        self.cst = sb("cst", [P, CONSTS.shape[1]])
        self.bf = {}
        for name in ("ident", "ones", "before", "neg_diag"):
            a, b = WHERE[name]
            self.bf[name] = sb(f"bf_{name}", [P, b - a], BF16)
        self.columns = sb("columns", [P, NCOL])
        self.w = {name: sb(name, [P, n]) for name, n in WEIGHTS}
        self.w["L1_attn_w_ff2"] = sb("L1_attn_w_ff2", [P, 4, C])
        self.tap = sb("tap", [P, 25])
        self.bn = sb("bn", [P, 2, 9])
        self.rot = sb("rot", [P, P])
        self.wt = {name: sb(name, [P, n]) for name, n in (
            ("qT", C), ("kT", C), ("vT", C), ("pT", C), ("f1T", 4 * C), ("f2T", 4 * C))}

    def c(self, name, rows=P):
        a, b = WHERE[name]
        return self.cst[0:rows, a:b]

    def col(self, name, k=0):
        a = COLUMN[name] + k
        return self.columns[:, a:a + 1]


def allocators(nc, ctx, tag):
    held = []

    def over():
        if held:
            nc.clear_and_free_semaphores(held)
            nc.all_engine_barrier()

    ctx.callback(over)

    def sb(name, shape, dt=F32):
        return ctx.enter_context(nc.sbuf_tensor(f"{tag}_{name}", shape, dt))

    def ps(name, shape, dt=F32):
        return ctx.enter_context(nc.psum_tensor(f"{tag}_{name}", shape, dt))

    def sem(name):
        held.append(nc.alloc_semaphore(name=f"{tag}_{name}"))
        return held[-1]

    return sb, ps, sem


def set_up(nc, R):
    ins = R.ins
    with ExitStack() as ctx:
        sb, ps, sem = allocators(nc, ctx, "setup")
        rows = sb("rows", [NCOL, C])
        raw = {s: sb(f"raw_{s}", [P, C]) for s in "qkvp"}
        raw_f1 = sb("raw_f1", [P, 4, C])
        raw_f2 = sb("raw_f2", [P, 4 * C])
        edge = sb("edge", [P, 5, 3])
        root = sb("root", [P, 9])
        pv = ps("pv", [P, 512])
        pt = ps("pt", [P, 4, 512])
        loaded, rot_zeroed, transposed, columns_ready, turned = (
            sem(n) for n in ("loaded", "rot_zeroed", "transposed", "columns_ready", "turned"))
        rot_loaded, rooted, order = sem("rot_loaded"), sem("rooted"), sem("order")
        block = ctx.enter_context(nc.Block())
        n_loads = 1 + len(VECTORS) + len(WEIGHTS) + 1 + 6
        bn_at = {"q": (0, 1), "k": (1, 1), "v": (2, 1), "p": (3, 1), "f1": (4, 4), "f2": (8, 1)}

        @block.sync
        def _(sp):
            sp.dma_start(R.cst[:, :], ins["consts"]).then_inc(loaded, 16)
            for name, n in WEIGHTS:
                sp.dma_start(R.w[name][:, :], ins[name]).then_inc(loaded, 16)
            sp.dma_start(R.w["L1_attn_w_ff2"][:, :, :],
                         ins["L1_attn_w_ff2"].rearrange("(k p) n -> p k n", p=P)).then_inc(loaded, 16)
            for s in "qkvp":
                sp.dma_start(raw[s][:, :], ins[f"L3_attn_{s}_w"]).then_inc(loaded, 16)
            sp.dma_start(raw_f1[:, :, :], ins["L3_attn_f1_w"].rearrange("(k p) n -> p k n", p=P)).then_inc(loaded, 16)
            sp.dma_start(raw_f2[:, :], ins["L3_attn_f2_w"]).then_inc(loaded, 16)

        @block.scalar
        def _(act):
            for name, n in VECTORS:
                a = COLUMN[name]
                src = ins[name]
                src = src.rearrange("a b o c -> (a b o) c") if name == "L0_tok_conv_w" else \
                    src.rearrange("(k p) -> k p", p=C)
                act.dma_start(rows[a:a + n, :], src).then_inc(loaded, 16)
            act.wait_ge(rot_zeroed, 1)
            for h in range(HEADS):
                act.dma_start(R.rot[HD * h:HD * h + HD, HD * h:HD * h + HD],
                              ins["L1_attn_rotations"]).then_inc(rot_loaded, 16)
            act.wait_ge(rot_loaded, 16 * HEADS)
            act.wait_ge(columns_ready, 2)
            for s, (a, n) in bn_at.items():
                last = act.activation(root[:, a:a + n], root[:, a:a + n], ACT.Sqrt)
            last.then_inc(rooted, 1)

        @block.tensor
        def _(pe):
            pe.wait_ge(loaded, 16 * n_loads)
            pe.transpose(pv[0:C, 0:NCOL], rows[:, :], R.c("ident")[0:NCOL, 0:NCOL]).then_inc(transposed, 1)
            for n, s in enumerate("qkvp"):
                last = pe.transpose(pt[:, 0, C * n:C * n + C], raw[s][:, :], R.c("ident"))
            last.then_inc(transposed, 1)
            for k in range(4):
                last = pe.transpose(pt[:, 1, C * k:C * k + C], raw_f1[:, k, :], R.c("ident"))
            last.then_inc(transposed, 1)
            for k in range(4):
                last = pe.transpose(pt[:, 2, C * k:C * k + C], raw_f2[:, C * k:C * k + C], R.c("ident"))
            last.then_inc(transposed, 1)

        @block.vector
        def _(dve):
            chain = Chain(dve, order)
            dve.memset(R.rot[:, :], 0.0).then_inc(rot_zeroed, 1)
            dve.wait_ge(loaded, 16 * n_loads)
            for name, t in R.bf.items():
                dve.tensor_copy(t[:, :], R.c(name))
            dve.wait_ge(transposed, 1)
            dve.tensor_copy(R.columns[:, :], pv[:, 0:NCOL]).then_inc(columns_ready, 1)
            dve.wait_ge(columns_ready, 1)
            for s, (a, n) in bn_at.items():
                v = COLUMN[f"L3_attn_{s}_v"]
                last = dve.tensor_scalar(root[:, a:a + n], R.columns[:, v:v + n], 1e-5, None, ALU.add)
            last.then_inc(columns_ready, 1)
            for k, n in enumerate("qkvp"):
                dve.wait_ge(transposed, 2)
                dve.tensor_copy(R.wt[f"{n}T"][:, :], pt[:, 0, C * k:C * k + C])
            dve.wait_ge(transposed, 3)
            dve.tensor_copy(R.wt["f1T"][:, :], pt[:, 1, :])
            dve.wait_ge(transposed, 4)
            dve.tensor_copy(R.wt["f2T"][:, :], pt[:, 2, :])
            w0 = COLUMN["L0_tok_conv_w"]
            tap = [R.columns[:, w0 + 3 * d:w0 + 3 * d + 3] for d in range(3)]
            chain(dve.tensor_tensor(edge[:, 1, :], tap[0], tap[1], ALU.add))
            dve.tensor_tensor(edge[:, 2, :], tap[1], tap[2], ALU.add)
            dve.tensor_copy(edge[:, 3, :], tap[0])
            dve.tensor_copy(edge[:, 4, :], tap[2])
            chain(dve.tensor_tensor(edge[:, 0, :], edge[:, 1, :], tap[2], ALU.add))
            t5 = R.tap[:, :].rearrange("p (r c) -> p r c", c=5)
            chain(dve.tensor_tensor(t5[:, :, 1], edge[:, :, 0], edge[:, :, 1], ALU.add))
            dve.tensor_tensor(t5[:, :, 2], edge[:, :, 1], edge[:, :, 2], ALU.add)
            dve.tensor_copy(t5[:, :, 3], edge[:, :, 0])
            dve.tensor_copy(t5[:, :, 4], edge[:, :, 2])
            chain(dve.tensor_tensor(t5[:, :, 0], t5[:, :, 1], edge[:, :, 2], ALU.add))
            dve.wait_ge(rooted, 1)
            chain(dve.reciprocal(root[:, :], root[:, :]))
            for s, (a, n) in bn_at.items():
                b, g, be, m = (COLUMN[f"L3_attn_{s}_{v}"] for v in ("b", "g", "be", "m"))
                dve.tensor_tensor(R.bn[:, 1, a:a + n], R.columns[:, b:b + n], R.columns[:, m:m + n], ALU.subtract)
                last = dve.tensor_tensor(R.bn[:, 0, a:a + n], root[:, a:a + n], R.columns[:, g:g + n], ALU.mult)
            chain(last)
            chain(dve.tensor_tensor(R.bn[:, 1, :], R.bn[:, 1, :], R.bn[:, 0, :], ALU.mult))
            for s, (a, n) in bn_at.items():
                be = COLUMN[f"L3_attn_{s}_be"]
                dve.tensor_tensor(R.bn[:, 1, a:a + n], R.bn[:, 1, a:a + n], R.columns[:, be:be + n], ALU.add)


def layer_norm(nc, R, tag, src, dst, eps=1e-5, gain=None, bias=None, residual=False):
    with ExitStack() as ctx:
        sb, ps, sem = allocators(nc, ctx, tag)
        squares, std, rstd = sb("squares", [P, 2, CH]), sb("std", [P, 2, CH]), sb("rstd", [P, 2, CH])
        centred, var = ps("centred", [P, 2, CH]), ps("var", [P, 2, CH])
        centred_ready, squared, var_ready, std_ready, done, order = (
            sem(n) for n in ("centred_ready", "squared", "var_ready", "std_ready", "done", "order"))
        block = ctx.enter_context(nc.Block())

        @block.tensor
        def _(pe):
            with pe.Fori(0, CHUNKS // 2) as i:
                for u in range(2):
                    pe.wait_ge(done, 2 * i + u + 1)
                    pe.matmul(centred[:, u, :], R.c("centre"), src[:, bass.ds(i * (2 * CH) + u * CH, CH)],
                              start=True, stop=True).then_inc(centred_ready, 1)
                for u in range(2):
                    pe.wait_ge(squared, 2 * i + u + 1)
                    pe.matmul(var[:, u, :], R.c("mean"), squares[:, u, :], start=True, stop=True).then_inc(var_ready, 1)

        @block.scalar
        def _(act):
            with act.Fori(0, CHUNKS // 2) as i:
                for u in range(2):
                    act.wait_ge(centred_ready, 2 * i + u + 1)
                    act.activation(squares[:, u, :], centred[:, u, :], ACT.Square).then_inc(squared, 1)
                for u in range(2):
                    act.wait_ge(var_ready, 2 * i + u + 1)
                    act.activation(std[:, u, :], var[:, u, :], ACT.Sqrt, bias=R_eps(R, eps)).then_inc(std_ready, 1)

        @block.vector
        def _(dve):
            dve.sem_inc(done, SLOTS)
            chain = Chain(dve, order)
            per = 2 * (1 + (gain is not None) + residual)
            with dve.Fori(0, CHUNKS // 2) as i:
                chain.turn(i, per)
                for u in range(2):
                    at = bass.ds(i * (2 * CH) + u * CH, CH)
                    dve.wait_ge(std_ready, 2 * i + u + 1)
                    chain(dve.reciprocal(rstd[:, u, :], std[:, u, :]))
                    if gain is None:
                        dve.tensor_tensor(dst[:, at], centred[:, u, :], rstd[:, u, :], ALU.mult).then_inc(done, 1)
                    else:
                        chain(dve.tensor_tensor(rstd[:, u, :], centred[:, u, :], rstd[:, u, :], ALU.mult))
                        if residual:
                            chain(dve.tensor_scalar(rstd[:, u, :], rstd[:, u, :], gain, bias, ALU.mult, ALU.add))
                            dve.tensor_tensor(dst[:, at], dst[:, at], rstd[:, u, :], ALU.add).then_inc(done, 1)
                        else:
                            dve.tensor_scalar(dst[:, at], rstd[:, u, :], gain, bias, ALU.mult, ALU.add).then_inc(done, 1)
                chain.close()


def R_eps(R, eps):
    return R.eps[eps][:, 0:1]


def tokens(nc, R):
    PART = 3 * PAD * 2
    CELLS = PAD * PAD
    with ExitStack() as ctx:
        sb, ps, sem = allocators(nc, ctx, "tok")
        xin = sb("xin", [P, 2, 32, C])
        inner = sb("inner", [P, 2, 4, C])
        win = sb("win", [P, 2 * 3 * 2 * 3 * CELLS + 3 * CELLS + 32])
        acc = sb("acc", [P, 2, 2, CELLS])
        txt = sb("txt", [P, 2, C])
        parts = ps("parts", [P, 2, 2, 512])
        ptxt = ps("ptxt", [P, 2, 512])
        x_loaded = [sem(f"x_loaded{u}") for u in range(2)]
        txt_loaded = [sem(f"txt_loaded{u}") for u in range(2)]
        inner_ready, parts_done, txt_done, copied, txt_copied, weighted, order, stored = (
            sem(n) for n in ("inner_ready", "parts_done", "txt_done", "copied", "txt_copied", "weighted", "order",
                             "stored"))
        win_zeroed = sem("win_zeroed")
        x_v = R.ins["x"].rearrange("b h (q j) c -> b (h q) (j c)", q=2)
        block = ctx.enter_context(nc.Block())
        W = 2 * 3 * 3 * CELLS

        def window(slot, part_c, part_r, shift):
            a = 16 + slot * W + part_c * (6 * CELLS) + part_r * CELLS + shift
            v = win[:, a:a + 6 * CELLS]
            return v.rearrange("p (m q) -> p m q", m=2)[:, :, 0:CELLS]

        @block.sync
        def _(sp):
            with sp.Fori(0, B // 2) as i:
                for u in range(2):
                    sp.wait_ge(parts_done, 2 * i + u + 1)
                    sp.dma_start(xin[:, u, :, :].rearrange("p j c -> p (j c)"),
                                 x_v[bass.ds(2 * i + u, 1)].rearrange("a p f -> (a p) f")).then_inc(x_loaded[u], 16)
                    sp.wait_ge(txt_done, 2 * i + u + 1)
                    sp.dma_start(txt[:, u, :],
                                 R.ins["txt"][bass.ds(2 * i + u, 1)].rearrange("a t c -> (a t) c")).then_inc(
                        txt_loaded[u], 16)

        @block.tensor
        def _(pe):
            pe.sem_inc(parts_done, SLOTS)
            pe.sem_inc(txt_done, SLOTS)
            with pe.Fori(0, B // 2) as i:
                for u in range(2):
                    pe.wait_ge(txt_loaded[u], 16 * i + 16)
                    pe.wait_ge(txt_copied, 2 * i + u + 1)
                    pe.transpose(ptxt[:, u, 0:C], txt[:, u, :], R.c("ident")).then_inc(txt_done, 1)
                    pe.wait_ge(inner_ready, 2 * i + u + 1)
                    pe.wait_ge(copied, 2 * i + u + 1)
                    for jq in range(4):
                        for part, lhsT in enumerate((inner[:, u, jq, :], xin[:, u, 8 * jq, :], xin[:, u, 8 * jq + 7, :])):
                            a = (jq % 2) * 3 * PART + part * PART
                            last = pe.matmul(parts[:, u, jq // 2, a:a + PART], lhsT, R.c("rows"), start=True, stop=True)
                    last.then_inc(parts_done, 1)

        @block.vector
        def _(dve):
            dve.memset(win[:, :], 0.0).then_inc(win_zeroed, 1)
            dve.memset(acc[:, :, :, :], 0.0)
            chain = Chain(dve, order)
            with dve.Fori(0, B // 4) as i:
                chain.turn(i, 48)
                for pair in range(2):
                    for u in range(2):
                        n = 4 * i + 2 * pair + u
                        dve.wait_ge(x_loaded[u], 32 * i + 16 * pair + 16)
                        v = xin[:, u, :, :].rearrange("p (q r) c -> p q c r", r=8)
                        dve.tensor_reduce(inner[:, u, :, :], v[:, :, :, 1:7], AX, ALU.add).then_inc(inner_ready, 1)
                    dve.wait_ge(copied, 4 * i + 2 * pair + 2 + SLOTS)
                    dve.wait_ge(stored, 2 * i + pair + 1)
                    first = True
                    out = acc[:, pair, :, :]
                    for r, (part_r, dr) in enumerate(((0, 0), (1, 0), (2, 0), (2, -1), (1, 1))):
                        for c, (part_c, dc) in enumerate(((0, 0), (1, 0), (2, 0), (2, -1), (1, 1))):
                            tap = R.tap[:, 5 * r + c:5 * r + c + 1]
                            src = window(pair, part_c, part_r, dr * PAD + dc)
                            if first:
                                chain(dve.tensor_scalar(out, src, tap, None, ALU.mult))
                            else:
                                ins = dve.scalar_tensor_tensor(out=out, in0=src, scalar=tap, in1=out,
                                                               op0=ALU.mult, op1=ALU.add)
                                if r == 4 and c == 4:
                                    ins.then_inc(weighted, 1)
                                else:
                                    chain(ins)
                            first = False
                chain.close()

        @block.scalar
        def _(act):
            act.sem_inc(copied, SLOTS)
            act.sem_inc(txt_copied, SLOTS)
            act.sem_inc(stored, SLOTS)
            act.wait_ge(win_zeroed, 1)
            with act.Fori(0, B // 4) as i:
                for pair in range(2):
                    act.wait_ge(stored, 2 * i + pair + 1)
                    for u in range(2):
                        act.wait_ge(txt_done, 4 * i + 2 * pair + u + 1 + SLOTS)
                        act.copy(R.hT[:, bass.ds(4 * i * T + (2 * pair + u) * T + IMG_TOKENS, TXT_TOKENS)],
                                 ptxt[:, u, 0:C]).then_inc(txt_copied, 1)
                        act.wait_ge(parts_done, 4 * i + 2 * pair + u + 1 + SLOTS)
                        for bank in range(2):
                            for part in range(3):
                                src = parts[:, u, bank, 0:6 * PART].rearrange("p (q k) -> p q k", q=2)
                                src = src[:, :, part * PART:(part + 1) * PART].rearrange("p q (r s) -> p q r s", s=2)
                                a = 16 + pair * W + part * 6 * CELLS + u * 3 * CELLS + 1 + 2 * bank
                                dst = win[:, a:a + 3 * CELLS].rearrange("p (r j) -> p r j", j=PAD)
                                dst = dst[:, :, 0:GRID].rearrange("p r (s q) -> p q r s", s=2)[:, 0:2]
                                last = act.copy(dst, src)
                        last.then_inc(copied, 1)
                    act.wait_ge(weighted, 2 * i + pair + 1)
                    src = acc[:, pair, :, :].rearrange("p m (r j) -> p m r j", j=PAD)[:, :, 1:GRID + 1, 1:GRID + 1]
                    for u in range(2):
                        last = act.activation(
                            R.hT[:, bass.ds(4 * i * T + (2 * pair + u) * T, IMG_TOKENS)].rearrange(
                                "p (r j) -> p r j", j=GRID),
                            src[:, u], ACT.Identity, scale=1.0 / IMG_TOKENS, bias=R.col("L0_tok_conv_b"))
                    last.then_inc(stored, 1)


def project(nc, R, tag, src, jobs, copies=()):
    J = len(jobs)
    with ExitStack() as ctx:
        sb, ps, sem = allocators(nc, ctx, tag)
        out = ps("out", [P, 2, J, CH])
        product_ready, evacuated, stored = sem("product_ready"), sem("evacuated"), sem("stored")
        block = ctx.enter_context(nc.Block())

        if copies:
            @block.sync
            def _(sp):
                with sp.Fori(0, CHUNKS) as i:
                    sp.wait_ge(evacuated, J * i + J + SLOTS * J)
                    for j, dram in copies:
                        at = bass.ds(i * CH, CH)
                        sp.dma_start(dram[:, at], jobs[j][1][:, at]).then_inc(stored, 16)
                sp.wait_ge(stored, 16 * CHUNKS * len(copies))

        @block.tensor
        def _(pe):
            with pe.Fori(0, CHUNKS // 2) as i:
                for u in range(2):
                    for j, (w, dst, func, scale, bias) in enumerate(jobs):
                        pe.wait_ge(evacuated, (2 * J) * i + u * J + j + 1)
                        pe.matmul(out[:, u, j, :], w, src[:, bass.ds(i * (2 * CH) + u * CH, CH)],
                                  start=True, stop=True).then_inc(product_ready, 1)

        @block.scalar
        def _(act):
            act.sem_inc(evacuated, SLOTS * J)
            with act.Fori(0, CHUNKS // 2) as i:
                for u in range(2):
                    for j, (w, dst, func, scale, bias) in enumerate(jobs):
                        act.wait_ge(product_ready, (2 * J) * i + u * J + j + 1)
                        act.activation(dst[:, bass.ds(i * (2 * CH) + u * CH, CH)], out[:, u, j, :], func,
                                       scale=scale, bias=bias).then_inc(evacuated, 1)


def attend(nc, R, tag, q_all, k_all, v_all, att, sums, scale, groups=None, self_value=None, own=None):
    SLOT = T // HEADS
    local = groups is None
    ROWS = HALF + 7
    with ExitStack() as ctx:
        sb, ps, sem = allocators(nc, ctx, tag)
        q16 = [sb(f"q16_{u}", [HALF + 1, HEADS, T]) for u in range(2)]
        k16 = [sb(f"k16_{u}", [HALF + 1, HEADS, T]) for u in range(2)]
        vin = [sb(f"vin_{u}", [HD, HEADS, T] if local else [P, T]) for u in range(2)]
        if local:
            raw = [sb(f"raw{u}", [HD, 3, HEADS, T]) for u in range(2)]
            moved_q, moved_kv = sem("moved_q"), sem("moved_kv")
        vrow = sb("vrow", [HALF, 2, 2, HEADS, 2 * HD])
        peak = sb("peak", [HALF, 2, 2 * HEADS])
        neg = sb("neg", [2 * HEADS, 2, HALF])
        prob = sb("prob", [HALF, 2, 2, T])
        o32 = [sb(f"o32_{u}", [2 * HD, HEADS, T]) for u in range(2)]
        pS, pT = ps("pS", [HALF, 2, 512]), ps("pT", [HALF, 2, 512])
        pO, pV, pM, pX = ps("pO", [2 * HD, 512]), ps("pV", [HALF, 512]), ps("pM", [2 * HEADS, 512]), ps("pX", [P, 512])
        loaded = [sem(f"loaded{u}") for u in range(2)]
        rows_loaded = [sem(f"rows_loaded{u}") for u in range(2)]
        stored = [sem(f"stored{u}") for u in range(2)]
        (cleared, v_turned, v_copied, scores_ready, max_done, floored, max_turned, neg_ready, shifted_ready, exp_done,
         weighted, o_copied, order, ones_set) = (sem(n) for n in (
             "cleared", "v_turned", "v_copied", "scores_ready", "max_done", "floored", "max_turned", "neg_ready",
             "shifted_ready", "exp_done", "weighted", "o_copied", "order", "ones_set"))
        if not local:
            qs_mask = [sb(f"qs_mask{u}", [ROWS, HEADS, T], BF16) for u in range(2)]
            ks_mask = [sb(f"ks_mask{u}", [ROWS, 2, HEADS, T], BF16) for u in range(2)]
            kt_mask = [sb(f"kt_mask{u}", [ROWS, HEADS, T], BF16) for u in range(2)]
            qt_mask = [sb(f"qt_mask{u}", [ROWS, 2, HEADS, T], BF16) for u in range(2)]
            spread_ready, own_ready = sem("spread_ready"), sem("own_ready")
        LOAD = 16 * (3 if local else 9)
        block = ctx.enter_context(nc.Block())

        def pick(t, h, half=None, rows=HALF):
            return t[0:rows, h, :] if half is None else t[0:rows, h, HALF * half:HALF * half + HALF]

        @block.sync
        def _(sp):
            def load(n, u):
                at = bass.ds(n * T, T)
                heads = "(s d) t -> d s t"
                if local:
                    for j, src in enumerate((q_all, k_all, v_all)):
                        sp.dma_start(raw[u][:, j, :, :], src[:, at].rearrange(heads, d=HD)).then_inc(loaded[u], 16)
                else:
                    sp.dma_start(q16[u][0:HD, :, :], q_all[:, at].rearrange(heads, d=HD)).then_inc(loaded[u], 16)
                    sp.dma_start(k16[u][0:HD, :, :], k_all[:, at].rearrange(heads, d=HD)).then_inc(loaded[u], 16)
                    sp.dma_start(vin[u][:, :], v_all[:, at]).then_inc(loaded[u], 16)
                    g = groups[:, at].rearrange("(h k c) t -> k c h t", h=HEADS, k=2)
                    for side, dst in ((0, qs_mask[u][HALF:ROWS, :, :]), (0, qt_mask[u][HALF:ROWS, 0, :, :]),
                                      (0, qt_mask[u][HALF:ROWS, 1, :, :]), (1, kt_mask[u][HALF:ROWS, :, :]),
                                      (1, ks_mask[u][HALF:ROWS, 0, :, :]), (1, ks_mask[u][HALF:ROWS, 1, :, :])):
                        sp.dma_start(dst, g[side, 0:7]).then_inc(loaded[u], 16)

            def store_max(n, u):
                sp.wait_ge(neg_ready, n + 2)
                for half in range(2):
                    src = neg[HEADS * half:HEADS * half + HEADS, u, :]
                    dst = q16[u][HALF:HALF + 1, :, HALF * half:HALF * half + HALF]
                    sp.dma_start(dst, src).then_inc(rows_loaded[u], 16)

            def store_out(n, u):
                at = bass.ds(n * T, T)
                sp.wait_ge(o_copied, 4 * n + 4 + 1)
                sp.dma_start(att[:, at].rearrange("(s d) t -> d s t", d=HD), o32[u][0:HD, :, :]).then_inc(stored[u], 16)
                sp.dma_start(sums[:, at].rearrange("(s d) t -> d s t", d=HD), o32[u][HD:2 * HD, :, :]).then_inc(
                    stored[u], 16)

            sp.sem_inc(stored[0], 32)
            sp.sem_inc(stored[1], 32)
            sp.wait_ge(cleared, 1)
            load(0, 0)
            load(1, 1)
            store_max(0, 0)
            with sp.Fori(0, B // 2 - 1) as i:
                for u in range(2):
                    store_max(2 * i + u + 1, 1 - u)
                    store_out(2 * i + u, u)
                    load(2 * i + u + 2, u)
            store_max(B - 1, 1)
            store_out(B - 2, 0)
            store_out(B - 1, 1)
            for u in range(2):
                sp.wait_ge(stored[u], 32 * (B // 2 + 1))

        @block.gpsimd
        def _(pool):
            for u in range(2):
                pool.memset(q16[u][:, :, :], 0.0)
                pool.memset(k16[u][:, :, :], 0.0)
            pool.memset(neg[:, :, :], 0.0).then_inc(order, 1)
            pool.wait_ge(order, 1)
            for u in range(2):
                last = pool.memset(k16[u][HALF:HALF + 1, :, :], 1.0)
            last.then_inc(order, 1)
            pool.wait_ge(order, 2)
            if not local:
                for u in range(2):
                    for t in (qs_mask, ks_mask, kt_mask, qt_mask):
                        last = pool.memset(t[u][:], 0.0)
                last.then_inc(order, 1)
                pool.wait_ge(order, 3)
                for u in range(2):
                    for h in range(HEADS):
                        for half in range(2):
                            mine = slice(HALF * half, HALF * half + HALF)
                            pool.tensor_copy(qs_mask[u][0:HALF, h, mine], R.bf["ident"][0:HALF, 0:HALF])
                            pool.tensor_copy(kt_mask[u][0:HALF, h, mine], R.bf["ident"][0:HALF, 0:HALF])
                            pool.tensor_copy(ks_mask[u][0:HALF, half, h, mine], R.bf["neg_diag"][0:HALF, :])
                            last = pool.tensor_copy(qt_mask[u][0:HALF, half, h, mine], R.bf["neg_diag"][0:HALF, :])
                last.then_inc(order, 1)
                pool.wait_ge(order, 4)
            pool.sem_inc(cleared, 1)

        MAXROWS = 32

        @block.tensor
        def _(pe):
            def values(n, u, turn):
                if local:
                    pe.wait_ge(moved_kv, n + 1)
                else:
                    pe.wait_ge(loaded[u], LOAD * turn + LOAD)
                pe.wait_ge(v_copied, n + 1)
                if local:
                    for half in range(2):
                        for h in range(HEADS):
                            a = (half * HEADS + h) * HD
                            last = pe.matmul(pV[:, a:a + HD], pick(vin[u], h, half, HD), R.c("ident")[0:HD, 0:HD],
                                             start=True, stop=True)
                else:
                    for half in range(2):
                        last = pe.transpose(pV[:, C * half:C * half + C], vin[u][:, HALF * half:HALF * half + HALF],
                                            R.c("ident"))
                last.then_inc(v_turned, 1)

            def scores(n, u):
                if local:
                    pe.wait_ge(moved_q, n + 1)
                for h in range(HEADS):
                    pe.wait_ge(max_done, HEADS * n + h + 1)
                    for half in range(2):
                        out = pS[:, h % 2, T * half:T * half + T]
                        if not local:
                            pe.matmul(out, qs_mask[u][:, h, HALF * half:HALF * half + HALF], ks_mask[u][:, half, h, :],
                                      start=True, stop=False)
                        last = pe.matmul(out, pick(q16[u], h, half), pick(k16[u], h), start=local, stop=True)
                    last.then_inc(scores_ready, 1)

            def maxima(n, u):
                if local:
                    pe.wait_ge(max_done, HEADS * n + HEADS + SLOTS)
                else:
                    pe.wait_ge(floored, n + 1)
                pe.wait_ge(neg_ready, n + 1)
                pe.transpose(pM[:, 0:HALF], peak[:, u, :], R.c("ident")[0:HALF, 0:HALF]).then_inc(max_turned, 1)

            def shifted(n, u, h, turn):
                if h == 0:
                    pe.wait_ge(rows_loaded[u], MAXROWS * turn + MAXROWS)
                pe.wait_ge(exp_done, HEADS * n + h + 1)
                for half in range(2):
                    out = pT[:, h % 2, T * half:T * half + T]
                    if not local:
                        pe.matmul(out, kt_mask[u][:, h, HALF * half:HALF * half + HALF], qt_mask[u][:, half, h, :],
                                  start=True, stop=False)
                    last = pe.matmul(out, pick(k16[u], h, half, HALF + 1), pick(q16[u], h, None, HALF + 1),
                                     start=local, stop=True)
                last.then_inc(shifted_ready, 1)

            def mix(n, u, h):
                if h == 0:
                    pe.wait_ge(v_copied, n + 2)
                if h % 2 == 0:
                    pe.wait_ge(o_copied, 4 * n + h // 2 + 1)
                pe.wait_ge(exp_done, HEADS * n + h + 1 + SLOTS)
                for half in range(2):
                    last = pe.matmul(pO[:, T * (h % 2):T * (h % 2) + T], vrow[:, u, half, h, :], prob[:, h % 2, half, :],
                                     start=(half == 0), stop=(half == 1))
                last.then_inc(weighted, 1)

            def own_spread(n, u):
                pe.wait_ge(neg_ready, n + 2)
                pe.wait_ge(own_ready, n + 1)
                for half in range(2):
                    last = pe.matmul(pX[:, HALF * half:HALF * half + HALF],
                                     R.c("spread", 2 * HEADS)[:, P * half:P * half + P], neg[:, u, :],
                                     start=True, stop=True)
                last.then_inc(spread_ready, 1)

            def sequence(n, u, nxt, turn):
                if nxt:
                    values(n + 1, 1 - u, turn + u)
                shifted(n, u, 0, turn)
                for h in range(3):
                    shifted(n, u, h + 1, turn)
                    mix(n, u, h)
                if nxt:
                    scores(n + 1, 1 - u)
                mix(n, u, 3)
                shifted(n, u, 4, turn)
                if nxt:
                    maxima(n + 1, 1 - u)
                for h in range(4, 7):
                    shifted(n, u, h + 1, turn)
                    mix(n, u, h)
                if nxt and not local:
                    own_spread(n + 1, 1 - u)
                mix(n, u, 7)

            pe.sem_inc(weighted, SLOTS)
            values(0, 0, 0)
            scores(0, 0)
            maxima(0, 0)
            if not local:
                own_spread(0, 0)
            with pe.Fori(0, B // 2 - 1) as i:
                for u in range(2):
                    sequence(2 * i + u, u, True, i)
            sequence(B - 2, 0, True, B // 2 - 1)
            sequence(B - 1, 1, False, B // 2 - 1)

        @block.scalar
        def _(act):
            act.sem_inc(v_copied, 1)
            act.sem_inc(neg_ready, 1)
            act.sem_inc(exp_done, SLOTS)
            if not local:
                act.sem_inc(own_ready, 1)

            def move(n, u, turn):
                act.wait_ge(loaded[u], LOAD * turn + LOAD)
                for j, dst in ((1, k16[u][0:HD]), (2, vin[u])):
                    last = act.copy(dst.rearrange("d h (s t) -> d h s t", s=HEADS),
                                    raw[u][:, j].rearrange("d s (h t) -> d h s t", h=HEADS))
                last.then_inc(moved_kv, 1)

            def values(n, u):
                act.wait_ge(v_turned, n + 1)
                if local:
                    src = pV[:, 0:2 * HEADS * HD].rearrange("p (g d) -> p g d", d=HD)
                else:
                    src = pV[:, 0:2 * C].rearrange("p (g d) -> p g d", d=HD)
                dst = vrow[:, u, :, :, 0:HD].rearrange("p a h d -> p (a h) d")
                act.copy(dst, src).then_inc(v_copied, 1)

            def maxima(n, u):
                act.wait_ge(max_turned, n + 1)
                act.mul(neg[:, u, :], pM[:, 0:HALF], -1.0).then_inc(neg_ready, 1)

            def own_term(n, u):
                act.wait_ge(spread_ready, n + 1)
                act.activation(own[:, bass.ds(n * T, T)], pX[:, 0:T], ACT.Exp, scale=scale,
                               bias=R.self_value[:, 0:1]).then_inc(own_ready, 1)

            def exps(n, u, lo, hi):
                for h in range(lo, hi):
                    act.wait_ge(shifted_ready, HEADS * n + h + 1)
                    act.wait_ge(weighted, HEADS * n + h + 1)
                    act.activation(prob[:, h % 2, :, :], pT[:, h % 2, 0:2 * T].rearrange("p (a t) -> p a t", a=2), ACT.Exp,
                                   scale=scale).then_inc(exp_done, 1)

            def sequence(n, u, nxt, turn):
                if nxt:
                    if local:
                        move(n + 1, 1 - u, turn + u)
                    values(n + 1, 1 - u)
                exps(n, u, 0, 5)
                if nxt:
                    maxima(n + 1, 1 - u)
                exps(n, u, 5, HEADS)
                if nxt and not local:
                    own_term(n + 1, 1 - u)

            act.wait_ge(ones_set, 1)
            act.wait_ge(cleared, 1)
            if local:
                move(0, 0, 0)
            values(0, 0)
            maxima(0, 0)
            if not local:
                own_term(0, 0)
            with act.Fori(0, B // 2 - 1) as i:
                for u in range(2):
                    sequence(2 * i + u, u, True, i)
            sequence(B - 2, 0, True, B // 2 - 1)
            sequence(B - 1, 1, False, B // 2 - 1)

        @block.vector
        def _(dve):
            dve.memset(vrow[:, :, :, :, :], 1.0).then_inc(ones_set, 1)
            dve.wait_ge(ones_set, 1)
            dve.sem_inc(max_done, SLOTS)
            dve.sem_inc(o_copied, 1)
            def maxima(n, u):
                for h in range(HEADS):
                    dve.wait_ge(scores_ready, HEADS * n + h + 1)
                    dst = peak[:, u, :].rearrange("p (a h) -> p a h", a=2)[:, :, h]
                    dve.tensor_reduce(dst, pS[:, h % 2, 0:2 * T].rearrange("p (a t) -> p a t", a=2), AX,
                                      ALU.max).then_inc(max_done, 1)
                if not local:
                    dve.wait_ge(max_done, HEADS * n + HEADS + SLOTS)
                    dve.tensor_scalar(peak[:, u, :], peak[:, u, :], self_value / scale, None, ALU.max).then_inc(floored, 1)

            def out(n, u, pair, turn):
                dve.wait_ge(weighted, HEADS * n + 2 * pair + 2 + SLOTS)
                if pair == 0:
                    dve.wait_ge(stored[u], 32 * turn + 32)
                src = pO[:, 0:2 * T]
                if local:
                    dst = o32[u][:, :, 2 * SLOT * pair:2 * SLOT * pair + 2 * SLOT].rearrange("p s (h t) -> p h s t", h=2)
                    src = src.rearrange("p (h s t) -> p h s t", h=2, s=HEADS)
                else:
                    dst = o32[u][:, 2 * pair:2 * pair + 2, :]
                    src = src.rearrange("p (h t) -> p h t", h=2)
                dve.tensor_copy(dst, src).then_inc(o_copied, 1)

            def move(n, u, turn):
                dve.wait_ge(loaded[u], LOAD * turn + LOAD)
                dve.tensor_copy(q16[u][0:HD].rearrange("d h (s t) -> d h s t", s=HEADS),
                                raw[u][:, 0].rearrange("d s (h t) -> d h s t", h=HEADS)).then_inc(moved_q, 1)

            def sequence(n, u, nxt, turn):
                if nxt and local:
                    move(n + 1, 1 - u, turn + u)
                out(n, u, 0, turn)
                if nxt:
                    maxima(n + 1, 1 - u)
                for pair in range(1, 4):
                    out(n, u, pair, turn)

            if local:
                dve.wait_ge(cleared, 1)
                move(0, 0, 0)
            maxima(0, 0)
            with dve.Fori(0, B // 2 - 1) as i:
                for u in range(2):
                    sequence(2 * i + u, u, True, i)
            sequence(B - 2, 0, True, B // 2 - 1)
            sequence(B - 1, 1, False, B // 2 - 1)


def attention_0(nc, R):
    with ExitStack() as ctx:
        sb, _, _ = allocators(nc, ctx, "a0")
        q, k, v = sb("q", [P, N]), sb("k", [P, N]), sb("v", [P, N])
        layer_norm(nc, R, "a0_ln", R.hT, R.xT)
        w = R.w["L0_attn_W_qkv"]
        project(nc, R, "a0_qkv", R.xT, [
            (w[:, C * n:C * n + C], dst, ACT.Identity, 1.0, R.col("L0_attn_b_qkv", n)) for n, dst in enumerate((q, k, v))],
            copies=[(n, R.scratch[n]) for n in range(3)])
        attend(nc, R, "a0", *R.scratch[0:5], 0.25)
        divide(nc, R, "a0_add", R.scratch[3], R.scratch[4], R.hT)


def divide(nc, R, tag, att, sums, dst, own=None, v=None):
    with ExitStack() as ctx:
        sb, ps, sem = allocators(nc, ctx, tag)
        a, s, t = sb("a", [P, 2, CH]), sb("s", [P, 2, CH]), sb("t", [P, 2, CH])
        loaded = [sem(f"loaded{u}") for u in range(2)]
        done, order = sem("done"), sem("order")
        block = ctx.enter_context(nc.Block())
        arrays = [(a, att), (s, sums)] + ([(t, v)] if own is not None else [])

        @block.sync
        def _(sp):
            with sp.Fori(0, CHUNKS // 2) as i:
                for u in range(2):
                    at = bass.ds(i * (2 * CH) + u * CH, CH)
                    sp.wait_ge(done, 2 * i + u + 1)
                    for tile, dram in arrays:
                        sp.dma_start(tile[:, u, :], dram[:, at]).then_inc(loaded[u], 16)

        @block.vector
        def _(dve):
            dve.sem_inc(done, SLOTS)
            chain = Chain(dve, order)
            load = 16 * len(arrays)
            with dve.Fori(0, CHUNKS // 2) as i:
                chain.turn(i, 8 if own is not None else 4)
                for u in range(2):
                    at = bass.ds(i * (2 * CH) + u * CH, CH)
                    dve.wait_ge(loaded[u], load * i + load)
                    if own is not None:
                        dve.tensor_tensor(t[:, u, :], own[:, at], t[:, u, :], ALU.mult)
                        chain(dve.tensor_tensor(s[:, u, :], own[:, at], s[:, u, :], ALU.add))
                        chain(dve.tensor_tensor(a[:, u, :], a[:, u, :], t[:, u, :], ALU.add))
                    chain(dve.reciprocal(s[:, u, :], s[:, u, :]))
                    if own is not None:
                        chain(dve.tensor_tensor(a[:, u, :], a[:, u, :], s[:, u, :], ALU.mult))
                        dve.tensor_copy(dst[:, at], a[:, u, :]).then_inc(done, 1)
                    else:
                        chain(dve.tensor_tensor(a[:, u, :], a[:, u, :], s[:, u, :], ALU.mult))
                        dve.tensor_tensor(dst[:, at], dst[:, at], a[:, u, :], ALU.add).then_inc(done, 1)
                chain.close()


def tile_of(t):
    return slice(P * t, P * t + P)


def route(nc, R, tag, w, E, logits, bias=None):
    with ExitStack() as ctx:
        sb, ps, sem = allocators(nc, ctx, tag)
        flat = sb("flat", [E, N])
        up = ps("up", [E, 2, CH])
        per_bank = 512 // E
        banks = -(-TILES // per_bank)
        turned = ps("turned", [P, banks, 512])
        product_ready, evacuated, turned_ready = sem("product_ready"), sem("evacuated"), sem("turned_ready")
        block = ctx.enter_context(nc.Block())

        @block.tensor
        def _(pe):
            with pe.Fori(0, CHUNKS // 2) as i:
                for u in range(2):
                    pe.wait_ge(evacuated, 2 * i + u + 1)
                    pe.matmul(up[:, u, :], w, R.xT[:, bass.ds(i * (2 * CH) + u * CH, CH)],
                              start=True, stop=True).then_inc(product_ready, 1)
            pe.wait_ge(evacuated, CHUNKS + SLOTS)
            for t in range(TILES):
                a = E * (t % per_bank)
                last = pe.transpose(turned[:, t // per_bank, a:a + E], flat[:, tile_of(t)], R.c("ident")[0:E, 0:E])
            last.then_inc(turned_ready, 1)

        @block.scalar
        def _(act):
            act.sem_inc(evacuated, SLOTS)
            with act.Fori(0, CHUNKS // 2) as i:
                for u in range(2):
                    act.wait_ge(product_ready, 2 * i + u + 1)
                    act.activation(flat[:, bass.ds(i * (2 * CH) + u * CH, CH)], up[:, u, :], ACT.Identity,
                                   bias=0.0 if bias is None else bias).then_inc(evacuated, 1)

        @block.vector
        def _(dve):
            dve.wait_ge(turned_ready, 1)
            for b in range(banks):
                n = min(per_bank, TILES - b * per_bank)
                dve.tensor_copy(logits[:, b * per_bank:b * per_bank + n, :],
                                turned[:, b, 0:n * E].rearrange("p (t e) -> p t e", e=E))


def top_gates(nc, R, tag, logits, E, K, gates, floor, capacity=None, dropped=None):
    TAKEN = 2.0
    with ExitStack() as ctx:
        sb, ps, sem = allocators(nc, ctx, tag)
        prob, marked = sb("prob", [P, TILES, E + 8]), sb("marked", [P, TILES, E + 8])
        top = sb("top", [P, TILES, 8])
        stat, total = sb("stat", [P, TILES]), sb("total", [P, TILES])
        count, before = sb("count", [P, TILES, E], BF16), sb("before", [P, TILES, E], BF16)
        place = ps("place", [P, 2, 512])
        shifted, exp_ready, counted, placed, order = (
            sem(n) for n in ("shifted", "exp_ready", "counted", "placed", "order"))
        block = ctx.enter_context(nc.Block())

        def wide(v):
            return v[:, :].unsqueeze(2).to_broadcast([P, TILES, E])

        @block.scalar
        def _(act):
            act.wait_ge(shifted, 1)
            act.activation(prob[:, :, 0:E], logits[:, :, :], ACT.Exp).then_inc(exp_ready, 1)

        @block.vector
        def _(dve):
            chain = Chain(dve, order)
            dve.memset(prob[:, :, E:E + 8], TAKEN)
            chain(dve.tensor_reduce(stat[:, :], logits[:, :, :], AX, ALU.max))
            dve.tensor_tensor(logits[:, :, :], logits[:, :, :], wide(stat), ALU.subtract).then_inc(shifted, 1)
            dve.wait_ge(exp_ready, 1)
            chain(dve.tensor_reduce(total[:, :], prob[:, :, 0:E], AX, ALU.add))
            chain(dve.reciprocal(total[:, :], total[:, :]))
            chain(dve.tensor_tensor(prob[:, :, 0:E], prob[:, :, 0:E], wide(total), ALU.mult))
            for t in range(TILES):
                last = dve.max(top[:, t, :], prob[:, t, 0:E])
            chain(last)
            chain(dve.tensor_reduce(stat[:, :], top[:, :, 0:K], AX, ALU.add))
            chain(dve.tensor_scalar(stat[:, :], stat[:, :], floor, None, ALU.max))
            dve.reciprocal(stat[:, :], stat[:, :])
            chain(dve.memset(top[:, :, K:8], TAKEN))
            for t in range(TILES):
                last = dve.match_replace(marked[:, t, :], top[:, t, :], prob[:, t, :], -1.0)
            chain(last)
            chain(dve.scalar_tensor_tensor(out=gates[:, :, :], in0=marked[:, :, 0:E], scalar=0.0, in1=prob[:, :, 0:E],
                                           op0=ALU.is_lt, op1=ALU.mult))
            chain(dve.tensor_tensor(gates[:, :, :], gates[:, :, :], wide(stat), ALU.mult))
            if capacity is None:
                return
            chain(dve.tensor_scalar(count[:, :, :], marked[:, :, 0:E], 0.0, None, ALU.is_lt))
            chain(dve.memset(before[:, 0, :], 0.0))
            for t in range(1, TILES):
                ins = dve.tensor_tensor(before[:, t, :], before[:, t - 1, :], count[:, t - 1, :], ALU.add)
                if t < TILES - 1:
                    chain(ins)
            ins.then_inc(counted, 1)
            dve.wait_ge(placed, 1)
            h = TILES // 2
            for b in range(2):
                g = gates[:, h * b:h * b + h, :].rearrange("p t e -> p (t e)")
                last = dve.scalar_tensor_tensor(out=g, in0=place[:, b, 0:h * E], scalar=float(capacity), in1=g,
                                                op0=ALU.is_lt, op1=ALU.mult)
            chain(last)
            chain(dve.tensor_reduce(dropped[:, :], gates[:, :, :], AX, ALU.add))
            dve.tensor_scalar(dropped[:, :], dropped[:, :], 1e-12, None, ALU.is_le)

        if capacity is not None:
            @block.tensor
            def _(pe):
                pe.wait_ge(counted, 1)
                h = TILES // 2
                for b in range(2):
                    out = place[:, b, 0:h * E]
                    pe.matmul(out, R.bf["before"][:, :], count[:, h * b:h * b + h, :].rearrange("p t e -> p (t e)"),
                              start=True, stop=False)
                    last = pe.matmul(out, R.bf["ones"][:, :],
                                     before[:, h * b:h * b + h, :].rearrange("p t e -> p (t e)"),
                                     start=False, stop=True)
                last.then_inc(placed, 1)


def experts(nc, R, tag, E, kind, weights, gates, acc, bias=None):
    ups, down = weights
    U = 4 if kind == "glu" else 1
    A = len(ups)
    PER = 2 * CHUNKS * U
    SUB = CH // P
    with ExitStack() as ctx:
        sb, ps, sem = allocators(nc, ctx, tag)
        wu = [sb(f"wu{u}", [P, A, U * P]) for u in range(2)]
        wd = [sb(f"wd{u}", [P, U, C]) for u in range(2)]
        first, hidden = sb("first", [P, 2, CH]), sb("hidden", [P, 2, CH])
        mixed = sb("mixed", [P, 2, CH]) if kind == "glu" else None
        bias_now, bias_copied = sb("bias_now", [P, 2, 1]), sem("bias_copied")
        up, back = ps("up", [P, 2, A, CH]), ps("back", [P, 2, CH])
        loaded = [sem(f"loaded{u}") for u in range(2)]
        up_ready, first_ready, up_used, hidden_ready, back_ready, added = (
            sem(n) for n in ("up_ready", "first_ready", "up_used", "hidden_ready", "back_ready", "added"))
        block = ctx.enter_context(nc.Block())

        @block.sync
        def _(sp):
            def load(e, u):
                for a, w in enumerate(ups):
                    sp.dma_start(wu[u][:, a, :], w[bass.ds(e, 1)].rearrange("o p h -> (o p) h")).then_inc(loaded[u], 16)
                sp.dma_start(wd[u][:, :, :],
                             down[bass.ds(e, 1)].rearrange("o (k p) d -> (o p) k d", p=P)).then_inc(loaded[u], 16)

            load(0, 0)
            load(1, 1)
            if E > 2:
                with sp.Fori(1, E // 2) as i:
                    for u in range(2):
                        sp.wait_ge(back_ready, PER * i - PER + (u + 1) * CHUNKS * U + SLOTS)
                        load(2 * i + u, u)

        LOAD = 16 * (A + 1)

        def unit(j):
            return j // (CHUNKS * U), (j // U) % CHUNKS, j % U

        @block.tensor
        def _(pe):
            pe.sem_inc(back_ready, SLOTS)

            def go_up(i, j):
                u, ch, k = unit(j)
                if ch == 0 and k == 0:
                    pe.wait_ge(loaded[u], LOAD * i + LOAD)
                pe.wait_ge(up_used, PER * i + j + 1)
                for a in range(A):
                    last = pe.matmul(up[:, j % 2, a, :], wu[u][:, a, P * k:P * k + P], R.xT[:, CH * ch:CH * ch + CH],
                                     start=True, stop=True)
                last.then_inc(up_ready, 1)

            def go_back(i, j):
                u, ch, k = unit(j)
                if k == 0:
                    pe.wait_ge(added, (PER // U) * i + j // U + 1)
                if kind == "glu":
                    pe.wait_ge(hidden_ready, PER * i + j + 1 + SLOTS)
                else:
                    pe.wait_ge(up_used, PER * i + j + 1 + SLOTS)
                for s in range(SUB):
                    last = pe.matmul(back[:, ch % 2, C * s:C * s + C], hidden[:, j % 2, P * s:P * s + P], wd[u][:, k, :],
                                     start=(k == 0 and s == 0), stop=(k == U - 1), skip_group_check=True)
                last.then_inc(back_ready, 1)

            go_up(0, 0)
            if E > 2:
                with pe.Fori(0, E // 2 - 1) as i:
                    for j in range(PER):
                        go_up(i + (j + 1) // PER, (j + 1) % PER)
                        go_back(i, j)
            for j in range(PER):
                if j + 1 < PER:
                    go_up(E // 2 - 1, j + 1)
                go_back(E // 2 - 1, j)

        @block.scalar
        def _(act):
            if kind == "relu":
                act.sem_inc(up_used, SLOTS)
            if kind == "glu":
                act.sem_inc(hidden_ready, SLOTS)

            def hide(i, j):
                n = PER * i + j
                u, ch, k = unit(j)
                if kind == "relu" and ch == 0:
                    act.copy(bias_now[:, u, :], bias[:, bass.ds(2 * i + u, 1)]).then_inc(bias_copied, 1)
                    act.wait_ge(bias_copied, 2 * i + u + 1)
                act.wait_ge(up_ready, n + 1)
                if kind == "glu":
                    act.wait_ge(up_used, n + 1)
                    act.copy(first[:, j % 2, :], up[:, j % 2, 0, :]).then_inc(first_ready, 1)
                elif kind == "swiglu":
                    act.wait_ge(up_used, n + 1)
                    act.activation(first[:, j % 2, :], up[:, j % 2, 0, :], ACT.Silu).then_inc(first_ready, 1)
                else:
                    act.wait_ge(back_ready, n + 1)
                    act.activation(hidden[:, j % 2, :], up[:, j % 2, 0, :], ACT.Relu, bias=bias_now[:, u, :]).then_inc(
                        up_used, 1)

            def bend(i, j):
                n = PER * i + j
                act.wait_ge(up_used, n + 1 + SLOTS)
                act.wait_ge(back_ready, n + 1)
                act.activation(hidden[:, j % 2, :], mixed[:, j % 2, :], ACT.Gelu).then_inc(hidden_ready, 1)

            if kind == "glu":
                hide(0, 0)
                if E > 2:
                    with act.Fori(0, E // 2 - 1) as i:
                        for j in range(PER):
                            hide(i + (j + 1) // PER, (j + 1) % PER)
                            bend(i, j)
                for j in range(PER):
                    if j + 1 < PER:
                        hide(E // 2 - 1, j + 1)
                    bend(E // 2 - 1, j)
            else:
                with act.Fori(0, E // 2) as i:
                    for j in range(PER):
                        hide(i, j)

        @block.vector
        def _(dve):
            if kind != "relu":
                dve.sem_inc(up_used, SLOTS)
            dve.sem_inc(added, SLOTS)

            def mix(i, j):
                n = PER * i + j
                if kind == "relu":
                    return
                dve.wait_ge(first_ready, n + 1)
                if kind == "glu":
                    dve.wait_ge(hidden_ready, n + 1)
                    dve.tensor_tensor(mixed[:, j % 2, :], up[:, j % 2, 1, :], first[:, j % 2, :], ALU.mult).then_inc(
                        up_used, 1)
                else:
                    dve.wait_ge(back_ready, n + 1)
                    dve.tensor_tensor(hidden[:, j % 2, :], up[:, j % 2, 1, :], first[:, j % 2, :], ALU.mult).then_inc(
                        up_used, 1)

            def add(i, j):
                u, ch, k = unit(j)
                if k != U - 1:
                    return
                dve.wait_ge(back_ready, PER * i + j + 1 + SLOTS)
                if j // U == 0:
                    dve.wait_ge(added, (PER // U) * i + SLOTS)
                elif ch == 0:
                    dve.wait_ge(added, (PER // U) * i + CHUNKS + SLOTS)
                for s in range(SUB):
                    t = SUB * ch + s
                    gate = 1.0 if gates is None else gates[:, t, :][:, bass.ds(2 * i + u, 1)]
                    last = dve.scalar_tensor_tensor(out=acc[:, t, :], in0=back[:, ch % 2, C * s:C * s + C], scalar=gate,
                                                    in1=acc[:, t, :], op0=ALU.mult, op1=ALU.add)
                last.then_inc(added, 1)

            mix(0, 0)
            if E > 2:
                with dve.Fori(0, E // 2 - 1) as i:
                    for j in range(PER):
                        mix(i + (j + 1) // PER, (j + 1) % PER)
                        add(i, j)
            for j in range(PER):
                if j + 1 < PER:
                    mix(E // 2 - 1, j + 1)
                add(E // 2 - 1, j)


def feed_forward_3(nc, R):
    E, K = 64, 6
    with ExitStack() as ctx:
        sb, _, _ = allocators(nc, ctx, "f3")
        gates, acc = sb("gates", [P, TILES, E]), sb("acc", [P, TILES, C])
        layer_norm(nc, R, "f3_ln", R.hT, R.xT)
        with ExitStack() as inner:
            sb2, _, _ = allocators(nc, inner, "f3r")
            logits = sb2("logits", [P, TILES, E])
            route(nc, R, "f3_route", R.w["L3_ffn_Wr"][:, :], E, logits)
            top_gates(nc, R, "f3_top", logits, E, K, gates, 0.0)
        zero(nc, acc)
        i = R.ins
        experts(nc, R, "f3_shared", 2, "swiglu", ((i["L3_ffn_sWg"], i["L3_ffn_sWu"]), i["L3_ffn_sWd"]), None, acc)
        experts(nc, R, "f3_routed", E, "swiglu", ((i["L3_ffn_Wg"], i["L3_ffn_Wu"]), i["L3_ffn_Wd"]), gates, acc)
        leave(nc, R, "f3_out", acc)


def zero(nc, acc):
    with nc.Block() as block:
        @block.vector
        def _(dve):
            dve.memset(acc[:, :, :], 0.0)


def leave(nc, R, tag, acc):
    with ExitStack() as ctx:
        sb, ps, sem = allocators(nc, ctx, tag)
        both = ps("both", [P, 2, 512])
        turned, summed, stored = sem("turned"), sem("summed"), sem("stored")
        block = ctx.enter_context(nc.Block())
        SUB = 4
        out = R.out.rearrange("b t c -> (b t) c").rearrange("(g s p) c -> g p s c", s=SUB, p=P)

        @block.tensor
        def _(pe):
            for g in range(TILES // SUB):
                if g >= 2:
                    pe.wait_ge(summed, g - 1)
                for s in range(SUB):
                    o = both[:, g % 2, C * s:C * s + C]
                    pe.matmul(o, R.hT[:, tile_of(SUB * g + s)], R.c("ident"), start=True, stop=False)
                    last = pe.matmul(o, R.xT[:, tile_of(SUB * g + s)], R.c("ident"), start=False, stop=True)
                last.then_inc(turned, 1)

        @block.vector
        def _(dve):
            for g in range(TILES // SUB):
                dve.wait_ge(turned, g + 1)
                a = acc[:, SUB * g:SUB * g + SUB, :].rearrange("p t c -> p (t c)")
                dve.tensor_tensor(a, both[:, g % 2, :], a, ALU.add).then_inc(summed, 1)

        @block.sync
        def _(sp):
            for g in range(TILES // SUB):
                sp.wait_ge(summed, g + 1)
                sp.dma_start(out[g], acc[:, SUB * g:SUB * g + SUB, :]).then_inc(stored, 16)
            sp.wait_ge(stored, 16 * (TILES // SUB))


def fold(nc, R, tag, acc, from_x, keep=None, gates=None, b2=None):
    SUB = CH // P
    with ExitStack() as ctx:
        sb, ps, sem = allocators(nc, ctx, tag)
        px, pb, py = ps("px", [P, 2, CH]), ps("pb", [P, 2, CH]), ps("py", [P, 2, CH])
        if b2 is not None:
            pg, gT = ps("pg", [32, 2, CH]), sb("gT", [32, 2, CH])
        g_turned, g_ready, x_ready, y_ready, y_turned, folded, order = (
            sem(n) for n in ("g_turned", "g_ready", "x_ready", "y_ready", "y_turned", "folded", "order"))
        block = ctx.enter_context(nc.Block())
        GROUPS = TILES // SUB

        @block.tensor
        def _(pe):
            def turn_gates(g):
                for s in range(SUB):
                    last = pe.transpose(pg[:, g % 2, P * s:P * s + P], gates[:, SUB * g + s, :], R.c("ident"))
                last.then_inc(g_turned, 1)

            def turn_x(g):
                if g >= 2:
                    pe.wait_ge(folded, g - 1)
                if b2 is not None:
                    pe.wait_ge(g_ready, g + 1)
                    for s in range(SUB):
                        pe.matmul(pb[:, g % 2, P * s:P * s + P], gT[:, g % 2, P * s:P * s + P], b2, start=True, stop=True)
                for s in range(SUB):
                    last = pe.transpose(px[:, g % 2, P * s:P * s + P], R.xT[:, tile_of(SUB * g + s)], R.c("ident"))
                last.then_inc(x_ready, 1)

            def turn_y(g):
                pe.wait_ge(y_ready, g + 1)
                for s in range(SUB):
                    last = pe.transpose(py[:, g % 2, P * s:P * s + P], acc[:, SUB * g + s, :], R.c("ident"))
                last.then_inc(y_turned, 1)

            for g in range(GROUPS):
                if b2 is not None:
                    turn_gates(g)
                turn_x(g)
                if g >= 1:
                    turn_y(g - 1)
            turn_y(GROUPS - 1)

        if b2 is not None:
            @block.scalar
            def _(act):
                for g in range(GROUPS):
                    act.wait_ge(g_turned, g + 1)
                    act.copy(gT[:, g % 2, :], pg[:, g % 2, :]).then_inc(g_ready, 1)

        @block.vector
        def _(dve):
            chain = Chain(dve, order)

            def make(g):
                dve.wait_ge(x_ready, g + 1)
                a = acc[:, SUB * g:SUB * g + SUB, :].rearrange("p t c -> p (t c)")
                if b2 is not None:
                    chain(dve.tensor_tensor(a, pb[:, g % 2, :], a, ALU.add))
                    for s in range(SUB):
                        t = SUB * g + s
                        last = dve.tensor_scalar(acc[:, t, :], acc[:, t, :], keep[:, t:t + 1], None, ALU.mult)
                    chain(last)
                for s in range(SUB):
                    t = SUB * g + s
                    last = dve.scalar_tensor_tensor(out=acc[:, t, :], in0=px[:, g % 2, P * s:P * s + P],
                                                    scalar=from_x[:, t:t + 1], in1=acc[:, t, :], op0=ALU.mult,
                                                    op1=ALU.add)
                last.then_inc(y_ready, 1)

            def put(g):
                dve.wait_ge(y_turned, g + 1)
                h = R.hT[:, CH * g:CH * g + CH]
                dve.tensor_tensor(h, py[:, g % 2, :], h, ALU.add).then_inc(folded, 1)

            for g in range(GROUPS):
                make(g)
                if g >= 1:
                    put(g - 1)
            put(GROUPS - 1)


def gates_0(nc, R, logits, gates, from_x):
    E = 8
    with ExitStack() as ctx:
        sb, ps, sem = allocators(nc, ctx, "g0")
        shape = [P, TILES, E]
        one, two, t1 = sb("one", shape), sb("two", shape), sb("t1", shape)
        m1, m2, i1, i2, s1, s2 = (sb(n, [P, TILES]) for n in ("m1", "m2", "i1", "i2", "s1", "s2"))
        keep = sb("keep", [P, 2, TILES])
        full = sb("full", [P, 2, E])
        one_bf, both_bf = sb("one_bf", shape, BF16), sb("both_bf", shape, BF16)
        tally = ps("tally", [P, 2, 512])
        gap_ready, exp_ready, chosen, tallied, order = (
            sem(n) for n in ("gap_ready", "exp_ready", "chosen", "tallied", "order"))
        block = ctx.enter_context(nc.Block())

        def wide(v):
            return v[:, :].unsqueeze(2).to_broadcast(shape)

        rev = R.c("rev8").unsqueeze(1).to_broadcast(shape)
        iota = R.c("iota8").unsqueeze(1).to_broadcast(shape)

        @block.scalar
        def _(act):
            act.wait_ge(gap_ready, 1)
            act.activation(s2[:, :], m2[:, :], ACT.Exp).then_inc(exp_ready, 1)

        @block.tensor
        def _(pe):
            pe.wait_ge(chosen, 1)
            for n, t in enumerate((one_bf, both_bf)):
                last = pe.matmul(tally[:, n, 0:TILES * E], R.bf["ones"][:, :], t[:, :, :].rearrange("p t e -> p (t e)"),
                                 start=True, stop=True)
            last.then_inc(tallied, 1)

        @block.vector
        def _(dve):
            chain = Chain(dve, order)

            def choose(best, at, out):
                chain(dve.tensor_reduce(best[:, :], logits[:, :, :], AX, ALU.max))
                chain(dve.tensor_tensor(t1[:, :, :], logits[:, :, :], wide(best), ALU.is_equal))
                chain(dve.tensor_tensor(t1[:, :, :], t1[:, :, :], rev, ALU.mult))
                chain(dve.tensor_reduce(at[:, :], t1[:, :, :], AX, ALU.max))
                chain(dve.tensor_tensor(out[:, :, :], rev, wide(at), ALU.is_equal))

            choose(m1, i1, one)
            chain(dve.scalar_tensor_tensor(out=logits[:, :, :], in0=one[:, :, :], scalar=-3e38, in1=logits[:, :, :],
                                           op0=ALU.mult, op1=ALU.add))
            choose(m2, i2, two)
            dve.tensor_copy(one_bf[:, :, :], one[:, :, :])
            dve.tensor_tensor(both_bf[:, :, :], one[:, :, :], two[:, :, :], ALU.add).then_inc(chosen, 1)
            dve.tensor_tensor(m2[:, :], m2[:, :], m1[:, :], ALU.subtract).then_inc(gap_ready, 1)
            dve.wait_ge(exp_ready, 1)
            chain(dve.tensor_scalar(s1[:, :], s2[:, :], 1.0, None, ALU.add))
            chain(dve.reciprocal(s1[:, :], s1[:, :]))
            chain(dve.tensor_tensor(s2[:, :], s2[:, :], s1[:, :], ALU.mult))
            dve.wait_ge(tallied, 1)
            for n in range(2):
                last = dve.tensor_reduce(full[:, n, :], tally[:, n, 0:TILES * E].rearrange("p (t e) -> p e t", e=E), AX,
                                         ALU.add)
            chain(last)
            chain(dve.tensor_scalar(full[:, :, :], full[:, :, :], float(N), R.c("last_row"), ALU.is_ge, ALU.mult))
            chain(dve.memset(keep[:, :, :], 1.0))
            for n, t in enumerate((one, two)):
                chain(dve.tensor_tensor(t1[:, n, :], t[:, TILES - 1, :], full[:, n, :], ALU.mult))
                chain(dve.tensor_reduce(keep[:, n, TILES - 1:TILES], t1[:, n, :], AX, ALU.add))
                chain(dve.tensor_scalar(keep[:, n, TILES - 1:TILES], keep[:, n, TILES - 1:TILES], -1.0, 1.0, ALU.mult,
                                        ALU.add))
            for n, t in enumerate((i1, i2)):
                chain(dve.tensor_scalar(t[:, :], t[:, :], -1.0, float(E), ALU.mult, ALU.add))
                chain(dve.tensor_tensor(t[:, :], t[:, :], keep[:, n, :], ALU.mult))
            chain(dve.tensor_tensor(i1[:, :], i1[:, :], i2[:, :], ALU.max))
            chain(dve.tensor_tensor(m1[:, :], s1[:, :], keep[:, 0, :], ALU.mult))
            chain(dve.tensor_tensor(m2[:, :], s2[:, :], keep[:, 1, :], ALU.mult))
            dve.tensor_tensor(s1[:, :], s1[:, :], m1[:, :], ALU.subtract)
            chain(dve.tensor_tensor(s2[:, :], s2[:, :], m2[:, :], ALU.subtract))
            dve.tensor_tensor(from_x[:, :], s1[:, :], s2[:, :], ALU.add)
            chain(dve.tensor_tensor(m1[:, :], m1[:, :], m2[:, :], ALU.add))
            chain(dve.tensor_tensor(gates[:, :, :], iota, wide(i1), ALU.is_equal))
            chain(dve.tensor_tensor(gates[:, :, :], gates[:, :, :], wide(m1), ALU.mult))


def feed_forward_0(nc, R):
    E = 8
    with ExitStack() as ctx:
        sb, _, _ = allocators(nc, ctx, "f0")
        gates, acc, from_x = sb("gates", [P, TILES, E]), sb("acc", [P, TILES, C]), sb("from_x", [P, TILES])
        logits, br = sb("logits", [P, TILES, E]), sb("br", [E, 1])
        layer_norm(nc, R, "f0_ln", R.hT, R.xT)
        with nc.semaphore("f0_bias") as loaded, nc.Block() as block:
            @block.sync
            def _(sp):
                sp.dma_start(br[:, :], R.ins["L0_ffn_br"].rearrange("(e o) -> e o", o=1)).then_inc(loaded, 16)
                sp.wait_ge(loaded, 16)
        route(nc, R, "f0_route", R.w["L0_ffn_Wr"][:, :], E, logits, br[:, 0:1])
        gates_0(nc, R, logits, gates, from_x)
        zero(nc, acc)
        i = R.ins
        experts(nc, R, "f0_experts", E, "glu", ((i["L0_ffn_W1"], i["L0_ffn_W2"]), i["L0_ffn_W3"]), gates, acc)
        fold(nc, R, "f0_fold", acc, from_x)


def feed_forward_1(nc, R):
    E, K = 32, 2
    capacity = -(-N * K * 5 // (4 * E))
    with ExitStack() as ctx:
        sb, _, _ = allocators(nc, ctx, "f1")
        gates, acc = sb("gates", [P, TILES, E]), sb("acc", [P, TILES, C])
        dropped, kept = sb("dropped", [P, TILES]), sb("kept", [P, TILES])
        logits, b1, b1T, b2 = sb("logits", [P, TILES, E]), sb("b1", [E, C]), sb("b1T", [P, E]), sb("b2", [E, C])
        layer_norm(nc, R, "f1_ln", R.hT, R.xT)
        route(nc, R, "f1_route", R.w["L1_ffn_Wg"][:, :], E, logits)
        top_gates(nc, R, "f1_top", logits, E, K, gates, 1e-9, capacity, dropped)
        with (nc.semaphore("f1_loaded") as loaded, nc.semaphore("f1_turned") as turned,
              nc.psum_tensor("f1_pb", [P, 512], F32) as pb, nc.Block() as block):
            @block.sync
            def _(sp):
                sp.dma_start(b1[:, :], R.ins["L1_ffn_b1"]).then_inc(loaded, 16)
                sp.dma_start(b2[:, :], R.ins["L1_ffn_b2"]).then_inc(loaded, 16)

            @block.tensor
            def _(pe):
                pe.wait_ge(loaded, 32)
                pe.transpose(pb[:, 0:E], b1[:, :], R.c("ident")[0:E, 0:E]).then_inc(turned, 1)

            @block.vector
            def _(dve):
                dve.memset(acc[:, :, :], 0.0)
                dve.tensor_scalar(kept[:, :], dropped[:, :], -1.0, 1.0, ALU.mult, ALU.add)
                dve.wait_ge(turned, 1)
                dve.tensor_copy(b1T[:, :], pb[:, 0:E])
        i = R.ins
        experts(nc, R, "f1_experts", E, "relu", ((i["L1_ffn_W1"],), i["L1_ffn_W2"]), gates, acc, b1T)
        fold(nc, R, "f1_fold", acc, dropped, kept, gates, b2[:, :])


def dense_mlp(nc, R, tag, src, w_up, up_scale, up_bias, w_down, finish):
    K = 4
    with ExitStack() as ctx:
        sb, ps, sem = allocators(nc, ctx, tag)
        hidden, t = sb("hidden", [P, 2, K, CH]), sb("t", [P, 2, CH])
        up, down = ps("up", [P, K, CH]), ps("down", [P, 2, CH])
        up_ready, hidden_ready, down_ready, evacuated, done, order = (
            sem(n) for n in ("up_ready", "hidden_ready", "down_ready", "evacuated", "done", "order"))
        block = ctx.enter_context(nc.Block())
        kind, p1, p2, p3 = finish

        @block.tensor
        def _(pe):
            pe.sem_inc(down_ready, SLOTS)
            with pe.Fori(0, CHUNKS // 2) as i:
                for u in range(2):
                    n = 2 * i + u
                    for k in range(K):
                        pe.wait_ge(hidden_ready, K * n + k + 1)
                        pe.matmul(up[:, k, :], w_up(k), src[:, bass.ds(i * (2 * CH) + u * CH, CH)], start=True,
                                  stop=True).then_inc(up_ready, 1)
                    pe.wait_ge(done, n + 1)
                    for k in range(K):
                        pe.wait_ge(hidden_ready, K * n + k + 1 + K)
                        last = pe.matmul(down[:, u, :], w_down(k), hidden[:, u, k, :], start=(k == 0), stop=(k == K - 1))
                    last.then_inc(down_ready, 1)

        @block.scalar
        def _(act):
            act.sem_inc(hidden_ready, K)
            with act.Fori(0, CHUNKS // 2) as i:
                for u in range(2):
                    n = 2 * i + u
                    for k in range(K):
                        act.wait_ge(up_ready, K * n + k + 1)
                        act.wait_ge(down_ready, n + 1)
                        act.activation(hidden[:, u, k, :], up[:, k, :], ACT.Relu, scale=up_scale(k),
                                       bias=up_bias(k)).then_inc(hidden_ready, 1)
                    if kind == "norm":
                        act.wait_ge(down_ready, n + 1 + SLOTS)
                        act.wait_ge(done, n + 1)
                        act.activation(t[:, u, :], down[:, u, :], ACT.Relu, scale=p1, bias=p2).then_inc(evacuated, 1)

        @block.vector
        def _(dve):
            dve.sem_inc(done, SLOTS)
            chain = Chain(dve, order)
            with dve.Fori(0, CHUNKS // 2) as i:
                chain.turn(i, 4 if kind == "half" else 2)
                for u in range(2):
                    n = 2 * i + u
                    at = bass.ds(i * (2 * CH) + u * CH, CH)
                    if kind == "half":
                        dve.wait_ge(down_ready, n + 1 + SLOTS)
                        chain(dve.scalar_tensor_tensor(out=t[:, u, :], in0=down[:, u, :], scalar=p1, in1=p2[:, at],
                                                       op0=ALU.add, op1=ALU.add))
                        chain(dve.tensor_tensor(t[:, u, :], t[:, u, :], p3[:, at], ALU.add))
                        dve.scalar_tensor_tensor(out=R.hT[:, at], in0=t[:, u, :], scalar=0.5, in1=R.hT[:, at],
                                                 op0=ALU.mult, op1=ALU.add).then_inc(done, 1)
                    else:
                        dve.wait_ge(evacuated, n + 1)
                        chain(dve.tensor_tensor(t[:, u, :], t[:, u, :], p3[:, at], ALU.add))
                        dve.tensor_tensor(R.hT[:, at], R.hT[:, at], t[:, u, :], ALU.add).then_inc(done, 1)
                chain.close()


def add_arrays(nc, R, tag, dst, a):
    with nc.Block() as block:
        @block.vector
        def _(dve):
            with dve.Fori(0, CHUNKS) as i:
                at = bass.ds(i * CH, CH)
                dve.tensor_tensor(dst[:, at], dst[:, at], a[:, at], ALU.add)


def unit_keys(nc, R, tag, q, dst, dram):
    with ExitStack() as ctx:
        sb, ps, sem = allocators(nc, ctx, tag)
        squares, norm = sb("squares", [P, 2, CH]), sb("norm", [P, 2, CH])
        total = ps("total", [P, 2, CH])
        squared, total_ready, norm_ready, done, stored, order = (
            sem(n) for n in ("squared", "total_ready", "norm_ready", "done", "stored", "order"))
        block = ctx.enter_context(nc.Block())

        @block.scalar
        def _(act):
            with act.Fori(0, CHUNKS // 2) as i:
                for u in range(2):
                    act.wait_ge(done, 2 * i + u + 1)
                    act.wait_ge(total_ready, SLOTS)
                    act.activation(squares[:, u, :], q[:, bass.ds(i * (2 * CH) + u * CH, CH)], ACT.Square).then_inc(
                        squared, 1)
                    act.wait_ge(total_ready, 2 * i + u + 1 + SLOTS)
                    act.activation(norm[:, u, :], total[:, u, :], ACT.Sqrt).then_inc(norm_ready, 1)

        @block.tensor
        def _(pe):
            pe.sem_inc(total_ready, SLOTS)
            with pe.Fori(0, CHUNKS // 2) as i:
                for u in range(2):
                    pe.wait_ge(squared, 2 * i + u + 1)
                    pe.matmul(total[:, u, :], R.c("head_block"), squares[:, u, :], start=True, stop=True).then_inc(
                        total_ready, 1)

        @block.vector
        def _(dve):
            dve.sem_inc(done, SLOTS)
            chain = Chain(dve, order)
            with dve.Fori(0, CHUNKS // 2) as i:
                chain.turn(i, 4)
                for u in range(2):
                    at = bass.ds(i * (2 * CH) + u * CH, CH)
                    dve.wait_ge(norm_ready, 2 * i + u + 1)
                    chain(dve.tensor_scalar(norm[:, u, :], norm[:, u, :], 1e-12, None, ALU.max))
                    chain(dve.reciprocal(norm[:, u, :], norm[:, u, :]))
                    dve.tensor_tensor(dst[:, at], q[:, at], norm[:, u, :], ALU.mult).then_inc(done, 1)
                chain.close()

        @block.sync
        def _(sp):
            with sp.Fori(0, CHUNKS) as i:
                at = bass.ds(i * CH, CH)
                sp.wait_ge(done, i + 1 + SLOTS)
                sp.dma_start(dram[:, at], dst[:, at]).then_inc(stored, 16)
            sp.wait_ge(stored, 16 * CHUNKS)


def hash_groups(nc, R, tag, q_all, groups):
    NB, G = 32, 2 * HEADS
    with ExitStack() as ctx:
        sb, ps, sem = allocators(nc, ctx, tag)
        q = sb("q", [P, 2, T])
        r = sb("r", [HALF, G, 2, NB // 2])
        eq = sb("eq", [HALF, G, NB])
        best, at_bucket, rank = sb("best", [HALF, G]), sb("at_bucket", [HALF, G]), sb("rank", [HALF, G])
        hot, below = sb("hot", [HALF, G, NB], BF16), sb("below", [HALF, G, NB], BF16)
        edge, chunk, reach = sb("edge", [HALF, G, 8]), sb("chunk", [HALF, G, 8]), sb("reach", [HALF, G, 8])
        sides = sb("sides", [HALF, 2, HEADS, 2, 8], BF16)
        flat = sb("flat", [P, 2, T], BF16)
        pr, pk, pt = ps("pr", [HALF, 2, 512]), ps("pk", [HALF, 512]), ps("pt", [P, 2 * T], BF16)
        copied, turned_q, hot_ready, ranked, sides_ready, flat_turned, flat_ready, order = (
            sem(n) for n in ("copied", "turned_q", "hot_ready", "ranked", "sides_ready", "flat_turned", "flat_ready",
                             "order"))
        stored = [sem(f"stored{u}") for u in range(2)]
        block = ctx.enter_context(nc.Block())
        wide_shape = [HALF, G, NB]

        @block.gpsimd
        def _(pool):
            with pool.Fori(0, B // 2) as i:
                for u in range(2):
                    pool.wait_ge(turned_q, 2 * i + u + 1)
                    pool.wait_ge(turned_q, SLOTS)
                    pool.tensor_copy(q[:, u, :], q_all[:, bass.ds(i * (2 * T) + u * T, T)]).then_inc(copied, 1)

        @block.tensor
        def _(pe):
            pe.sem_inc(turned_q, SLOTS)

            def rotate(n, u):
                pe.wait_ge(copied, n + 1)
                pe.wait_ge(hot_ready, n + 1)
                for half in range(2):
                    last = pe.matmul(pr[:, u, P * half:P * half + P], q[:, u, HALF * half:HALF * half + HALF], R.rot[:, :],
                                     start=True, stop=True)
                last.then_inc(turned_q, 1)

            def ranks(n, u):
                pe.wait_ge(hot_ready, n + 1 + SLOTS)
                for half in range(2):
                    out = pk[:, 256 * half:256 * half + 256]
                    one, before = R.bf["ones"][0:HALF, 0:HALF], R.bf["before"][0:HALF, 0:HALF]
                    terms = [(before, hot, half), (one, below, 0), (one, below, 1)] + ([(one, hot, 0)] if half else [])
                    for m, (lhsT, t, side) in enumerate(terms):
                        rhs = t[:, HEADS * side:HEADS * side + HEADS, :].rearrange("p h b -> p (h b)")
                        last = pe.matmul(out, lhsT, rhs, start=(m == 0), stop=(m == len(terms) - 1))
                last.then_inc(ranked, 1)

            def turn(n, u):
                pe.wait_ge(sides_ready, n + 1)
                pe.wait_ge(flat_ready, n + 1)
                for half in range(2):
                    last = pe.transpose(pt[:, HALF * half:HALF * half + HALF],
                                        sides[:, half].rearrange("p h k c -> p (h k c)"), R.bf["ident"][0:HALF, 0:HALF])
                last.then_inc(flat_turned, 1)

            with pe.Fori(0, B // 2) as i:
                for u in range(2):
                    rotate(2 * i + u, u)
                    ranks(2 * i + u, u)
                    turn(2 * i + u, u)

        @block.scalar
        def _(act):
            act.sem_inc(flat_ready, 1)
            with act.Fori(0, B // 2) as i:
                for u in range(2):
                    act.wait_ge(flat_turned, 2 * i + u + 1)
                    act.wait_ge(stored[u], 16 * i + 16)
                    act.copy(flat[:, u, :], pt[:, 0:T]).then_inc(flat_ready, 1)

        @block.sync
        def _(sp):
            for u in range(2):
                sp.sem_inc(stored[u], 16)
            with sp.Fori(0, B // 2) as i:
                for u in range(2):
                    sp.wait_ge(flat_ready, 2 * i + u + 2)
                    sp.dma_start(groups[:, bass.ds(i * (2 * T) + u * T, T)], flat[:, u, :]).then_inc(stored[u], 16)
            for u in range(2):
                sp.wait_ge(stored[u], 16 * (B // 2 + 1))

        @block.vector
        def _(dve):
            chain = Chain(dve, order)
            rev = R.c("rev32", HALF).unsqueeze(1).to_broadcast(wide_shape)
            edges = R.c("chunk_edge", HALF).unsqueeze(1).to_broadcast([HALF, G, 8])

            def wide(v, n=NB):
                return v[:, :].unsqueeze(2).to_broadcast([HALF, G, n])

            chain(dve.memset(sides[:, :, :, :, :], 0.0))
            dve.memset(sides[:, :, :, 0, 6:7], 1.0)
            dve.memset(sides[:, :, :, 1, 6:7], -BIG)
            dve.sem_inc(hot_ready, SLOTS)
            with dve.Fori(0, B // 2) as i:
                chain.turn(i, 2 * 12, 1)
                for u in range(2):
                    n = 2 * i + u
                    dve.wait_ge(turned_q, n + 1 + SLOTS)
                    src = pr[:, u, 0:2 * P].rearrange("p (g b) -> p g b", b=NB // 2)
                    dve.tensor_copy(r[:, :, 0, :], src)
                    chain(dve.tensor_scalar(r[:, :, 1, :], src, -1.0, None, ALU.mult))
                    rr = r[:, :, :, :].rearrange("p g s b -> p g (s b)")
                    chain(dve.tensor_reduce(best[:, :], rr, AX, ALU.max))
                    chain(dve.tensor_tensor(eq[:, :, :], rr, wide(best), ALU.is_equal))
                    chain(dve.tensor_tensor(eq[:, :, :], eq[:, :, :], rev, ALU.mult))
                    chain(dve.tensor_reduce(at_bucket[:, :], eq[:, :, :], AX, ALU.max))
                    chain(dve.tensor_tensor(hot[:, :, :], rev, wide(at_bucket), ALU.is_equal))
                    dve.tensor_tensor(below[:, :, :], rev, wide(at_bucket), ALU.is_lt).then_inc(hot_ready, 1)
                    dve.wait_ge(ranked, n + 1)
                    chain(dve.tensor_tensor(eq[:, :, :], pk[:, 0:512].rearrange("p (g b) -> p g b", b=NB), hot[:, :, :],
                                            ALU.mult))
                    chain(dve.tensor_reduce(rank[:, :], eq[:, :, :], AX, ALU.add))
                    chain(dve.tensor_tensor(edge[:, :, :], wide(rank, 8), edges, ALU.is_ge))
                    chain(dve.tensor_tensor(chunk[:, :, 0:6], edge[:, :, 0:6], edge[:, :, 1:7], ALU.subtract))
                    dve.tensor_tensor(reach[:, :, 1:6], chunk[:, :, 1:6], chunk[:, :, 0:5], ALU.add)
                    chain(dve.tensor_tensor(reach[:, :, 0:1], chunk[:, :, 0:1], chunk[:, :, 5:6], ALU.add))
                    dve.wait_ge(flat_ready, n + 1)
                    s = sides[:, :, :, :, :].rearrange("p a h k c -> p (a h) k c")
                    chain(dve.tensor_copy(s[:, :, 0, 0:6], chunk[:, :, 0:6]))
                    dve.tensor_scalar(s[:, :, 1, 0:6], reach[:, :, 0:6], BIG, None, ALU.mult).then_inc(sides_ready, 1)
                chain.close()


def add_projection(nc, R, tag, src, w, bias, x, dst):
    with ExitStack() as ctx:
        sb, ps, sem = allocators(nc, ctx, tag)
        out = ps("out", [P, 2, CH])
        product_ready, done = sem("product_ready"), sem("done")
        block = ctx.enter_context(nc.Block())

        @block.tensor
        def _(pe):
            with pe.Fori(0, CHUNKS // 2) as i:
                for u in range(2):
                    pe.wait_ge(done, 2 * i + u + 1)
                    pe.matmul(out[:, u, :], w, src[:, bass.ds(i * (2 * CH) + u * CH, CH)], start=True,
                              stop=True).then_inc(product_ready, 1)

        @block.vector
        def _(dve):
            dve.sem_inc(done, SLOTS)
            with dve.Fori(0, CHUNKS // 2) as i:
                for u in range(2):
                    at = bass.ds(i * (2 * CH) + u * CH, CH)
                    dve.wait_ge(product_ready, 2 * i + u + 1)
                    dve.scalar_tensor_tensor(out=dst[:, at], in0=out[:, u, :], scalar=bias, in1=x[:, at], op0=ALU.add,
                                             op1=ALU.add).then_inc(done, 1)


def attention_1(nc, R):
    with ExitStack() as ctx:
        sb, _, _ = allocators(nc, ctx, "a1")
        own, y1, h1 = sb("own", [P, N]), sb("y1", [P, N]), sb("h1", [P, N])
        layer_norm(nc, R, "a1_ln", R.hT, R.xT)
        layer_norm(nc, R, "a1_ln1", R.xT, h1, 1e-5, R.col("L1_attn_ln1_g"), R.col("L1_attn_ln1_b"))
        project(nc, R, "a1_qv", h1, [(R.w["L1_attn_w_qk"][:, :], own, ACT.Identity, 1.0, 0.0),
                                     (R.w["L1_attn_w_v"][:, :], y1, ACT.Identity, 1.0, 0.0)],
                copies=[(0, R.scratch[0]), (1, R.scratch[2])])
        unit_keys(nc, R, "a1_keys", own, y1, R.scratch[1])
        hash_groups(nc, R, "a1_hash", own, R.groups)
        attend(nc, R, "a1", *R.scratch[0:5], HD ** -0.5, R.groups, -50000.0, own)
        divide(nc, R, "a1_div", R.scratch[3], R.scratch[4], h1, own, R.scratch[2])
        add_projection(nc, R, "a1_out", h1, R.w["L1_attn_w_out"][:, :], R.col("L1_attn_b_out"), R.xT, y1)
        layer_norm(nc, R, "a1_ln2", y1, h1, 1e-5, R.col("L1_attn_ln2_g"), R.col("L1_attn_ln2_b"))
        dense_mlp(nc, R, "a1_mlp", h1, lambda k: R.w["L1_attn_w_ff1"][:, C * k:C * k + C], lambda k: 1.0,
                  lambda k: R.col("L1_attn_b_ff1", k), lambda k: R.w["L1_attn_w_ff2"][:, k, :],
                  ("half", R.col("L1_attn_b_ff2"), R.xT, y1))


def attention_2(nc, R):
    with ExitStack() as ctx:
        sb, _, _ = allocators(nc, ctx, "a2")
        q, k, v, o = sb("q", [P, N]), sb("k", [P, N]), sb("v", [P, N]), sb("o", [P, N])
        layer_norm(nc, R, "a2_ln", R.hT, R.xT)
        project(nc, R, "a2_qkv", R.xT, [(R.w[f"L2_attn_W{n}"][:, :], dst, ACT.Relu, 1.0, R.col(f"L2_attn_b{n}"))
                                        for n, dst in (("q", q), ("k", k), ("v", v))])
        one_head(nc, R, "a2", q, k, v, o, HD ** -0.5)
        project(nc, R, "a2_out", o, [(R.w["L2_attn_Wo"][:, :], q, ACT.Relu, 1.0, R.col("L2_attn_bo"))])
        layer_norm(nc, R, "a2_norm", q, R.hT, 1e-3, R.col("L2_attn_gamma"), R.col("L2_attn_beta"), residual=True)


def one_head(nc, R, tag, q_all, k_all, v_all, o_all, scale):
    with ExitStack() as ctx:
        sb, ps, sem = allocators(nc, ctx, tag)
        qkv = sb("qkv", [P, 2, 3, T])
        peak, total = sb("peak", [HALF, 2, 2]), sb("total", [HALF, 2, 2])
        prob, probT, vrow = sb("prob", [HALF, 2, 2, T]), sb("probT", [HALF, 2, 2, T]), sb("vrow", [HALF, 2, 2, C])
        pS, pV, pT, pO = ps("pS", [HALF, 2, 512]), ps("pV", [HALF, 2, 512]), ps("pT", [HALF, 2, 512]), ps("pO", [P, 2, 512])
        loaded = [sem(f"loaded{u}") for u in range(2)]
        scores_ready, v_ready, peak_ready, exp_done, scaled, turned, copied, mixed, done, order = (
            sem(n) for n in ("scores_ready", "v_ready", "peak_ready", "exp_done", "scaled", "turned", "copied", "mixed",
                             "done", "order"))
        block = ctx.enter_context(nc.Block())

        @block.sync
        def _(sp):
            with sp.Fori(0, B // 2) as i:
                for u in range(2):
                    sp.wait_ge(done, 2 * i + u + 1)
                    for j, src in enumerate((q_all, k_all, v_all)):
                        sp.dma_start(qkv[:, u, j, :], src[:, bass.ds(i * (2 * T) + u * T, T)]).then_inc(loaded[u], 16)

        @block.tensor
        def _(pe):
            def scores(n, u, turn):
                pe.wait_ge(loaded[u], 48 * turn + 48)
                pe.wait_ge(done, n + 1)
                for half in range(2):
                    last = pe.matmul(pS[:, u, T * half:T * half + T], qkv[:, u, 0, HALF * half:HALF * half + HALF],
                                     qkv[:, u, 1, :], start=True, stop=True)
                last.then_inc(scores_ready, 1)
                for half in range(2):
                    last = pe.transpose(pV[:, u, C * half:C * half + C], qkv[:, u, 2, HALF * half:HALF * half + HALF],
                                        R.c("ident"))
                last.then_inc(v_ready, 1)

            def mix(n, u):
                pe.wait_ge(scaled, n + 1)
                for a in range(2):
                    for b in range(2):
                        last = pe.transpose(pT[:, u, T * b + HALF * a:T * b + HALF * a + HALF],
                                            prob[:, u, a, HALF * b:HALF * b + HALF], R.c("ident")[0:HALF, 0:HALF])
                last.then_inc(turned, 1)
                pe.wait_ge(copied, 2 * n + 2)
                for b in range(2):
                    last = pe.matmul(pO[:, u, 0:T], vrow[:, u, b, :], probT[:, u, b, :], start=(b == 0), stop=(b == 1))
                last.then_inc(mixed, 1)

            scores(0, 0, 0)
            with pe.Fori(0, B // 2 - 1) as i:
                for u in range(2):
                    scores(2 * i + u + 1, 1 - u, i + u)
                    mix(2 * i + u, u)
            scores(B - 1, 1, B // 2 - 1)
            mix(B - 2, 0)
            mix(B - 1, 1)

        @block.scalar
        def _(act):
            with act.Fori(0, B // 2) as i:
                for u in range(2):
                    n = 2 * i + u
                    act.wait_ge(v_ready, n + 1)
                    act.copy(vrow[:, u, :, :].rearrange("p a c -> p (a c)"), pV[:, u, 0:2 * C]).then_inc(copied, 1)
                    act.wait_ge(peak_ready, n + 1)
                    for half in range(2):
                        last = act.activation(prob[:, u, half, :], pS[:, u, T * half:T * half + T], ACT.Exp, scale=scale,
                                              bias=peak[:, u, half:half + 1], accum_out=total[:, u, half:half + 1])
                    last.then_inc(exp_done, 1)
                    act.wait_ge(turned, n + 1)
                    act.copy(probT[:, u, :, :].rearrange("p a c -> p (a c)"), pT[:, u, 0:2 * T]).then_inc(copied, 1)

        @block.vector
        def _(dve):
            dve.sem_inc(done, SLOTS)
            chain = Chain(dve, order)
            with dve.Fori(0, B // 2) as i:
                chain.turn(i, 4)
                for u in range(2):
                    n = 2 * i + u
                    dve.wait_ge(scores_ready, n + 1)
                    chain(dve.tensor_reduce(peak[:, u, :], pS[:, u, 0:2 * T].rearrange("p (a t) -> p a t", a=2), AX,
                                            ALU.max))
                    dve.tensor_scalar(peak[:, u, :], peak[:, u, :], -scale, None, ALU.mult).then_inc(peak_ready, 1)
                    dve.wait_ge(exp_done, n + 1)
                    chain(dve.reciprocal(total[:, u, :], total[:, u, :]))
                    for half in range(2):
                        last = dve.tensor_scalar(prob[:, u, half, :], prob[:, u, half, :], total[:, u, half:half + 1], None,
                                                 ALU.mult)
                    last.then_inc(scaled, 1)
                    dve.wait_ge(mixed, n + 1)
                    dve.tensor_copy(o_all[:, bass.ds(i * (2 * T) + u * T, T)], pO[:, u, 0:T]).then_inc(done, 1)
                chain.close()


def attention_3(nc, R):
    with ExitStack() as ctx:
        sb, _, _ = allocators(nc, ctx, "a3")
        q, k, v, o = sb("q", [P, N]), sb("k", [P, N]), sb("v", [P, N]), sb("o", [P, N])
        layer_norm(nc, R, "a3_ln", R.hT, R.xT)
        project(nc, R, "a3_qkv", R.xT, [
            (R.wt[f"{s}T"][:, :], dst, ACT.Relu, R.bn[:, 0, n:n + 1], R.bn[:, 1, n:n + 1])
            for n, (s, dst) in enumerate((("q", q), ("k", k), ("v", v)))])
        linear_heads(nc, R, "a3", q, k, v, o, 0.125)
        project(nc, R, "a3_out", o, [(R.wt["pT"][:, :], q, ACT.Relu, R.bn[:, 0, 3:4], R.bn[:, 1, 3:4])])
        add_arrays(nc, R, "a3_x1", q, R.xT)
        dense_mlp(nc, R, "a3_mlp", q, lambda n: R.wt["f1T"][:, C * n:C * n + C], lambda n: R.bn[:, 0, 4 + n:5 + n],
                  lambda n: R.bn[:, 1, 4 + n:5 + n], lambda n: R.wt["f2T"][:, C * n:C * n + C],
                  ("norm", R.bn[:, 0, 8:9], R.bn[:, 1, 8:9], q))


def linear_heads(nc, R, tag, q_all, k_all, v_all, o_all, scale):
    with ExitStack() as ctx:
        sb, ps, sem = allocators(nc, ctx, tag)
        kv = sb("kv", [P, 2, 2, T])
        rows, state = sb("rows", [HALF, 2, 2, 2, C]), sb("state", [P, 2, C])
        pR, pS, pO = ps("pR", [HALF, 2, 512]), ps("pS", [P, 2, 512]), ps("pO", [P, 2, 512])
        loaded = [sem(f"loaded{u}") for u in range(2)]
        turned, rows_ready, product_ready, state_ready, mixed, done = (
            sem(n) for n in ("turned", "rows_ready", "product_ready", "state_ready", "mixed", "done"))
        block = ctx.enter_context(nc.Block())

        @block.sync
        def _(sp):
            with sp.Fori(0, B // 2) as i:
                for u in range(2):
                    sp.wait_ge(done, 2 * i + u + 1)
                    for j, src in enumerate((k_all, v_all)):
                        sp.dma_start(kv[:, u, j, :], src[:, bass.ds(i * (2 * T) + u * T, T)]).then_inc(loaded[u], 16)

        @block.tensor
        def _(pe):
            def turn(n, u, t):
                pe.wait_ge(loaded[u], 32 * t + 32)
                pe.wait_ge(done, n + 1)
                for j in range(2):
                    for half in range(2):
                        a = C * (2 * j + half)
                        last = pe.transpose(pR[:, u, a:a + C], kv[:, u, j, HALF * half:HALF * half + HALF], R.c("ident"))
                last.then_inc(turned, 1)

            def mix(n, u, i):
                pe.wait_ge(rows_ready, n + 1)
                for half in range(2):
                    last = pe.matmul(pS[:, u, 0:C], rows[:, u, 0, half, :], rows[:, u, 1, half, :], start=(half == 0),
                                     stop=(half == 1))
                last.then_inc(product_ready, 1)
                pe.wait_ge(state_ready, n + 1)
                pe.matmul(pO[:, u, 0:T], state[:, u, :], q_all[:, bass.ds(n * T, T)], start=True, stop=True).then_inc(mixed, 1)

            turn(0, 0, 0)
            with pe.Fori(0, B // 2 - 1) as i:
                for u in range(2):
                    turn(2 * i + u + 1, 1 - u, i + u)
                    mix(2 * i + u, u, i)
            turn(B - 1, 1, B // 2 - 1)
            mix(B - 2, 0, 0)
            mix(B - 1, 1, 0)

        @block.scalar
        def _(act):
            act.sem_inc(done, SLOTS)
            with act.Fori(0, B // 2) as i:
                for u in range(2):
                    n = 2 * i + u
                    act.wait_ge(turned, n + 1)
                    act.copy(rows[:, u].rearrange("p j a c -> p (j a c)"), pR[:, u, :]).then_inc(rows_ready, 1)
                    act.wait_ge(mixed, n + 1)
                    act.activation(o_all[:, bass.ds(i * (2 * T) + u * T, T)], pO[:, u, 0:T], ACT.Relu).then_inc(done, 1)

        @block.vector
        def _(dve):
            with dve.Fori(0, B // 2) as i:
                for u in range(2):
                    dve.wait_ge(product_ready, 2 * i + u + 1)
                    dve.scalar_tensor_tensor(out=state[:, u, :], in0=pS[:, u, 0:C], scalar=scale, in1=R.c("head_block"),
                                             op0=ALU.mult, op1=ALU.mult).then_inc(state_ready, 1)


N_IN, N_PROC, N_OUT, D_PV = 512, 256, 512, 64
K_IN, K_PROC, K_OUT = 64, 128, 64


def pattern_weights(nc, R, w):
    with ExitStack() as ctx:
        sb, ps, sem = allocators(nc, ctx, "f2w")
        raw_in, raw_p, raw_o = sb("raw_in", [P, 4, C]), sb("raw_p", [P, 2, N_IN]), sb("raw_o", [P, 4, D_PV])
        pi, pp, po = ps("pi", [P, 512]), ps("pp", [P, 2, 512]), ps("po", [D_PV, 512])
        loaded, zeroed, turned = sem("loaded"), sem("zeroed"), sem("turned")
        block = ctx.enter_context(nc.Block())
        i = R.ins

        @block.sync
        def _(sp):
            sp.wait_ge(zeroed, 1)
            for dst, src in ((raw_in[:, :, :], i["L2_ffn_input_patterns"].rearrange("(k p) d -> p k d", p=P)),
                             (raw_p[:, :, :], i["L2_ffn_process_input_weights"].rearrange("(k p) n -> p k n", p=P)),
                             (raw_o[:, :, :], i["L2_ffn_output_input_weights"].rearrange("(k p) d -> p k d", p=P)),
                             (w["pv"][:, :, 0:D_PV], i["L2_ffn_process_values"].rearrange("(k p) d -> p k d", p=P)),
                             (w["op"][:, :, :], i["L2_ffn_output_patterns"].rearrange("(k p) m -> p k m", p=P))):
                sp.dma_start(dst, src).then_inc(loaded, 16)

        @block.tensor
        def _(pe):
            pe.wait_ge(loaded, 80)
            for k in range(4):
                pe.transpose(pi[:, P * k:P * k + P], raw_in[:, k, :], R.c("ident"))
                pe.transpose(po[:, P * k:P * k + P], raw_o[:, k, :], R.c("ident"))
            for k in range(2):
                for n in range(4):
                    a = 256 * n + P * k
                    last = pe.transpose(pp[:, a // 512, a % 512:a % 512 + P], raw_p[:, k, P * n:P * n + P], R.c("ident"))
            last.then_inc(turned, 1)

        @block.vector
        def _(dve):
            dve.memset(w["pv"][:, :, :], 0.0)
            dve.memset(w["oiT"][:, :], 0.0).then_inc(zeroed, 1)
            dve.wait_ge(turned, 1)
            dve.wait_ge(zeroed, 1)
            dve.tensor_copy(w["ipT"][:, :], pi[:, :])
            dve.tensor_copy(w["oiT"][0:D_PV, :], po[:, :])
            dve.tensor_copy(w["piT"][:, :, :].rearrange("p n k -> p (n k)"), pp[:, :, :].rearrange("p a b -> p (a b)"))


def feed_forward_2(nc, R):
    NEVER = -1e30
    with ExitStack() as ctx:
        sb, ps, sem = allocators(nc, ctx, "f2")
        layer_norm(nc, R, "f2_ln", R.hT, R.xT)
        w = {"ipT": sb("ipT", [P, N_IN]), "piT": sb("piT", [P, 4, N_PROC]), "pv": sb("pv", [P, 2, C]),
             "oiT": sb("oiT", [P, N_OUT]), "op": sb("op", [P, 4, C])}
        pattern_weights(nc, R, w)
        x = sb("x", [P, 2, P])
        act_in, act_proc, act_out = sb("act_in", [P, 2, N_IN]), sb("act_proc", [P, 2, N_PROC]), sb("act_out", [P, 2, N_OUT])
        sel_in, sel_proc, sel_out = sb("sel_in", [P, 2, N_IN]), sb("sel_proc", [P, 2, N_PROC]), sb("sel_out", [P, 2, N_OUT])
        soft = sb("soft", [P, 2, N_PROC])
        inT, procT, outT, aggT = sb("inT", [P, 2, N_IN]), sb("procT", [P, 2, N_PROC]), sb("outT", [P, 2, N_OUT]), sb(
            "aggT", [P, 2, P])
        top, peak, total = sb("top", [P, 2, 8]), sb("peak", [P, 2, 1]), sb("total", [P, 2, 1])
        bank = [ps(f"bank{u}", [P, 512]) for u in range(2)]
        turn = [ps(f"turn{u}", [P, 512]) for u in range(2)]
        small = [ps(f"small{u}", [P, 512]) for u in range(2)]
        names = ("copied", "in_ready", "in_acted", "in_selected", "in_turned", "in_evacuated", "proc_ready", "proc_acted",
                 "peak_ready", "soft_ready", "proc_selected", "proc_turned", "proc_evacuated", "agg_ready", "agg_evacuated",
                 "out_ready", "out_acted", "out_selected", "out_turned", "out_evacuated", "y_ready", "done", "order")
        s = {n: sem(n) for n in names}
        block = ctx.enter_context(nc.Block())
        PAIRS = TILES // 2

        @block.gpsimd
        def _(pool):
            with pool.Fori(0, PAIRS) as i:
                for u in range(2):
                    pool.wait_ge(s["in_ready"], 2 * i + u + 1)
                    pool.wait_ge(s["in_ready"], SLOTS)
                    pool.tensor_copy(x[:, u, :], R.xT[:, bass.ds(i * (2 * P) + u * P, P)]).then_inc(s["copied"], 1)

        @block.tensor
        def _(pe):
            pe.sem_inc(s["in_ready"], SLOTS)

            def product_in(n, u):
                pe.wait_ge(s["copied"], n + 1)
                pe.wait_ge(s["out_acted"], n + 1)
                pe.matmul(bank[u][:, :], x[:, u, :], w["ipT"][:, :], start=True, stop=True).then_inc(s["in_ready"], 1)

            def turned(src, n_blocks, selected, count, signal, u):
                pe.wait_ge(s[selected], count)
                for k in range(n_blocks):
                    last = pe.transpose(turn[u][:, P * k:P * k + P], src[:, u, P * k:P * k + P], R.c("ident"))
                last.then_inc(s[signal], 1)

            for u in range(2):
                product_in(u, u)

            def pair(i, more):
                for u in range(2):
                    n = 2 * i + u
                    turned(sel_in, 4, "in_selected", n + 1 + SLOTS, "in_turned", u)
                    pe.wait_ge(s["in_evacuated"], n + 1)
                    for k in range(4):
                        last = pe.matmul(bank[u][:, 0:N_PROC], inT[:, u, P * k:P * k + P], w["piT"][:, k, :],
                                         start=(k == 0), stop=(k == 3))
                    last.then_inc(s["proc_ready"], 1)
                for u in range(2):
                    n = 2 * i + u
                    turned(sel_proc, 2, "proc_selected", n + 1, "proc_turned", u)
                    pe.wait_ge(s["proc_evacuated"], n + 1)
                    pe.wait_ge(s["done"], n + 1)
                    for k in range(2):
                        last = pe.matmul(small[u][:, 0:P], w["pv"][:, k, :], procT[:, u, P * k:P * k + P],
                                         start=(k == 0), stop=(k == 1))
                    last.then_inc(s["agg_ready"], 1)
                    pe.wait_ge(s["agg_evacuated"], n + 1)
                    pe.matmul(bank[u][:, :], aggT[:, u, :], w["oiT"][:, :], start=True, stop=True).then_inc(
                        s["out_ready"], 1)
                if more:
                    for u in range(2):
                        product_in(2 * i + 2 + u, u)
                for u in range(2):
                    n = 2 * i + u
                    turned(sel_out, 4, "out_selected", n + 1, "out_turned", u)
                    pe.wait_ge(s["out_evacuated"], n + 1)
                    for k in range(4):
                        last = pe.matmul(small[u][:, P:2 * P], w["op"][:, k, :], outT[:, u, P * k:P * k + P],
                                         start=(k == 0), stop=(k == 3))
                    last.then_inc(s["y_ready"], 1)

            with pe.Fori(0, PAIRS - 1) as i:
                pair(i, True)
            pair(PAIRS - 1, False)

        @block.scalar
        def _(act):
            act.sem_inc(s["out_acted"], SLOTS)

            def gelu_in(n, u):
                act.wait_ge(s["in_ready"], n + 1 + SLOTS)
                act.wait_ge(s["in_selected"], n + 1)
                act.activation(act_in[:, u, :], bank[u][:, :], ACT.Gelu).then_inc(s["in_acted"], 1)

            for u in range(2):
                gelu_in(u, u)

            def pair(i, more):
                for u in range(2):
                    n = 2 * i + u
                    act.wait_ge(s["in_turned"], n + 1)
                    act.copy(inT[:, u, :], turn[u][:, :]).then_inc(s["in_evacuated"], 1)
                    act.wait_ge(s["proc_ready"], n + 1)
                    act.activation(act_proc[:, u, :], bank[u][:, 0:N_PROC], ACT.Gelu).then_inc(s["proc_acted"], 1)
                for u in range(2):
                    n = 2 * i + u
                    act.wait_ge(s["peak_ready"], n + 1)
                    act.activation(soft[:, u, :], act_proc[:, u, :], ACT.Exp, bias=peak[:, u, :]).then_inc(
                        s["soft_ready"], 1)
                for u in range(2):
                    n = 2 * i + u
                    act.wait_ge(s["proc_turned"], n + 1)
                    act.copy(procT[:, u, :], turn[u][:, 0:N_PROC]).then_inc(s["proc_evacuated"], 1)
                    act.wait_ge(s["agg_ready"], n + 1)
                    act.copy(aggT[:, u, :], small[u][:, 0:P]).then_inc(s["agg_evacuated"], 1)
                    act.wait_ge(s["out_ready"], n + 1)
                    act.activation(act_out[:, u, :], bank[u][:, :], ACT.Gelu).then_inc(s["out_acted"], 1)
                if more:
                    for u in range(2):
                        gelu_in(2 * i + 2 + u, u)
                for u in range(2):
                    n = 2 * i + u
                    act.wait_ge(s["out_turned"], n + 1)
                    act.copy(outT[:, u, :], turn[u][:, :]).then_inc(s["out_evacuated"], 1)

            with act.Fori(0, PAIRS - 1) as i:
                pair(i, True)
            pair(PAIRS - 1, False)

        @block.vector
        def _(dve):
            dve.sem_inc(s["done"], SLOTS)
            dve.sem_inc(s["in_selected"], SLOTS)
            chain = Chain(dve, s["order"])

            def select(src, marked, u, k, peaks=False, n=None):
                chain(dve.memset(top[:, u, :], 0.0))
                for r in range(k // 8):
                    a = src if r == 0 else marked
                    chain(dve.max(top[:, u, :], a[:, u, :]))
                    if peaks and r == 0:
                        dve.tensor_scalar(peak[:, u, :], top[:, u, 0:1], -1.0, None, ALU.mult).then_inc(s["peak_ready"], 1)
                    chain(dve.match_replace(marked[:, u, :], top[:, u, :], a[:, u, :], NEVER))

            with dve.Fori(0, PAIRS) as i:
                chain.restart()
                for u in range(2):
                    n = 2 * i + u
                    dve.wait_ge(s["in_acted"], n + 1)
                    select(act_in, sel_in, u, K_IN)
                    dve.scalar_tensor_tensor(out=sel_in[:, u, :], in0=sel_in[:, u, :], scalar=NEVER, in1=act_in[:, u, :],
                                             op0=ALU.is_equal, op1=ALU.mult).then_inc(s["in_selected"], 1)
                for u in range(2):
                    n = 2 * i + u
                    dve.wait_ge(s["proc_acted"], n + 1)
                    select(act_proc, sel_proc, u, K_PROC, True, n)
                    dve.wait_ge(s["soft_ready"], n + 1)
                    chain(dve.scalar_tensor_tensor(out=sel_proc[:, u, :], in0=sel_proc[:, u, :], scalar=NEVER,
                                                   in1=soft[:, u, :], op0=ALU.is_equal, op1=ALU.mult,
                                                   accum_out=total[:, u, :]))
                    chain(dve.reciprocal(total[:, u, :], total[:, u, :]))
                    dve.tensor_scalar(sel_proc[:, u, :], sel_proc[:, u, :], total[:, u, :], None, ALU.mult).then_inc(
                        s["proc_selected"], 1)
                for u in range(2):
                    n = 2 * i + u
                    dve.wait_ge(s["out_acted"], n + 1 + SLOTS)
                    select(act_out, sel_out, u, K_OUT)
                    dve.scalar_tensor_tensor(out=sel_out[:, u, :], in0=sel_out[:, u, :], scalar=NEVER,
                                             in1=act_out[:, u, :], op0=ALU.is_equal, op1=ALU.mult).then_inc(
                        s["out_selected"], 1)
                for u in range(2):
                    n = 2 * i + u
                    at = bass.ds(i * (2 * P) + u * P, P)
                    dve.wait_ge(s["y_ready"], n + 1)
                    dve.tensor_tensor(R.hT[:, at], small[u][:, P:2 * P], R.hT[:, at], ALU.add).then_inc(s["done"], 1)


STAGES = {
    "tokens": tokens,
    "attention_0": attention_0,
    "feed_forward_0": feed_forward_0,
    "attention_1": attention_1,
    "feed_forward_1": feed_forward_1,
    "attention_2": attention_2,
    "feed_forward_2": feed_forward_2,
    "attention_3": attention_3,
    "feed_forward_3": feed_forward_3,
}


def program(nc, ins, out, only=None, h_in=None, dump=None):
    with ExitStack() as ctx:
        R = Resident(nc, ctx, ins, out)
        R.eps = {e: ctx.enter_context(nc.sbuf_tensor(f"eps{k}", [P, 1], F32)) for k, e in enumerate((1e-5, 1e-3))}
        R.scratch = [nc.dram_tensor(f"scratch{n}", (P, N), F32, kind="Internal").ap() for n in range(6)]
        R.groups = nc.dram_tensor("lsh_groups", (P, N), BF16, kind="Internal").ap()
        R.self_value = ctx.enter_context(nc.sbuf_tensor("self_value", [P, 1], F32))
        with nc.Block() as block:
            @block.vector
            def _(dve):
                for e, t in R.eps.items():
                    dve.memset(t[:, :], e)
                dve.memset(R.self_value[:, :], -50000.0)
        set_up(nc, R)
        if h_in is not None:
            with nc.semaphore("hin") as s, nc.Block() as block:
                @block.sync
                def _(sp):
                    sp.dma_start(R.hT[:, :], h_in).then_inc(s, 16)
                    sp.wait_ge(s, 16)
        for name in (only or STAGES):
            STAGES[name](nc, R)
        if dump is not None:
            with nc.semaphore("hdump") as s, nc.Block() as block:
                @block.sync
                def _(sp):
                    sp.dma_start(dump, (R.hT if only[-1] != "ln" else R.xT)[:, :]).then_inc(s, 16)
                    sp.wait_ge(s, 16)


def kernel(**inputs):
    import concourse.bacc as bacc
    from concourse.bass_utils import run_bass_kernel_spmd

    nc = bacc.Bacc("TRN2", target_bir_lowering=False, num_devices=1)
    arrays, ins = {}, {}
    for name, a in list(inputs.items()) + [("consts", CONSTS)]:
        a = np.ascontiguousarray(a)
        arrays[f"in_{name}_dram"] = a
        ins[name] = nc.dram_tensor(f"in_{name}_dram", a.shape, mybir.dt.from_np(a.dtype), kind="ExternalInput").ap()
    out = nc.dram_tensor("out_0_dram", (B, T, C), F32, kind="ExternalOutput").ap()
    program(nc, ins, out)
    r = run_bass_kernel_spmd(nc, [arrays], core_ids=[0])
    return r.results[0]["out_0_dram"]
```

```python
from contextlib import ExitStack

import numpy as np

import concourse.bass as bass
from concourse import mybir

ALU = mybir.AluOpType
ACT = mybir.ActivationFunctionType
AX = mybir.AxisListType.X
F32 = mybir.dt.float32
BF16 = mybir.dt.bfloat16

P = 128
C = 128
B = 16
GRID = 8
IMG_TOKENS = GRID * GRID
TXT_TOKENS = 128
T = IMG_TOKENS + TXT_TOKENS
N = B * T
HALF = T // 2
HEADS = 8
HD = C // HEADS
TILES = N // P
CH = 512
CHUNKS = N // CH
BIG = 2.0 ** 100
PAD = GRID + 2
SLOTS = 2


def shape_constants():
    parts, at = {}, 0
    out = []

    def put(name, a):
        nonlocal at
        full = np.zeros((P, a.shape[1]), np.float32)
        full[:a.shape[0]] = a
        out.append(full)
        parts[name] = (at, at + a.shape[1])
        at += a.shape[1]

    eye = np.eye(P, dtype=np.float32)
    put("ident", eye)
    put("centre", eye - np.float32(1.0 / C))
    put("mean", np.full((P, P), 1.0 / C, np.float32))
    put("ones", np.ones((P, P), np.float32))
    rows = np.zeros((P, 3, PAD, 2), np.float32)
    for p in range(P):
        row, side = p // 2, p % 2
        kind = {0: 1, 7: 2}.get(row % 8, 0)
        rows[p, kind, row // 8 + 1, side] = 1.0
    put("rows", rows.reshape(P, -1))
    block = np.kron(np.eye(HEADS, dtype=np.float32), np.ones((HD, HD), np.float32))
    put("head_block", block)
    put("before", np.triu(np.ones((P, P), np.float32), 1))
    put("neg_diag", (-BIG * eye[:, :HALF]).astype(np.float32))
    put("rev32", np.tile(32.0 - np.arange(32, dtype=np.float32), (P, 1)))
    put("rev8", np.tile(8.0 - np.arange(8, dtype=np.float32), (P, 1)))
    put("iota8", np.tile(np.arange(8, dtype=np.float32), (P, 1)))
    put("chunk_edge", np.tile(32.0 * np.arange(8, dtype=np.float32), (P, 1)))
    last = np.zeros((P, 1), np.float32)
    last[P - 1] = 1.0
    put("last_row", last)
    spread = np.zeros((2 * HEADS, 2, HEADS, HD), np.float32)
    for h in range(HEADS):
        for s in range(2):
            spread[HEADS * s + h, s, h] = 1.0
    put("spread", spread.reshape(2 * HEADS, -1))
    return np.concatenate(out, 1), parts


CONSTS, WHERE = shape_constants()

VECTORS = [
    ("L0_tok_conv_b", 1), ("L0_attn_b_qkv", 3),
    ("L1_attn_b_out", 1), ("L1_attn_ln1_g", 1), ("L1_attn_ln1_b", 1), ("L1_attn_b_ff1", 4), ("L1_attn_b_ff2", 1),
    ("L1_attn_ln2_g", 1), ("L1_attn_ln2_b", 1),
    ("L2_attn_bq", 1), ("L2_attn_bk", 1), ("L2_attn_bv", 1), ("L2_attn_bo", 1), ("L2_attn_gamma", 1),
    ("L2_attn_beta", 1),
]
for _s in ("q", "k", "v", "p", "f1", "f2"):
    for _v in ("b", "g", "be", "m", "v"):
        VECTORS.append((f"L3_attn_{_s}_{_v}", 4 if _s == "f1" else 1))
VECTORS.append(("L0_tok_conv_w", 9))
COLUMN, _at = {}, 0
for _n, _k in VECTORS:
    COLUMN[_n] = _at
    _at += _k
NCOL = _at

WEIGHTS = [
    ("L0_attn_W_qkv", 3 * C), ("L1_attn_w_qk", C), ("L1_attn_w_v", C), ("L1_attn_w_out", C), ("L1_attn_w_ff1", 4 * C),
    ("L2_attn_Wq", C), ("L2_attn_Wk", C), ("L2_attn_Wv", C), ("L2_attn_Wo", C), ("L1_ffn_Wg", 32), ("L0_ffn_Wr", 8),
    ("L3_ffn_Wr", 64),
]


class Chain:

    def __init__(self, eng, sem):
        self.eng, self.sem, self.base, self.n = eng, sem, 0, 0

    def __call__(self, ins):
        ins.then_inc(self.sem, 1)
        self.n += 1
        self.eng.wait_ge(self.sem, self.base + self.n)

    def turn(self, i, per, before=0):
        self.base, self.n = i * per + before, 0
        self.per = per

    def late(self, ins):
        ins.then_inc(self.sem, 1)
        self.n += 1
        if self.n > 1:
            self.eng.wait_ge(self.sem, self.base + self.n - 1)

    def catch_up(self):
        self.eng.wait_ge(self.sem, self.base + self.n)

    def restart(self):
        self.eng.sem_clear(self.sem)
        self.n = 0

    def close(self):
        assert self.n == self.per, (self.n, self.per)

    def after(self, total):
        self.base, self.n = total, 0


class Resident:

    def __init__(self, nc, ctx, ins, out):
        self.ins, self.out = ins, out

        def sb(name, shape, dt=F32):
            return ctx.enter_context(nc.sbuf_tensor(name, shape, dt))

        self.hT = sb("hT", [P, N])
        self.xT = sb("xT", [P, N])
        self.cst = sb("cst", [P, CONSTS.shape[1]])
        self.bf = {}
        for name in ("ident", "ones", "before", "neg_diag"):
            a, b = WHERE[name]
            self.bf[name] = sb(f"bf_{name}", [P, b - a], BF16)
        self.columns = sb("columns", [P, NCOL])
        self.w = {name: sb(name, [P, n]) for name, n in WEIGHTS}
        self.w["L1_attn_w_ff2"] = sb("L1_attn_w_ff2", [P, 4, C])
        self.tap = sb("tap", [P, 25])
        self.bn = sb("bn", [P, 2, 9])
        self.rot = sb("rot", [P, P])
        self.wt = {name: sb(name, [P, n]) for name, n in (
            ("qT", C), ("kT", C), ("vT", C), ("pT", C), ("f1T", 4 * C), ("f2T", 4 * C))}

    def c(self, name, rows=P):
        a, b = WHERE[name]
        return self.cst[0:rows, a:b]

    def col(self, name, k=0):
        a = COLUMN[name] + k
        return self.columns[:, a:a + 1]


def allocators(nc, ctx, tag):
    held = []

    def over():
        if held:
            nc.clear_and_free_semaphores(held)
            nc.all_engine_barrier()

    ctx.callback(over)

    def sb(name, shape, dt=F32):
        return ctx.enter_context(nc.sbuf_tensor(f"{tag}_{name}", shape, dt))

    def ps(name, shape, dt=F32):
        return ctx.enter_context(nc.psum_tensor(f"{tag}_{name}", shape, dt))

    def sem(name):
        held.append(nc.alloc_semaphore(name=f"{tag}_{name}"))
        return held[-1]

    return sb, ps, sem


def set_up(nc, R):
    ins = R.ins
    with ExitStack() as ctx:
        sb, ps, sem = allocators(nc, ctx, "setup")
        rows = sb("rows", [NCOL, C])
        raw = {s: sb(f"raw_{s}", [P, C]) for s in "qkvp"}
        raw_f1 = sb("raw_f1", [P, 4, C])
        raw_f2 = sb("raw_f2", [P, 4 * C])
        edge = sb("edge", [P, 5, 3])
        root = sb("root", [P, 9])
        pv = ps("pv", [P, 512])
        pt = ps("pt", [P, 4, 512])
        loaded, rot_zeroed, transposed, columns_ready, turned = (
            sem(n) for n in ("loaded", "rot_zeroed", "transposed", "columns_ready", "turned"))
        rot_loaded, rooted, order = sem("rot_loaded"), sem("rooted"), sem("order")
        block = ctx.enter_context(nc.Block())
        n_loads = 1 + len(VECTORS) + len(WEIGHTS) + 1 + 6
        bn_at = {"q": (0, 1), "k": (1, 1), "v": (2, 1), "p": (3, 1), "f1": (4, 4), "f2": (8, 1)}

        @block.sync
        def _(sp):
            sp.dma_start(R.cst[:, :], ins["consts"]).then_inc(loaded, 16)
            for name, n in WEIGHTS:
                sp.dma_start(R.w[name][:, :], ins[name]).then_inc(loaded, 16)
            sp.dma_start(R.w["L1_attn_w_ff2"][:, :, :],
                         ins["L1_attn_w_ff2"].rearrange("(k p) n -> p k n", p=P)).then_inc(loaded, 16)
            for s in "qkvp":
                sp.dma_start(raw[s][:, :], ins[f"L3_attn_{s}_w"]).then_inc(loaded, 16)
            sp.dma_start(raw_f1[:, :, :], ins["L3_attn_f1_w"].rearrange("(k p) n -> p k n", p=P)).then_inc(loaded, 16)
            sp.dma_start(raw_f2[:, :], ins["L3_attn_f2_w"]).then_inc(loaded, 16)

        @block.scalar
        def _(act):
            for name, n in VECTORS:
                a = COLUMN[name]
                src = ins[name]
                src = src.rearrange("a b o c -> (a b o) c") if name == "L0_tok_conv_w" else \
                    src.rearrange("(k p) -> k p", p=C)
                act.dma_start(rows[a:a + n, :], src).then_inc(loaded, 16)
            act.wait_ge(rot_zeroed, 1)
            for h in range(HEADS):
                act.dma_start(R.rot[HD * h:HD * h + HD, HD * h:HD * h + HD],
                              ins["L1_attn_rotations"]).then_inc(rot_loaded, 16)
            act.wait_ge(rot_loaded, 16 * HEADS)
            act.wait_ge(columns_ready, 2)
            for s, (a, n) in bn_at.items():
                last = act.activation(root[:, a:a + n], root[:, a:a + n], ACT.Sqrt)
            last.then_inc(rooted, 1)

        @block.tensor
        def _(pe):
            pe.wait_ge(loaded, 16 * n_loads)
            pe.transpose(pv[0:C, 0:NCOL], rows[:, :], R.c("ident")[0:NCOL, 0:NCOL]).then_inc(transposed, 1)
            for n, s in enumerate("qkvp"):
                last = pe.transpose(pt[:, 0, C * n:C * n + C], raw[s][:, :], R.c("ident"))
            last.then_inc(transposed, 1)
            for k in range(4):
                last = pe.transpose(pt[:, 1, C * k:C * k + C], raw_f1[:, k, :], R.c("ident"))
            last.then_inc(transposed, 1)
            for k in range(4):
                last = pe.transpose(pt[:, 2, C * k:C * k + C], raw_f2[:, C * k:C * k + C], R.c("ident"))
            last.then_inc(transposed, 1)

        @block.vector
        def _(dve):
            chain = Chain(dve, order)
            dve.memset(R.rot[:, :], 0.0).then_inc(rot_zeroed, 1)
            dve.wait_ge(loaded, 16 * n_loads)
            for name, t in R.bf.items():
                dve.tensor_copy(t[:, :], R.c(name))
            dve.wait_ge(transposed, 1)
            dve.tensor_copy(R.columns[:, :], pv[:, 0:NCOL]).then_inc(columns_ready, 1)
            dve.wait_ge(columns_ready, 1)
            for s, (a, n) in bn_at.items():
                v = COLUMN[f"L3_attn_{s}_v"]
                last = dve.tensor_scalar(root[:, a:a + n], R.columns[:, v:v + n], 1e-5, None, ALU.add)
            last.then_inc(columns_ready, 1)
            for k, n in enumerate("qkvp"):
                dve.wait_ge(transposed, 2)
                dve.tensor_copy(R.wt[f"{n}T"][:, :], pt[:, 0, C * k:C * k + C])
            dve.wait_ge(transposed, 3)
            dve.tensor_copy(R.wt["f1T"][:, :], pt[:, 1, :])
            dve.wait_ge(transposed, 4)
            dve.tensor_copy(R.wt["f2T"][:, :], pt[:, 2, :])
            w0 = COLUMN["L0_tok_conv_w"]
            tap = [R.columns[:, w0 + 3 * d:w0 + 3 * d + 3] for d in range(3)]
            chain(dve.tensor_tensor(edge[:, 1, :], tap[0], tap[1], ALU.add))
            dve.tensor_tensor(edge[:, 2, :], tap[1], tap[2], ALU.add)
            dve.tensor_copy(edge[:, 3, :], tap[0])
            dve.tensor_copy(edge[:, 4, :], tap[2])
            chain(dve.tensor_tensor(edge[:, 0, :], edge[:, 1, :], tap[2], ALU.add))
            t5 = R.tap[:, :].rearrange("p (r c) -> p r c", c=5)
            chain(dve.tensor_tensor(t5[:, :, 1], edge[:, :, 0], edge[:, :, 1], ALU.add))
            dve.tensor_tensor(t5[:, :, 2], edge[:, :, 1], edge[:, :, 2], ALU.add)
            dve.tensor_copy(t5[:, :, 3], edge[:, :, 0])
            dve.tensor_copy(t5[:, :, 4], edge[:, :, 2])
            chain(dve.tensor_tensor(t5[:, :, 0], t5[:, :, 1], edge[:, :, 2], ALU.add))
            dve.wait_ge(rooted, 1)
            chain(dve.reciprocal(root[:, :], root[:, :]))
            for s, (a, n) in bn_at.items():
                b, g, be, m = (COLUMN[f"L3_attn_{s}_{v}"] for v in ("b", "g", "be", "m"))
                dve.tensor_tensor(R.bn[:, 1, a:a + n], R.columns[:, b:b + n], R.columns[:, m:m + n], ALU.subtract)
                last = dve.tensor_tensor(R.bn[:, 0, a:a + n], root[:, a:a + n], R.columns[:, g:g + n], ALU.mult)
            chain(last)
            chain(dve.tensor_tensor(R.bn[:, 1, :], R.bn[:, 1, :], R.bn[:, 0, :], ALU.mult))
            for s, (a, n) in bn_at.items():
                be = COLUMN[f"L3_attn_{s}_be"]
                dve.tensor_tensor(R.bn[:, 1, a:a + n], R.bn[:, 1, a:a + n], R.columns[:, be:be + n], ALU.add)


def layer_norm(nc, R, tag, src, dst, eps=1e-5, gain=None, bias=None, residual=False):
    WAVE = 3
    SUB = CH // P
    with ExitStack() as ctx:
        sb, ps, sem = allocators(nc, ctx, tag)
        squares, rstd, scaled = sb("squares", [P, WAVE, CH]), sb("rstd", [P, WAVE, CH]), sb("scaled", [P, WAVE, CH])
        diag, root = sb("diag", [P, WAVE, CH]), sb("root", [P, WAVE, SUB])
        inverse = sb("inverse", [P, WAVE, SUB])
        centred, spread = ps("centred", [P, WAVE, CH]), ps("spread", [P, WAVE, CH])
        centred_ready, squared, var_ready, rooted, diag_ready, spread_ready, rstd_ready, done, order = (
            sem(n) for n in ("centred_ready", "squared", "var_ready", "rooted", "diag_ready", "spread_ready",
                             "rstd_ready", "done", "order"))
        block = ctx.enter_context(nc.Block())

        @block.tensor
        def _(pe):
            with pe.Fori(0, CHUNKS // WAVE) as i:
                for u in range(WAVE):
                    pe.wait_ge(done, WAVE * i + u + 1)
                    pe.matmul(centred[:, u, :], R.c("centre"), src[:, bass.ds(i * (WAVE * CH) + u * CH, CH)],
                              start=True, stop=True).then_inc(centred_ready, 1)
                for u in range(WAVE):
                    pe.wait_ge(squared, WAVE * i + u + 1)
                    for s in range(SUB):
                        last = pe.matmul(spread[:, u, s:s + 1], squares[:, u, P * s:P * s + P], R.c("mean")[:, 0:1],
                                         start=(s == 0), stop=(s == SUB - 1), skip_group_check=True)
                    last.then_inc(var_ready, 1)
                for u in range(WAVE):
                    pe.wait_ge(diag_ready, WAVE * i + u + 1)
                    pe.matmul(spread[:, u, :], R.c("mean"), diag[:, u, :], start=True, stop=True).then_inc(
                        spread_ready, 1)

        @block.scalar
        def _(act):
            with act.Fori(0, CHUNKS // WAVE) as i:
                for u in range(WAVE):
                    act.wait_ge(centred_ready, WAVE * i + u + 1)
                    act.activation(squares[:, u, :], centred[:, u, :], ACT.Square).then_inc(squared, 1)
                for u in range(WAVE):
                    act.wait_ge(var_ready, WAVE * i + u + 1)
                    act.activation(root[:, u, :], spread[:, u, 0:SUB], ACT.Sqrt, bias=R_eps(R, eps)).then_inc(rooted, 1)
                for u in range(WAVE):
                    act.wait_ge(spread_ready, WAVE * i + u + 1)
                    act.copy(rstd[:, u, :], spread[:, u, :]).then_inc(rstd_ready, 1)

        @block.vector
        def _(dve):
            dve.sem_inc(done, WAVE)
            chain = Chain(dve, order)
            with dve.Fori(0, CHUNKS // WAVE) as i:
                chain.turn(i, WAVE * (1 + (gain is not None) + residual))
                for u in range(WAVE):
                    dve.wait_ge(rooted, WAVE * i + u + 1)
                    chain(dve.reciprocal(inverse[:, u, :], root[:, u, :]))
                    for s in range(SUB):
                        last = dve.tensor_scalar(diag[:, u, P * s:P * s + P], R.c("ident"), inverse[:, u, s:s + 1],
                                                 float(P), ALU.mult, ALU.mult)
                    last.then_inc(diag_ready, 1)
                for u in range(WAVE):
                    at = bass.ds(i * (WAVE * CH) + u * CH, CH)
                    dve.wait_ge(rstd_ready, WAVE * i + u + 1)
                    if gain is None:
                        dve.tensor_tensor(dst[:, at], centred[:, u, :], rstd[:, u, :], ALU.mult).then_inc(done, 1)
                        continue
                    chain(dve.tensor_tensor(scaled[:, u, :], centred[:, u, :], rstd[:, u, :], ALU.mult))
                    if residual:
                        chain(dve.tensor_scalar(scaled[:, u, :], scaled[:, u, :], gain, bias, ALU.mult, ALU.add))
                        dve.tensor_tensor(dst[:, at], dst[:, at], scaled[:, u, :], ALU.add).then_inc(done, 1)
                    else:
                        dve.tensor_scalar(dst[:, at], scaled[:, u, :], gain, bias, ALU.mult, ALU.add).then_inc(done, 1)
                chain.close()


def R_eps(R, eps):
    return R.eps[eps][:, 0:1]


def tokens(nc, R):
    PART = 3 * PAD * 2
    CELLS = PAD * PAD
    with ExitStack() as ctx:
        sb, ps, sem = allocators(nc, ctx, "tok")
        xin = sb("xin", [P, 2, 32, C])
        inner = sb("inner", [P, 2, 4, C])
        win = sb("win", [P, 2 * 3 * 2 * 3 * CELLS + 3 * CELLS + 32])
        acc = sb("acc", [P, 2, 2, CELLS])
        txt = sb("txt", [P, 2, C])
        parts = ps("parts", [P, 2, 2, 512])
        ptxt = ps("ptxt", [P, 2, 512])
        x_loaded = [sem(f"x_loaded{u}") for u in range(2)]
        txt_loaded = [sem(f"txt_loaded{u}") for u in range(2)]
        inner_ready, parts_done, txt_done, copied, txt_copied, weighted, order, stored = (
            sem(n) for n in ("inner_ready", "parts_done", "txt_done", "copied", "txt_copied", "weighted", "order",
                             "stored"))
        win_zeroed = sem("win_zeroed")
        x_v = R.ins["x"].rearrange("b h (q j) c -> b (h q) (j c)", q=2)
        block = ctx.enter_context(nc.Block())
        W = 2 * 3 * 3 * CELLS

        def window(slot, part_c, part_r, shift):
            a = 16 + slot * W + part_c * (6 * CELLS) + part_r * CELLS + shift
            v = win[:, a:a + 6 * CELLS]
            return v.rearrange("p (m q) -> p m q", m=2)[:, :, 0:CELLS]

        @block.sync
        def _(sp):
            with sp.Fori(0, B // 2) as i:
                for u in range(2):
                    sp.wait_ge(parts_done, 2 * i + u + 1)
                    sp.dma_start(xin[:, u, :, :].rearrange("p j c -> p (j c)"),
                                 x_v[bass.ds(2 * i + u, 1)].rearrange("a p f -> (a p) f")).then_inc(x_loaded[u], 16)
                    sp.wait_ge(txt_done, 2 * i + u + 1)
                    sp.dma_start(txt[:, u, :],
                                 R.ins["txt"][bass.ds(2 * i + u, 1)].rearrange("a t c -> (a t) c")).then_inc(
                        txt_loaded[u], 16)

        @block.tensor
        def _(pe):
            pe.sem_inc(parts_done, SLOTS)
            pe.sem_inc(txt_done, SLOTS)
            with pe.Fori(0, B // 2) as i:
                for u in range(2):
                    pe.wait_ge(txt_loaded[u], 16 * i + 16)
                    pe.wait_ge(txt_copied, 2 * i + u + 1)
                    pe.transpose(ptxt[:, u, 0:C], txt[:, u, :], R.c("ident")).then_inc(txt_done, 1)
                    pe.wait_ge(inner_ready, 2 * i + u + 1)
                    pe.wait_ge(copied, 2 * i + u + 1)
                    for jq in range(4):
                        for part, lhsT in enumerate((inner[:, u, jq, :], xin[:, u, 8 * jq, :], xin[:, u, 8 * jq + 7, :])):
                            a = (jq % 2) * 3 * PART + part * PART
                            last = pe.matmul(parts[:, u, jq // 2, a:a + PART], lhsT, R.c("rows"), start=True, stop=True)
                    last.then_inc(parts_done, 1)

        @block.vector
        def _(dve):
            dve.memset(win[:, :], 0.0).then_inc(win_zeroed, 1)
            dve.memset(acc[:, :, :, :], 0.0)
            chain = Chain(dve, order)
            with dve.Fori(0, B // 4) as i:
                chain.turn(i, 48)
                for pair in range(2):
                    for u in range(2):
                        n = 4 * i + 2 * pair + u
                        dve.wait_ge(x_loaded[u], 32 * i + 16 * pair + 16)
                        v = xin[:, u, :, :].rearrange("p (q r) c -> p q c r", r=8)
                        dve.tensor_reduce(inner[:, u, :, :], v[:, :, :, 1:7], AX, ALU.add).then_inc(inner_ready, 1)
                    dve.wait_ge(copied, 4 * i + 2 * pair + 2 + SLOTS)
                    dve.wait_ge(stored, 2 * i + pair + 1)
                    first = True
                    out = acc[:, pair, :, :]
                    for r, (part_r, dr) in enumerate(((0, 0), (1, 0), (2, 0), (2, -1), (1, 1))):
                        for c, (part_c, dc) in enumerate(((0, 0), (1, 0), (2, 0), (2, -1), (1, 1))):
                            tap = R.tap[:, 5 * r + c:5 * r + c + 1]
                            src = window(pair, part_c, part_r, dr * PAD + dc)
                            if first:
                                chain(dve.tensor_scalar(out, src, tap, None, ALU.mult))
                            else:
                                ins = dve.scalar_tensor_tensor(out=out, in0=src, scalar=tap, in1=out,
                                                               op0=ALU.mult, op1=ALU.add)
                                if r == 4 and c == 4:
                                    ins.then_inc(weighted, 1)
                                else:
                                    chain(ins)
                            first = False
                chain.close()

        @block.scalar
        def _(act):
            act.sem_inc(copied, SLOTS)
            act.sem_inc(txt_copied, SLOTS)
            act.sem_inc(stored, SLOTS)
            act.wait_ge(win_zeroed, 1)
            with act.Fori(0, B // 4) as i:
                for pair in range(2):
                    act.wait_ge(stored, 2 * i + pair + 1)
                    for u in range(2):
                        act.wait_ge(txt_done, 4 * i + 2 * pair + u + 1 + SLOTS)
                        act.copy(R.hT[:, bass.ds(4 * i * T + (2 * pair + u) * T + IMG_TOKENS, TXT_TOKENS)],
                                 ptxt[:, u, 0:C]).then_inc(txt_copied, 1)
                        act.wait_ge(parts_done, 4 * i + 2 * pair + u + 1 + SLOTS)
                        for bank in range(2):
                            for part in range(3):
                                src = parts[:, u, bank, 0:6 * PART].rearrange("p (q k) -> p q k", q=2)
                                src = src[:, :, part * PART:(part + 1) * PART].rearrange("p q (r s) -> p q r s", s=2)
                                a = 16 + pair * W + part * 6 * CELLS + u * 3 * CELLS + 1 + 2 * bank
                                dst = win[:, a:a + 3 * CELLS].rearrange("p (r j) -> p r j", j=PAD)
                                dst = dst[:, :, 0:GRID].rearrange("p r (s q) -> p q r s", s=2)[:, 0:2]
                                last = act.copy(dst, src)
                        last.then_inc(copied, 1)
                    act.wait_ge(weighted, 2 * i + pair + 1)
                    src = acc[:, pair, :, :].rearrange("p m (r j) -> p m r j", j=PAD)[:, :, 1:GRID + 1, 1:GRID + 1]
                    for u in range(2):
                        last = act.activation(
                            R.hT[:, bass.ds(4 * i * T + (2 * pair + u) * T, IMG_TOKENS)].rearrange(
                                "p (r j) -> p r j", j=GRID),
                            src[:, u], ACT.Identity, scale=1.0 / IMG_TOKENS, bias=R.col("L0_tok_conv_b"))
                    last.then_inc(stored, 1)


def project(nc, R, tag, src, jobs, copies=()):
    J = len(jobs)
    with ExitStack() as ctx:
        sb, ps, sem = allocators(nc, ctx, tag)
        out = ps("out", [P, 2, J, CH])
        product_ready, evacuated, stored = sem("product_ready"), sem("evacuated"), sem("stored")
        block = ctx.enter_context(nc.Block())

        if copies:
            @block.sync
            def _(sp):
                with sp.Fori(0, CHUNKS) as i:
                    sp.wait_ge(evacuated, J * i + J + SLOTS * J)
                    for j, dram in copies:
                        at = bass.ds(i * CH, CH)
                        sp.dma_start(dram[:, at], jobs[j][1][:, at]).then_inc(stored, 16)
                sp.wait_ge(stored, 16 * CHUNKS * len(copies))

        @block.tensor
        def _(pe):
            with pe.Fori(0, CHUNKS // 2) as i:
                for u in range(2):
                    for j, (w, dst, func, scale, bias) in enumerate(jobs):
                        pe.wait_ge(evacuated, (2 * J) * i + u * J + j + 1)
                        pe.matmul(out[:, u, j, :], w, src[:, bass.ds(i * (2 * CH) + u * CH, CH)],
                                  start=True, stop=True).then_inc(product_ready, 1)

        @block.scalar
        def _(act):
            act.sem_inc(evacuated, SLOTS * J)
            with act.Fori(0, CHUNKS // 2) as i:
                for u in range(2):
                    for j, (w, dst, func, scale, bias) in enumerate(jobs):
                        act.wait_ge(product_ready, (2 * J) * i + u * J + j + 1)
                        act.activation(dst[:, bass.ds(i * (2 * CH) + u * CH, CH)], out[:, u, j, :], func,
                                       scale=scale, bias=bias).then_inc(evacuated, 1)


def attend(nc, R, tag, q_all, k_all, v_all, att, sums, scale, groups=None, self_value=None, own=None):
    SLOT = T // HEADS
    local = groups is None
    ROWS = HALF + 7
    with ExitStack() as ctx:
        sb, ps, sem = allocators(nc, ctx, tag)
        q16 = [sb(f"q16_{u}", [HALF + 1, HEADS, T]) for u in range(2)]
        k16 = [sb(f"k16_{u}", [HALF + 1, HEADS, T]) for u in range(2)]
        vin = [sb(f"vin_{u}", [HD, HEADS, T] if local else [P, T]) for u in range(2)]
        if local:
            raw = [sb(f"raw{u}", [HD, 3, HEADS, T]) for u in range(2)]
            moved_qk, moved_v = sem("moved_qk"), sem("moved_v")
        vrow = sb("vrow", [HALF, 2, 2, HEADS, 2 * HD])
        peak = sb("peak", [HALF, 2, 2 * HEADS])
        neg = sb("neg", [2 * HEADS, 2, HALF])
        prob = sb("prob", [HALF, 2, 2, T])
        o32 = [sb(f"o32_{u}", [2 * HD, HEADS, T]) for u in range(2)]
        pS, pT = ps("pS", [HALF, 2, 512]), ps("pT", [HALF, 2, 512])
        pO, pV, pM, pX = ps("pO", [2 * HD, 512]), ps("pV", [HALF, 512]), ps("pM", [2 * HEADS, 512]), ps("pX", [P, 512])
        loaded = [sem(f"loaded{u}") for u in range(2)]
        rows_loaded = [sem(f"rows_loaded{u}") for u in range(2)]
        stored = [sem(f"stored{u}") for u in range(2)]
        (cleared, v_turned, v_copied, scores_ready, max_done, floored, max_turned, neg_ready, shifted_ready, exp_done,
         weighted, o_copied, order, ones_set) = (sem(n) for n in (
             "cleared", "v_turned", "v_copied", "scores_ready", "max_done", "floored", "max_turned", "neg_ready",
             "shifted_ready", "exp_done", "weighted", "o_copied", "order", "ones_set"))
        if not local:
            qs_mask = [sb(f"qs_mask{u}", [ROWS, HEADS, T], BF16) for u in range(2)]
            ks_mask = [sb(f"ks_mask{u}", [ROWS, 2, HEADS, T], BF16) for u in range(2)]
            kt_mask = [sb(f"kt_mask{u}", [ROWS, HEADS, T], BF16) for u in range(2)]
            qt_mask = [sb(f"qt_mask{u}", [ROWS, 2, HEADS, T], BF16) for u in range(2)]
            pool_masks, masks_zeroed = sem("pool_masks"), [sem(f"masks_zeroed{u}") for u in range(2)]
            spread_ready, own_ready, masks_ready = sem("spread_ready"), sem("own_ready"), sem("masks_ready")
        LOAD = 16 * (3 if local else 9)
        block = ctx.enter_context(nc.Block())

        def pick(t, h, half=None, rows=HALF):
            return t[0:rows, h, :] if half is None else t[0:rows, h, HALF * half:HALF * half + HALF]

        @block.sync
        def _(sp):
            def load(n, u):
                at = bass.ds(n * T, T)
                heads = "(s d) t -> d s t"
                if local:
                    for j, src in enumerate((q_all, k_all, v_all)):
                        sp.dma_start(raw[u][:, j, :, :], src[:, at].rearrange(heads, d=HD)).then_inc(loaded[u], 16)
                else:
                    sp.dma_start(q16[u][0:HD, :, :], q_all[:, at].rearrange(heads, d=HD)).then_inc(loaded[u], 16)
                    sp.dma_start(k16[u][0:HD, :, :], k_all[:, at].rearrange(heads, d=HD)).then_inc(loaded[u], 16)
                    sp.dma_start(vin[u][:, :], v_all[:, at]).then_inc(loaded[u], 16)
                    g = groups[:, at].rearrange("(h k c) t -> k c h t", h=HEADS, k=2)
                    for side, dst in ((0, qs_mask[u][HALF:ROWS, :, :]), (0, qt_mask[u][HALF:ROWS, 0, :, :]),
                                      (0, qt_mask[u][HALF:ROWS, 1, :, :]), (1, kt_mask[u][HALF:ROWS, :, :]),
                                      (1, ks_mask[u][HALF:ROWS, 0, :, :]), (1, ks_mask[u][HALF:ROWS, 1, :, :])):
                        sp.dma_start(dst, g[side, 0:7]).then_inc(loaded[u], 16)

            def store_max(n, u):
                sp.wait_ge(neg_ready, n + 2)
                for half in range(2):
                    src = neg[HEADS * half:HEADS * half + HEADS, u, :]
                    dst = q16[u][HALF:HALF + 1, :, HALF * half:HALF * half + HALF]
                    sp.dma_start(dst, src).then_inc(rows_loaded[u], 16)

            def store_out(n, u):
                at = bass.ds(n * T, T)
                sp.wait_ge(o_copied, 4 * n + 4 + 1)
                sp.dma_start(att[:, at].rearrange("(s d) t -> d s t", d=HD), o32[u][0:HD, :, :]).then_inc(stored[u], 16)
                sp.dma_start(sums[:, at].rearrange("(s d) t -> d s t", d=HD), o32[u][HD:2 * HD, :, :]).then_inc(
                    stored[u], 16)

            sp.sem_inc(stored[0], 32)
            sp.sem_inc(stored[1], 32)
            for u in range(2):
                if not local:
                    sp.wait_ge(cleared, 1)
                    sp.wait_ge(masks_ready, u + 1)
                load(u, u)
            store_max(0, 0)
            with sp.Fori(0, B // 2 - 1) as i:
                for u in range(2):
                    n = 2 * i + u
                    if local:
                        sp.wait_ge(moved_qk, n + 1)
                        sp.wait_ge(moved_v, n + 1)
                        load(n + 2, u)
                    store_max(n + 1, 1 - u)
                    if not local:
                        sp.wait_ge(shifted_ready, HEADS * n + HEADS)
                        load(n + 2, u)
                    store_out(n, u)
            store_max(B - 1, 1)
            store_out(B - 2, 0)
            store_out(B - 1, 1)
            for u in range(2):
                sp.wait_ge(stored[u], 32 * (B // 2 + 1))

        def masks(eng, u):
            for t in (qs_mask, ks_mask, kt_mask, qt_mask):
                last = eng.memset(t[u][:], 0.0)
            last.then_inc(masks_zeroed[u], 1)
            eng.wait_ge(masks_zeroed[u], 1)
            shape = [HALF, HEADS, HALF]
            plus, minus = (R.bf[m][0:HALF, 0:HALF].unsqueeze(1).to_broadcast(shape) for m in ("ident", "neg_diag"))
            for half in range(2):
                mine = slice(HALF * half, HALF * half + HALF)
                eng.tensor_copy(qs_mask[u][0:HALF, :, mine], plus)
                eng.tensor_copy(kt_mask[u][0:HALF, :, mine], plus)
                eng.tensor_copy(ks_mask[u][0:HALF, half, :, mine], minus)
                last = eng.tensor_copy(qt_mask[u][0:HALF, half, :, mine], minus)
            return last

        if not local:
            @block.gpsimd
            def _(pool):
                last = masks(pool, 1)
                last.then_inc(pool_masks, 1)
                pool.wait_ge(pool_masks, 1)
                pool.wait_ge(masks_ready, 1)
                pool.sem_inc(masks_ready, 1)

        MAXROWS = 32

        @block.tensor
        def _(pe):
            def values(n, u, turn):
                if local:
                    pe.wait_ge(moved_v, n + 1)
                else:
                    pe.wait_ge(loaded[u], LOAD * turn + LOAD)
                pe.wait_ge(v_copied, n + 1)
                if local:
                    for half in range(2):
                        for h in range(HEADS):
                            a = (half * HEADS + h) * HD
                            last = pe.matmul(pV[:, a:a + HD], pick(vin[u], h, half, HD), R.c("ident")[0:HD, 0:HD],
                                             start=True, stop=True)
                else:
                    for half in range(2):
                        last = pe.transpose(pV[:, C * half:C * half + C], vin[u][:, HALF * half:HALF * half + HALF],
                                            R.c("ident"))
                last.then_inc(v_turned, 1)

            def scores(n, u):
                if local:
                    pe.wait_ge(moved_qk, n + 1)
                for h in range(HEADS):
                    pe.wait_ge(max_done, HEADS * n + h + 1)
                    for half in range(2):
                        out = pS[:, h % 2, T * half:T * half + T]
                        if not local:
                            pe.matmul(out, qs_mask[u][:, h, HALF * half:HALF * half + HALF], ks_mask[u][:, half, h, :],
                                      start=True, stop=False)
                        last = pe.matmul(out, pick(q16[u], h, half), pick(k16[u], h), start=local, stop=True)
                    last.then_inc(scores_ready, 1)

            def maxima(n, u):
                if local:
                    pe.wait_ge(max_done, HEADS * n + HEADS + SLOTS)
                else:
                    pe.wait_ge(floored, n + 1)
                pe.wait_ge(neg_ready, n + 1)
                pe.transpose(pM[:, 0:HALF], peak[:, u, :], R.c("ident")[0:HALF, 0:HALF]).then_inc(max_turned, 1)

            def shifted(n, u, h, turn):
                if h == 0:
                    pe.wait_ge(rows_loaded[u], MAXROWS * turn + MAXROWS)
                pe.wait_ge(exp_done, HEADS * n + h + 1)
                for half in range(2):
                    out = pT[:, h % 2, T * half:T * half + T]
                    if not local:
                        pe.matmul(out, kt_mask[u][:, h, HALF * half:HALF * half + HALF], qt_mask[u][:, half, h, :],
                                  start=True, stop=False)
                    last = pe.matmul(out, pick(k16[u], h, half, HALF + 1), pick(q16[u], h, None, HALF + 1),
                                     start=local, stop=True)
                last.then_inc(shifted_ready, 1)

            def mix(n, u, h):
                if h == 0:
                    pe.wait_ge(v_copied, n + 2)
                if h % 2 == 0:
                    pe.wait_ge(o_copied, 4 * n + h // 2 + 1)
                pe.wait_ge(exp_done, HEADS * n + h + 1 + SLOTS)
                for half in range(2):
                    last = pe.matmul(pO[:, T * (h % 2):T * (h % 2) + T], vrow[:, u, half, h, :], prob[:, h % 2, half, :],
                                     start=(half == 0), stop=(half == 1))
                last.then_inc(weighted, 1)

            def own_spread(n, u):
                pe.wait_ge(neg_ready, n + 2)
                pe.wait_ge(own_ready, n + 1)
                for half in range(2):
                    last = pe.matmul(pX[:, HALF * half:HALF * half + HALF],
                                     R.c("spread", 2 * HEADS)[:, P * half:P * half + P], neg[:, u, :],
                                     start=True, stop=True)
                last.then_inc(spread_ready, 1)

            def sequence(n, u, nxt, turn):
                shifted(n, u, 0, turn)
                for h in range(3):
                    shifted(n, u, h + 1, turn)
                    mix(n, u, h)
                if nxt:
                    values(n + 1, 1 - u, turn + u)
                    scores(n + 1, 1 - u)
                mix(n, u, 3)
                shifted(n, u, 4, turn)
                if nxt:
                    maxima(n + 1, 1 - u)
                for h in range(4, 7):
                    shifted(n, u, h + 1, turn)
                    mix(n, u, h)
                if nxt and not local:
                    own_spread(n + 1, 1 - u)
                mix(n, u, 7)

            pe.sem_inc(weighted, SLOTS)
            values(0, 0, 0)
            scores(0, 0)
            maxima(0, 0)
            if not local:
                own_spread(0, 0)
            with pe.Fori(0, B // 2 - 1) as i:
                for u in range(2):
                    sequence(2 * i + u, u, True, i)
            sequence(B - 2, 0, True, B // 2 - 1)
            sequence(B - 1, 1, False, B // 2 - 1)

        @block.scalar
        def _(act):
            act.sem_inc(v_copied, 1)
            act.sem_inc(neg_ready, 1)
            act.sem_inc(exp_done, SLOTS)
            if not local:
                act.sem_inc(own_ready, 1)

            def move(n, u, turn):
                act.wait_ge(loaded[u], LOAD * turn + LOAD)
                act.copy(vin[u].rearrange("d h (s t) -> d h s t", s=HEADS),
                         raw[u][:, 2].rearrange("d s (h t) -> d h s t", h=HEADS)).then_inc(moved_v, 1)

            def values(n, u):
                act.wait_ge(v_turned, n + 1)
                if local:
                    src = pV[:, 0:2 * HEADS * HD].rearrange("p (g d) -> p g d", d=HD)
                else:
                    src = pV[:, 0:2 * C].rearrange("p (g d) -> p g d", d=HD)
                dst = vrow[:, u, :, :, 0:HD].rearrange("p a h d -> p (a h) d")
                act.copy(dst, src).then_inc(v_copied, 1)

            def maxima(n, u):
                act.wait_ge(max_turned, n + 1)
                act.mul(neg[:, u, :], pM[:, 0:HALF], -1.0).then_inc(neg_ready, 1)

            def own_term(n, u):
                act.wait_ge(spread_ready, n + 1)
                act.activation(own[:, bass.ds(n * T, T)], pX[:, 0:T], ACT.Exp, scale=scale,
                               bias=R.self_value[:, 0:1]).then_inc(own_ready, 1)

            def exps(n, u, lo, hi):
                for h in range(lo, hi):
                    act.wait_ge(shifted_ready, HEADS * n + h + 1)
                    act.wait_ge(weighted, HEADS * n + h + 1)
                    act.activation(prob[:, h % 2, :, :], pT[:, h % 2, 0:2 * T].rearrange("p (a t) -> p a t", a=2), ACT.Exp,
                                   scale=scale).then_inc(exp_done, 1)

            def sequence(n, u, nxt, turn):
                exps(n, u, 0, 2)
                if nxt and local:
                    move(n + 1, 1 - u, turn + u)
                exps(n, u, 2, 4)
                if nxt:
                    values(n + 1, 1 - u)
                exps(n, u, 4, 5)
                if nxt:
                    maxima(n + 1, 1 - u)
                exps(n, u, 5, HEADS)
                if nxt and not local:
                    own_term(n + 1, 1 - u)

            act.wait_ge(ones_set, 1)
            if local:
                move(0, 0, 0)
            values(0, 0)
            maxima(0, 0)
            if not local:
                own_term(0, 0)
            with act.Fori(0, B // 2 - 1) as i:
                for u in range(2):
                    sequence(2 * i + u, u, True, i)
            sequence(B - 2, 0, True, B // 2 - 1)
            sequence(B - 1, 1, False, B // 2 - 1)

        @block.vector
        def _(dve):
            for u in range(2):
                dve.memset(q16[u][:, :, :], 0.0)
                dve.memset(k16[u][:, :, :], 0.0)
            dve.memset(neg[:, :, :], 0.0).then_inc(order, 1)
            dve.wait_ge(order, 1)
            for u in range(2):
                dve.memset(k16[u][HALF:HALF + 1, :, :], 1.0)
            dve.memset(vrow[:, :, :, :, :], 1.0).then_inc(ones_set, 1)
            dve.wait_ge(ones_set, 1)
            if not local:
                dve.sem_inc(cleared, 1)
                masks(dve, 0).then_inc(masks_ready, 1)
            dve.sem_inc(max_done, SLOTS)
            dve.sem_inc(o_copied, 1)
            def maxima(n, u):
                for h in range(HEADS):
                    dve.wait_ge(scores_ready, HEADS * n + h + 1)
                    dst = peak[:, u, :].rearrange("p (a h) -> p a h", a=2)[:, :, h]
                    dve.tensor_reduce(dst, pS[:, h % 2, 0:2 * T].rearrange("p (a t) -> p a t", a=2), AX,
                                      ALU.max).then_inc(max_done, 1)
                if not local:
                    dve.wait_ge(max_done, HEADS * n + HEADS + SLOTS)
                    dve.tensor_scalar(peak[:, u, :], peak[:, u, :], self_value / scale, None, ALU.max).then_inc(floored, 1)

            def out(n, u, pair, turn):
                dve.wait_ge(weighted, HEADS * n + 2 * pair + 2 + SLOTS)
                if pair == 0:
                    dve.wait_ge(stored[u], 32 * turn + 32)
                src = pO[:, 0:2 * T]
                if local:
                    dst = o32[u][:, :, 2 * SLOT * pair:2 * SLOT * pair + 2 * SLOT].rearrange("p s (h t) -> p h s t", h=2)
                    src = src.rearrange("p (h s t) -> p h s t", h=2, s=HEADS)
                else:
                    dst = o32[u][:, 2 * pair:2 * pair + 2, :]
                    src = src.rearrange("p (h t) -> p h t", h=2)
                dve.tensor_copy(dst, src).then_inc(o_copied, 1)

            def move(n, u, turn):
                dve.wait_ge(loaded[u], LOAD * turn + LOAD)
                for j, dst in enumerate((q16[u], k16[u])):
                    last = dve.tensor_copy(dst[0:HD].rearrange("d h (s t) -> d h s t", s=HEADS),
                                           raw[u][:, j].rearrange("d s (h t) -> d h s t", h=HEADS))
                last.then_inc(moved_qk, 1)

            def sequence(n, u, nxt, turn):
                if nxt and local:
                    move(n + 1, 1 - u, turn + u)
                out(n, u, 0, turn)
                if nxt:
                    maxima(n + 1, 1 - u)
                for pair in range(1, 4):
                    out(n, u, pair, turn)

            if local:
                move(0, 0, 0)
            maxima(0, 0)
            with dve.Fori(0, B // 2 - 1) as i:
                for u in range(2):
                    sequence(2 * i + u, u, True, i)
            sequence(B - 2, 0, True, B // 2 - 1)
            sequence(B - 1, 1, False, B // 2 - 1)


def attention_0(nc, R):
    with ExitStack() as ctx:
        sb, _, _ = allocators(nc, ctx, "a0")
        q, k, v = sb("q", [P, N]), sb("k", [P, N]), sb("v", [P, N])
        layer_norm(nc, R, "a0_ln", R.hT, R.xT)
        w = R.w["L0_attn_W_qkv"]
        project(nc, R, "a0_qkv", R.xT, [
            (w[:, C * n:C * n + C], dst, ACT.Identity, 1.0, R.col("L0_attn_b_qkv", n)) for n, dst in enumerate((q, k, v))],
            copies=[(n, R.scratch[n]) for n in range(3)])
        attend(nc, R, "a0", *R.scratch[0:5], 0.25)
        divide(nc, R, "a0_add", R.scratch[3], R.scratch[4], R.hT)


def divide(nc, R, tag, att, sums, dst, own=None, v=None):
    with ExitStack() as ctx:
        sb, ps, sem = allocators(nc, ctx, tag)
        a, s, t = sb("a", [P, 2, CH]), sb("s", [P, 2, CH]), sb("t", [P, 2, CH])
        loaded = [sem(f"loaded{u}") for u in range(2)]
        done, order = sem("done"), sem("order")
        block = ctx.enter_context(nc.Block())
        arrays = [(a, att), (s, sums)] + ([(t, v)] if own is not None else [])

        @block.sync
        def _(sp):
            with sp.Fori(0, CHUNKS // 2) as i:
                for u in range(2):
                    at = bass.ds(i * (2 * CH) + u * CH, CH)
                    sp.wait_ge(done, 2 * i + u + 1)
                    for tile, dram in arrays:
                        sp.dma_start(tile[:, u, :], dram[:, at]).then_inc(loaded[u], 16)

        @block.vector
        def _(dve):
            dve.sem_inc(done, SLOTS)
            chain = Chain(dve, order)
            load = 16 * len(arrays)
            with dve.Fori(0, CHUNKS // 2) as i:
                chain.turn(i, 8 if own is not None else 4)
                for u in range(2):
                    at = bass.ds(i * (2 * CH) + u * CH, CH)
                    dve.wait_ge(loaded[u], load * i + load)
                    if own is not None:
                        dve.tensor_tensor(t[:, u, :], own[:, at], t[:, u, :], ALU.mult)
                        chain(dve.tensor_tensor(s[:, u, :], own[:, at], s[:, u, :], ALU.add))
                        chain(dve.tensor_tensor(a[:, u, :], a[:, u, :], t[:, u, :], ALU.add))
                    chain(dve.reciprocal(s[:, u, :], s[:, u, :]))
                    if own is not None:
                        chain(dve.tensor_tensor(a[:, u, :], a[:, u, :], s[:, u, :], ALU.mult))
                        dve.tensor_copy(dst[:, at], a[:, u, :]).then_inc(done, 1)
                    else:
                        chain(dve.tensor_tensor(a[:, u, :], a[:, u, :], s[:, u, :], ALU.mult))
                        dve.tensor_tensor(dst[:, at], dst[:, at], a[:, u, :], ALU.add).then_inc(done, 1)
                chain.close()


def tile_of(t):
    return slice(P * t, P * t + P)


def route(nc, R, tag, w, E, logits, bias=None):
    with ExitStack() as ctx:
        sb, ps, sem = allocators(nc, ctx, tag)
        flat = sb("flat", [E, N])
        up = ps("up", [E, 2, CH])
        per_bank = 512 // E
        banks = -(-TILES // per_bank)
        turned = ps("turned", [P, banks, 512])
        product_ready, evacuated, turned_ready = sem("product_ready"), sem("evacuated"), sem("turned_ready")
        block = ctx.enter_context(nc.Block())

        @block.tensor
        def _(pe):
            with pe.Fori(0, CHUNKS // 2) as i:
                for u in range(2):
                    pe.wait_ge(evacuated, 2 * i + u + 1)
                    pe.matmul(up[:, u, :], w, R.xT[:, bass.ds(i * (2 * CH) + u * CH, CH)],
                              start=True, stop=True).then_inc(product_ready, 1)
            pe.wait_ge(evacuated, CHUNKS + SLOTS)
            for t in range(TILES):
                a = E * (t % per_bank)
                last = pe.transpose(turned[:, t // per_bank, a:a + E], flat[:, tile_of(t)], R.c("ident")[0:E, 0:E])
            last.then_inc(turned_ready, 1)

        @block.scalar
        def _(act):
            act.sem_inc(evacuated, SLOTS)
            with act.Fori(0, CHUNKS // 2) as i:
                for u in range(2):
                    act.wait_ge(product_ready, 2 * i + u + 1)
                    act.activation(flat[:, bass.ds(i * (2 * CH) + u * CH, CH)], up[:, u, :], ACT.Identity,
                                   bias=0.0 if bias is None else bias).then_inc(evacuated, 1)

        @block.vector
        def _(dve):
            dve.wait_ge(turned_ready, 1)
            for b in range(banks):
                n = min(per_bank, TILES - b * per_bank)
                dve.tensor_copy(logits[:, b * per_bank:b * per_bank + n, :],
                                turned[:, b, 0:n * E].rearrange("p (t e) -> p t e", e=E))


def top_gates(nc, R, tag, logits, E, K, gates, floor, capacity=None, dropped=None):
    TAKEN = 2.0
    with ExitStack() as ctx:
        sb, ps, sem = allocators(nc, ctx, tag)
        prob, marked = sb("prob", [P, TILES, E + 8]), sb("marked", [P, TILES, E + 8])
        top = sb("top", [P, TILES, 8])
        stat, total = sb("stat", [P, TILES]), sb("total", [P, TILES])
        count, before = sb("count", [P, TILES, E], BF16), sb("before", [P, TILES, E], BF16)
        place = ps("place", [P, 2, 512])
        shifted, exp_ready, counted, placed, order = (
            sem(n) for n in ("shifted", "exp_ready", "counted", "placed", "order"))
        block = ctx.enter_context(nc.Block())

        def wide(v):
            return v[:, :].unsqueeze(2).to_broadcast([P, TILES, E])

        @block.scalar
        def _(act):
            act.wait_ge(shifted, 1)
            act.activation(prob[:, :, 0:E], logits[:, :, :], ACT.Exp).then_inc(exp_ready, 1)

        @block.vector
        def _(dve):
            chain = Chain(dve, order)
            dve.memset(prob[:, :, E:E + 8], TAKEN)
            chain(dve.tensor_reduce(stat[:, :], logits[:, :, :], AX, ALU.max))
            dve.tensor_tensor(logits[:, :, :], logits[:, :, :], wide(stat), ALU.subtract).then_inc(shifted, 1)
            dve.wait_ge(exp_ready, 1)
            chain(dve.tensor_reduce(total[:, :], prob[:, :, 0:E], AX, ALU.add))
            chain(dve.reciprocal(total[:, :], total[:, :]))
            chain(dve.tensor_tensor(prob[:, :, 0:E], prob[:, :, 0:E], wide(total), ALU.mult))
            for t in range(TILES):
                last = dve.max(top[:, t, :], prob[:, t, 0:E])
            chain(last)
            chain(dve.tensor_reduce(stat[:, :], top[:, :, 0:K], AX, ALU.add))
            chain(dve.tensor_scalar(stat[:, :], stat[:, :], floor, None, ALU.max))
            dve.reciprocal(stat[:, :], stat[:, :])
            chain(dve.memset(top[:, :, K:8], TAKEN))
            for t in range(TILES):
                last = dve.match_replace(marked[:, t, :], top[:, t, :], prob[:, t, :], -1.0)
            chain(last)
            chain(dve.scalar_tensor_tensor(out=gates[:, :, :], in0=marked[:, :, 0:E], scalar=0.0, in1=prob[:, :, 0:E],
                                           op0=ALU.is_lt, op1=ALU.mult))
            chain(dve.tensor_tensor(gates[:, :, :], gates[:, :, :], wide(stat), ALU.mult))
            if capacity is None:
                return
            chain(dve.tensor_scalar(count[:, :, :], marked[:, :, 0:E], 0.0, None, ALU.is_lt))
            chain(dve.memset(before[:, 0, :], 0.0))
            for t in range(1, TILES):
                ins = dve.tensor_tensor(before[:, t, :], before[:, t - 1, :], count[:, t - 1, :], ALU.add)
                if t < TILES - 1:
                    chain(ins)
            ins.then_inc(counted, 1)
            dve.wait_ge(placed, 1)
            h = TILES // 2
            for b in range(2):
                g = gates[:, h * b:h * b + h, :].rearrange("p t e -> p (t e)")
                last = dve.scalar_tensor_tensor(out=g, in0=place[:, b, 0:h * E], scalar=float(capacity), in1=g,
                                                op0=ALU.is_lt, op1=ALU.mult)
            chain(last)
            chain(dve.tensor_reduce(dropped[:, :], gates[:, :, :], AX, ALU.add))
            dve.tensor_scalar(dropped[:, :], dropped[:, :], 1e-12, None, ALU.is_le)

        if capacity is not None:
            @block.tensor
            def _(pe):
                pe.wait_ge(counted, 1)
                h = TILES // 2
                for b in range(2):
                    out = place[:, b, 0:h * E]
                    pe.matmul(out, R.bf["before"][:, :], count[:, h * b:h * b + h, :].rearrange("p t e -> p (t e)"),
                              start=True, stop=False)
                    last = pe.matmul(out, R.bf["ones"][:, :],
                                     before[:, h * b:h * b + h, :].rearrange("p t e -> p (t e)"),
                                     start=False, stop=True)
                last.then_inc(placed, 1)


def experts(nc, R, tag, E, kind, weights, gates, acc, bias=None):
    ups, down = weights
    U = 4 if kind == "glu" else 1
    A = len(ups)
    PER = 2 * CHUNKS * U
    SUB = CH // P
    with ExitStack() as ctx:
        sb, ps, sem = allocators(nc, ctx, tag)
        wu = [sb(f"wu{u}", [P, A, U * P]) for u in range(2)]
        wd = [sb(f"wd{u}", [P, U, C]) for u in range(2)]
        first, hidden = sb("first", [P, 2, CH]), sb("hidden", [P, 2, CH])
        mixed = sb("mixed", [P, 2, CH]) if kind == "glu" else None
        bias_now, bias_copied = sb("bias_now", [P, 2, 1]), sem("bias_copied")
        up, back = ps("up", [P, 2, A, CH]), ps("back", [P, 2, CH])
        loaded = [sem(f"loaded{u}") for u in range(2)]
        up_ready, first_ready, up_used, hidden_ready, back_ready, added = (
            sem(n) for n in ("up_ready", "first_ready", "up_used", "hidden_ready", "back_ready", "added"))
        block = ctx.enter_context(nc.Block())

        @block.sync
        def _(sp):
            def load(e, u):
                for a, w in enumerate(ups):
                    sp.dma_start(wu[u][:, a, :], w[bass.ds(e, 1)].rearrange("o p h -> (o p) h")).then_inc(loaded[u], 16)
                sp.dma_start(wd[u][:, :, :],
                             down[bass.ds(e, 1)].rearrange("o (k p) d -> (o p) k d", p=P)).then_inc(loaded[u], 16)

            load(0, 0)
            load(1, 1)
            if E > 2:
                with sp.Fori(1, E // 2) as i:
                    for u in range(2):
                        sp.wait_ge(back_ready, PER * i - PER + (u + 1) * CHUNKS * U + SLOTS)
                        load(2 * i + u, u)

        LOAD = 16 * (A + 1)

        def unit(j):
            return j // (CHUNKS * U), (j // U) % CHUNKS, j % U

        @block.tensor
        def _(pe):
            pe.sem_inc(back_ready, SLOTS)

            def go_up(i, j):
                u, ch, k = unit(j)
                if ch == 0 and k == 0:
                    pe.wait_ge(loaded[u], LOAD * i + LOAD)
                pe.wait_ge(up_used, PER * i + j + 1)
                for a in range(A):
                    last = pe.matmul(up[:, j % 2, a, :], wu[u][:, a, P * k:P * k + P], R.xT[:, CH * ch:CH * ch + CH],
                                     start=True, stop=True)
                last.then_inc(up_ready, 1)

            def go_back(i, j):
                u, ch, k = unit(j)
                if k == 0:
                    pe.wait_ge(added, (PER // U) * i + j // U + 1)
                if kind == "glu":
                    pe.wait_ge(hidden_ready, PER * i + j + 1 + SLOTS)
                else:
                    pe.wait_ge(up_used, PER * i + j + 1 + SLOTS)
                for s in range(SUB):
                    last = pe.matmul(back[:, ch % 2, C * s:C * s + C], hidden[:, j % 2, P * s:P * s + P], wd[u][:, k, :],
                                     start=(k == 0 and s == 0), stop=(k == U - 1), skip_group_check=True)
                last.then_inc(back_ready, 1)

            go_up(0, 0)
            if E > 2:
                with pe.Fori(0, E // 2 - 1) as i:
                    for j in range(PER):
                        go_up(i + (j + 1) // PER, (j + 1) % PER)
                        go_back(i, j)
            for j in range(PER):
                if j + 1 < PER:
                    go_up(E // 2 - 1, j + 1)
                go_back(E // 2 - 1, j)

        @block.scalar
        def _(act):
            if kind == "relu":
                act.sem_inc(up_used, SLOTS)
            if kind == "glu":
                act.sem_inc(hidden_ready, SLOTS)

            def hide(i, j):
                n = PER * i + j
                u, ch, k = unit(j)
                if kind == "relu" and ch == 0:
                    act.copy(bias_now[:, u, :], bias[:, bass.ds(2 * i + u, 1)]).then_inc(bias_copied, 1)
                    act.wait_ge(bias_copied, 2 * i + u + 1)
                act.wait_ge(up_ready, n + 1)
                if kind == "glu":
                    act.wait_ge(up_used, n + 1)
                    act.copy(first[:, j % 2, :], up[:, j % 2, 0, :]).then_inc(first_ready, 1)
                elif kind == "swiglu":
                    act.wait_ge(up_used, n + 1)
                    act.activation(first[:, j % 2, :], up[:, j % 2, 0, :], ACT.Silu).then_inc(first_ready, 1)
                else:
                    act.wait_ge(back_ready, n + 1)
                    act.activation(hidden[:, j % 2, :], up[:, j % 2, 0, :], ACT.Relu, bias=bias_now[:, u, :]).then_inc(
                        up_used, 1)

            def bend(i, j):
                n = PER * i + j
                act.wait_ge(up_used, n + 1 + SLOTS)
                act.wait_ge(back_ready, n + 1)
                act.activation(hidden[:, j % 2, :], mixed[:, j % 2, :], ACT.Gelu).then_inc(hidden_ready, 1)

            if kind == "glu":
                with act.Fori(0, E // 2) as i:
                    for j in range(PER):
                        hide(i, j)
                        bend(i, j)
            else:
                with act.Fori(0, E // 2) as i:
                    for j in range(PER):
                        hide(i, j)

        @block.vector
        def _(dve):
            if kind != "relu":
                dve.sem_inc(up_used, SLOTS)
            dve.sem_inc(added, SLOTS)

            def mix(i, j):
                n = PER * i + j
                if kind == "relu":
                    return
                dve.wait_ge(first_ready, n + 1)
                if kind == "glu":
                    dve.wait_ge(hidden_ready, n + 1)
                    dve.tensor_tensor(mixed[:, j % 2, :], up[:, j % 2, 1, :], first[:, j % 2, :], ALU.mult).then_inc(
                        up_used, 1)
                else:
                    dve.wait_ge(back_ready, n + 1)
                    dve.tensor_tensor(hidden[:, j % 2, :], up[:, j % 2, 1, :], first[:, j % 2, :], ALU.mult).then_inc(
                        up_used, 1)

            def add(i, j):
                u, ch, k = unit(j)
                if k != U - 1:
                    return
                dve.wait_ge(back_ready, PER * i + j + 1 + SLOTS)
                if j // U == 0:
                    dve.wait_ge(added, (PER // U) * i + SLOTS)
                elif ch == 0:
                    dve.wait_ge(added, (PER // U) * i + CHUNKS + SLOTS)
                for s in range(SUB):
                    t = SUB * ch + s
                    gate = 1.0 if gates is None else gates[:, t, :][:, bass.ds(2 * i + u, 1)]
                    last = dve.scalar_tensor_tensor(out=acc[:, t, :], in0=back[:, ch % 2, C * s:C * s + C], scalar=gate,
                                                    in1=acc[:, t, :], op0=ALU.mult, op1=ALU.add)
                last.then_inc(added, 1)

            mix(0, 0)
            if E > 2:
                with dve.Fori(0, E // 2 - 1) as i:
                    for j in range(PER):
                        mix(i + (j + 1) // PER, (j + 1) % PER)
                        add(i, j)
            for j in range(PER):
                if j + 1 < PER:
                    mix(E // 2 - 1, j + 1)
                add(E // 2 - 1, j)


def feed_forward_3(nc, R):
    E, K = 64, 6
    with ExitStack() as ctx:
        sb, _, _ = allocators(nc, ctx, "f3")
        gates, acc = sb("gates", [P, TILES, E]), sb("acc", [P, TILES, C])
        layer_norm(nc, R, "f3_ln", R.hT, R.xT)
        with ExitStack() as inner:
            sb2, _, _ = allocators(nc, inner, "f3r")
            logits = sb2("logits", [P, TILES, E])
            route(nc, R, "f3_route", R.w["L3_ffn_Wr"][:, :], E, logits)
            top_gates(nc, R, "f3_top", logits, E, K, gates, 0.0)
        zero(nc, acc)
        i = R.ins
        experts(nc, R, "f3_shared", 2, "swiglu", ((i["L3_ffn_sWg"], i["L3_ffn_sWu"]), i["L3_ffn_sWd"]), None, acc)
        experts(nc, R, "f3_routed", E, "swiglu", ((i["L3_ffn_Wg"], i["L3_ffn_Wu"]), i["L3_ffn_Wd"]), gates, acc)
        leave(nc, R, "f3_out", acc)


def zero(nc, acc):
    with nc.Block() as block:
        @block.vector
        def _(dve):
            dve.memset(acc[:, :, :], 0.0)


def leave(nc, R, tag, acc):
    with ExitStack() as ctx:
        sb, ps, sem = allocators(nc, ctx, tag)
        both = ps("both", [P, 2, 512])
        turned, summed, stored = sem("turned"), sem("summed"), sem("stored")
        block = ctx.enter_context(nc.Block())
        SUB = 4
        out = R.out.rearrange("b t c -> (b t) c").rearrange("(g s p) c -> g p s c", s=SUB, p=P)

        @block.tensor
        def _(pe):
            for g in range(TILES // SUB):
                if g >= 2:
                    pe.wait_ge(summed, g - 1)
                for s in range(SUB):
                    o = both[:, g % 2, C * s:C * s + C]
                    pe.matmul(o, R.hT[:, tile_of(SUB * g + s)], R.c("ident"), start=True, stop=False)
                    last = pe.matmul(o, R.xT[:, tile_of(SUB * g + s)], R.c("ident"), start=False, stop=True)
                last.then_inc(turned, 1)

        @block.vector
        def _(dve):
            for g in range(TILES // SUB):
                dve.wait_ge(turned, g + 1)
                a = acc[:, SUB * g:SUB * g + SUB, :].rearrange("p t c -> p (t c)")
                dve.tensor_tensor(a, both[:, g % 2, :], a, ALU.add).then_inc(summed, 1)

        @block.sync
        def _(sp):
            for g in range(TILES // SUB):
                sp.wait_ge(summed, g + 1)
                sp.dma_start(out[g], acc[:, SUB * g:SUB * g + SUB, :]).then_inc(stored, 16)
            sp.wait_ge(stored, 16 * (TILES // SUB))


def fold(nc, R, tag, acc, from_x, keep=None, gates=None, b2=None):
    SUB = CH // P
    with ExitStack() as ctx:
        sb, ps, sem = allocators(nc, ctx, tag)
        px, pb, py = ps("px", [P, 2, CH]), ps("pb", [P, 2, CH]), ps("py", [P, 2, CH])
        if b2 is not None:
            pg, gT = ps("pg", [32, 2, CH]), sb("gT", [32, 2, CH])
        g_turned, g_ready, x_ready, y_ready, y_turned, folded, order = (
            sem(n) for n in ("g_turned", "g_ready", "x_ready", "y_ready", "y_turned", "folded", "order"))
        block = ctx.enter_context(nc.Block())
        GROUPS = TILES // SUB

        @block.tensor
        def _(pe):
            def turn_gates(g):
                for s in range(SUB):
                    last = pe.transpose(pg[:, g % 2, P * s:P * s + P], gates[:, SUB * g + s, :], R.c("ident"))
                last.then_inc(g_turned, 1)

            def turn_x(g):
                if g >= 2:
                    pe.wait_ge(folded, g - 1)
                if b2 is not None:
                    pe.wait_ge(g_ready, g + 1)
                    for s in range(SUB):
                        pe.matmul(pb[:, g % 2, P * s:P * s + P], gT[:, g % 2, P * s:P * s + P], b2, start=True, stop=True)
                for s in range(SUB):
                    last = pe.transpose(px[:, g % 2, P * s:P * s + P], R.xT[:, tile_of(SUB * g + s)], R.c("ident"))
                last.then_inc(x_ready, 1)

            def turn_y(g):
                pe.wait_ge(y_ready, g + 1)
                for s in range(SUB):
                    last = pe.transpose(py[:, g % 2, P * s:P * s + P], acc[:, SUB * g + s, :], R.c("ident"))
                last.then_inc(y_turned, 1)

            for g in range(GROUPS):
                if b2 is not None:
                    turn_gates(g)
                turn_x(g)
                if g >= 1:
                    turn_y(g - 1)
            turn_y(GROUPS - 1)

        if b2 is not None:
            @block.scalar
            def _(act):
                for g in range(GROUPS):
                    act.wait_ge(g_turned, g + 1)
                    act.copy(gT[:, g % 2, :], pg[:, g % 2, :]).then_inc(g_ready, 1)

        @block.vector
        def _(dve):
            chain = Chain(dve, order)

            def make(g):
                dve.wait_ge(x_ready, g + 1)
                a = acc[:, SUB * g:SUB * g + SUB, :].rearrange("p t c -> p (t c)")
                if b2 is not None:
                    chain(dve.tensor_tensor(a, pb[:, g % 2, :], a, ALU.add))
                    for s in range(SUB):
                        t = SUB * g + s
                        last = dve.tensor_scalar(acc[:, t, :], acc[:, t, :], keep[:, t:t + 1], None, ALU.mult)
                    chain(last)
                for s in range(SUB):
                    t = SUB * g + s
                    last = dve.scalar_tensor_tensor(out=acc[:, t, :], in0=px[:, g % 2, P * s:P * s + P],
                                                    scalar=from_x[:, t:t + 1], in1=acc[:, t, :], op0=ALU.mult,
                                                    op1=ALU.add)
                last.then_inc(y_ready, 1)

            def put(g):
                dve.wait_ge(y_turned, g + 1)
                h = R.hT[:, CH * g:CH * g + CH]
                dve.tensor_tensor(h, py[:, g % 2, :], h, ALU.add).then_inc(folded, 1)

            for g in range(GROUPS):
                make(g)
                if g >= 1:
                    put(g - 1)
            put(GROUPS - 1)


def gates_0(nc, R, logits, gates, from_x):
    E = 8
    with ExitStack() as ctx:
        sb, ps, sem = allocators(nc, ctx, "g0")
        shape = [P, TILES, E]
        one, two, t1 = sb("one", shape), sb("two", shape), sb("t1", shape)
        m1, m2, i1, i2, s1, s2 = (sb(n, [P, TILES]) for n in ("m1", "m2", "i1", "i2", "s1", "s2"))
        keep = sb("keep", [P, 2, TILES])
        full = sb("full", [P, 2, E])
        one_bf, both_bf = sb("one_bf", shape, BF16), sb("both_bf", shape, BF16)
        tally = ps("tally", [P, 2, 512])
        gap_ready, exp_ready, chosen, tallied, order = (
            sem(n) for n in ("gap_ready", "exp_ready", "chosen", "tallied", "order"))
        block = ctx.enter_context(nc.Block())

        def wide(v):
            return v[:, :].unsqueeze(2).to_broadcast(shape)

        rev = R.c("rev8").unsqueeze(1).to_broadcast(shape)
        iota = R.c("iota8").unsqueeze(1).to_broadcast(shape)

        @block.scalar
        def _(act):
            act.wait_ge(gap_ready, 1)
            act.activation(s2[:, :], m2[:, :], ACT.Exp).then_inc(exp_ready, 1)

        @block.tensor
        def _(pe):
            pe.wait_ge(chosen, 1)
            for n, t in enumerate((one_bf, both_bf)):
                last = pe.matmul(tally[:, n, 0:TILES * E], R.bf["ones"][:, :], t[:, :, :].rearrange("p t e -> p (t e)"),
                                 start=True, stop=True)
            last.then_inc(tallied, 1)

        @block.vector
        def _(dve):
            chain = Chain(dve, order)

            def choose(best, at, out):
                chain(dve.tensor_reduce(best[:, :], logits[:, :, :], AX, ALU.max))
                chain(dve.tensor_tensor(t1[:, :, :], logits[:, :, :], wide(best), ALU.is_equal))
                chain(dve.tensor_tensor(t1[:, :, :], t1[:, :, :], rev, ALU.mult))
                chain(dve.tensor_reduce(at[:, :], t1[:, :, :], AX, ALU.max))
                chain(dve.tensor_tensor(out[:, :, :], rev, wide(at), ALU.is_equal))

            choose(m1, i1, one)
            chain(dve.scalar_tensor_tensor(out=logits[:, :, :], in0=one[:, :, :], scalar=-3e38, in1=logits[:, :, :],
                                           op0=ALU.mult, op1=ALU.add))
            choose(m2, i2, two)
            dve.tensor_copy(one_bf[:, :, :], one[:, :, :])
            dve.tensor_tensor(both_bf[:, :, :], one[:, :, :], two[:, :, :], ALU.add).then_inc(chosen, 1)
            dve.tensor_tensor(m2[:, :], m2[:, :], m1[:, :], ALU.subtract).then_inc(gap_ready, 1)
            dve.wait_ge(exp_ready, 1)
            chain(dve.tensor_scalar(s1[:, :], s2[:, :], 1.0, None, ALU.add))
            chain(dve.reciprocal(s1[:, :], s1[:, :]))
            chain(dve.tensor_tensor(s2[:, :], s2[:, :], s1[:, :], ALU.mult))
            dve.wait_ge(tallied, 1)
            for n in range(2):
                last = dve.tensor_reduce(full[:, n, :], tally[:, n, 0:TILES * E].rearrange("p (t e) -> p e t", e=E), AX,
                                         ALU.add)
            chain(last)
            chain(dve.tensor_scalar(full[:, :, :], full[:, :, :], float(N), R.c("last_row"), ALU.is_ge, ALU.mult))
            chain(dve.memset(keep[:, :, :], 1.0))
            for n, t in enumerate((one, two)):
                chain(dve.tensor_tensor(t1[:, n, :], t[:, TILES - 1, :], full[:, n, :], ALU.mult))
                chain(dve.tensor_reduce(keep[:, n, TILES - 1:TILES], t1[:, n, :], AX, ALU.add))
                chain(dve.tensor_scalar(keep[:, n, TILES - 1:TILES], keep[:, n, TILES - 1:TILES], -1.0, 1.0, ALU.mult,
                                        ALU.add))
            for n, t in enumerate((i1, i2)):
                chain(dve.tensor_scalar(t[:, :], t[:, :], -1.0, float(E), ALU.mult, ALU.add))
                chain(dve.tensor_tensor(t[:, :], t[:, :], keep[:, n, :], ALU.mult))
            chain(dve.tensor_tensor(i1[:, :], i1[:, :], i2[:, :], ALU.max))
            chain(dve.tensor_tensor(m1[:, :], s1[:, :], keep[:, 0, :], ALU.mult))
            chain(dve.tensor_tensor(m2[:, :], s2[:, :], keep[:, 1, :], ALU.mult))
            dve.tensor_tensor(s1[:, :], s1[:, :], m1[:, :], ALU.subtract)
            chain(dve.tensor_tensor(s2[:, :], s2[:, :], m2[:, :], ALU.subtract))
            dve.tensor_tensor(from_x[:, :], s1[:, :], s2[:, :], ALU.add)
            chain(dve.tensor_tensor(m1[:, :], m1[:, :], m2[:, :], ALU.add))
            chain(dve.tensor_tensor(gates[:, :, :], iota, wide(i1), ALU.is_equal))
            chain(dve.tensor_tensor(gates[:, :, :], gates[:, :, :], wide(m1), ALU.mult))


def feed_forward_0(nc, R):
    E = 8
    with ExitStack() as ctx:
        sb, _, _ = allocators(nc, ctx, "f0")
        gates, acc, from_x = sb("gates", [P, TILES, E]), sb("acc", [P, TILES, C]), sb("from_x", [P, TILES])
        logits, br = sb("logits", [P, TILES, E]), sb("br", [E, 1])
        layer_norm(nc, R, "f0_ln", R.hT, R.xT)
        with nc.semaphore("f0_bias") as loaded, nc.Block() as block:
            @block.sync
            def _(sp):
                sp.dma_start(br[:, :], R.ins["L0_ffn_br"].rearrange("(e o) -> e o", o=1)).then_inc(loaded, 16)
                sp.wait_ge(loaded, 16)
        route(nc, R, "f0_route", R.w["L0_ffn_Wr"][:, :], E, logits, br[:, 0:1])
        gates_0(nc, R, logits, gates, from_x)
        zero(nc, acc)
        i = R.ins
        experts(nc, R, "f0_experts", E, "glu", ((i["L0_ffn_W1"], i["L0_ffn_W2"]), i["L0_ffn_W3"]), gates, acc)
        fold(nc, R, "f0_fold", acc, from_x)


def feed_forward_1(nc, R):
    E, K = 32, 2
    capacity = -(-N * K * 5 // (4 * E))
    with ExitStack() as ctx:
        sb, _, _ = allocators(nc, ctx, "f1")
        gates, acc = sb("gates", [P, TILES, E]), sb("acc", [P, TILES, C])
        dropped, kept = sb("dropped", [P, TILES]), sb("kept", [P, TILES])
        logits, b1, b1T, b2 = sb("logits", [P, TILES, E]), sb("b1", [E, C]), sb("b1T", [P, E]), sb("b2", [E, C])
        layer_norm(nc, R, "f1_ln", R.hT, R.xT)
        route(nc, R, "f1_route", R.w["L1_ffn_Wg"][:, :], E, logits)
        top_gates(nc, R, "f1_top", logits, E, K, gates, 1e-9, capacity, dropped)
        with (nc.semaphore("f1_loaded") as loaded, nc.semaphore("f1_turned") as turned,
              nc.psum_tensor("f1_pb", [P, 512], F32) as pb, nc.Block() as block):
            @block.sync
            def _(sp):
                sp.dma_start(b1[:, :], R.ins["L1_ffn_b1"]).then_inc(loaded, 16)
                sp.dma_start(b2[:, :], R.ins["L1_ffn_b2"]).then_inc(loaded, 16)

            @block.tensor
            def _(pe):
                pe.wait_ge(loaded, 32)
                pe.transpose(pb[:, 0:E], b1[:, :], R.c("ident")[0:E, 0:E]).then_inc(turned, 1)

            @block.vector
            def _(dve):
                dve.memset(acc[:, :, :], 0.0)
                dve.tensor_scalar(kept[:, :], dropped[:, :], -1.0, 1.0, ALU.mult, ALU.add)
                dve.wait_ge(turned, 1)
                dve.tensor_copy(b1T[:, :], pb[:, 0:E])
        i = R.ins
        experts(nc, R, "f1_experts", E, "relu", ((i["L1_ffn_W1"],), i["L1_ffn_W2"]), gates, acc, b1T)
        fold(nc, R, "f1_fold", acc, dropped, kept, gates, b2[:, :])


def dense_mlp(nc, R, tag, src, w_up, up_scale, up_bias, w_down, finish):
    K = 4
    with ExitStack() as ctx:
        sb, ps, sem = allocators(nc, ctx, tag)
        hidden, t = sb("hidden", [P, 2, K, CH]), sb("t", [P, 2, CH])
        up, down = ps("up", [P, K, CH]), ps("down", [P, 2, CH])
        up_ready, hidden_ready, down_ready, evacuated, done, order = (
            sem(n) for n in ("up_ready", "hidden_ready", "down_ready", "evacuated", "done", "order"))
        block = ctx.enter_context(nc.Block())
        kind, p1, p2, p3 = finish

        @block.tensor
        def _(pe):
            pe.sem_inc(down_ready, SLOTS)
            with pe.Fori(0, CHUNKS // 2) as i:
                for u in range(2):
                    n = 2 * i + u
                    for k in range(K):
                        pe.wait_ge(hidden_ready, K * n + k + 1)
                        pe.matmul(up[:, k, :], w_up(k), src[:, bass.ds(i * (2 * CH) + u * CH, CH)], start=True,
                                  stop=True).then_inc(up_ready, 1)
                    pe.wait_ge(done, n + 1)
                    for k in range(K):
                        pe.wait_ge(hidden_ready, K * n + k + 1 + K)
                        last = pe.matmul(down[:, u, :], w_down(k), hidden[:, u, k, :], start=(k == 0), stop=(k == K - 1))
                    last.then_inc(down_ready, 1)

        @block.scalar
        def _(act):
            act.sem_inc(hidden_ready, K)
            with act.Fori(0, CHUNKS // 2) as i:
                for u in range(2):
                    n = 2 * i + u
                    for k in range(K):
                        act.wait_ge(up_ready, K * n + k + 1)
                        act.wait_ge(down_ready, n + 1)
                        act.activation(hidden[:, u, k, :], up[:, k, :], ACT.Relu, scale=up_scale(k),
                                       bias=up_bias(k)).then_inc(hidden_ready, 1)
                    if kind == "norm":
                        act.wait_ge(down_ready, n + 1 + SLOTS)
                        act.wait_ge(done, n + 1)
                        act.activation(t[:, u, :], down[:, u, :], ACT.Relu, scale=p1, bias=p2).then_inc(evacuated, 1)

        @block.vector
        def _(dve):
            dve.sem_inc(done, SLOTS)
            chain = Chain(dve, order)
            with dve.Fori(0, CHUNKS // 2) as i:
                chain.turn(i, 4 if kind == "half" else 2)
                for u in range(2):
                    n = 2 * i + u
                    at = bass.ds(i * (2 * CH) + u * CH, CH)
                    if kind == "half":
                        dve.wait_ge(down_ready, n + 1 + SLOTS)
                        chain(dve.scalar_tensor_tensor(out=t[:, u, :], in0=down[:, u, :], scalar=p1, in1=p2[:, at],
                                                       op0=ALU.add, op1=ALU.add))
                        chain(dve.tensor_tensor(t[:, u, :], t[:, u, :], p3[:, at], ALU.add))
                        dve.scalar_tensor_tensor(out=R.hT[:, at], in0=t[:, u, :], scalar=0.5, in1=R.hT[:, at],
                                                 op0=ALU.mult, op1=ALU.add).then_inc(done, 1)
                    else:
                        dve.wait_ge(evacuated, n + 1)
                        chain(dve.tensor_tensor(t[:, u, :], t[:, u, :], p3[:, at], ALU.add))
                        dve.tensor_tensor(R.hT[:, at], R.hT[:, at], t[:, u, :], ALU.add).then_inc(done, 1)
                chain.close()


def add_arrays(nc, R, tag, dst, a):
    with nc.Block() as block:
        @block.vector
        def _(dve):
            with dve.Fori(0, CHUNKS) as i:
                at = bass.ds(i * CH, CH)
                dve.tensor_tensor(dst[:, at], dst[:, at], a[:, at], ALU.add)


def unit_keys(nc, R, tag, q, dst, dram):
    with ExitStack() as ctx:
        sb, ps, sem = allocators(nc, ctx, tag)
        squares, norm = sb("squares", [P, 2, CH]), sb("norm", [P, 2, CH])
        total = ps("total", [P, 2, CH])
        squared, total_ready, norm_ready, done, stored, order = (
            sem(n) for n in ("squared", "total_ready", "norm_ready", "done", "stored", "order"))
        block = ctx.enter_context(nc.Block())

        @block.scalar
        def _(act):
            with act.Fori(0, CHUNKS // 2) as i:
                for u in range(2):
                    act.wait_ge(done, 2 * i + u + 1)
                    act.wait_ge(total_ready, SLOTS)
                    act.activation(squares[:, u, :], q[:, bass.ds(i * (2 * CH) + u * CH, CH)], ACT.Square).then_inc(
                        squared, 1)
                    act.wait_ge(total_ready, 2 * i + u + 1 + SLOTS)
                    act.activation(norm[:, u, :], total[:, u, :], ACT.Sqrt).then_inc(norm_ready, 1)

        @block.tensor
        def _(pe):
            pe.sem_inc(total_ready, SLOTS)
            with pe.Fori(0, CHUNKS // 2) as i:
                for u in range(2):
                    pe.wait_ge(squared, 2 * i + u + 1)
                    pe.matmul(total[:, u, :], R.c("head_block"), squares[:, u, :], start=True, stop=True).then_inc(
                        total_ready, 1)

        @block.vector
        def _(dve):
            dve.sem_inc(done, SLOTS)
            chain = Chain(dve, order)
            with dve.Fori(0, CHUNKS // 2) as i:
                chain.turn(i, 4)
                for u in range(2):
                    at = bass.ds(i * (2 * CH) + u * CH, CH)
                    dve.wait_ge(norm_ready, 2 * i + u + 1)
                    chain(dve.tensor_scalar(norm[:, u, :], norm[:, u, :], 1e-12, None, ALU.max))
                    chain(dve.reciprocal(norm[:, u, :], norm[:, u, :]))
                    dve.tensor_tensor(dst[:, at], q[:, at], norm[:, u, :], ALU.mult).then_inc(done, 1)
                chain.close()

        @block.sync
        def _(sp):
            with sp.Fori(0, CHUNKS) as i:
                at = bass.ds(i * CH, CH)
                sp.wait_ge(done, i + 1 + SLOTS)
                sp.dma_start(dram[:, at], dst[:, at]).then_inc(stored, 16)
            sp.wait_ge(stored, 16 * CHUNKS)


def hash_groups(nc, R, tag, q_all, groups):
    NB, G = 32, 2 * HEADS
    with ExitStack() as ctx:
        sb, ps, sem = allocators(nc, ctx, tag)
        q = sb("q", [P, 2, T])
        r = sb("r", [HALF, G, 2, NB // 2])
        eq = sb("eq", [HALF, G, NB])
        best, at_bucket, rank = sb("best", [HALF, G]), sb("at_bucket", [HALF, G]), sb("rank", [HALF, G])
        hot, below = sb("hot", [HALF, G, NB], BF16), sb("below", [HALF, G, NB], BF16)
        edge, chunk, reach = sb("edge", [HALF, G, 8]), sb("chunk", [HALF, G, 8]), sb("reach", [HALF, G, 8])
        sides = sb("sides", [HALF, 2, HEADS, 2, 8], BF16)
        flat = sb("flat", [P, 2, T], BF16)
        pr, pk, pt = ps("pr", [HALF, 2, 512]), ps("pk", [HALF, 512]), ps("pt", [P, 2 * T], BF16)
        copied, turned_q, hot_ready, ranked, sides_ready, flat_turned, flat_ready, order = (
            sem(n) for n in ("copied", "turned_q", "hot_ready", "ranked", "sides_ready", "flat_turned", "flat_ready",
                             "order"))
        stored = [sem(f"stored{u}") for u in range(2)]
        block = ctx.enter_context(nc.Block())
        wide_shape = [HALF, G, NB]

        @block.gpsimd
        def _(pool):
            with pool.Fori(0, B // 2) as i:
                for u in range(2):
                    pool.wait_ge(turned_q, 2 * i + u + 1)
                    pool.wait_ge(turned_q, SLOTS)
                    pool.tensor_copy(q[:, u, :], q_all[:, bass.ds(i * (2 * T) + u * T, T)]).then_inc(copied, 1)

        @block.tensor
        def _(pe):
            pe.sem_inc(turned_q, SLOTS)

            def rotate(n, u):
                pe.wait_ge(copied, n + 1)
                pe.wait_ge(hot_ready, n + 1)
                for half in range(2):
                    last = pe.matmul(pr[:, u, P * half:P * half + P], q[:, u, HALF * half:HALF * half + HALF], R.rot[:, :],
                                     start=True, stop=True)
                last.then_inc(turned_q, 1)

            def ranks(n, u):
                pe.wait_ge(hot_ready, n + 1 + SLOTS)
                for half in range(2):
                    out = pk[:, 256 * half:256 * half + 256]
                    one, before = R.bf["ones"][0:HALF, 0:HALF], R.bf["before"][0:HALF, 0:HALF]
                    terms = [(before, hot, half), (one, below, 0), (one, below, 1)] + ([(one, hot, 0)] if half else [])
                    for m, (lhsT, t, side) in enumerate(terms):
                        rhs = t[:, HEADS * side:HEADS * side + HEADS, :].rearrange("p h b -> p (h b)")
                        last = pe.matmul(out, lhsT, rhs, start=(m == 0), stop=(m == len(terms) - 1))
                last.then_inc(ranked, 1)

            def turn(n, u):
                pe.wait_ge(sides_ready, n + 1)
                pe.wait_ge(flat_ready, n + 1)
                for half in range(2):
                    last = pe.transpose(pt[:, HALF * half:HALF * half + HALF],
                                        sides[:, half].rearrange("p h k c -> p (h k c)"), R.bf["ident"][0:HALF, 0:HALF])
                last.then_inc(flat_turned, 1)

            with pe.Fori(0, B // 2) as i:
                for u in range(2):
                    rotate(2 * i + u, u)
                    ranks(2 * i + u, u)
                    turn(2 * i + u, u)

        @block.scalar
        def _(act):
            act.sem_inc(flat_ready, 1)
            with act.Fori(0, B // 2) as i:
                for u in range(2):
                    act.wait_ge(flat_turned, 2 * i + u + 1)
                    act.wait_ge(stored[u], 16 * i + 16)
                    act.copy(flat[:, u, :], pt[:, 0:T]).then_inc(flat_ready, 1)

        @block.sync
        def _(sp):
            for u in range(2):
                sp.sem_inc(stored[u], 16)
            with sp.Fori(0, B // 2) as i:
                for u in range(2):
                    sp.wait_ge(flat_ready, 2 * i + u + 2)
                    sp.dma_start(groups[:, bass.ds(i * (2 * T) + u * T, T)], flat[:, u, :]).then_inc(stored[u], 16)
            for u in range(2):
                sp.wait_ge(stored[u], 16 * (B // 2 + 1))

        @block.vector
        def _(dve):
            chain = Chain(dve, order)
            rev = R.c("rev32", HALF).unsqueeze(1).to_broadcast(wide_shape)
            edges = R.c("chunk_edge", HALF).unsqueeze(1).to_broadcast([HALF, G, 8])

            def wide(v, n=NB):
                return v[:, :].unsqueeze(2).to_broadcast([HALF, G, n])

            chain(dve.memset(sides[:, :, :, :, :], 0.0))
            dve.memset(sides[:, :, :, 0, 6:7], 1.0)
            dve.memset(sides[:, :, :, 1, 6:7], -BIG)
            dve.sem_inc(hot_ready, SLOTS)
            with dve.Fori(0, B // 2) as i:
                chain.turn(i, 2 * 12, 1)
                for u in range(2):
                    n = 2 * i + u
                    dve.wait_ge(turned_q, n + 1 + SLOTS)
                    src = pr[:, u, 0:2 * P].rearrange("p (g b) -> p g b", b=NB // 2)
                    dve.tensor_copy(r[:, :, 0, :], src)
                    chain(dve.tensor_scalar(r[:, :, 1, :], src, -1.0, None, ALU.mult))
                    rr = r[:, :, :, :].rearrange("p g s b -> p g (s b)")
                    chain(dve.tensor_reduce(best[:, :], rr, AX, ALU.max))
                    chain(dve.tensor_tensor(eq[:, :, :], rr, wide(best), ALU.is_equal))
                    chain(dve.tensor_tensor(eq[:, :, :], eq[:, :, :], rev, ALU.mult))
                    chain(dve.tensor_reduce(at_bucket[:, :], eq[:, :, :], AX, ALU.max))
                    chain(dve.tensor_tensor(hot[:, :, :], rev, wide(at_bucket), ALU.is_equal))
                    dve.tensor_tensor(below[:, :, :], rev, wide(at_bucket), ALU.is_lt).then_inc(hot_ready, 1)
                    dve.wait_ge(ranked, n + 1)
                    chain(dve.tensor_tensor(eq[:, :, :], pk[:, 0:512].rearrange("p (g b) -> p g b", b=NB), hot[:, :, :],
                                            ALU.mult))
                    chain(dve.tensor_reduce(rank[:, :], eq[:, :, :], AX, ALU.add))
                    chain(dve.tensor_tensor(edge[:, :, :], wide(rank, 8), edges, ALU.is_ge))
                    chain(dve.tensor_tensor(chunk[:, :, 0:6], edge[:, :, 0:6], edge[:, :, 1:7], ALU.subtract))
                    dve.tensor_tensor(reach[:, :, 1:6], chunk[:, :, 1:6], chunk[:, :, 0:5], ALU.add)
                    chain(dve.tensor_tensor(reach[:, :, 0:1], chunk[:, :, 0:1], chunk[:, :, 5:6], ALU.add))
                    dve.wait_ge(flat_ready, n + 1)
                    s = sides[:, :, :, :, :].rearrange("p a h k c -> p (a h) k c")
                    chain(dve.tensor_copy(s[:, :, 0, 0:6], chunk[:, :, 0:6]))
                    dve.tensor_scalar(s[:, :, 1, 0:6], reach[:, :, 0:6], BIG, None, ALU.mult).then_inc(sides_ready, 1)
                chain.close()


def add_projection(nc, R, tag, src, w, bias, x, dst):
    with ExitStack() as ctx:
        sb, ps, sem = allocators(nc, ctx, tag)
        out = ps("out", [P, 2, CH])
        product_ready, done = sem("product_ready"), sem("done")
        block = ctx.enter_context(nc.Block())

        @block.tensor
        def _(pe):
            with pe.Fori(0, CHUNKS // 2) as i:
                for u in range(2):
                    pe.wait_ge(done, 2 * i + u + 1)
                    pe.matmul(out[:, u, :], w, src[:, bass.ds(i * (2 * CH) + u * CH, CH)], start=True,
                              stop=True).then_inc(product_ready, 1)

        @block.vector
        def _(dve):
            dve.sem_inc(done, SLOTS)
            with dve.Fori(0, CHUNKS // 2) as i:
                for u in range(2):
                    at = bass.ds(i * (2 * CH) + u * CH, CH)
                    dve.wait_ge(product_ready, 2 * i + u + 1)
                    dve.scalar_tensor_tensor(out=dst[:, at], in0=out[:, u, :], scalar=bias, in1=x[:, at], op0=ALU.add,
                                             op1=ALU.add).then_inc(done, 1)


def attention_1(nc, R):
    with ExitStack() as ctx:
        sb, _, _ = allocators(nc, ctx, "a1")
        own, y1, h1 = sb("own", [P, N]), sb("y1", [P, N]), sb("h1", [P, N])
        layer_norm(nc, R, "a1_ln", R.hT, R.xT)
        layer_norm(nc, R, "a1_ln1", R.xT, h1, 1e-5, R.col("L1_attn_ln1_g"), R.col("L1_attn_ln1_b"))
        project(nc, R, "a1_qv", h1, [(R.w["L1_attn_w_qk"][:, :], own, ACT.Identity, 1.0, 0.0),
                                     (R.w["L1_attn_w_v"][:, :], y1, ACT.Identity, 1.0, 0.0)],
                copies=[(0, R.scratch[0]), (1, R.scratch[2])])
        unit_keys(nc, R, "a1_keys", own, y1, R.scratch[1])
        hash_groups(nc, R, "a1_hash", own, R.groups)
        attend(nc, R, "a1", *R.scratch[0:5], HD ** -0.5, R.groups, -50000.0, own)
        divide(nc, R, "a1_div", R.scratch[3], R.scratch[4], h1, own, R.scratch[2])
        add_projection(nc, R, "a1_out", h1, R.w["L1_attn_w_out"][:, :], R.col("L1_attn_b_out"), R.xT, y1)
        layer_norm(nc, R, "a1_ln2", y1, h1, 1e-5, R.col("L1_attn_ln2_g"), R.col("L1_attn_ln2_b"))
        dense_mlp(nc, R, "a1_mlp", h1, lambda k: R.w["L1_attn_w_ff1"][:, C * k:C * k + C], lambda k: 1.0,
                  lambda k: R.col("L1_attn_b_ff1", k), lambda k: R.w["L1_attn_w_ff2"][:, k, :],
                  ("half", R.col("L1_attn_b_ff2"), R.xT, y1))


def attention_2(nc, R):
    with ExitStack() as ctx:
        sb, _, _ = allocators(nc, ctx, "a2")
        q, k, v, o = sb("q", [P, N]), sb("k", [P, N]), sb("v", [P, N]), sb("o", [P, N])
        layer_norm(nc, R, "a2_ln", R.hT, R.xT)
        project(nc, R, "a2_qkv", R.xT, [(R.w[f"L2_attn_W{n}"][:, :], dst, ACT.Relu, 1.0, R.col(f"L2_attn_b{n}"))
                                        for n, dst in (("q", q), ("k", k), ("v", v))])
        one_head(nc, R, "a2", q, k, v, o, HD ** -0.5)
        project(nc, R, "a2_out", o, [(R.w["L2_attn_Wo"][:, :], q, ACT.Relu, 1.0, R.col("L2_attn_bo"))])
        layer_norm(nc, R, "a2_norm", q, R.hT, 1e-3, R.col("L2_attn_gamma"), R.col("L2_attn_beta"), residual=True)


def one_head(nc, R, tag, q_all, k_all, v_all, o_all, scale):
    with ExitStack() as ctx:
        sb, ps, sem = allocators(nc, ctx, tag)
        qkv = sb("qkv", [P, 2, 3, T])
        peak, total = sb("peak", [HALF, 2, 2]), sb("total", [HALF, 2, 2])
        prob, probT, vrow = sb("prob", [HALF, 2, 2, T]), sb("probT", [HALF, 2, 2, T]), sb("vrow", [HALF, 2, 2, C])
        pS, pV, pT, pO = ps("pS", [HALF, 2, 512]), ps("pV", [HALF, 2, 512]), ps("pT", [HALF, 2, 512]), ps("pO", [P, 2, 512])
        loaded = [sem(f"loaded{u}") for u in range(2)]
        scores_ready, v_ready, peak_ready, exp_done, scaled, turned, copied, mixed, done, order = (
            sem(n) for n in ("scores_ready", "v_ready", "peak_ready", "exp_done", "scaled", "turned", "copied", "mixed",
                             "done", "order"))
        block = ctx.enter_context(nc.Block())

        @block.sync
        def _(sp):
            with sp.Fori(0, B // 2) as i:
                for u in range(2):
                    sp.wait_ge(done, 2 * i + u + 1)
                    for j, src in enumerate((q_all, k_all, v_all)):
                        sp.dma_start(qkv[:, u, j, :], src[:, bass.ds(i * (2 * T) + u * T, T)]).then_inc(loaded[u], 16)

        @block.tensor
        def _(pe):
            def scores(n, u, turn):
                pe.wait_ge(loaded[u], 48 * turn + 48)
                pe.wait_ge(done, n + 1)
                for half in range(2):
                    last = pe.matmul(pS[:, u, T * half:T * half + T], qkv[:, u, 0, HALF * half:HALF * half + HALF],
                                     qkv[:, u, 1, :], start=True, stop=True)
                last.then_inc(scores_ready, 1)
                for half in range(2):
                    last = pe.transpose(pV[:, u, C * half:C * half + C], qkv[:, u, 2, HALF * half:HALF * half + HALF],
                                        R.c("ident"))
                last.then_inc(v_ready, 1)

            def mix(n, u):
                pe.wait_ge(scaled, n + 1)
                for a in range(2):
                    for b in range(2):
                        last = pe.transpose(pT[:, u, T * b + HALF * a:T * b + HALF * a + HALF],
                                            prob[:, u, a, HALF * b:HALF * b + HALF], R.c("ident")[0:HALF, 0:HALF])
                last.then_inc(turned, 1)
                pe.wait_ge(copied, 2 * n + 2)
                for b in range(2):
                    last = pe.matmul(pO[:, u, 0:T], vrow[:, u, b, :], probT[:, u, b, :], start=(b == 0), stop=(b == 1))
                last.then_inc(mixed, 1)

            scores(0, 0, 0)
            with pe.Fori(0, B // 2 - 1) as i:
                for u in range(2):
                    scores(2 * i + u + 1, 1 - u, i + u)
                    mix(2 * i + u, u)
            scores(B - 1, 1, B // 2 - 1)
            mix(B - 2, 0)
            mix(B - 1, 1)

        @block.scalar
        def _(act):
            with act.Fori(0, B // 2) as i:
                for u in range(2):
                    n = 2 * i + u
                    act.wait_ge(v_ready, n + 1)
                    act.copy(vrow[:, u, :, :].rearrange("p a c -> p (a c)"), pV[:, u, 0:2 * C]).then_inc(copied, 1)
                    act.wait_ge(peak_ready, n + 1)
                    for half in range(2):
                        last = act.activation(prob[:, u, half, :], pS[:, u, T * half:T * half + T], ACT.Exp, scale=scale,
                                              bias=peak[:, u, half:half + 1], accum_out=total[:, u, half:half + 1])
                    last.then_inc(exp_done, 1)
                    act.wait_ge(turned, n + 1)
                    act.copy(probT[:, u, :, :].rearrange("p a c -> p (a c)"), pT[:, u, 0:2 * T]).then_inc(copied, 1)

        @block.vector
        def _(dve):
            dve.sem_inc(done, SLOTS)
            chain = Chain(dve, order)
            with dve.Fori(0, B // 2) as i:
                chain.turn(i, 4)
                for u in range(2):
                    n = 2 * i + u
                    dve.wait_ge(scores_ready, n + 1)
                    chain(dve.tensor_reduce(peak[:, u, :], pS[:, u, 0:2 * T].rearrange("p (a t) -> p a t", a=2), AX,
                                            ALU.max))
                    dve.tensor_scalar(peak[:, u, :], peak[:, u, :], -scale, None, ALU.mult).then_inc(peak_ready, 1)
                    dve.wait_ge(exp_done, n + 1)
                    chain(dve.reciprocal(total[:, u, :], total[:, u, :]))
                    for half in range(2):
                        last = dve.tensor_scalar(prob[:, u, half, :], prob[:, u, half, :], total[:, u, half:half + 1], None,
                                                 ALU.mult)
                    last.then_inc(scaled, 1)
                    dve.wait_ge(mixed, n + 1)
                    dve.tensor_copy(o_all[:, bass.ds(i * (2 * T) + u * T, T)], pO[:, u, 0:T]).then_inc(done, 1)
                chain.close()


def attention_3(nc, R):
    with ExitStack() as ctx:
        sb, _, _ = allocators(nc, ctx, "a3")
        q, k, v, o = sb("q", [P, N]), sb("k", [P, N]), sb("v", [P, N]), sb("o", [P, N])
        layer_norm(nc, R, "a3_ln", R.hT, R.xT)
        project(nc, R, "a3_qkv", R.xT, [
            (R.wt[f"{s}T"][:, :], dst, ACT.Relu, R.bn[:, 0, n:n + 1], R.bn[:, 1, n:n + 1])
            for n, (s, dst) in enumerate((("q", q), ("k", k), ("v", v)))])
        linear_heads(nc, R, "a3", q, k, v, o, 0.125)
        project(nc, R, "a3_out", o, [(R.wt["pT"][:, :], q, ACT.Relu, R.bn[:, 0, 3:4], R.bn[:, 1, 3:4])])
        add_arrays(nc, R, "a3_x1", q, R.xT)
        dense_mlp(nc, R, "a3_mlp", q, lambda n: R.wt["f1T"][:, C * n:C * n + C], lambda n: R.bn[:, 0, 4 + n:5 + n],
                  lambda n: R.bn[:, 1, 4 + n:5 + n], lambda n: R.wt["f2T"][:, C * n:C * n + C],
                  ("norm", R.bn[:, 0, 8:9], R.bn[:, 1, 8:9], q))


def linear_heads(nc, R, tag, q_all, k_all, v_all, o_all, scale):
    with ExitStack() as ctx:
        sb, ps, sem = allocators(nc, ctx, tag)
        kv = sb("kv", [P, 2, 2, T])
        rows, state = sb("rows", [HALF, 2, 2, 2, C]), sb("state", [P, 2, C])
        pR, pS, pO = ps("pR", [HALF, 2, 512]), ps("pS", [P, 2, 512]), ps("pO", [P, 2, 512])
        loaded = [sem(f"loaded{u}") for u in range(2)]
        turned, rows_ready, product_ready, state_ready, mixed, done = (
            sem(n) for n in ("turned", "rows_ready", "product_ready", "state_ready", "mixed", "done"))
        block = ctx.enter_context(nc.Block())

        @block.sync
        def _(sp):
            with sp.Fori(0, B // 2) as i:
                for u in range(2):
                    sp.wait_ge(done, 2 * i + u + 1)
                    for j, src in enumerate((k_all, v_all)):
                        sp.dma_start(kv[:, u, j, :], src[:, bass.ds(i * (2 * T) + u * T, T)]).then_inc(loaded[u], 16)

        @block.tensor
        def _(pe):
            def turn(n, u, t):
                pe.wait_ge(loaded[u], 32 * t + 32)
                pe.wait_ge(done, n + 1)
                for j in range(2):
                    for half in range(2):
                        a = C * (2 * j + half)
                        last = pe.transpose(pR[:, u, a:a + C], kv[:, u, j, HALF * half:HALF * half + HALF], R.c("ident"))
                last.then_inc(turned, 1)

            def mix(n, u, i):
                pe.wait_ge(rows_ready, n + 1)
                for half in range(2):
                    last = pe.matmul(pS[:, u, 0:C], rows[:, u, 0, half, :], rows[:, u, 1, half, :], start=(half == 0),
                                     stop=(half == 1))
                last.then_inc(product_ready, 1)
                pe.wait_ge(state_ready, n + 1)
                pe.matmul(pO[:, u, 0:T], state[:, u, :], q_all[:, bass.ds(n * T, T)], start=True, stop=True).then_inc(mixed, 1)

            turn(0, 0, 0)
            with pe.Fori(0, B // 2 - 1) as i:
                for u in range(2):
                    turn(2 * i + u + 1, 1 - u, i + u)
                    mix(2 * i + u, u, i)
            turn(B - 1, 1, B // 2 - 1)
            mix(B - 2, 0, 0)
            mix(B - 1, 1, 0)

        @block.scalar
        def _(act):
            act.sem_inc(done, SLOTS)
            with act.Fori(0, B // 2) as i:
                for u in range(2):
                    n = 2 * i + u
                    act.wait_ge(turned, n + 1)
                    act.copy(rows[:, u].rearrange("p j a c -> p (j a c)"), pR[:, u, :]).then_inc(rows_ready, 1)
                    act.wait_ge(mixed, n + 1)
                    act.activation(o_all[:, bass.ds(i * (2 * T) + u * T, T)], pO[:, u, 0:T], ACT.Relu).then_inc(done, 1)

        @block.vector
        def _(dve):
            with dve.Fori(0, B // 2) as i:
                for u in range(2):
                    dve.wait_ge(product_ready, 2 * i + u + 1)
                    dve.scalar_tensor_tensor(out=state[:, u, :], in0=pS[:, u, 0:C], scalar=scale, in1=R.c("head_block"),
                                             op0=ALU.mult, op1=ALU.mult).then_inc(state_ready, 1)


N_IN, N_PROC, N_OUT, D_PV = 512, 256, 512, 64
K_IN, K_PROC, K_OUT = 64, 128, 64


def pattern_weights(nc, R, w):
    with ExitStack() as ctx:
        sb, ps, sem = allocators(nc, ctx, "f2w")
        raw_in, raw_p, raw_o = sb("raw_in", [P, 4, C]), sb("raw_p", [P, 2, N_IN]), sb("raw_o", [P, 4, D_PV])
        pi, pp, po = ps("pi", [P, 512]), ps("pp", [P, 2, 512]), ps("po", [D_PV, 512])
        loaded, zeroed, turned = sem("loaded"), sem("zeroed"), sem("turned")
        block = ctx.enter_context(nc.Block())
        i = R.ins

        @block.sync
        def _(sp):
            sp.wait_ge(zeroed, 1)
            for dst, src in ((raw_in[:, :, :], i["L2_ffn_input_patterns"].rearrange("(k p) d -> p k d", p=P)),
                             (raw_p[:, :, :], i["L2_ffn_process_input_weights"].rearrange("(k p) n -> p k n", p=P)),
                             (raw_o[:, :, :], i["L2_ffn_output_input_weights"].rearrange("(k p) d -> p k d", p=P)),
                             (w["pv"][:, :, 0:D_PV], i["L2_ffn_process_values"].rearrange("(k p) d -> p k d", p=P)),
                             (w["op"][:, :, :], i["L2_ffn_output_patterns"].rearrange("(k p) m -> p k m", p=P))):
                sp.dma_start(dst, src).then_inc(loaded, 16)

        @block.tensor
        def _(pe):
            pe.wait_ge(loaded, 80)
            for k in range(4):
                pe.transpose(pi[:, P * k:P * k + P], raw_in[:, k, :], R.c("ident"))
                pe.transpose(po[:, P * k:P * k + P], raw_o[:, k, :], R.c("ident"))
            for k in range(2):
                for n in range(4):
                    a = 256 * n + P * k
                    last = pe.transpose(pp[:, a // 512, a % 512:a % 512 + P], raw_p[:, k, P * n:P * n + P], R.c("ident"))
            last.then_inc(turned, 1)

        @block.vector
        def _(dve):
            dve.memset(w["pv"][:, :, :], 0.0)
            dve.memset(w["oiT"][:, :], 0.0).then_inc(zeroed, 1)
            dve.wait_ge(turned, 1)
            dve.wait_ge(zeroed, 1)
            dve.tensor_copy(w["ipT"][:, :], pi[:, :])
            dve.tensor_copy(w["oiT"][0:D_PV, :], po[:, :])
            dve.tensor_copy(w["piT"][:, :, :].rearrange("p n k -> p (n k)"), pp[:, :, :].rearrange("p a b -> p (a b)"))


def feed_forward_2(nc, R):
    NEVER = -1e30
    QUAD, PAIRS = 4, ((0, 1), (2, 3))
    TURNS = TILES // QUAD
    with ExitStack() as ctx:
        sb, ps, sem = allocators(nc, ctx, "f2")
        layer_norm(nc, R, "f2_ln", R.hT, R.xT)
        w = {"ipT": sb("ipT", [P, N_IN]), "piT": sb("piT", [P, 4, N_PROC]), "pv": sb("pv", [P, 2, C]),
             "oiT": sb("oiT", [P, N_OUT]), "op": sb("op", [P, 4, C])}
        pattern_weights(nc, R, w)
        x, y = sb("x", [P, QUAD, P]), sb("y", [P, 2, P])
        act_in, act_proc, act_out = sb("act_in", [P, QUAD, N_IN]), sb("act_proc", [P, QUAD, N_PROC]), sb(
            "act_out", [P, QUAD, N_OUT])
        sel_in, sel_proc, sel_out = sb("sel_in", [P, QUAD, N_IN]), sb("sel_proc", [P, QUAD, N_PROC]), sb(
            "sel_out", [P, QUAD, N_OUT])
        soft = sb("soft", [P, QUAD, N_PROC])
        inT, procT, outT, aggT = sb("inT", [P, 2, N_IN]), sb("procT", [P, 2, N_PROC]), sb("outT", [P, 2, N_OUT]), sb(
            "aggT", [P, 2, P])
        top, peak, total = sb("top", [P, QUAD, 8]), sb("peak", [P, QUAD, 1]), sb("total", [P, QUAD, 1])
        bank = [ps(f"bank{t}", [P, 512]) for t in range(QUAD)]
        turn = [ps(f"turn{u}", [P, 512]) for u in range(2)]
        small = [ps(f"small{u}", [P, 512]) for u in range(2)]
        names = ("copied", "in_ready", "in_acted", "in_selected", "in_turned", "in_evacuated", "proc_ready", "proc_acted",
                 "peak_ready", "soft_ready", "proc_selected", "proc_turned", "proc_evacuated", "agg_ready", "agg_evacuated",
                 "out_ready", "out_acted", "out_selected", "out_turned", "out_evacuated", "y_ready", "done", "added", "order")
        s = {n: sem(n) for n in names}
        block = ctx.enter_context(nc.Block())

        @block.gpsimd
        def _(pool):
            pool.sem_inc(s["added"], 2)

            def copy_in(i):
                for t in range(QUAD):
                    pool.wait_ge(s["in_ready"], QUAD * i + t + 1)
                    pool.tensor_copy(x[:, t, :], R.xT[:, bass.ds(i * (QUAD * P) + t * P, P)]).then_inc(s["copied"], 1)

            def add_out(i):
                for t in range(QUAD):
                    at = bass.ds(i * (QUAD * P) + t * P, P)
                    pool.wait_ge(s["done"], QUAD * i + t + 1 + 2)
                    pool.tensor_tensor(R.hT[:, at], y[:, t % 2, :], R.hT[:, at], ALU.add).then_inc(s["added"], 1)

            copy_in(0)
            with pool.Fori(0, TURNS - 1) as i:
                copy_in(i + 1)
                add_out(i)
            add_out(TURNS - 1)

        @block.tensor
        def _(pe):
            pe.sem_inc(s["in_ready"], QUAD)

            def product_in(n, t):
                pe.wait_ge(s["copied"], n + 1)
                pe.wait_ge(s["out_acted"], n + 1)
                pe.matmul(bank[t][:, :], x[:, t, :], w["ipT"][:, :], start=True, stop=True).then_inc(s["in_ready"], 1)

            def turned(src, n_blocks, selected, count, signal, t):
                pe.wait_ge(s[selected], count)
                for k in range(n_blocks):
                    last = pe.transpose(turn[t % 2][:, P * k:P * k + P], src[:, t, P * k:P * k + P], R.c("ident"))
                last.then_inc(s[signal], 1)

            for t in range(QUAD):
                product_in(t, t)

            def quad(i, more):
                for pair in PAIRS:
                    for t in pair:
                        n = QUAD * i + t
                        turned(sel_in, 4, "in_selected", n + 1 + QUAD, "in_turned", t)
                    for t in pair:
                        n = QUAD * i + t
                        pe.wait_ge(s["in_evacuated"], n + 1)
                        for k in range(4):
                            last = pe.matmul(bank[t][:, 0:N_PROC], inT[:, t % 2, P * k:P * k + P], w["piT"][:, k, :],
                                             start=(k == 0), stop=(k == 3))
                        last.then_inc(s["proc_ready"], 1)
                for pair in PAIRS:
                    for t in pair:
                        n = QUAD * i + t
                        turned(sel_proc, 2, "proc_selected", n + 1, "proc_turned", t)
                    for t in pair:
                        n = QUAD * i + t
                        pe.wait_ge(s["proc_evacuated"], n + 1)
                        pe.wait_ge(s["done"], QUAD * i + (t % 2) + 1)
                        for k in range(2):
                            last = pe.matmul(small[t % 2][:, 0:P], w["pv"][:, k, :], procT[:, t % 2, P * k:P * k + P],
                                             start=(k == 0), stop=(k == 1))
                        last.then_inc(s["agg_ready"], 1)
                    for t in pair:
                        n = QUAD * i + t
                        pe.wait_ge(s["agg_evacuated"], n + 1)
                        pe.matmul(bank[t][:, :], aggT[:, t % 2, :], w["oiT"][:, :], start=True, stop=True).then_inc(
                            s["out_ready"], 1)
                if more:
                    for t in range(QUAD):
                        product_in(QUAD * i + QUAD + t, t)
                for pair in PAIRS:
                    for t in pair:
                        n = QUAD * i + t
                        turned(sel_out, 4, "out_selected", n + 1, "out_turned", t)
                    for t in pair:
                        n = QUAD * i + t
                        pe.wait_ge(s["out_evacuated"], n + 1)
                        pe.wait_ge(s["done"], n + 1)
                        for k in range(4):
                            last = pe.matmul(small[t % 2][:, P:2 * P], w["op"][:, k, :], outT[:, t % 2, P * k:P * k + P],
                                             start=(k == 0), stop=(k == 3))
                        last.then_inc(s["y_ready"], 1)

            with pe.Fori(0, TURNS - 1) as i:
                quad(i, True)
            quad(TURNS - 1, False)

        @block.scalar
        def _(act):
            act.sem_inc(s["out_acted"], QUAD)
            act.sem_inc(s["done"], 2)

            def gelu_in(n, t):
                act.wait_ge(s["in_ready"], n + 1 + QUAD)
                act.wait_ge(s["in_selected"], n + 1)
                act.activation(act_in[:, t, :], bank[t][:, :], ACT.Gelu).then_inc(s["in_acted"], 1)

            for t in range(QUAD):
                gelu_in(t, t)

            def quad(i, more):
                for pair in PAIRS:
                    for t in pair:
                        act.wait_ge(s["in_turned"], QUAD * i + t + 1)
                        act.copy(inT[:, t % 2, :], turn[t % 2][:, :]).then_inc(s["in_evacuated"], 1)
                    for t in pair:
                        act.wait_ge(s["proc_ready"], QUAD * i + t + 1)
                        act.activation(act_proc[:, t, :], bank[t][:, 0:N_PROC], ACT.Gelu).then_inc(s["proc_acted"], 1)
                for pair in PAIRS:
                    for t in pair:
                        act.wait_ge(s["peak_ready"], QUAD * i + t + 1)
                        act.activation(soft[:, t, :], act_proc[:, t, :], ACT.Exp, bias=peak[:, t, :]).then_inc(
                            s["soft_ready"], 1)
                    for t in pair:
                        act.wait_ge(s["proc_turned"], QUAD * i + t + 1)
                        act.copy(procT[:, t % 2, :], turn[t % 2][:, 0:N_PROC]).then_inc(s["proc_evacuated"], 1)
                    for t in pair:
                        act.wait_ge(s["agg_ready"], QUAD * i + t + 1)
                        act.copy(aggT[:, t % 2, :], small[t % 2][:, 0:P]).then_inc(s["agg_evacuated"], 1)
                    for t in pair:
                        act.wait_ge(s["out_ready"], QUAD * i + t + 1)
                        act.activation(act_out[:, t, :], bank[t][:, :], ACT.Gelu).then_inc(s["out_acted"], 1)
                if more:
                    for t in range(QUAD):
                        gelu_in(QUAD * i + QUAD + t, t)
                for pair in PAIRS:
                    for t in pair:
                        act.wait_ge(s["out_turned"], QUAD * i + t + 1)
                        act.copy(outT[:, t % 2, :], turn[t % 2][:, :]).then_inc(s["out_evacuated"], 1)
                    for t in pair:
                        act.wait_ge(s["y_ready"], QUAD * i + t + 1)
                        act.wait_ge(s["added"], QUAD * i + t + 1)
                        act.copy(y[:, t % 2, :], small[t % 2][:, P:2 * P]).then_inc(s["done"], 1)

            with act.Fori(0, TURNS - 1) as i:
                quad(i, True)
            quad(TURNS - 1, False)

        @block.vector
        def _(dve):
            dve.sem_inc(s["in_selected"], QUAD)
            chain = Chain(dve, s["order"])

            def select(src, marked, pair, k, peaks=False):
                for t in pair:
                    chain.late(dve.memset(top[:, t, :], 0.0))
                for r in range(k // 8):
                    a = src if r == 0 else marked
                    for t in pair:
                        chain.late(dve.max(top[:, t, :], a[:, t, :]))
                    if peaks and r == 0:
                        chain.catch_up()
                        for t in pair:
                            dve.tensor_scalar(peak[:, t, :], top[:, t, 0:1], -1.0, None, ALU.mult).then_inc(
                                s["peak_ready"], 1)
                    for t in pair:
                        chain.late(dve.match_replace(marked[:, t, :], top[:, t, :], a[:, t, :], NEVER))

            with dve.Fori(0, TURNS) as i:
                chain.restart()
                for src, marked, acted, before, k, signal in ((act_in, sel_in, "in_acted", 0, K_IN, "in_selected"),
                                                              (act_proc, sel_proc, "proc_acted", 0, K_PROC, None),
                                                              (act_out, sel_out, "out_acted", QUAD, K_OUT, "out_selected")):
                    for pair in PAIRS:
                        dve.wait_ge(s[acted], QUAD * i + pair[1] + 1 + before)
                        select(src, marked, pair, k, signal is None)
                        for t in pair:
                            if signal is not None:
                                dve.scalar_tensor_tensor(out=marked[:, t, :], in0=marked[:, t, :], scalar=NEVER,
                                                         in1=src[:, t, :], op0=ALU.is_equal, op1=ALU.mult).then_inc(
                                    s[signal], 1)
                                if t == pair[0]:
                                    chain.catch_up()
                                continue
                            dve.wait_ge(s["soft_ready"], QUAD * i + t + 1)
                            chain.late(dve.scalar_tensor_tensor(out=marked[:, t, :], in0=marked[:, t, :], scalar=NEVER,
                                                                in1=soft[:, t, :], op0=ALU.is_equal, op1=ALU.mult,
                                                                accum_out=total[:, t, :]))
                        if signal is None:
                            for t in pair:
                                chain.late(dve.reciprocal(total[:, t, :], total[:, t, :]))
                            chain.catch_up()
                            for t in pair:
                                dve.tensor_scalar(marked[:, t, :], marked[:, t, :], total[:, t, :], None,
                                                  ALU.mult).then_inc(s["proc_selected"], 1)


STAGES = {
    "tokens": tokens,
    "attention_0": attention_0,
    "feed_forward_0": feed_forward_0,
    "attention_1": attention_1,
    "feed_forward_1": feed_forward_1,
    "attention_2": attention_2,
    "feed_forward_2": feed_forward_2,
    "attention_3": attention_3,
    "feed_forward_3": feed_forward_3,
}


def program(nc, ins, out, only=None, h_in=None, dump=None):
    with ExitStack() as ctx:
        R = Resident(nc, ctx, ins, out)
        R.eps = {e: ctx.enter_context(nc.sbuf_tensor(f"eps{k}", [P, 1], F32)) for k, e in enumerate((1e-5, 1e-3))}
        R.scratch = [nc.dram_tensor(f"scratch{n}", (P, N), F32, kind="Internal").ap() for n in range(6)]
        R.groups = nc.dram_tensor("lsh_groups", (P, N), BF16, kind="Internal").ap()
        R.self_value = ctx.enter_context(nc.sbuf_tensor("self_value", [P, 1], F32))
        with nc.Block() as block:
            @block.vector
            def _(dve):
                for e, t in R.eps.items():
                    dve.memset(t[:, :], e)
                dve.memset(R.self_value[:, :], -50000.0)
        set_up(nc, R)
        if h_in is not None:
            with nc.semaphore("hin") as s, nc.Block() as block:
                @block.sync
                def _(sp):
                    sp.dma_start(R.hT[:, :], h_in).then_inc(s, 16)
                    sp.wait_ge(s, 16)
        for name in (only or STAGES):
            STAGES[name](nc, R)
        if dump is not None:
            with nc.semaphore("hdump") as s, nc.Block() as block:
                @block.sync
                def _(sp):
                    sp.dma_start(dump, (R.hT if only[-1] != "ln" else R.xT)[:, :]).then_inc(s, 16)
                    sp.wait_ge(s, 16)


def kernel(**inputs):
    import concourse.bacc as bacc
    from concourse.bass_utils import run_bass_kernel_spmd

    nc = bacc.Bacc("TRN2", target_bir_lowering=False, num_devices=1)
    arrays, ins = {}, {}
    for name, a in list(inputs.items()) + [("consts", CONSTS)]:
        a = np.ascontiguousarray(a)
        arrays[f"in_{name}_dram"] = a
        ins[name] = nc.dram_tensor(f"in_{name}_dram", a.shape, mybir.dt.from_np(a.dtype), kind="ExternalInput").ap()
    out = nc.dram_tensor("out_0_dram", (B, T, C), F32, kind="ExternalOutput").ap()
    program(nc, ins, out)
    r = run_bass_kernel_spmd(nc, [arrays], core_ids=[0])
    return r.results[0]["out_0_dram"]
```

```python
from contextlib import ExitStack

import numpy as np

import concourse.bass as bass
from concourse import mybir

ALU = mybir.AluOpType
ACT = mybir.ActivationFunctionType
AX = mybir.AxisListType.X
F32 = mybir.dt.float32
BF16 = mybir.dt.bfloat16
F32R, U32 = mybir.dt.float32r, mybir.dt.uint32
HIGH_BITS = 0xFFFFF000

P = 128
C = 128
B = 16
GRID = 8
IMG_TOKENS = GRID * GRID
TXT_TOKENS = 128
T = IMG_TOKENS + TXT_TOKENS
N = B * T
HALF = T // 2
HEADS = 8
HD = C // HEADS
TILES = N // P
CH = 512
CHUNKS = N // CH
BIG = 2.0 ** 100
PAD = GRID + 2
SLOTS = 2


def shape_constants():
    parts, at = {}, 0
    out = []

    def put(name, a):
        nonlocal at
        full = np.zeros((P, a.shape[1]), np.float32)
        full[:a.shape[0]] = a
        out.append(full)
        parts[name] = (at, at + a.shape[1])
        at += a.shape[1]

    eye = np.eye(P, dtype=np.float32)
    put("ident", eye)
    put("centre", eye - np.float32(1.0 / C))
    put("mean", np.full((P, P), 1.0 / C, np.float32))
    put("ones", np.ones((P, P), np.float32))
    rows = np.zeros((P, 3, PAD, 2), np.float32)
    for p in range(P):
        row, side = p // 2, p % 2
        kind = {0: 1, 7: 2}.get(row % 8, 0)
        rows[p, kind, row // 8 + 1, side] = 1.0
    put("rows", rows.reshape(P, -1))
    block = np.kron(np.eye(HEADS, dtype=np.float32), np.ones((HD, HD), np.float32))
    put("head_block", block)
    put("before", np.triu(np.ones((P, P), np.float32), 1))
    put("neg_diag", (-BIG * eye[:, :HALF]).astype(np.float32))
    put("rev32", np.tile(32.0 - np.arange(32, dtype=np.float32), (P, 1)))
    put("rev8", np.tile(8.0 - np.arange(8, dtype=np.float32), (P, 1)))
    put("iota8", np.tile(np.arange(8, dtype=np.float32), (P, 1)))
    put("chunk_edge", np.tile(32.0 * np.arange(8, dtype=np.float32), (P, 1)))
    last = np.zeros((P, 1), np.float32)
    last[P - 1] = 1.0
    put("last_row", last)
    spread = np.zeros((2 * HEADS, 2, HEADS, HD), np.float32)
    for h in range(HEADS):
        for s in range(2):
            spread[HEADS * s + h, s, h] = 1.0
    put("spread", spread.reshape(2 * HEADS, -1))
    return np.concatenate(out, 1), parts


CONSTS, WHERE = shape_constants()

VECTORS = [
    ("L0_tok_conv_b", 1), ("L0_attn_b_qkv", 3),
    ("L1_attn_b_out", 1), ("L1_attn_ln1_g", 1), ("L1_attn_ln1_b", 1), ("L1_attn_b_ff1", 4), ("L1_attn_b_ff2", 1),
    ("L1_attn_ln2_g", 1), ("L1_attn_ln2_b", 1),
    ("L2_attn_bq", 1), ("L2_attn_bk", 1), ("L2_attn_bv", 1), ("L2_attn_bo", 1), ("L2_attn_gamma", 1),
    ("L2_attn_beta", 1),
]
for _s in ("q", "k", "v", "p", "f1", "f2"):
    for _v in ("b", "g", "be", "m", "v"):
        VECTORS.append((f"L3_attn_{_s}_{_v}", 4 if _s == "f1" else 1))
VECTORS.append(("L0_tok_conv_w", 9))
COLUMN, _at = {}, 0
for _n, _k in VECTORS:
    COLUMN[_n] = _at
    _at += _k
NCOL = _at

WEIGHTS = [
    ("L0_attn_W_qkv", 3 * C), ("L1_attn_w_qk", C), ("L1_attn_w_v", C), ("L1_attn_w_out", C), ("L1_attn_w_ff1", 4 * C),
    ("L2_attn_Wq", C), ("L2_attn_Wk", C), ("L2_attn_Wv", C), ("L2_attn_Wo", C), ("L1_ffn_Wg", 32), ("L0_ffn_Wr", 8),
    ("L3_ffn_Wr", 64), ("L1_attn_w_ff2", 4 * C),
]
WEIGHT_AT, _at = {}, 0
for _n, _k in WEIGHTS:
    WEIGHT_AT[_n] = _at
    _at += _k
N_WEIGHTS = _at


def packed(inputs):
    vectors = np.concatenate([np.asarray(inputs[name]).reshape(k, C) for name, k in VECTORS], axis=0)
    down = np.asarray(inputs["L1_attn_w_ff2"]).reshape(4, P, C).transpose(1, 0, 2).reshape(P, 4 * C)
    wide = [down if name == "L1_attn_w_ff2" else np.asarray(inputs[name]) for name, _ in WEIGHTS]
    return {"vectors": vectors, "weights": np.concatenate(wide, axis=1)}


class Chain:

    def __init__(self, eng, sem):
        self.eng, self.sem, self.base, self.n = eng, sem, 0, 0

    def __call__(self, ins):
        ins.then_inc(self.sem, 1)
        self.n += 1
        self.eng.wait_ge(self.sem, self.base + self.n)

    def turn(self, i, per, before=0):
        self.base, self.n = i * per + before, 0
        self.per = per

    def late(self, ins):
        ins.then_inc(self.sem, 1)
        self.n += 1
        if self.n > 1:
            self.eng.wait_ge(self.sem, self.base + self.n - 1)

    def catch_up(self):
        self.eng.wait_ge(self.sem, self.base + self.n)

    def restart(self):
        self.eng.sem_clear(self.sem)
        self.n = 0

    def close(self):
        assert self.n == self.per, (self.n, self.per)

    def after(self, total):
        self.base, self.n = total, 0


class Resident:

    def __init__(self, nc, ctx, ins, out):
        self.ins, self.out = ins, out

        def sb(name, shape, dt=F32):
            return ctx.enter_context(nc.sbuf_tensor(name, shape, dt))

        self.hT = sb("hT", [P, N])
        self.xT = sb("xT", [P, N])
        self.cst = sb("cst", [P, CONSTS.shape[1]])
        self.bf = {}
        for name in ("ident", "ones", "before", "neg_diag"):
            a, b = WHERE[name]
            self.bf[name] = sb(f"bf_{name}", [P, b - a], BF16)
        self.columns = sb("columns", [P, NCOL])
        self.weights = sb("weights", [P, N_WEIGHTS])
        self.w = {name: self.weights[:, WEIGHT_AT[name]:WEIGHT_AT[name] + n] for name, n in WEIGHTS}
        self.w["L1_attn_w_ff2"] = self.w["L1_attn_w_ff2"].rearrange("p (k n) -> p k n", k=4)
        self.tap = sb("tap", [P, 25])
        self.bn = sb("bn", [P, 2, 9])
        self.rot = sb("rot", [P, P])
        self.wt = {name: sb(name, [P, n]) for name, n in (
            ("qT", C), ("kT", C), ("vT", C), ("pT", C), ("f1T", 4 * C), ("f2T", 4 * C))}

    def c(self, name, rows=P):
        a, b = WHERE[name]
        return self.cst[0:rows, a:b]

    def col(self, name, k=0):
        a = COLUMN[name] + k
        return self.columns[:, a:a + 1]


def allocators(nc, ctx, tag):
    held = []

    def over():
        if held:
            nc.clear_and_free_semaphores(held)
            nc.all_engine_barrier()

    ctx.callback(over)

    def sb(name, shape, dt=F32):
        return ctx.enter_context(nc.sbuf_tensor(f"{tag}_{name}", shape, dt))

    def ps(name, shape, dt=F32):
        return ctx.enter_context(nc.psum_tensor(f"{tag}_{name}", shape, dt))

    def sem(name):
        held.append(nc.alloc_semaphore(name=f"{tag}_{name}"))
        return held[-1]

    return sb, ps, sem


def set_up(nc, R):
    ins = R.ins
    with ExitStack() as ctx:
        sb, ps, sem = allocators(nc, ctx, "setup")
        rows = sb("rows", [NCOL, C])
        raw = {s: sb(f"raw_{s}", [P, C]) for s in "qkvp"}
        raw_f1 = sb("raw_f1", [P, 4, C])
        raw_f2 = sb("raw_f2", [P, 4 * C])
        edge = sb("edge", [P, 5, 3])
        root = sb("root", [P, 9])
        pv = ps("pv", [P, 512])
        pt = ps("pt", [P, 4, 512])
        loaded, rot_zeroed, transposed, columns_ready, turned = (
            sem(n) for n in ("loaded", "rot_zeroed", "transposed", "columns_ready", "turned"))
        rot_loaded, rooted, order = sem("rot_loaded"), sem("rooted"), sem("order")
        block = ctx.enter_context(nc.Block())
        n_loads = 3 + 6
        bn_at = {"q": (0, 1), "k": (1, 1), "v": (2, 1), "p": (3, 1), "f1": (4, 4), "f2": (8, 1)}

        @block.sync
        def _(sp):
            sp.dma_start(R.cst[:, :], ins["consts"]).then_inc(loaded, 16)
            sp.dma_start(rows[:, :], ins["vectors"]).then_inc(loaded, 16)
            sp.dma_start(R.weights[:, :], ins["weights"]).then_inc(loaded, 16)
            for s in "qkvp":
                sp.dma_start(raw[s][:, :], ins[f"L3_attn_{s}_w"]).then_inc(loaded, 16)
            sp.dma_start(raw_f1[:, :, :], ins["L3_attn_f1_w"].rearrange("(k p) n -> p k n", p=P)).then_inc(loaded, 16)
            sp.dma_start(raw_f2[:, :], ins["L3_attn_f2_w"]).then_inc(loaded, 16)

        @block.scalar
        def _(act):
            act.wait_ge(rot_zeroed, 1)
            for h in range(HEADS):
                act.dma_start(R.rot[HD * h:HD * h + HD, HD * h:HD * h + HD],
                              ins["L1_attn_rotations"]).then_inc(rot_loaded, 16)
            act.wait_ge(rot_loaded, 16 * HEADS)
            act.wait_ge(columns_ready, 2)
            for s, (a, n) in bn_at.items():
                last = act.activation(root[:, a:a + n], root[:, a:a + n], ACT.Sqrt)
            last.then_inc(rooted, 1)

        @block.tensor
        def _(pe):
            pe.wait_ge(loaded, 16 * n_loads)
            pe.transpose(pv[0:C, 0:NCOL], rows[:, :], R.c("ident")[0:NCOL, 0:NCOL]).then_inc(transposed, 1)
            for n, s in enumerate("qkvp"):
                last = pe.transpose(pt[:, 0, C * n:C * n + C], raw[s][:, :], R.c("ident"))
            last.then_inc(transposed, 1)
            for k in range(4):
                last = pe.transpose(pt[:, 1, C * k:C * k + C], raw_f1[:, k, :], R.c("ident"))
            last.then_inc(transposed, 1)
            for k in range(4):
                last = pe.transpose(pt[:, 2, C * k:C * k + C], raw_f2[:, C * k:C * k + C], R.c("ident"))
            last.then_inc(transposed, 1)

        @block.vector
        def _(dve):
            chain = Chain(dve, order)
            dve.memset(R.rot[:, :], 0.0).then_inc(rot_zeroed, 1)
            dve.wait_ge(loaded, 16 * n_loads)
            for name, t in R.bf.items():
                dve.tensor_copy(t[:, :], R.c(name))
            dve.wait_ge(transposed, 1)
            dve.tensor_copy(R.columns[:, :], pv[:, 0:NCOL]).then_inc(columns_ready, 1)
            dve.wait_ge(columns_ready, 1)
            for s, (a, n) in bn_at.items():
                v = COLUMN[f"L3_attn_{s}_v"]
                last = dve.tensor_scalar(root[:, a:a + n], R.columns[:, v:v + n], 1e-5, None, ALU.add)
            last.then_inc(columns_ready, 1)
            for k, n in enumerate("qkvp"):
                dve.wait_ge(transposed, 2)
                dve.tensor_copy(R.wt[f"{n}T"][:, :], pt[:, 0, C * k:C * k + C])
            dve.wait_ge(transposed, 3)
            dve.tensor_copy(R.wt["f1T"][:, :], pt[:, 1, :])
            dve.wait_ge(transposed, 4)
            dve.tensor_copy(R.wt["f2T"][:, :], pt[:, 2, :])
            w0 = COLUMN["L0_tok_conv_w"]
            tap = [R.columns[:, w0 + 3 * d:w0 + 3 * d + 3] for d in range(3)]
            chain(dve.tensor_tensor(edge[:, 1, :], tap[0], tap[1], ALU.add))
            dve.tensor_tensor(edge[:, 2, :], tap[1], tap[2], ALU.add)
            dve.tensor_copy(edge[:, 3, :], tap[0])
            dve.tensor_copy(edge[:, 4, :], tap[2])
            chain(dve.tensor_tensor(edge[:, 0, :], edge[:, 1, :], tap[2], ALU.add))
            t5 = R.tap[:, :].rearrange("p (r c) -> p r c", c=5)
            chain(dve.tensor_tensor(t5[:, :, 1], edge[:, :, 0], edge[:, :, 1], ALU.add))
            dve.tensor_tensor(t5[:, :, 2], edge[:, :, 1], edge[:, :, 2], ALU.add)
            dve.tensor_copy(t5[:, :, 3], edge[:, :, 0])
            dve.tensor_copy(t5[:, :, 4], edge[:, :, 2])
            chain(dve.tensor_tensor(t5[:, :, 0], t5[:, :, 1], edge[:, :, 2], ALU.add))
            dve.wait_ge(rooted, 1)
            chain(dve.reciprocal(root[:, :], root[:, :]))
            for s, (a, n) in bn_at.items():
                b, g, be, m = (COLUMN[f"L3_attn_{s}_{v}"] for v in ("b", "g", "be", "m"))
                dve.tensor_tensor(R.bn[:, 1, a:a + n], R.columns[:, b:b + n], R.columns[:, m:m + n], ALU.subtract)
                last = dve.tensor_tensor(R.bn[:, 0, a:a + n], root[:, a:a + n], R.columns[:, g:g + n], ALU.mult)
            chain(last)
            chain(dve.tensor_tensor(R.bn[:, 1, :], R.bn[:, 1, :], R.bn[:, 0, :], ALU.mult))
            for s, (a, n) in bn_at.items():
                be = COLUMN[f"L3_attn_{s}_be"]
                dve.tensor_tensor(R.bn[:, 1, a:a + n], R.bn[:, 1, a:a + n], R.columns[:, be:be + n], ALU.add)


def layer_norm(nc, R, tag, src, dst, eps=1e-5, gain=None, bias=None, residual=False):
    SUB = CH // P
    LEAD = 2
    POOLED = 3
    with ExitStack() as ctx:
        sb, ps, sem = allocators(nc, ctx, tag)
        squares, rstd, scaled = sb("squares", [P, CHUNKS, CH]), sb("rstd", [P, CHUNKS, CH]), sb("scaled", [P, CHUNKS, CH])
        diag, root, inverse = sb("diag", [P, CHUNKS, CH]), sb("root", [P, TILES]), sb("inverse", [P, TILES])
        table = sb("table", [P, 1])
        centred, spread = ps("centred", [P, CHUNKS, CH]), ps("spread", [P, 2, CH])
        centred_ready, squared, var_ready, rooted, inverted, diag_ready, spread_ready, rstd_ready, done = (
            sem(n) for n in ("centred_ready", "squared", "var_ready", "rooted", "inverted", "diag_ready", "spread_ready",
                             "rstd_ready", "done"))
        pool_diag_ready = sem("pool_diag_ready")
        block = ctx.enter_context(nc.Block())

        @block.tensor
        def _(pe):
            def centre(c):
                pe.matmul(centred[:, c, :], R.c("centre"), src[:, CH * c:CH * c + CH], start=True, stop=True).then_inc(
                    centred_ready, 1)

            def variances(c):
                pe.wait_ge(squared, c + 1)
                for s in range(SUB):
                    last = pe.matmul(spread[:, 0, SUB * c + s:SUB * c + s + 1], squares[:, c, P * s:P * s + P],
                                     R.c("mean")[:, 0:1], start=(c == 0 and s == 0), stop=True, skip_group_check=True)
                return last

            for c in range(CHUNKS + LEAD):
                if c < CHUNKS:
                    centre(c)
                if c >= LEAD:
                    last = variances(c - LEAD)
            last.then_inc(var_ready, 1)
            for c in range(CHUNKS):
                if c < POOLED:
                    pe.wait_ge(diag_ready, c + 1)
                else:
                    pe.wait_ge(pool_diag_ready, c - POOLED + 1)
                if c >= 2:
                    pe.wait_ge(rstd_ready, c - 1)
                pe.matmul(spread[:, c % 2, :], R.c("ones"), diag[:, c, :], start=True, stop=True).then_inc(
                    spread_ready, 1)

        def diagonal(eng, c):
            shape = [P, SUB, P]
            return eng.tensor_tensor(diag[:, c, :].rearrange("p (s t) -> p s t", s=SUB),
                                     R.c("ident").unsqueeze(1).to_broadcast(shape),
                                     inverse[:, SUB * c:SUB * c + SUB].unsqueeze(2).to_broadcast(shape), ALU.mult)

        @block.gpsimd
        def _(pool):
            pool.wait_ge(inverted, 1)
            for c in range(POOLED, CHUNKS):
                diagonal(pool, c).then_inc(pool_diag_ready, 1)

        @block.scalar
        def _(act):
            act.activation(table[:, :], R_eps(R, eps), ACT.Sqrt)
            for c in range(CHUNKS):
                act.wait_ge(centred_ready, c + 1)
                act.activation(squares[:, c, :], centred[:, c, :], ACT.Square).then_inc(squared, 1)
            act.wait_ge(var_ready, 1)
            act.activation(root[:, :], spread[:, 0, 0:TILES], ACT.Sqrt, bias=R_eps(R, eps)).then_inc(rooted, 1)
            for c in range(CHUNKS):
                act.wait_ge(spread_ready, c + 1)
                if gain is None:
                    act.copy(rstd[:, c, :], spread[:, c % 2, :]).then_inc(rstd_ready, 1)
                else:
                    act.mul(rstd[:, c, :], spread[:, c % 2, :], gain).then_inc(rstd_ready, 1)

        @block.vector
        def _(dve):
            def scale(c):
                dve.wait_ge(rstd_ready, c + 1)
                to = dst[:, CH * c:CH * c + CH] if gain is None else scaled[:, c, :]
                dve.tensor_tensor(to, centred[:, c, :], rstd[:, c, :], ALU.mult).then_inc(done, 1)

            def shift(c):
                at = slice(CH * c, CH * c + CH)
                dve.wait_ge(done, c + 1)
                if residual:
                    dve.scalar_tensor_tensor(out=dst[:, at], in0=scaled[:, c, :], scalar=bias, in1=dst[:, at],
                                             op0=ALU.add, op1=ALU.add)
                else:
                    dve.tensor_scalar(dst[:, at], scaled[:, c, :], bias, None, ALU.add)

            dve.wait_ge(rooted, 1)
            dve.reciprocal(inverse[:, :], root[:, :]).then_inc(inverted, 1)
            dve.wait_ge(inverted, 1)
            for c in range(POOLED):
                diagonal(dve, c).then_inc(diag_ready, 1)
            for c in range(CHUNKS):
                scale(c)
                if gain is not None and c > 0:
                    shift(c - 1)
            if gain is not None:
                shift(CHUNKS - 1)


def R_eps(R, eps):
    return R.eps[eps][:, 0:1]


def tokens(nc, R):
    PART = 3 * PAD * 2
    CELLS = PAD * PAD
    with ExitStack() as ctx:
        sb, ps, sem = allocators(nc, ctx, "tok")
        xin = sb("xin", [P, 2, 32, C])
        inner = sb("inner", [P, 2, 4, C])
        win = sb("win", [P, 2 * 3 * 2 * 3 * CELLS + 3 * CELLS + 32])
        acc = sb("acc", [P, 2, 2, CELLS])
        txt = sb("txt", [P, 2, C])
        parts = ps("parts", [P, 2, 2, 512])
        ptxt = ps("ptxt", [P, 2, 512])
        x_loaded = [sem(f"x_loaded{u}") for u in range(2)]
        txt_loaded = [sem(f"txt_loaded{u}") for u in range(2)]
        inner_ready, parts_done, txt_done, copied, txt_copied, weighted, order, stored = (
            sem(n) for n in ("inner_ready", "parts_done", "txt_done", "copied", "txt_copied", "weighted", "order",
                             "stored"))
        win_zeroed = sem("win_zeroed")
        x_v = R.ins["x"].rearrange("b h (q j) c -> b (h q) (j c)", q=2)
        block = ctx.enter_context(nc.Block())
        W = 2 * 3 * 3 * CELLS

        def window(slot, part_c, part_r, shift):
            a = 16 + slot * W + part_c * (6 * CELLS) + part_r * CELLS + shift
            v = win[:, a:a + 6 * CELLS]
            return v.rearrange("p (m q) -> p m q", m=2)[:, :, 0:CELLS]

        @block.sync
        def _(sp):
            with sp.Fori(0, B // 2) as i:
                for u in range(2):
                    sp.wait_ge(parts_done, 2 * i + u + 1)
                    sp.dma_start(xin[:, u, :, :].rearrange("p j c -> p (j c)"),
                                 x_v[bass.ds(2 * i + u, 1)].rearrange("a p f -> (a p) f")).then_inc(x_loaded[u], 16)
                    sp.wait_ge(txt_done, 2 * i + u + 1)
                    sp.dma_start(txt[:, u, :],
                                 R.ins["txt"][bass.ds(2 * i + u, 1)].rearrange("a t c -> (a t) c")).then_inc(
                        txt_loaded[u], 16)

        @block.tensor
        def _(pe):
            pe.sem_inc(parts_done, SLOTS)
            pe.sem_inc(txt_done, SLOTS)
            with pe.Fori(0, B // 2) as i:
                for u in range(2):
                    pe.wait_ge(txt_loaded[u], 16 * i + 16)
                    pe.wait_ge(txt_copied, 2 * i + u + 1)
                    pe.transpose(ptxt[:, u, 0:C], txt[:, u, :], R.c("ident")).then_inc(txt_done, 1)
                    pe.wait_ge(inner_ready, 2 * i + u + 1)
                    pe.wait_ge(copied, 2 * i + u + 1)
                    for jq in range(4):
                        for part, lhsT in enumerate((inner[:, u, jq, :], xin[:, u, 8 * jq, :], xin[:, u, 8 * jq + 7, :])):
                            a = (jq % 2) * 3 * PART + part * PART
                            last = pe.matmul(parts[:, u, jq // 2, a:a + PART], lhsT, R.c("rows"), start=True, stop=True)
                    last.then_inc(parts_done, 1)

        @block.vector
        def _(dve):
            dve.memset(win[:, :], 0.0).then_inc(win_zeroed, 1)
            dve.memset(acc[:, :, :, :], 0.0)
            chain = Chain(dve, order)

            def reduce(i, pair):
                for u in range(2):
                    n = 4 * i + 2 * pair + u
                    dve.wait_ge(x_loaded[u], 32 * i + 16 * pair + 16)
                    dve.wait_ge(parts_done, n + 1)
                    v = xin[:, u, :, :].rearrange("p (q r) c -> p q c r", r=8)
                    dve.tensor_reduce(inner[:, u, :, :], v[:, :, :, 1:7], AX, ALU.add).then_inc(inner_ready, 1)

            def weight(i, pair):
                dve.wait_ge(copied, 4 * i + 2 * pair + 2 + SLOTS)
                dve.wait_ge(stored, 2 * i + pair + 1)
                first = True
                out = acc[:, pair, :, :]
                for r, (part_r, dr) in enumerate(((0, 0), (1, 0), (2, 0), (2, -1), (1, 1))):
                    for c, (part_c, dc) in enumerate(((0, 0), (1, 0), (2, 0), (2, -1), (1, 1))):
                        tap = R.tap[:, 5 * r + c:5 * r + c + 1]
                        src = window(pair, part_c, part_r, dr * PAD + dc)
                        if first:
                            chain(dve.tensor_scalar(out, src, tap, None, ALU.mult))
                        else:
                            ins = dve.scalar_tensor_tensor(out=out, in0=src, scalar=tap, in1=out,
                                                           op0=ALU.mult, op1=ALU.add)
                            if r == 4 and c == 4:
                                ins.then_inc(weighted, 1)
                            else:
                                chain(ins)
                        first = False

            reduce(0, 0)
            with dve.Fori(0, B // 4 - 1) as i:
                chain.turn(i, 48)
                for pair in range(2):
                    reduce(i + (pair + 1) // 2, (pair + 1) % 2)
                    weight(i, pair)
                chain.close()
            chain.after(48 * (B // 4 - 1))
            reduce(B // 4 - 1, 1)
            weight(B // 4 - 1, 0)
            weight(B // 4 - 1, 1)

        @block.scalar
        def _(act):
            act.sem_inc(copied, SLOTS)
            act.sem_inc(txt_copied, SLOTS)
            act.sem_inc(stored, SLOTS)
            act.wait_ge(win_zeroed, 1)
            with act.Fori(0, B // 4) as i:
                for pair in range(2):
                    act.wait_ge(stored, 2 * i + pair + 1)
                    for u in range(2):
                        act.wait_ge(txt_done, 4 * i + 2 * pair + u + 1 + SLOTS)
                        act.copy(R.hT[:, bass.ds(4 * i * T + (2 * pair + u) * T + IMG_TOKENS, TXT_TOKENS)],
                                 ptxt[:, u, 0:C]).then_inc(txt_copied, 1)
                        act.wait_ge(parts_done, 4 * i + 2 * pair + u + 1 + SLOTS)
                        for bank in range(2):
                            for part in range(3):
                                src = parts[:, u, bank, 0:6 * PART].rearrange("p (q k) -> p q k", q=2)
                                src = src[:, :, part * PART:(part + 1) * PART].rearrange("p q (r s) -> p q r s", s=2)
                                a = 16 + pair * W + part * 6 * CELLS + u * 3 * CELLS + 1 + 2 * bank
                                dst = win[:, a:a + 3 * CELLS].rearrange("p (r j) -> p r j", j=PAD)
                                dst = dst[:, :, 0:GRID].rearrange("p r (s q) -> p q r s", s=2)[:, 0:2]
                                last = act.copy(dst, src)
                        last.then_inc(copied, 1)
                    act.wait_ge(weighted, 2 * i + pair + 1)
                    src = acc[:, pair, :, :].rearrange("p m (r j) -> p m r j", j=PAD)[:, :, 1:GRID + 1, 1:GRID + 1]
                    for u in range(2):
                        last = act.activation(
                            R.hT[:, bass.ds(4 * i * T + (2 * pair + u) * T, IMG_TOKENS)].rearrange(
                                "p (r j) -> p r j", j=GRID),
                            src[:, u], ACT.Identity, scale=1.0 / IMG_TOKENS, bias=R.col("L0_tok_conv_b"))
                    last.then_inc(stored, 1)


def project(nc, R, tag, src, jobs, copies=()):
    J = len(jobs)
    with ExitStack() as ctx:
        sb, ps, sem = allocators(nc, ctx, tag)
        out = ps("out", [P, 2, J, CH])
        product_ready, evacuated, stored = sem("product_ready"), sem("evacuated"), sem("stored")
        block = ctx.enter_context(nc.Block())

        if copies:
            @block.sync
            def _(sp):
                with sp.Fori(0, CHUNKS) as i:
                    sp.wait_ge(evacuated, J * i + J + SLOTS * J)
                    for j, dram in copies:
                        at = bass.ds(i * CH, CH)
                        sp.dma_start(dram[:, at], jobs[j][1][:, at]).then_inc(stored, 16)
                sp.wait_ge(stored, 16 * CHUNKS * len(copies))

        @block.tensor
        def _(pe):
            with pe.Fori(0, CHUNKS // 2) as i:
                for u in range(2):
                    for j, (w, dst, func, scale, bias) in enumerate(jobs):
                        pe.wait_ge(evacuated, (2 * J) * i + u * J + j + 1)
                        pe.matmul(out[:, u, j, :], w, src[:, bass.ds(i * (2 * CH) + u * CH, CH)],
                                  start=True, stop=True).then_inc(product_ready, 1)

        @block.scalar
        def _(act):
            act.sem_inc(evacuated, SLOTS * J)
            with act.Fori(0, CHUNKS // 2) as i:
                for u in range(2):
                    for j, (w, dst, func, scale, bias) in enumerate(jobs):
                        act.wait_ge(product_ready, (2 * J) * i + u * J + j + 1)
                        act.activation(dst[:, bass.ds(i * (2 * CH) + u * CH, CH)], out[:, u, j, :], func,
                                       scale=scale, bias=bias).then_inc(evacuated, 1)


def attend(nc, R, tag, q_all, k_all, v_all, att, sums, scale, groups=None, self_value=None, own=None):
    SLOT = T // HEADS
    local = groups is None
    ROWS = HALF + 7
    with ExitStack() as ctx:
        sb, ps, sem = allocators(nc, ctx, tag)
        q16 = [sb(f"q16_{u}", [HALF + 1, HEADS, T]) for u in range(2)]
        k16 = [sb(f"k16_{u}", [HALF + 1, HEADS, T]) for u in range(2)]
        vin = [sb(f"vin_{u}", [HD, HEADS, T] if local else [P, T]) for u in range(2)]
        if local:
            raw = [sb(f"raw{u}", [HD, 3, HEADS, T]) for u in range(2)]
            moved_qk, moved_v = sem("moved_qk"), sem("moved_v")
        vrow = sb("vrow", [HALF, 2, 2, HEADS, 2 * HD])
        peak = sb("peak", [HALF, 2, 2 * HEADS])
        neg = sb("neg", [2 * HEADS, 2, HALF])
        prob = sb("prob", [HALF, 2, 2, T])
        SIDES = 2
        o_shape = [HEADS, HALF] if local else [HEADS // SIDES, T]
        o32 = [sb(f"o32_{u}", [2 * HD * SIDES] + o_shape) for u in range(2)]
        pS, pT = ps("pS", [HALF, 2, 512]), ps("pT", [HALF, 2, 512])
        pO, pV, pM, pX = ps("pO", [2 * HD * SIDES, 512]), ps("pV", [HALF, 512]), ps("pM", [2 * HEADS, 512]), ps("pX", [P, 512])
        loaded = [sem(f"loaded{u}") for u in range(2)]
        rows_loaded = [sem(f"rows_loaded{u}") for u in range(2)]
        stored = [sem(f"stored{u}") for u in range(2)]
        (cleared, v_turned, v_copied, scores_ready, max_done, floored, max_turned, neg_ready, shifted_ready, exp_done,
         weighted, o_copied, order, ones_set) = (sem(n) for n in (
             "cleared", "v_turned", "v_copied", "scores_ready", "max_done", "floored", "max_turned", "neg_ready",
             "shifted_ready", "exp_done", "weighted", "o_copied", "order", "ones_set"))
        if not local:
            qs_mask = [sb(f"qs_mask{u}", [ROWS, HEADS, T], BF16) for u in range(2)]
            ks_mask = [sb(f"ks_mask{u}", [ROWS, 2, HEADS, T], BF16) for u in range(2)]
            kt_mask = [sb(f"kt_mask{u}", [ROWS, HEADS, T], BF16) for u in range(2)]
            qt_mask = [sb(f"qt_mask{u}", [ROWS, 2, HEADS, T], BF16) for u in range(2)]
            pool_masks, masks_zeroed = sem("pool_masks"), [sem(f"masks_zeroed{u}") for u in range(2)]
            spread_ready, own_ready, masks_ready = sem("spread_ready"), sem("own_ready"), sem("masks_ready")
        LOAD, STORE = 16 * (3 if local else 9), 32 * SIDES
        block = ctx.enter_context(nc.Block())

        def pick(t, h, half=None, rows=HALF):
            return t[0:rows, h, :] if half is None else t[0:rows, h, HALF * half:HALF * half + HALF]

        @block.sync
        def _(sp):
            def load(n, u):
                at = bass.ds(n * T, T)
                heads = "(s d) t -> d s t"
                if local:
                    for j, src in enumerate((q_all, k_all, v_all)):
                        sp.dma_start(raw[u][:, j, :, :], src[:, at].rearrange(heads, d=HD)).then_inc(loaded[u], 16)
                else:
                    sp.dma_start(q16[u][0:HD, :, :], q_all[:, at].rearrange(heads, d=HD)).then_inc(loaded[u], 16)
                    sp.dma_start(k16[u][0:HD, :, :], k_all[:, at].rearrange(heads, d=HD)).then_inc(loaded[u], 16)
                    sp.dma_start(vin[u][:, :], v_all[:, at]).then_inc(loaded[u], 16)
                    g = groups[:, at].rearrange("(h k c) t -> k c h t", h=HEADS, k=2)
                    for side, dst in ((0, qs_mask[u][HALF:ROWS, :, :]), (0, qt_mask[u][HALF:ROWS, 0, :, :]),
                                      (0, qt_mask[u][HALF:ROWS, 1, :, :]), (1, kt_mask[u][HALF:ROWS, :, :]),
                                      (1, ks_mask[u][HALF:ROWS, 0, :, :]), (1, ks_mask[u][HALF:ROWS, 1, :, :])):
                        sp.dma_start(dst, g[side, 0:7]).then_inc(loaded[u], 16)

            def store_max(n, u):
                sp.wait_ge(neg_ready, n + 2)
                for half in range(2):
                    src = neg[HEADS * half:HEADS * half + HEADS, u, :]
                    dst = q16[u][HALF:HALF + 1, :, HALF * half:HALF * half + HALF]
                    sp.dma_start(dst, src).then_inc(rows_loaded[u], 16)

            def store_out(n, u):
                at = bass.ds(n * T, T)
                sp.wait_ge(o_copied, 4 * n + 4 + 1)
                for side in range(SIDES):
                    for k, dram in enumerate((att, sums)):
                        rows = slice(HD * (2 * side + k), HD * (2 * side + k + 1))
                        if local:
                            to = dram[:, bass.ds(n * T + HALF * side, HALF)].rearrange("(s d) t -> d s t", d=HD)
                        else:
                            to = dram[:, at].rearrange("(s g d) t -> g d s t", g=SIDES, d=HD)[side]
                        sp.dma_start(to, o32[u][rows, :, :]).then_inc(stored[u], 16)

            sp.sem_inc(stored[0], STORE)
            sp.sem_inc(stored[1], STORE)
            for u in range(2):
                if not local:
                    sp.wait_ge(cleared, 1)
                    sp.wait_ge(masks_ready, u + 1)
                load(u, u)
            store_max(0, 0)
            with sp.Fori(0, B // 2 - 1) as i:
                for u in range(2):
                    n = 2 * i + u
                    if local:
                        sp.wait_ge(moved_qk, n + 1)
                        sp.wait_ge(moved_v, n + 1)
                        load(n + 2, u)
                    store_max(n + 1, 1 - u)
                    if not local:
                        sp.wait_ge(shifted_ready, HEADS * n + HEADS)
                        load(n + 2, u)
                    store_out(n, u)
            store_max(B - 1, 1)
            store_out(B - 2, 0)
            store_out(B - 1, 1)
            for u in range(2):
                sp.wait_ge(stored[u], STORE * (B // 2 + 1))

        def masks(eng, u):
            for t in (qs_mask, ks_mask, kt_mask, qt_mask):
                last = eng.memset(t[u][:], 0.0)
            last.then_inc(masks_zeroed[u], 1)
            eng.wait_ge(masks_zeroed[u], 1)
            shape = [HALF, HEADS, HALF]
            plus, minus = (R.bf[m][0:HALF, 0:HALF].unsqueeze(1).to_broadcast(shape) for m in ("ident", "neg_diag"))
            for half in range(2):
                mine = slice(HALF * half, HALF * half + HALF)
                eng.tensor_copy(qs_mask[u][0:HALF, :, mine], plus)
                eng.tensor_copy(kt_mask[u][0:HALF, :, mine], plus)
                eng.tensor_copy(ks_mask[u][0:HALF, half, :, mine], minus)
                last = eng.tensor_copy(qt_mask[u][0:HALF, half, :, mine], minus)
            return last

        if not local:
            @block.gpsimd
            def _(pool):
                last = masks(pool, 1)
                last.then_inc(pool_masks, 1)
                pool.wait_ge(pool_masks, 1)
                pool.wait_ge(masks_ready, 1)
                pool.sem_inc(masks_ready, 1)

        MAXROWS = 32

        @block.tensor
        def _(pe):
            def values(n, u, turn):
                if local:
                    pe.wait_ge(moved_v, n + 1)
                else:
                    pe.wait_ge(loaded[u], LOAD * turn + LOAD)
                pe.wait_ge(v_copied, n + 1)
                if local:
                    for half in range(2):
                        for h in range(HEADS):
                            a = (half * HEADS + h) * HD
                            last = pe.matmul(pV[:, a:a + HD], pick(vin[u], h, half, HD), R.c("ident")[0:HD, 0:HD],
                                             start=True, stop=True)
                else:
                    for half in range(2):
                        last = pe.transpose(pV[:, C * half:C * half + C], vin[u][:, HALF * half:HALF * half + HALF],
                                            R.c("ident"))
                last.then_inc(v_turned, 1)

            def scores(n, u):
                if local:
                    pe.wait_ge(moved_qk, n + 1)
                for h in range(HEADS):
                    pe.wait_ge(max_done, HEADS * n + h + 1)
                    for half in range(2):
                        out = pS[:, h % 2, T * half:T * half + T]
                        if not local:
                            pe.matmul(out, qs_mask[u][:, h, HALF * half:HALF * half + HALF], ks_mask[u][:, half, h, :],
                                      start=True, stop=False)
                        last = pe.matmul(out, pick(q16[u], h, half), pick(k16[u], h), start=local, stop=True)
                    last.then_inc(scores_ready, 1)

            def maxima(n, u):
                if local:
                    pe.wait_ge(max_done, HEADS * n + HEADS + SLOTS)
                else:
                    pe.wait_ge(floored, n + 1)
                pe.wait_ge(neg_ready, n + 1)
                pe.transpose(pM[:, 0:HALF], peak[:, u, :], R.c("ident")[0:HALF, 0:HALF]).then_inc(max_turned, 1)

            def shifted(n, u, h, turn):
                if h == 0:
                    pe.wait_ge(rows_loaded[u], MAXROWS * turn + MAXROWS)
                pe.wait_ge(exp_done, HEADS * n + h + 1)
                for half in range(2):
                    out = pT[:, h % 2, T * half:T * half + T]
                    if not local:
                        pe.matmul(out, kt_mask[u][:, h, HALF * half:HALF * half + HALF], qt_mask[u][:, half, h, :],
                                  start=True, stop=False)
                    last = pe.matmul(out, pick(k16[u], h, half, HALF + 1), pick(q16[u], h, None, HALF + 1),
                                     start=local, stop=True)
                last.then_inc(shifted_ready, 1)

            def mix(n, u, h):
                if h == 0:
                    pe.wait_ge(v_copied, n + 2)
                if h % 2 == 0:
                    pe.wait_ge(o_copied, 4 * n + h // 2 + 1)
                pe.wait_ge(exp_done, HEADS * n + h + 1 + SLOTS)
                to = pO[2 * HD * (h % 2):2 * HD * (h % 2) + 2 * HD, 0:T]
                for half in range(2):
                    last = pe.matmul(to, vrow[:, u, half, h, :], prob[:, h % 2, half, :], start=(half == 0),
                                     stop=(half == 1))
                last.then_inc(weighted, 1)

            def own_spread(n, u):
                pe.wait_ge(neg_ready, n + 2)
                pe.wait_ge(own_ready, n + 1)
                for half in range(2):
                    last = pe.matmul(pX[:, HALF * half:HALF * half + HALF],
                                     R.c("spread", 2 * HEADS)[:, P * half:P * half + P], neg[:, u, :],
                                     start=True, stop=True)
                last.then_inc(spread_ready, 1)

            def sequence(n, u, nxt, turn):
                shifted(n, u, 0, turn)
                for h in range(3):
                    shifted(n, u, h + 1, turn)
                    mix(n, u, h)
                if nxt:
                    values(n + 1, 1 - u, turn + u)
                    scores(n + 1, 1 - u)
                mix(n, u, 3)
                shifted(n, u, 4, turn)
                if nxt:
                    maxima(n + 1, 1 - u)
                for h in range(4, 7):
                    shifted(n, u, h + 1, turn)
                    mix(n, u, h)
                if nxt and not local:
                    own_spread(n + 1, 1 - u)
                mix(n, u, 7)

            pe.sem_inc(weighted, SLOTS)
            values(0, 0, 0)
            scores(0, 0)
            maxima(0, 0)
            if not local:
                own_spread(0, 0)
            with pe.Fori(0, B // 2 - 1) as i:
                for u in range(2):
                    sequence(2 * i + u, u, True, i)
            sequence(B - 2, 0, True, B // 2 - 1)
            sequence(B - 1, 1, False, B // 2 - 1)

        @block.scalar
        def _(act):
            act.sem_inc(v_copied, 1)
            act.sem_inc(neg_ready, 1)
            act.sem_inc(exp_done, SLOTS)
            if not local:
                act.sem_inc(own_ready, 1)

            def move(n, u, turn):
                act.wait_ge(loaded[u], LOAD * turn + LOAD)
                act.copy(vin[u].rearrange("d h (s t) -> d h s t", s=HEADS),
                         raw[u][:, 2].rearrange("d s (h t) -> d h s t", h=HEADS)).then_inc(moved_v, 1)

            def values(n, u):
                act.wait_ge(v_turned, n + 1)
                if local:
                    src = pV[:, 0:2 * HEADS * HD].rearrange("p (g d) -> p g d", d=HD)
                else:
                    src = pV[:, 0:2 * C].rearrange("p (g d) -> p g d", d=HD)
                dst = vrow[:, u, :, :, 0:HD].rearrange("p a h d -> p (a h) d")
                act.copy(dst, src).then_inc(v_copied, 1)

            def maxima(n, u):
                act.wait_ge(max_turned, n + 1)
                act.mul(neg[:, u, :], pM[:, 0:HALF], -1.0).then_inc(neg_ready, 1)

            def own_term(n, u):
                act.wait_ge(spread_ready, n + 1)
                act.activation(own[:, bass.ds(n * T, T)], pX[:, 0:T], ACT.Exp, scale=scale,
                               bias=R.self_value[:, 0:1]).then_inc(own_ready, 1)

            def exps(n, u, lo, hi):
                for h in range(lo, hi):
                    act.wait_ge(shifted_ready, HEADS * n + h + 1)
                    act.wait_ge(weighted, HEADS * n + h + 1)
                    act.activation(prob[:, h % 2, :, :], pT[:, h % 2, 0:2 * T].rearrange("p (a t) -> p a t", a=2), ACT.Exp,
                                   scale=scale).then_inc(exp_done, 1)

            def sequence(n, u, nxt, turn):
                exps(n, u, 0, 2)
                if nxt and local:
                    move(n + 1, 1 - u, turn + u)
                exps(n, u, 2, 4)
                if nxt:
                    values(n + 1, 1 - u)
                exps(n, u, 4, 5)
                if nxt:
                    maxima(n + 1, 1 - u)
                exps(n, u, 5, HEADS)
                if nxt and not local:
                    own_term(n + 1, 1 - u)

            act.wait_ge(ones_set, 1)
            if local:
                move(0, 0, 0)
            values(0, 0)
            maxima(0, 0)
            if not local:
                own_term(0, 0)
            with act.Fori(0, B // 2 - 1) as i:
                for u in range(2):
                    sequence(2 * i + u, u, True, i)
            sequence(B - 2, 0, True, B // 2 - 1)
            sequence(B - 1, 1, False, B // 2 - 1)

        @block.vector
        def _(dve):
            for u in range(2):
                dve.memset(q16[u][:, :, :], 0.0)
                dve.memset(k16[u][:, :, :], 0.0)
            dve.memset(neg[:, :, :], 0.0).then_inc(order, 1)
            dve.wait_ge(order, 1)
            for u in range(2):
                dve.memset(k16[u][HALF:HALF + 1, :, :], 1.0)
            dve.memset(vrow[:, :, :, :, :], 1.0).then_inc(ones_set, 1)
            dve.wait_ge(ones_set, 1)
            if not local:
                dve.sem_inc(cleared, 1)
                masks(dve, 0).then_inc(masks_ready, 1)
            dve.sem_inc(max_done, SLOTS)
            dve.sem_inc(o_copied, 1)
            def maxima(n, u):
                for h in range(HEADS):
                    dve.wait_ge(scores_ready, HEADS * n + h + 1)
                    dst = peak[:, u, :].rearrange("p (a h) -> p a h", a=2)[:, :, h]
                    dve.tensor_reduce(dst, pS[:, h % 2, 0:2 * T].rearrange("p (a t) -> p a t", a=2), AX,
                                      ALU.max).then_inc(max_done, 1)
                if not local:
                    dve.wait_ge(max_done, HEADS * n + HEADS + SLOTS)
                    dve.tensor_scalar(peak[:, u, :], peak[:, u, :], self_value / scale, None, ALU.max).then_inc(floored, 1)

            def out(n, u, pair, turn):
                dve.wait_ge(weighted, HEADS * n + 2 * pair + 2 + SLOTS)
                if pair == 0:
                    dve.wait_ge(stored[u], STORE * turn + STORE)
                src = pO[:, 0:T]
                if local:
                    dst = o32[u][:, :, SLOT * pair:SLOT * pair + SLOT]
                    src = src.rearrange("p (s t) -> p s t", s=HEADS)
                else:
                    dst = o32[u][:, pair, :]
                dve.tensor_copy(dst, src).then_inc(o_copied, 1)

            def move(n, u, turn):
                dve.wait_ge(loaded[u], LOAD * turn + LOAD)
                for j, dst in enumerate((q16[u], k16[u])):
                    last = dve.tensor_copy(dst[0:HD].rearrange("d h (s t) -> d h s t", s=HEADS),
                                           raw[u][:, j].rearrange("d s (h t) -> d h s t", h=HEADS))
                last.then_inc(moved_qk, 1)

            def sequence(n, u, nxt, turn):
                if nxt and local:
                    move(n + 1, 1 - u, turn + u)
                out(n, u, 0, turn)
                if nxt:
                    maxima(n + 1, 1 - u)
                for pair in range(1, 4):
                    out(n, u, pair, turn)

            if local:
                move(0, 0, 0)
            maxima(0, 0)
            with dve.Fori(0, B // 2 - 1) as i:
                for u in range(2):
                    sequence(2 * i + u, u, True, i)
            sequence(B - 2, 0, True, B // 2 - 1)
            sequence(B - 1, 1, False, B // 2 - 1)


def attention_0(nc, R):
    with ExitStack() as ctx:
        sb, _, _ = allocators(nc, ctx, "a0")
        q, k, v = sb("q", [P, N]), sb("k", [P, N]), sb("v", [P, N])
        layer_norm(nc, R, "a0_ln", R.hT, R.xT)
        w = R.w["L0_attn_W_qkv"]
        project(nc, R, "a0_qkv", R.xT, [
            (w[:, C * n:C * n + C], dst, ACT.Identity, 1.0, R.col("L0_attn_b_qkv", n)) for n, dst in enumerate((q, k, v))],
            copies=[(n, R.scratch[n]) for n in range(3)])
        attend(nc, R, "a0", *R.scratch[0:5], 0.25)
        divide(nc, R, "a0_add", R.scratch[3], R.scratch[4], R.hT)


def divide(nc, R, tag, att, sums, dst, own=None, v=None):
    with ExitStack() as ctx:
        sb, ps, sem = allocators(nc, ctx, tag)
        W = 2 * T if own is None else CH
        a, s, t = sb("a", [P, 2, W]), sb("s", [P, 2, W]), sb("t", [P, 2, W])
        loaded = [sem(f"loaded{u}") for u in range(2)]
        done, order = sem("done"), sem("order")
        block = ctx.enter_context(nc.Block())
        arrays = [(a, att), (s, sums)] + ([(t, v)] if own is not None else [])

        @block.sync
        def _(sp):
            with sp.Fori(0, N // W // 2) as i:
                for u in range(2):
                    at = bass.ds(i * (2 * W) + u * W, W)
                    sp.wait_ge(done, 2 * i + u + 1)
                    for tile, dram in arrays:
                        sp.dma_start(tile[:, u, :], dram[:, at]).then_inc(loaded[u], 16)

        @block.vector
        def _(dve):
            dve.sem_inc(done, SLOTS)
            chain = Chain(dve, order)
            load = 16 * len(arrays)
            with dve.Fori(0, N // W // 2) as i:
                chain.turn(i, 8 if own is not None else 4)
                for u in range(2):
                    at = bass.ds(i * (2 * W) + u * W, W)
                    dve.wait_ge(loaded[u], load * i + load)
                    if own is not None:
                        dve.tensor_tensor(t[:, u, :], own[:, at], t[:, u, :], ALU.mult)
                        chain(dve.tensor_tensor(s[:, u, :], own[:, at], s[:, u, :], ALU.add))
                        chain(dve.tensor_tensor(a[:, u, :], a[:, u, :], t[:, u, :], ALU.add))
                    chain(dve.reciprocal(s[:, u, :], s[:, u, :]))
                    if own is not None:
                        chain(dve.tensor_tensor(a[:, u, :], a[:, u, :], s[:, u, :], ALU.mult))
                        dve.tensor_copy(dst[:, at], a[:, u, :]).then_inc(done, 1)
                    else:
                        chain(dve.tensor_tensor(a[:, u, :], a[:, u, :], s[:, u, :], ALU.mult))
                        for q in range(2):
                            there = dst[:, bass.ds(i * (2 * W) + u * W + q * T, T)].rearrange(
                                "p (k g t) -> p g k t", g=2, k=HEADS // 2)
                            here = a[:, u, T * q:T * q + T].rearrange("p (g k t) -> p g k t", g=2, k=HEADS // 2)
                            last = dve.tensor_tensor(there, there, here, ALU.add)
                        last.then_inc(done, 1)
                chain.close()


def tile_of(t):
    return slice(P * t, P * t + P)


def route(nc, R, tag, w, E, logits, bias=None):
    with ExitStack() as ctx:
        sb, ps, sem = allocators(nc, ctx, tag)
        flat = sb("flat", [E, N])
        up = ps("up", [E, 2, CH])
        per_bank = 512 // E
        banks = -(-TILES // per_bank)
        turned = ps("turned", [P, banks, 512])
        product_ready, evacuated, turned_ready = sem("product_ready"), sem("evacuated"), sem("turned_ready")
        block = ctx.enter_context(nc.Block())

        @block.tensor
        def _(pe):
            with pe.Fori(0, CHUNKS // 2) as i:
                for u in range(2):
                    pe.wait_ge(evacuated, 2 * i + u + 1)
                    pe.matmul(up[:, u, :], w, R.xT[:, bass.ds(i * (2 * CH) + u * CH, CH)],
                              start=True, stop=True).then_inc(product_ready, 1)
            pe.wait_ge(evacuated, CHUNKS + SLOTS)
            for t in range(TILES):
                a = E * (t % per_bank)
                last = pe.transpose(turned[:, t // per_bank, a:a + E], flat[:, tile_of(t)], R.c("ident")[0:E, 0:E])
            last.then_inc(turned_ready, 1)

        @block.scalar
        def _(act):
            act.sem_inc(evacuated, SLOTS)
            with act.Fori(0, CHUNKS // 2) as i:
                for u in range(2):
                    act.wait_ge(product_ready, 2 * i + u + 1)
                    act.activation(flat[:, bass.ds(i * (2 * CH) + u * CH, CH)], up[:, u, :], ACT.Identity,
                                   bias=0.0 if bias is None else bias).then_inc(evacuated, 1)

        @block.vector
        def _(dve):
            dve.wait_ge(turned_ready, 1)
            for b in range(banks):
                n = min(per_bank, TILES - b * per_bank)
                dve.tensor_copy(logits[:, b * per_bank:b * per_bank + n, :],
                                turned[:, b, 0:n * E].rearrange("p (t e) -> p t e", e=E))


def top_gates(nc, R, tag, logits, E, K, gates, floor, capacity=None, dropped=None):
    TAKEN = 2.0
    with ExitStack() as ctx:
        sb, ps, sem = allocators(nc, ctx, tag)
        prob, marked = sb("prob", [P, TILES, E + 8]), sb("marked", [P, TILES, E + 8])
        top = sb("top", [P, TILES, 8])
        stat, total = sb("stat", [P, TILES]), sb("total", [P, TILES])
        count, before = sb("count", [P, TILES, E], BF16), sb("before", [P, TILES, E], BF16)
        place = ps("place", [P, 2, 512])
        shifted, exp_ready, counted, placed, order = (
            sem(n) for n in ("shifted", "exp_ready", "counted", "placed", "order"))
        block = ctx.enter_context(nc.Block())

        def wide(v):
            return v[:, :].unsqueeze(2).to_broadcast([P, TILES, E])

        @block.scalar
        def _(act):
            act.wait_ge(shifted, 1)
            act.activation(prob[:, :, 0:E], logits[:, :, :], ACT.Exp).then_inc(exp_ready, 1)

        @block.vector
        def _(dve):
            chain = Chain(dve, order)
            dve.memset(prob[:, :, E:E + 8], TAKEN)
            chain(dve.tensor_reduce(stat[:, :], logits[:, :, :], AX, ALU.max))
            dve.tensor_tensor(logits[:, :, :], logits[:, :, :], wide(stat), ALU.subtract).then_inc(shifted, 1)
            dve.wait_ge(exp_ready, 1)
            chain(dve.tensor_reduce(total[:, :], prob[:, :, 0:E], AX, ALU.add))
            chain(dve.reciprocal(total[:, :], total[:, :]))
            chain(dve.tensor_tensor(prob[:, :, 0:E], prob[:, :, 0:E], wide(total), ALU.mult))
            for t in range(TILES):
                last = dve.max(top[:, t, :], prob[:, t, 0:E])
            chain(last)
            chain(dve.tensor_reduce(stat[:, :], top[:, :, 0:K], AX, ALU.add))
            chain(dve.tensor_scalar(stat[:, :], stat[:, :], floor, None, ALU.max))
            dve.reciprocal(stat[:, :], stat[:, :])
            chain(dve.memset(top[:, :, K:8], TAKEN))
            for t in range(TILES):
                last = dve.match_replace(marked[:, t, :], top[:, t, :], prob[:, t, :], -1.0)
            chain(last)
            chain(dve.scalar_tensor_tensor(out=gates[:, :, :], in0=marked[:, :, 0:E], scalar=0.0, in1=prob[:, :, 0:E],
                                           op0=ALU.is_lt, op1=ALU.mult))
            chain(dve.tensor_tensor(gates[:, :, :], gates[:, :, :], wide(stat), ALU.mult))
            if capacity is None:
                return
            chain(dve.tensor_scalar(count[:, :, :], marked[:, :, 0:E], 0.0, None, ALU.is_lt))
            chain(dve.memset(before[:, 0, :], 0.0))
            for t in range(1, TILES):
                ins = dve.tensor_tensor(before[:, t, :], before[:, t - 1, :], count[:, t - 1, :], ALU.add)
                if t < TILES - 1:
                    chain(ins)
            ins.then_inc(counted, 1)
            dve.wait_ge(placed, 1)
            h = TILES // 2
            for b in range(2):
                g = gates[:, h * b:h * b + h, :].rearrange("p t e -> p (t e)")
                last = dve.scalar_tensor_tensor(out=g, in0=place[:, b, 0:h * E], scalar=float(capacity), in1=g,
                                                op0=ALU.is_lt, op1=ALU.mult)
            chain(last)
            chain(dve.tensor_reduce(dropped[:, :], gates[:, :, :], AX, ALU.add))
            dve.tensor_scalar(dropped[:, :], dropped[:, :], 1e-12, None, ALU.is_le)

        if capacity is not None:
            @block.tensor
            def _(pe):
                pe.wait_ge(counted, 1)
                h = TILES // 2
                for b in range(2):
                    out = place[:, b, 0:h * E]
                    pe.matmul(out, R.bf["before"][:, :], count[:, h * b:h * b + h, :].rearrange("p t e -> p (t e)"),
                              start=True, stop=False)
                    last = pe.matmul(out, R.bf["ones"][:, :],
                                     before[:, h * b:h * b + h, :].rearrange("p t e -> p (t e)"),
                                     start=False, stop=True)
                last.then_inc(placed, 1)


def experts(nc, R, tag, E, kind, weights, gates, acc, bias=None):
    ups, down = weights
    U = 4 if kind == "glu" else 1
    A = len(ups)
    PER = 2 * CHUNKS * U
    SUB = CH // P
    with ExitStack() as ctx:
        sb, ps, sem = allocators(nc, ctx, tag)
        wu = [sb(f"wu{u}", [P, A * U * P]) for u in range(2)]
        wu_hi, wu_lo = ([sb(f"wu_{part}{u}", [P, A * U * P], F32R) for u in range(2)] for part in ("hi", "lo"))
        x_hi, x_lo = sb("x_hi", [P, N], F32R), sb("x_lo", [P, N], F32R)
        high_w, high_x = sb("high_w", [P, 2, A * U * P]), sb("high_x", [P, 2, CH])
        wd = [sb(f"wd{u}", [P, U, C]) for u in range(2)]
        first, hidden = sb("first", [P, 2, CH]), sb("hidden", [P, 2, CH])
        mixed = sb("mixed", [P, 2, CH]) if kind == "glu" else None
        bias_now, bias_copied = sb("bias_now", [P, 2, 1]), sem("bias_copied")
        up, back = ps("up", [P, 2, A, CH]), ps("back", [P, 2, CH])
        ups_loaded, down_loaded = ([sem(f"{what}_loaded{u}") for u in range(2)] for what in ("ups", "down"))
        x_halved, x_split, w_halved, w_split = (sem(n) for n in ("x_halved", "x_split", "w_halved", "w_split"))
        up_ready, first_ready, up_used, hidden_ready, back_ready, added = (
            sem(n) for n in ("up_ready", "first_ready", "up_used", "hidden_ready", "back_ready", "added"))
        block = ctx.enter_context(nc.Block())

        @block.sync
        def _(sp):
            def load_ups(e, u):
                for a, w in enumerate(ups):
                    sp.dma_start(wu[u][:, U * P * a:U * P * a + U * P],
                                 w[bass.ds(e, 1)].rearrange("o p h -> (o p) h")).then_inc(ups_loaded[u], 16)

            def load_down(e, u):
                sp.dma_start(wd[u][:, :, :],
                             down[bass.ds(e, 1)].rearrange("o (k p) d -> (o p) k d", p=P)).then_inc(down_loaded[u], 16)

            for u in range(2):
                load_ups(u, u)
                load_down(u, u)
            if E > 2:
                for u in range(2):
                    sp.wait_ge(w_split, u + 1)
                    load_ups(2 + u, u)
                with sp.Fori(1, E // 2 - 1) as i:
                    for u in range(2):
                        sp.wait_ge(back_ready, PER * i - PER + (u + 1) * CHUNKS * U + SLOTS)
                        load_down(2 * i + u, u)
                        sp.wait_ge(w_split, 2 * i + u + 1)
                        load_ups(2 * i + 2 + u, u)
                for u in range(2):
                    sp.wait_ge(back_ready, PER * (E // 2 - 2) + (u + 1) * CHUNKS * U + SLOTS)
                    load_down(E - 2 + u, u)

        def unit(j):
            return j // (CHUNKS * U), (j // U) % CHUNKS, j % U

        @block.tensor
        def _(pe):
            pe.sem_inc(back_ready, SLOTS)

            def go_up(i, j):
                u, ch, k = unit(j)
                if ch == 0 and k == 0:
                    pe.wait_ge(w_split, 2 * i + u + 1)
                if k == 0:
                    pe.wait_ge(x_split, ch + 1)
                pe.wait_ge(up_used, PER * i + j + 1)
                for a in range(A):
                    for m, (w, x) in enumerate(((wu_hi, x_lo), (wu_lo, x_hi), (wu_hi, x_hi))):
                        last = pe.matmul(up[:, j % 2, a, :], w[u][:, P * (U * a + k):P * (U * a + k) + P],
                                         x[:, CH * ch:CH * ch + CH], start=(m == 0), stop=(m == 2))
                last.then_inc(up_ready, 1)

            def go_back(i, j):
                u, ch, k = unit(j)
                if ch == 0 and k == 0:
                    pe.wait_ge(down_loaded[u], 16 * i + 16)
                if k == 0:
                    pe.wait_ge(added, (PER // U) * i + j // U + 1)
                if kind == "glu":
                    pe.wait_ge(hidden_ready, PER * i + j + 1 + SLOTS)
                else:
                    pe.wait_ge(up_used, PER * i + j + 1 + SLOTS)
                for s in range(SUB):
                    last = pe.matmul(back[:, ch % 2, C * s:C * s + C], hidden[:, j % 2, P * s:P * s + P], wd[u][:, k, :],
                                     start=(k == 0 and s == 0), stop=(k == U - 1), skip_group_check=True)
                last.then_inc(back_ready, 1)

            go_up(0, 0)
            if E > 2:
                with pe.Fori(0, E // 2 - 1) as i:
                    for j in range(PER):
                        go_up(i + (j + 1) // PER, (j + 1) % PER)
                        go_back(i, j)
            for j in range(PER):
                if j + 1 < PER:
                    go_up(E // 2 - 1, j + 1)
                go_back(E // 2 - 1, j)

        @block.scalar
        def _(act):
            if kind == "relu":
                act.sem_inc(up_used, SLOTS)
            if kind == "glu":
                act.sem_inc(hidden_ready, SLOTS)

            def hide(i, j):
                n = PER * i + j
                u, ch, k = unit(j)
                if kind == "relu" and ch == 0:
                    act.copy(bias_now[:, u, :], bias[:, bass.ds(2 * i + u, 1)]).then_inc(bias_copied, 1)
                    act.wait_ge(bias_copied, 2 * i + u + 1)
                act.wait_ge(up_ready, n + 1)
                if kind == "glu":
                    act.wait_ge(up_used, n + 1)
                    act.copy(first[:, j % 2, :], up[:, j % 2, 0, :]).then_inc(first_ready, 1)
                elif kind == "swiglu":
                    act.wait_ge(up_used, n + 1)
                    act.activation(first[:, j % 2, :], up[:, j % 2, 0, :], ACT.Silu).then_inc(first_ready, 1)
                else:
                    act.wait_ge(back_ready, n + 1)
                    act.activation(hidden[:, j % 2, :], up[:, j % 2, 0, :], ACT.Relu, bias=bias_now[:, u, :]).then_inc(
                        up_used, 1)

            def bend(i, j):
                n = PER * i + j
                act.wait_ge(up_used, n + 1 + SLOTS)
                act.wait_ge(back_ready, n + 1)
                act.activation(hidden[:, j % 2, :], mixed[:, j % 2, :], ACT.Gelu).then_inc(hidden_ready, 1)

            if kind == "glu":
                with act.Fori(0, E // 2) as i:
                    for j in range(PER):
                        hide(i, j)
                        bend(i, j)
            else:
                with act.Fori(0, E // 2) as i:
                    for j in range(PER):
                        hide(i, j)

        @block.vector
        def _(dve):
            if kind != "relu":
                dve.sem_inc(up_used, SLOTS)
            dve.sem_inc(added, SLOTS)

            def split_weights(i, u, first=False):
                dve.wait_ge(ups_loaded[u], 16 * A * i + 16 * A)
                if not first:
                    dve.wait_ge(w_split, 2 * i + u - 1)
                dve.tensor_scalar(high_w[:, u, :].bitcast(U32), wu[u][:, :].bitcast(U32), HIGH_BITS, None,
                                  ALU.bitwise_and).then_inc(w_halved, 1)
                dve.wait_ge(w_halved, 2 * i + u + 1)
                dve.tensor_copy(wu_hi[u][:, :], high_w[:, u, :])
                dve.tensor_tensor(wu_lo[u][:, :], wu[u][:, :], high_w[:, u, :], ALU.subtract).then_inc(w_split, 1)

            def split_chunk(ch):
                at = slice(CH * ch, CH * ch + CH)
                high = high_x[:, ch % 2, :]
                if ch >= 2:
                    dve.wait_ge(x_split, ch - 1)
                dve.tensor_scalar(high.bitcast(U32), R.xT[:, at].bitcast(U32), HIGH_BITS, None,
                                  ALU.bitwise_and).then_inc(x_halved, 1)
                dve.wait_ge(x_halved, ch + 1)
                dve.tensor_copy(x_hi[:, at], high)
                dve.tensor_tensor(x_lo[:, at], R.xT[:, at], high, ALU.subtract).then_inc(x_split, 1)

            def mix(i, j):
                n = PER * i + j
                if kind == "relu":
                    return
                dve.wait_ge(first_ready, n + 1)
                if kind == "glu":
                    dve.wait_ge(hidden_ready, n + 1)
                    dve.tensor_tensor(mixed[:, j % 2, :], up[:, j % 2, 1, :], first[:, j % 2, :], ALU.mult).then_inc(
                        up_used, 1)
                else:
                    dve.wait_ge(back_ready, n + 1)
                    dve.tensor_tensor(hidden[:, j % 2, :], up[:, j % 2, 1, :], first[:, j % 2, :], ALU.mult).then_inc(
                        up_used, 1)

            def add(i, j):
                u, ch, k = unit(j)
                if k != U - 1:
                    return
                dve.wait_ge(back_ready, PER * i + j + 1 + SLOTS)
                if j // U == 0:
                    dve.wait_ge(added, (PER // U) * i + SLOTS)
                elif ch == 0:
                    dve.wait_ge(added, (PER // U) * i + CHUNKS + SLOTS)
                for s in range(SUB):
                    t = SUB * ch + s
                    gate = 1.0 if gates is None else gates[:, t, :][:, bass.ds(2 * i + u, 1)]
                    last = dve.scalar_tensor_tensor(out=acc[:, t, :], in0=back[:, ch % 2, C * s:C * s + C], scalar=gate,
                                                    in1=acc[:, t, :], op0=ALU.mult, op1=ALU.add)
                last.then_inc(added, 1)

            split_chunk(0)
            split_weights(0, 0, True)
            for ch in range(1, CHUNKS):
                split_chunk(ch)
            split_weights(0, 1, True)
            mix(0, 0)
            if E > 2:
                with dve.Fori(0, E // 2 - 1) as i:
                    for j in range(PER):
                        mix(i + (j + 1) // PER, (j + 1) % PER)
                        if j % (PER // 2) == PER // 2 - 1:
                            dve.wait_ge(up_ready, PER * i + j + 1)
                            split_weights(i + 1, j // (PER // 2))
                        add(i, j)
            for j in range(PER):
                if j + 1 < PER:
                    mix(E // 2 - 1, j + 1)
                add(E // 2 - 1, j)


def feed_forward_3(nc, R):
    E, K = 64, 6
    with ExitStack() as ctx:
        sb, _, _ = allocators(nc, ctx, "f3")
        gates, acc = sb("gates", [P, TILES, E]), sb("acc", [P, TILES, C])
        layer_norm(nc, R, "f3_ln", R.hT, R.xT)
        with ExitStack() as inner:
            sb2, _, _ = allocators(nc, inner, "f3r")
            logits = sb2("logits", [P, TILES, E])
            route(nc, R, "f3_route", R.w["L3_ffn_Wr"][:, :], E, logits)
            top_gates(nc, R, "f3_top", logits, E, K, gates, 0.0)
        zero(nc, acc)
        i = R.ins
        experts(nc, R, "f3_shared", 2, "swiglu", ((i["L3_ffn_sWg"], i["L3_ffn_sWu"]), i["L3_ffn_sWd"]), None, acc)
        experts(nc, R, "f3_routed", E, "swiglu", ((i["L3_ffn_Wg"], i["L3_ffn_Wu"]), i["L3_ffn_Wd"]), gates, acc)
        leave(nc, R, "f3_out", acc)


def zero(nc, acc):
    with nc.Block() as block:
        @block.vector
        def _(dve):
            dve.memset(acc[:, :, :], 0.0)


def leave(nc, R, tag, acc):
    with ExitStack() as ctx:
        sb, ps, sem = allocators(nc, ctx, tag)
        both = ps("both", [P, 2, 512])
        turned, summed, stored = sem("turned"), sem("summed"), sem("stored")
        block = ctx.enter_context(nc.Block())
        SUB = 4
        out = R.out.rearrange("b t c -> (b t) c").rearrange("(g s p) c -> g p s c", s=SUB, p=P)

        @block.tensor
        def _(pe):
            for g in range(TILES // SUB):
                if g >= 2:
                    pe.wait_ge(summed, g - 1)
                for s in range(SUB):
                    o = both[:, g % 2, C * s:C * s + C]
                    pe.matmul(o, R.hT[:, tile_of(SUB * g + s)], R.c("ident"), start=True, stop=False)
                    last = pe.matmul(o, R.xT[:, tile_of(SUB * g + s)], R.c("ident"), start=False, stop=True)
                last.then_inc(turned, 1)

        @block.vector
        def _(dve):
            for g in range(TILES // SUB):
                dve.wait_ge(turned, g + 1)
                a = acc[:, SUB * g:SUB * g + SUB, :].rearrange("p t c -> p (t c)")
                dve.tensor_tensor(a, both[:, g % 2, :], a, ALU.add).then_inc(summed, 1)

        @block.sync
        def _(sp):
            for g in range(TILES // SUB):
                sp.wait_ge(summed, g + 1)
                sp.dma_start(out[g], acc[:, SUB * g:SUB * g + SUB, :]).then_inc(stored, 16)
            sp.wait_ge(stored, 16 * (TILES // SUB))


def fold(nc, R, tag, acc, from_x, keep=None, gates=None, b2=None):
    SUB = CH // P
    with ExitStack() as ctx:
        sb, ps, sem = allocators(nc, ctx, tag)
        px, pb, py = ps("px", [P, 2, CH]), ps("pb", [P, 2, CH]), ps("py", [P, 2, CH])
        if b2 is not None:
            pg, gT = ps("pg", [32, 2, CH]), sb("gT", [32, 2, CH])
        g_turned, g_ready, x_ready, y_ready, y_turned, folded, order = (
            sem(n) for n in ("g_turned", "g_ready", "x_ready", "y_ready", "y_turned", "folded", "order"))
        block = ctx.enter_context(nc.Block())
        GROUPS = TILES // SUB

        @block.tensor
        def _(pe):
            def turn_gates(g):
                for s in range(SUB):
                    last = pe.transpose(pg[:, g % 2, P * s:P * s + P], gates[:, SUB * g + s, :], R.c("ident"))
                last.then_inc(g_turned, 1)

            def turn_x(g):
                if g >= 2:
                    pe.wait_ge(folded, g - 1)
                if b2 is not None:
                    pe.wait_ge(g_ready, g + 1)
                    for s in range(SUB):
                        pe.matmul(pb[:, g % 2, P * s:P * s + P], gT[:, g % 2, P * s:P * s + P], b2, start=True, stop=True)
                for s in range(SUB):
                    last = pe.transpose(px[:, g % 2, P * s:P * s + P], R.xT[:, tile_of(SUB * g + s)], R.c("ident"))
                last.then_inc(x_ready, 1)

            def turn_y(g):
                pe.wait_ge(y_ready, g + 1)
                for s in range(SUB):
                    last = pe.transpose(py[:, g % 2, P * s:P * s + P], acc[:, SUB * g + s, :], R.c("ident"))
                last.then_inc(y_turned, 1)

            for g in range(GROUPS):
                if b2 is not None:
                    turn_gates(g)
                turn_x(g)
                if g >= 1:
                    turn_y(g - 1)
            turn_y(GROUPS - 1)

        if b2 is not None:
            @block.scalar
            def _(act):
                for g in range(GROUPS):
                    act.wait_ge(g_turned, g + 1)
                    act.copy(gT[:, g % 2, :], pg[:, g % 2, :]).then_inc(g_ready, 1)

        @block.vector
        def _(dve):
            chain = Chain(dve, order)

            def make(g):
                dve.wait_ge(x_ready, g + 1)
                a = acc[:, SUB * g:SUB * g + SUB, :].rearrange("p t c -> p (t c)")
                if b2 is not None:
                    chain(dve.tensor_tensor(a, pb[:, g % 2, :], a, ALU.add))
                    for s in range(SUB):
                        t = SUB * g + s
                        last = dve.tensor_scalar(acc[:, t, :], acc[:, t, :], keep[:, t:t + 1], None, ALU.mult)
                    chain(last)
                for s in range(SUB):
                    t = SUB * g + s
                    last = dve.scalar_tensor_tensor(out=acc[:, t, :], in0=px[:, g % 2, P * s:P * s + P],
                                                    scalar=from_x[:, t:t + 1], in1=acc[:, t, :], op0=ALU.mult,
                                                    op1=ALU.add)
                last.then_inc(y_ready, 1)

            def put(g):
                dve.wait_ge(y_turned, g + 1)
                h = R.hT[:, CH * g:CH * g + CH]
                dve.tensor_tensor(h, py[:, g % 2, :], h, ALU.add).then_inc(folded, 1)

            for g in range(GROUPS):
                make(g)
                if g >= 1:
                    put(g - 1)
            put(GROUPS - 1)


def gates_0(nc, R, logits, gates, from_x):
    E = 8
    with ExitStack() as ctx:
        sb, ps, sem = allocators(nc, ctx, "g0")
        shape = [P, TILES, E]
        one, two, t1 = sb("one", shape), sb("two", shape), sb("t1", shape)
        m1, m2, i1, i2, s1, s2 = (sb(n, [P, TILES]) for n in ("m1", "m2", "i1", "i2", "s1", "s2"))
        keep = sb("keep", [P, 2, TILES])
        full = sb("full", [P, 2, E])
        one_bf, both_bf = sb("one_bf", shape, BF16), sb("both_bf", shape, BF16)
        tally = ps("tally", [P, 2, 512])
        gap_ready, exp_ready, chosen, tallied, order = (
            sem(n) for n in ("gap_ready", "exp_ready", "chosen", "tallied", "order"))
        block = ctx.enter_context(nc.Block())

        def wide(v):
            return v[:, :].unsqueeze(2).to_broadcast(shape)

        rev = R.c("rev8").unsqueeze(1).to_broadcast(shape)
        iota = R.c("iota8").unsqueeze(1).to_broadcast(shape)

        @block.scalar
        def _(act):
            act.wait_ge(gap_ready, 1)
            act.activation(s2[:, :], m2[:, :], ACT.Exp).then_inc(exp_ready, 1)

        @block.tensor
        def _(pe):
            pe.wait_ge(chosen, 1)
            for n, t in enumerate((one_bf, both_bf)):
                last = pe.matmul(tally[:, n, 0:TILES * E], R.bf["ones"][:, :], t[:, :, :].rearrange("p t e -> p (t e)"),
                                 start=True, stop=True)
            last.then_inc(tallied, 1)

        @block.vector
        def _(dve):
            chain = Chain(dve, order)

            def choose(best, at, out):
                chain(dve.tensor_reduce(best[:, :], logits[:, :, :], AX, ALU.max))
                chain(dve.tensor_tensor(t1[:, :, :], logits[:, :, :], wide(best), ALU.is_equal))
                chain(dve.tensor_tensor(t1[:, :, :], t1[:, :, :], rev, ALU.mult))
                chain(dve.tensor_reduce(at[:, :], t1[:, :, :], AX, ALU.max))
                chain(dve.tensor_tensor(out[:, :, :], rev, wide(at), ALU.is_equal))

            choose(m1, i1, one)
            chain(dve.scalar_tensor_tensor(out=logits[:, :, :], in0=one[:, :, :], scalar=-3e38, in1=logits[:, :, :],
                                           op0=ALU.mult, op1=ALU.add))
            choose(m2, i2, two)
            dve.tensor_copy(one_bf[:, :, :], one[:, :, :])
            dve.tensor_tensor(both_bf[:, :, :], one[:, :, :], two[:, :, :], ALU.add).then_inc(chosen, 1)
            dve.tensor_tensor(m2[:, :], m2[:, :], m1[:, :], ALU.subtract).then_inc(gap_ready, 1)
            dve.wait_ge(exp_ready, 1)
            chain(dve.tensor_scalar(s1[:, :], s2[:, :], 1.0, None, ALU.add))
            chain(dve.reciprocal(s1[:, :], s1[:, :]))
            chain(dve.tensor_tensor(s2[:, :], s2[:, :], s1[:, :], ALU.mult))
            dve.wait_ge(tallied, 1)
            for n in range(2):
                last = dve.tensor_reduce(full[:, n, :], tally[:, n, 0:TILES * E].rearrange("p (t e) -> p e t", e=E), AX,
                                         ALU.add)
            chain(last)
            chain(dve.tensor_scalar(full[:, :, :], full[:, :, :], float(N), R.c("last_row"), ALU.is_ge, ALU.mult))
            chain(dve.memset(keep[:, :, :], 1.0))
            for n, t in enumerate((one, two)):
                chain(dve.tensor_tensor(t1[:, n, :], t[:, TILES - 1, :], full[:, n, :], ALU.mult))
                chain(dve.tensor_reduce(keep[:, n, TILES - 1:TILES], t1[:, n, :], AX, ALU.add))
                chain(dve.tensor_scalar(keep[:, n, TILES - 1:TILES], keep[:, n, TILES - 1:TILES], -1.0, 1.0, ALU.mult,
                                        ALU.add))
            for n, t in enumerate((i1, i2)):
                chain(dve.tensor_scalar(t[:, :], t[:, :], -1.0, float(E), ALU.mult, ALU.add))
                chain(dve.tensor_tensor(t[:, :], t[:, :], keep[:, n, :], ALU.mult))
            chain(dve.tensor_tensor(i1[:, :], i1[:, :], i2[:, :], ALU.max))
            chain(dve.tensor_tensor(m1[:, :], s1[:, :], keep[:, 0, :], ALU.mult))
            chain(dve.tensor_tensor(m2[:, :], s2[:, :], keep[:, 1, :], ALU.mult))
            dve.tensor_tensor(s1[:, :], s1[:, :], m1[:, :], ALU.subtract)
            chain(dve.tensor_tensor(s2[:, :], s2[:, :], m2[:, :], ALU.subtract))
            dve.tensor_tensor(from_x[:, :], s1[:, :], s2[:, :], ALU.add)
            chain(dve.tensor_tensor(m1[:, :], m1[:, :], m2[:, :], ALU.add))
            chain(dve.tensor_tensor(gates[:, :, :], iota, wide(i1), ALU.is_equal))
            chain(dve.tensor_tensor(gates[:, :, :], gates[:, :, :], wide(m1), ALU.mult))


def feed_forward_0(nc, R):
    E = 8
    with ExitStack() as ctx:
        sb, _, _ = allocators(nc, ctx, "f0")
        gates, acc, from_x = sb("gates", [P, TILES, E]), sb("acc", [P, TILES, C]), sb("from_x", [P, TILES])
        logits, br = sb("logits", [P, TILES, E]), sb("br", [E, 1])
        layer_norm(nc, R, "f0_ln", R.hT, R.xT)
        with nc.semaphore("f0_bias") as loaded, nc.Block() as block:
            @block.sync
            def _(sp):
                sp.dma_start(br[:, :], R.ins["L0_ffn_br"].rearrange("(e o) -> e o", o=1)).then_inc(loaded, 16)
                sp.wait_ge(loaded, 16)
        route(nc, R, "f0_route", R.w["L0_ffn_Wr"][:, :], E, logits, br[:, 0:1])
        gates_0(nc, R, logits, gates, from_x)
        zero(nc, acc)
        i = R.ins
        experts(nc, R, "f0_experts", E, "glu", ((i["L0_ffn_W1"], i["L0_ffn_W2"]), i["L0_ffn_W3"]), gates, acc)
        fold(nc, R, "f0_fold", acc, from_x)


def feed_forward_1(nc, R):
    E, K = 32, 2
    capacity = -(-N * K * 5 // (4 * E))
    with ExitStack() as ctx:
        sb, _, _ = allocators(nc, ctx, "f1")
        gates, acc = sb("gates", [P, TILES, E]), sb("acc", [P, TILES, C])
        dropped, kept = sb("dropped", [P, TILES]), sb("kept", [P, TILES])
        logits, b1, b1T, b2 = sb("logits", [P, TILES, E]), sb("b1", [E, C]), sb("b1T", [P, E]), sb("b2", [E, C])
        layer_norm(nc, R, "f1_ln", R.hT, R.xT)
        route(nc, R, "f1_route", R.w["L1_ffn_Wg"][:, :], E, logits)
        top_gates(nc, R, "f1_top", logits, E, K, gates, 1e-9, capacity, dropped)
        with (nc.semaphore("f1_loaded") as loaded, nc.semaphore("f1_turned") as turned,
              nc.psum_tensor("f1_pb", [P, 512], F32) as pb, nc.Block() as block):
            @block.sync
            def _(sp):
                sp.dma_start(b1[:, :], R.ins["L1_ffn_b1"]).then_inc(loaded, 16)
                sp.dma_start(b2[:, :], R.ins["L1_ffn_b2"]).then_inc(loaded, 16)

            @block.tensor
            def _(pe):
                pe.wait_ge(loaded, 32)
                pe.transpose(pb[:, 0:E], b1[:, :], R.c("ident")[0:E, 0:E]).then_inc(turned, 1)

            @block.vector
            def _(dve):
                dve.memset(acc[:, :, :], 0.0)
                dve.tensor_scalar(kept[:, :], dropped[:, :], -1.0, 1.0, ALU.mult, ALU.add)
                dve.wait_ge(turned, 1)
                dve.tensor_copy(b1T[:, :], pb[:, 0:E])
        i = R.ins
        experts(nc, R, "f1_experts", E, "relu", ((i["L1_ffn_W1"],), i["L1_ffn_W2"]), gates, acc, b1T)
        fold(nc, R, "f1_fold", acc, dropped, kept, gates, b2[:, :])


def dense_mlp(nc, R, tag, src, w_up, up_scale, up_bias, w_down, finish):
    K = 4
    with ExitStack() as ctx:
        sb, ps, sem = allocators(nc, ctx, tag)
        hidden, t = sb("hidden", [P, 2, K, CH]), sb("t", [P, 2, CH])
        up, down = ps("up", [P, K, CH]), ps("down", [P, 2, CH])
        up_ready, hidden_ready, down_ready, evacuated, done, order = (
            sem(n) for n in ("up_ready", "hidden_ready", "down_ready", "evacuated", "done", "order"))
        block = ctx.enter_context(nc.Block())
        kind, p1, p2, p3 = finish

        @block.tensor
        def _(pe):
            pe.sem_inc(down_ready, SLOTS)
            with pe.Fori(0, CHUNKS // 2) as i:
                for u in range(2):
                    n = 2 * i + u
                    for k in range(K):
                        pe.wait_ge(hidden_ready, K * n + k + 1)
                        pe.matmul(up[:, k, :], w_up(k), src[:, bass.ds(i * (2 * CH) + u * CH, CH)], start=True,
                                  stop=True).then_inc(up_ready, 1)
                    pe.wait_ge(done, n + 1)
                    for k in range(K):
                        pe.wait_ge(hidden_ready, K * n + k + 1 + K)
                        last = pe.matmul(down[:, u, :], w_down(k), hidden[:, u, k, :], start=(k == 0), stop=(k == K - 1))
                    last.then_inc(down_ready, 1)

        @block.scalar
        def _(act):
            act.sem_inc(hidden_ready, K)
            with act.Fori(0, CHUNKS // 2) as i:
                for u in range(2):
                    n = 2 * i + u
                    for k in range(K):
                        act.wait_ge(up_ready, K * n + k + 1)
                        act.wait_ge(down_ready, n + 1)
                        act.activation(hidden[:, u, k, :], up[:, k, :], ACT.Relu, scale=up_scale(k),
                                       bias=up_bias(k)).then_inc(hidden_ready, 1)
                    if kind == "norm":
                        act.wait_ge(down_ready, n + 1 + SLOTS)
                        act.wait_ge(done, n + 1)
                        act.activation(t[:, u, :], down[:, u, :], ACT.Relu, scale=p1, bias=p2).then_inc(evacuated, 1)

        @block.vector
        def _(dve):
            dve.sem_inc(done, SLOTS)
            chain = Chain(dve, order)
            with dve.Fori(0, CHUNKS // 2) as i:
                chain.turn(i, 4 if kind == "half" else 2)
                for u in range(2):
                    n = 2 * i + u
                    at = bass.ds(i * (2 * CH) + u * CH, CH)
                    if kind == "half":
                        dve.wait_ge(down_ready, n + 1 + SLOTS)
                        chain(dve.scalar_tensor_tensor(out=t[:, u, :], in0=down[:, u, :], scalar=p1, in1=p2[:, at],
                                                       op0=ALU.add, op1=ALU.add))
                        chain(dve.tensor_tensor(t[:, u, :], t[:, u, :], p3[:, at], ALU.add))
                        dve.scalar_tensor_tensor(out=R.hT[:, at], in0=t[:, u, :], scalar=0.5, in1=R.hT[:, at],
                                                 op0=ALU.mult, op1=ALU.add).then_inc(done, 1)
                    else:
                        dve.wait_ge(evacuated, n + 1)
                        chain(dve.tensor_tensor(t[:, u, :], t[:, u, :], p3[:, at], ALU.add))
                        dve.tensor_tensor(R.hT[:, at], R.hT[:, at], t[:, u, :], ALU.add).then_inc(done, 1)
                chain.close()


def add_arrays(nc, R, tag, dst, a):
    with nc.Block() as block:
        @block.vector
        def _(dve):
            with dve.Fori(0, CHUNKS) as i:
                at = bass.ds(i * CH, CH)
                dve.tensor_tensor(dst[:, at], dst[:, at], a[:, at], ALU.add)


def unit_keys(nc, R, tag, q, dst, dram):
    with ExitStack() as ctx:
        sb, ps, sem = allocators(nc, ctx, tag)
        squares, norm = sb("squares", [P, 2, CH]), sb("norm", [P, 2, CH])
        total = ps("total", [P, 2, CH])
        squared, total_ready, norm_ready, done, stored, order = (
            sem(n) for n in ("squared", "total_ready", "norm_ready", "done", "stored", "order"))
        block = ctx.enter_context(nc.Block())

        @block.scalar
        def _(act):
            with act.Fori(0, CHUNKS // 2) as i:
                for u in range(2):
                    act.wait_ge(done, 2 * i + u + 1)
                    act.wait_ge(total_ready, SLOTS)
                    act.activation(squares[:, u, :], q[:, bass.ds(i * (2 * CH) + u * CH, CH)], ACT.Square).then_inc(
                        squared, 1)
                    act.wait_ge(total_ready, 2 * i + u + 1 + SLOTS)
                    act.activation(norm[:, u, :], total[:, u, :], ACT.Sqrt).then_inc(norm_ready, 1)

        @block.tensor
        def _(pe):
            pe.sem_inc(total_ready, SLOTS)
            with pe.Fori(0, CHUNKS // 2) as i:
                for u in range(2):
                    pe.wait_ge(squared, 2 * i + u + 1)
                    pe.matmul(total[:, u, :], R.c("head_block"), squares[:, u, :], start=True, stop=True).then_inc(
                        total_ready, 1)

        @block.vector
        def _(dve):
            dve.sem_inc(done, SLOTS)
            chain = Chain(dve, order)
            with dve.Fori(0, CHUNKS // 2) as i:
                chain.turn(i, 4)
                for u in range(2):
                    at = bass.ds(i * (2 * CH) + u * CH, CH)
                    dve.wait_ge(norm_ready, 2 * i + u + 1)
                    chain(dve.tensor_scalar(norm[:, u, :], norm[:, u, :], 1e-12, None, ALU.max))
                    chain(dve.reciprocal(norm[:, u, :], norm[:, u, :]))
                    dve.tensor_tensor(dst[:, at], q[:, at], norm[:, u, :], ALU.mult).then_inc(done, 1)
                chain.close()

        @block.sync
        def _(sp):
            with sp.Fori(0, CHUNKS) as i:
                at = bass.ds(i * CH, CH)
                sp.wait_ge(done, i + 1 + SLOTS)
                sp.dma_start(dram[:, at], dst[:, at]).then_inc(stored, 16)
            sp.wait_ge(stored, 16 * CHUNKS)


def hash_groups(nc, R, tag, q_all, groups):
    NB, G = 32, 2 * HEADS
    with ExitStack() as ctx:
        sb, ps, sem = allocators(nc, ctx, tag)
        q = sb("q", [P, 2, T])
        r = sb("r", [HALF, G, 2, NB // 2])
        eq = sb("eq", [HALF, G, NB])
        best, at_bucket, rank = sb("best", [HALF, G]), sb("at_bucket", [HALF, G]), sb("rank", [HALF, G])
        big = sb("big", [HALF, G, 6])
        hot, below = ([sb(f"{what}{u}", [HALF, G, NB], BF16) for u in range(2)] for what in ("hot", "below"))
        edge, chunk, reach = sb("edge", [HALF, 2, G, 8]), sb("chunk", [HALF, G, 8]), sb("reach", [HALF, G, 8])
        sides = sb("sides", [HALF, 2, HEADS, 2, 8], BF16)
        flat = sb("flat", [P, 2, T], BF16)
        pr, pk, pt = ps("pr", [HALF, 2, 512]), ps("pk", [HALF, 512]), ps("pt", [P, 2 * T], BF16)
        copied, turned_q, hot_ready, ranked, sides_ready, flat_turned, flat_ready, order = (
            sem(n) for n in ("copied", "turned_q", "hot_ready", "ranked", "sides_ready", "flat_turned", "flat_ready",
                             "order"))
        stored = [sem(f"stored{u}") for u in range(2)]
        block = ctx.enter_context(nc.Block())
        wide_shape = [HALF, G, NB]

        edge_ready, steps = sem("edge_ready"), sem("steps")

        @block.gpsimd
        def _(pool):
            chain = Chain(pool, steps)
            pool.sem_inc(sides_ready, SLOTS)
            pool.memset(big[:, :, :], BIG)
            chain(pool.memset(sides[:, :, :, :, :], 0.0))
            pool.memset(sides[:, :, :, 0, 6:7], 1.0)
            chain(pool.memset(sides[:, :, :, 1, 6:7], -BIG))

            def copy_in(n, u):
                pool.wait_ge(turned_q, n + 1)
                pool.wait_ge(turned_q, SLOTS)
                pool.tensor_copy(q[:, u, :], q_all[:, bass.ds(n * T, T)]).then_inc(copied, 1)

            def sides_of(n, u):
                pool.wait_ge(edge_ready, n + 2)
                chain(pool.tensor_tensor(chunk[:, :, 0:6], edge[:, u, :, 0:6], edge[:, u, :, 1:7], ALU.subtract))
                pool.tensor_tensor(reach[:, :, 1:6], chunk[:, :, 1:6], chunk[:, :, 0:5], ALU.add)
                chain(pool.tensor_tensor(reach[:, :, 0:1], chunk[:, :, 0:1], chunk[:, :, 5:6], ALU.add))
                pool.wait_ge(flat_ready, n + 1)
                pool.wait_ge(turned_q, SLOTS)
                s = sides[:, :, :, :, :].rearrange("p a h k c -> p (a h) k c")
                chain(pool.tensor_tensor(s[:, :, 0, 0:6], edge[:, u, :, 0:6], edge[:, u, :, 1:7], ALU.subtract))
                pool.tensor_tensor(s[:, :, 1, 0:6], reach[:, :, 0:6], big[:, :, :], ALU.mult).then_inc(sides_ready, 1)

            copy_in(0, 0)
            copy_in(1, 1)
            with pool.Fori(0, B // 2 - 1) as i:
                chain.turn(i, 2 * 3, 2)
                for u in range(2):
                    copy_in(2 * i + u + 2, u)
                    sides_of(2 * i + u, u)
                chain.close()
            chain.after(2 + 2 * 3 * (B // 2 - 1))
            sides_of(B - 2, 0)
            sides_of(B - 1, 1)

        @block.tensor
        def _(pe):
            pe.sem_inc(turned_q, SLOTS)

            def rotate(n, u):
                pe.wait_ge(copied, n + 1)
                pe.wait_ge(hot_ready, n + 1)
                for half in range(2):
                    last = pe.matmul(pr[:, u, P * half:P * half + P], q[:, u, HALF * half:HALF * half + HALF], R.rot[:, :],
                                     start=True, stop=True)
                last.then_inc(turned_q, 1)

            def ranks(n, u):
                pe.wait_ge(hot_ready, n + 1 + SLOTS)
                pe.wait_ge(edge_ready, n + 1)
                for half in range(2):
                    out = pk[:, 256 * half:256 * half + 256]
                    one, before = R.bf["ones"][0:HALF, 0:HALF], R.bf["before"][0:HALF, 0:HALF]
                    terms = [(before, hot[u], half), (one, below[u], 0), (one, below[u], 1)] + (
                        [(one, hot[u], 0)] if half else [])
                    for m, (lhsT, t, side) in enumerate(terms):
                        rhs = t[:, HEADS * side:HEADS * side + HEADS, :].rearrange("p h b -> p (h b)")
                        last = pe.matmul(out, lhsT, rhs, start=(m == 0), stop=(m == len(terms) - 1))
                last.then_inc(ranked, 1)

            def turn(n, u):
                pe.wait_ge(sides_ready, n + 1 + SLOTS)
                pe.wait_ge(flat_ready, n + 1)
                for half in range(2):
                    last = pe.transpose(pt[:, HALF * half:HALF * half + HALF],
                                        sides[:, half].rearrange("p h k c -> p (h k c)"), R.bf["ident"][0:HALF, 0:HALF])
                last.then_inc(flat_turned, 1)

            rotate(0, 0)
            rotate(1, 1)
            ranks(0, 0)
            with pe.Fori(0, B // 2 - 1) as i:
                for u in range(2):
                    rotate(2 * i + u + 2, u)
                    ranks(2 * i + u + 1, 1 - u)
                    turn(2 * i + u, u)
            ranks(B - 1, 1)
            turn(B - 2, 0)
            turn(B - 1, 1)

        @block.scalar
        def _(act):
            act.sem_inc(flat_ready, 1)
            with act.Fori(0, B // 2) as i:
                for u in range(2):
                    act.wait_ge(flat_turned, 2 * i + u + 1)
                    act.wait_ge(stored[u], 16 * i + 16)
                    act.copy(flat[:, u, :], pt[:, 0:T]).then_inc(flat_ready, 1)

        @block.sync
        def _(sp):
            for u in range(2):
                sp.sem_inc(stored[u], 16)
            with sp.Fori(0, B // 2) as i:
                for u in range(2):
                    sp.wait_ge(flat_ready, 2 * i + u + 2)
                    sp.dma_start(groups[:, bass.ds(i * (2 * T) + u * T, T)], flat[:, u, :]).then_inc(stored[u], 16)
            for u in range(2):
                sp.wait_ge(stored[u], 16 * (B // 2 + 1))

        @block.vector
        def _(dve):
            chain = Chain(dve, order)
            rev = R.c("rev32", HALF).unsqueeze(1).to_broadcast(wide_shape)

            edges = R.c("chunk_edge", HALF).unsqueeze(1).to_broadcast([HALF, G, 8])

            def wide(v):
                return v[:, :].unsqueeze(2).to_broadcast([HALF, G, NB])

            dve.sem_inc(hot_ready, SLOTS)

            def buckets(n, u):
                dve.wait_ge(turned_q, n + 1 + SLOTS)
                src = pr[:, u, 0:2 * P].rearrange("p (g b) -> p g b", b=NB // 2)
                dve.tensor_copy(r[:, :, 0, :], src)
                chain(dve.tensor_scalar(r[:, :, 1, :], src, -1.0, None, ALU.mult))
                rr = r[:, :, :, :].rearrange("p g s b -> p g (s b)")
                chain(dve.tensor_reduce(best[:, :], rr, AX, ALU.max))
                chain(dve.tensor_tensor(eq[:, :, :], rr, wide(best), ALU.is_equal))
                chain(dve.tensor_tensor(eq[:, :, :], eq[:, :, :], rev, ALU.mult))
                chain(dve.tensor_reduce(at_bucket[:, :], eq[:, :, :], AX, ALU.max))
                chain(dve.tensor_tensor(hot[u][:, :, :], rev, wide(at_bucket), ALU.is_equal))
                dve.tensor_tensor(below[u][:, :, :], rev, wide(at_bucket), ALU.is_lt).then_inc(hot_ready, 1)
                dve.wait_ge(hot_ready, n + 1 + SLOTS)

            def chunks(n, u):
                dve.wait_ge(ranked, n + 1)
                chain(dve.tensor_tensor(eq[:, :, :], pk[:, 0:512].rearrange("p (g b) -> p g b", b=NB), hot[u][:, :, :],
                                        ALU.mult))
                chain(dve.tensor_reduce(rank[:, :], eq[:, :, :], AX, ALU.add))
                dve.wait_ge(sides_ready, n + 1)
                dve.tensor_tensor(edge[:, u, :, :], rank[:, :].unsqueeze(2).to_broadcast([HALF, G, 8]), edges,
                                  ALU.is_ge).then_inc(edge_ready, 1)

            dve.sem_inc(edge_ready, 1)
            buckets(0, 0)
            with dve.Fori(0, B // 2 - 1) as i:
                chain.turn(i, 2 * 8, 6)
                for u in range(2):
                    buckets(2 * i + u + 1, 1 - u)
                    chunks(2 * i + u, u)
                chain.close()
            chain.after(6 + 2 * 8 * (B // 2 - 1))
            buckets(B - 1, 1)
            chunks(B - 2, 0)
            chunks(B - 1, 1)


def add_projection(nc, R, tag, src, w, bias, x, dst):
    with ExitStack() as ctx:
        sb, ps, sem = allocators(nc, ctx, tag)
        out = ps("out", [P, 2, CH])
        product_ready, done = sem("product_ready"), sem("done")
        block = ctx.enter_context(nc.Block())

        @block.tensor
        def _(pe):
            with pe.Fori(0, CHUNKS // 2) as i:
                for u in range(2):
                    pe.wait_ge(done, 2 * i + u + 1)
                    pe.matmul(out[:, u, :], w, src[:, bass.ds(i * (2 * CH) + u * CH, CH)], start=True,
                              stop=True).then_inc(product_ready, 1)

        @block.vector
        def _(dve):
            dve.sem_inc(done, SLOTS)
            with dve.Fori(0, CHUNKS // 2) as i:
                for u in range(2):
                    at = bass.ds(i * (2 * CH) + u * CH, CH)
                    dve.wait_ge(product_ready, 2 * i + u + 1)
                    dve.scalar_tensor_tensor(out=dst[:, at], in0=out[:, u, :], scalar=bias, in1=x[:, at], op0=ALU.add,
                                             op1=ALU.add).then_inc(done, 1)


def attention_1(nc, R):
    with ExitStack() as ctx:
        sb, _, _ = allocators(nc, ctx, "a1")
        own, y1, h1 = sb("own", [P, N]), sb("y1", [P, N]), sb("h1", [P, N])
        layer_norm(nc, R, "a1_ln", R.hT, R.xT)
        layer_norm(nc, R, "a1_ln1", R.xT, h1, 1e-5, R.col("L1_attn_ln1_g"), R.col("L1_attn_ln1_b"))
        project(nc, R, "a1_qv", h1, [(R.w["L1_attn_w_qk"][:, :], own, ACT.Identity, 1.0, 0.0),
                                     (R.w["L1_attn_w_v"][:, :], y1, ACT.Identity, 1.0, 0.0)],
                copies=[(0, R.scratch[0]), (1, R.scratch[2])])
        unit_keys(nc, R, "a1_keys", own, y1, R.scratch[1])
        hash_groups(nc, R, "a1_hash", own, R.groups)
        attend(nc, R, "a1", *R.scratch[0:5], HD ** -0.5, R.groups, -50000.0, own)
        divide(nc, R, "a1_div", R.scratch[3], R.scratch[4], h1, own, R.scratch[2])
        add_projection(nc, R, "a1_out", h1, R.w["L1_attn_w_out"][:, :], R.col("L1_attn_b_out"), R.xT, y1)
        layer_norm(nc, R, "a1_ln2", y1, h1, 1e-5, R.col("L1_attn_ln2_g"), R.col("L1_attn_ln2_b"))
        dense_mlp(nc, R, "a1_mlp", h1, lambda k: R.w["L1_attn_w_ff1"][:, C * k:C * k + C], lambda k: 1.0,
                  lambda k: R.col("L1_attn_b_ff1", k), lambda k: R.w["L1_attn_w_ff2"][:, k, :],
                  ("half", R.col("L1_attn_b_ff2"), R.xT, y1))


def attention_2(nc, R):
    with ExitStack() as ctx:
        sb, _, _ = allocators(nc, ctx, "a2")
        q, k, v, o = sb("q", [P, N]), sb("k", [P, N]), sb("v", [P, N]), sb("o", [P, N])
        layer_norm(nc, R, "a2_ln", R.hT, R.xT)
        project(nc, R, "a2_qkv", R.xT, [(R.w[f"L2_attn_W{n}"][:, :], dst, ACT.Relu, 1.0, R.col(f"L2_attn_b{n}"))
                                        for n, dst in (("q", q), ("k", k), ("v", v))])
        one_head(nc, R, "a2", q, k, v, o, HD ** -0.5)
        project(nc, R, "a2_out", o, [(R.w["L2_attn_Wo"][:, :], q, ACT.Relu, 1.0, R.col("L2_attn_bo"))])
        layer_norm(nc, R, "a2_norm", q, R.hT, 1e-3, R.col("L2_attn_gamma"), R.col("L2_attn_beta"), residual=True)


def one_head(nc, R, tag, q_all, k_all, v_all, o_all, scale):
    with ExitStack() as ctx:
        sb, ps, sem = allocators(nc, ctx, tag)
        qkv = sb("qkv", [P, 2, 3, T])
        peak, total = sb("peak", [HALF, 2, 2]), sb("total", [HALF, 2, 2])
        prob, probT, vrow = sb("prob", [HALF, 2, 2, T]), sb("probT", [HALF, 2, 2, T]), sb("vrow", [HALF, 2, 2, C])
        pS, pV, pT, pO = ps("pS", [HALF, 2, 512]), ps("pV", [HALF, 2, 512]), ps("pT", [HALF, 2, 512]), ps("pO", [P, 2, 512])
        loaded = [sem(f"loaded{u}") for u in range(2)]
        scores_ready, v_turned, v_copied, peak_ready, exp_done, scaled, turned, copied, mixed, done, order = (
            sem(n) for n in ("scores_ready", "v_turned", "v_copied", "peak_ready", "exp_done", "scaled", "turned", "copied",
                             "mixed", "done", "order"))
        block = ctx.enter_context(nc.Block())

        @block.sync
        def _(sp):
            with sp.Fori(0, B // 2) as i:
                for u in range(2):
                    sp.wait_ge(v_turned, 2 * i + u + 1)
                    for j, src in enumerate((q_all, k_all, v_all)):
                        sp.dma_start(qkv[:, u, j, :], src[:, bass.ds(i * (2 * T) + u * T, T)]).then_inc(loaded[u], 16)

        @block.tensor
        def _(pe):
            pe.sem_inc(v_turned, SLOTS)
            pe.sem_inc(mixed, SLOTS)

            def scores(n, u, turn):
                pe.wait_ge(loaded[u], 48 * turn + 48)
                pe.wait_ge(exp_done, n + 1)
                for half in range(2):
                    last = pe.matmul(pS[:, u, T * half:T * half + T], qkv[:, u, 0, HALF * half:HALF * half + HALF],
                                     qkv[:, u, 1, :], start=True, stop=True)
                last.then_inc(scores_ready, 1)
                pe.wait_ge(v_copied, n + 1)
                for half in range(2):
                    last = pe.transpose(pV[:, u, C * half:C * half + C], qkv[:, u, 2, HALF * half:HALF * half + HALF],
                                        R.c("ident"))
                last.then_inc(v_turned, 1)

            def mix(n, u):
                pe.wait_ge(scaled, n + 1)
                for a in range(2):
                    for b in range(2):
                        last = pe.transpose(pT[:, u, T * b + HALF * a:T * b + HALF * a + HALF],
                                            prob[:, u, a, HALF * b:HALF * b + HALF], R.c("ident")[0:HALF, 0:HALF])
                last.then_inc(turned, 1)
                pe.wait_ge(v_copied, n + 1 + SLOTS)
                pe.wait_ge(copied, n + 1)
                pe.wait_ge(done, n + 1)
                for b in range(2):
                    last = pe.matmul(pO[:, u, 0:T], vrow[:, u, b, :], probT[:, u, b, :], start=(b == 0), stop=(b == 1))
                last.then_inc(mixed, 1)

            scores(0, 0, 0)
            with pe.Fori(0, B // 2 - 1) as i:
                for u in range(2):
                    scores(2 * i + u + 1, 1 - u, i + u)
                    mix(2 * i + u, u)
            scores(B - 1, 1, B // 2 - 1)
            mix(B - 2, 0)
            mix(B - 1, 1)

        @block.scalar
        def _(act):
            act.sem_inc(exp_done, SLOTS)
            act.sem_inc(v_copied, SLOTS)

            def exps(n, u):
                act.wait_ge(peak_ready, n + 1)
                for half in range(2):
                    last = act.activation(prob[:, u, half, :], pS[:, u, T * half:T * half + T], ACT.Exp, scale=scale,
                                          bias=peak[:, u, half:half + 1], accum_out=total[:, u, half:half + 1])
                last.then_inc(exp_done, 1)

            def values(n, u):
                act.wait_ge(v_turned, n + 1 + SLOTS)
                act.wait_ge(mixed, n + 1)
                act.copy(vrow[:, u, :, :].rearrange("p a c -> p (a c)"), pV[:, u, 0:2 * C]).then_inc(v_copied, 1)

            def turn_out(n, u):
                act.wait_ge(turned, n + 1)
                act.copy(probT[:, u, :, :].rearrange("p a c -> p (a c)"), pT[:, u, 0:2 * T]).then_inc(copied, 1)

            exps(0, 0)
            values(0, 0)
            with act.Fori(0, B // 2 - 1) as i:
                for u in range(2):
                    turn_out(2 * i + u, u)
                    exps(2 * i + u + 1, 1 - u)
                    values(2 * i + u + 1, 1 - u)
            turn_out(B - 2, 0)
            exps(B - 1, 1)
            values(B - 1, 1)
            turn_out(B - 1, 1)

        @block.vector
        def _(dve):
            dve.sem_inc(done, SLOTS)
            chain = Chain(dve, order)

            def peaks(n, u):
                dve.wait_ge(scores_ready, n + 1)
                chain(dve.tensor_reduce(peak[:, u, :], pS[:, u, 0:2 * T].rearrange("p (a t) -> p a t", a=2), AX, ALU.max))
                dve.tensor_scalar(peak[:, u, :], peak[:, u, :], -scale, None, ALU.mult).then_inc(peak_ready, 1)

            def weights(n, u):
                dve.wait_ge(exp_done, n + 1 + SLOTS)
                chain(dve.reciprocal(total[:, u, :], total[:, u, :]))
                for half in range(2):
                    last = dve.tensor_scalar(prob[:, u, half, :], prob[:, u, half, :], total[:, u, half:half + 1], None,
                                             ALU.mult)
                last.then_inc(scaled, 1)

            def out(n, u):
                dve.wait_ge(mixed, n + 1 + SLOTS)
                dve.tensor_copy(o_all[:, bass.ds(n * T, T)], pO[:, u, 0:T]).then_inc(done, 1)

            peaks(0, 0)
            with dve.Fori(0, B // 2 - 1) as i:
                chain.turn(i, 4, 1)
                for u in range(2):
                    weights(2 * i + u, u)
                    peaks(2 * i + u + 1, 1 - u)
                    out(2 * i + u, u)
                chain.close()
            chain.after(1 + 4 * (B // 2 - 1))
            weights(B - 2, 0)
            peaks(B - 1, 1)
            out(B - 2, 0)
            weights(B - 1, 1)
            out(B - 1, 1)


def attention_3(nc, R):
    with ExitStack() as ctx:
        sb, _, _ = allocators(nc, ctx, "a3")
        q, k, v, o = sb("q", [P, N]), sb("k", [P, N]), sb("v", [P, N]), sb("o", [P, N])
        layer_norm(nc, R, "a3_ln", R.hT, R.xT)
        project(nc, R, "a3_qkv", R.xT, [
            (R.wt[f"{s}T"][:, :], dst, ACT.Relu, R.bn[:, 0, n:n + 1], R.bn[:, 1, n:n + 1])
            for n, (s, dst) in enumerate((("q", q), ("k", k), ("v", v)))])
        linear_heads(nc, R, "a3", q, k, v, o, 0.125)
        project(nc, R, "a3_out", o, [(R.wt["pT"][:, :], q, ACT.Relu, R.bn[:, 0, 3:4], R.bn[:, 1, 3:4])])
        add_arrays(nc, R, "a3_x1", q, R.xT)
        dense_mlp(nc, R, "a3_mlp", q, lambda n: R.wt["f1T"][:, C * n:C * n + C], lambda n: R.bn[:, 0, 4 + n:5 + n],
                  lambda n: R.bn[:, 1, 4 + n:5 + n], lambda n: R.wt["f2T"][:, C * n:C * n + C],
                  ("norm", R.bn[:, 0, 8:9], R.bn[:, 1, 8:9], q))


def linear_heads(nc, R, tag, q_all, k_all, v_all, o_all, scale):
    with ExitStack() as ctx:
        sb, ps, sem = allocators(nc, ctx, tag)
        kv = sb("kv", [P, 2, 2, T])
        rows, state = sb("rows", [HALF, 2, 2, 2, C]), sb("state", [P, 2, C])
        pR, pS, pO = ps("pR", [HALF, 2, 512]), ps("pS", [P, 2, 512]), ps("pO", [P, 2, 512])
        loaded = [sem(f"loaded{u}") for u in range(2)]
        turned, rows_ready, product_ready, state_ready, mixed, done = (
            sem(n) for n in ("turned", "rows_ready", "product_ready", "state_ready", "mixed", "done"))
        block = ctx.enter_context(nc.Block())

        @block.sync
        def _(sp):
            with sp.Fori(0, B // 2) as i:
                for u in range(2):
                    sp.wait_ge(turned, 2 * i + u + 1)
                    for j, src in enumerate((k_all, v_all)):
                        sp.dma_start(kv[:, u, j, :], src[:, bass.ds(i * (2 * T) + u * T, T)]).then_inc(loaded[u], 16)

        @block.tensor
        def _(pe):
            def turn(n, u, t):
                pe.wait_ge(loaded[u], 32 * t + 32)
                pe.wait_ge(rows_ready, n + 1)
                for j in range(2):
                    for half in range(2):
                        a = C * (2 * j + half)
                        last = pe.transpose(pR[:, u, a:a + C], kv[:, u, j, HALF * half:HALF * half + HALF], R.c("ident"))
                last.then_inc(turned, 1)

            def products(n, u):
                pe.wait_ge(rows_ready, n + 1 + SLOTS)
                pe.wait_ge(state_ready, n + 1)
                for half in range(2):
                    last = pe.matmul(pS[:, u, 0:C], rows[:, u, 0, half, :], rows[:, u, 1, half, :], start=(half == 0),
                                     stop=(half == 1))
                last.then_inc(product_ready, 1)

            def mix(n, u):
                pe.wait_ge(state_ready, n + 1 + SLOTS)
                pe.wait_ge(done, n + 1)
                pe.matmul(pO[:, u, 0:T], state[:, u, :], q_all[:, bass.ds(n * T, T)], start=True, stop=True).then_inc(mixed, 1)

            pe.sem_inc(turned, SLOTS)
            pe.sem_inc(mixed, SLOTS)
            turn(0, 0, 0)
            turn(1, 1, 0)
            products(0, 0)
            with pe.Fori(0, B // 2 - 1) as i:
                for u in range(2):
                    turn(2 * i + u + 2, u, i + 1)
                    products(2 * i + u + 1, 1 - u)
                    mix(2 * i + u, u)
            products(B - 1, 1)
            mix(B - 2, 0)
            mix(B - 1, 1)

        @block.scalar
        def _(act):
            act.sem_inc(done, SLOTS)
            act.sem_inc(rows_ready, SLOTS)

            def rows_out(n, u):
                act.wait_ge(turned, n + 1 + SLOTS)
                act.wait_ge(product_ready, n + 1)
                act.copy(rows[:, u].rearrange("p j a c -> p (j a c)"), pR[:, u, :]).then_inc(rows_ready, 1)

            def out(n, u):
                act.wait_ge(mixed, n + 1 + SLOTS)
                act.activation(o_all[:, bass.ds(n * T, T)], pO[:, u, 0:T], ACT.Relu).then_inc(done, 1)

            rows_out(0, 0)
            rows_out(1, 1)
            with act.Fori(0, B // 2 - 1) as i:
                for u in range(2):
                    rows_out(2 * i + u + 2, u)
                    out(2 * i + u, u)
            out(B - 2, 0)
            out(B - 1, 1)

        @block.vector
        def _(dve):
            dve.sem_inc(state_ready, SLOTS)
            dve.sem_inc(product_ready, SLOTS)
            with dve.Fori(0, B // 2) as i:
                for u in range(2):
                    dve.wait_ge(product_ready, 2 * i + u + 1 + SLOTS)
                    dve.wait_ge(mixed, 2 * i + u + 1)
                    dve.scalar_tensor_tensor(out=state[:, u, :], in0=pS[:, u, 0:C], scalar=scale, in1=R.c("head_block"),
                                             op0=ALU.mult, op1=ALU.mult).then_inc(state_ready, 1)


N_IN, N_PROC, N_OUT, D_PV = 512, 256, 512, 64
K_IN, K_PROC, K_OUT = 64, 128, 64


def pattern_weights(nc, R, w):
    with ExitStack() as ctx:
        sb, ps, sem = allocators(nc, ctx, "f2w")
        raw_in, raw_p, raw_o = sb("raw_in", [P, 4, C]), sb("raw_p", [P, 2, N_IN]), sb("raw_o", [P, 4, D_PV])
        pi, pp, po = ps("pi", [P, 512]), ps("pp", [P, 2, 512]), ps("po", [D_PV, 512])
        loaded, zeroed, turned = sem("loaded"), sem("zeroed"), sem("turned")
        block = ctx.enter_context(nc.Block())
        i = R.ins

        @block.sync
        def _(sp):
            sp.wait_ge(zeroed, 1)
            for dst, src in ((raw_in[:, :, :], i["L2_ffn_input_patterns"].rearrange("(k p) d -> p k d", p=P)),
                             (raw_p[:, :, :], i["L2_ffn_process_input_weights"].rearrange("(k p) n -> p k n", p=P)),
                             (raw_o[:, :, :], i["L2_ffn_output_input_weights"].rearrange("(k p) d -> p k d", p=P)),
                             (w["pv"][:, :, 0:D_PV], i["L2_ffn_process_values"].rearrange("(k p) d -> p k d", p=P)),
                             (w["op"][:, :, :], i["L2_ffn_output_patterns"].rearrange("(k p) m -> p k m", p=P))):
                sp.dma_start(dst, src).then_inc(loaded, 16)

        @block.tensor
        def _(pe):
            pe.wait_ge(loaded, 80)
            for k in range(4):
                pe.transpose(pi[:, P * k:P * k + P], raw_in[:, k, :], R.c("ident"))
                pe.transpose(po[:, P * k:P * k + P], raw_o[:, k, :], R.c("ident"))
            for k in range(2):
                for n in range(4):
                    a = 256 * n + P * k
                    last = pe.transpose(pp[:, a // 512, a % 512:a % 512 + P], raw_p[:, k, P * n:P * n + P], R.c("ident"))
            last.then_inc(turned, 1)

        @block.vector
        def _(dve):
            dve.memset(w["pv"][:, :, :], 0.0)
            dve.memset(w["oiT"][:, :], 0.0).then_inc(zeroed, 1)
            dve.wait_ge(turned, 1)
            dve.wait_ge(zeroed, 1)
            dve.tensor_copy(w["ipT"][:, :], pi[:, :])
            dve.tensor_copy(w["oiT"][0:D_PV, :], po[:, :])
            dve.tensor_copy(w["piT"][:, :, :].rearrange("p n k -> p (n k)"), pp[:, :, :].rearrange("p a b -> p (a b)"))


def feed_forward_2(nc, R):
    NEVER = -1e30
    QUAD, PAIRS = 4, ((0, 1), (2, 3))
    TURNS = TILES // QUAD
    with ExitStack() as ctx:
        sb, ps, sem = allocators(nc, ctx, "f2")
        layer_norm(nc, R, "f2_ln", R.hT, R.xT)
        w = {"ipT": sb("ipT", [P, N_IN]), "piT": sb("piT", [P, 4, N_PROC]), "pv": sb("pv", [P, 2, C]),
             "oiT": sb("oiT", [P, N_OUT]), "op": sb("op", [P, 4, C])}
        pattern_weights(nc, R, w)
        x, y = sb("x", [P, QUAD, P]), sb("y", [P, 2, P])
        act_in, act_proc, act_out = sb("act_in", [P, QUAD, N_IN]), sb("act_proc", [P, QUAD, N_PROC]), sb(
            "act_out", [P, QUAD, N_OUT])
        sel_in, sel_proc, sel_out = sb("sel_in", [P, QUAD, N_IN]), sb("sel_proc", [P, QUAD, N_PROC]), sb(
            "sel_out", [P, QUAD, N_OUT])
        soft = sb("soft", [P, QUAD, N_PROC])
        inT, procT, outT, aggT = sb("inT", [P, 2, N_IN]), sb("procT", [P, 2, N_PROC]), sb("outT", [P, 2, N_OUT]), sb(
            "aggT", [P, 2, P])
        top, peak, total = sb("top", [P, QUAD, 8]), sb("peak", [P, QUAD, 1]), sb("total", [P, QUAD, 1])
        bank = [ps(f"bank{t}", [P, 512]) for t in range(QUAD)]
        turn = [ps(f"turn{u}", [P, 512]) for u in range(2)]
        small = [ps(f"small{u}", [P, 512]) for u in range(2)]
        names = ("copied", "in_ready", "in_acted", "in_selected", "in_turned", "in_evacuated", "proc_ready", "proc_acted",
                 "peak_ready", "soft_ready", "proc_selected", "proc_turned", "proc_evacuated", "agg_ready", "agg_evacuated",
                 "out_ready", "out_acted", "out_selected", "out_turned", "out_evacuated", "y_ready", "done", "added", "order")
        s = {n: sem(n) for n in names}
        block = ctx.enter_context(nc.Block())

        @block.gpsimd
        def _(pool):
            pool.sem_inc(s["added"], 2)

            def copy_in(i):
                for t in range(QUAD):
                    pool.wait_ge(s["in_ready"], QUAD * i + t + 1)
                    pool.tensor_copy(x[:, t, :], R.xT[:, bass.ds(i * (QUAD * P) + t * P, P)]).then_inc(s["copied"], 1)

            def add_out(i):
                for t in range(QUAD):
                    at = bass.ds(i * (QUAD * P) + t * P, P)
                    pool.wait_ge(s["done"], QUAD * i + t + 1 + 2)
                    pool.tensor_tensor(R.hT[:, at], y[:, t % 2, :], R.hT[:, at], ALU.add).then_inc(s["added"], 1)

            copy_in(0)
            with pool.Fori(0, TURNS - 1) as i:
                copy_in(i + 1)
                add_out(i)
            add_out(TURNS - 1)

        @block.tensor
        def _(pe):
            pe.sem_inc(s["in_ready"], QUAD)

            def product_in(n, t):
                pe.wait_ge(s["copied"], n + 1)
                pe.wait_ge(s["out_acted"], n + 1)
                pe.matmul(bank[t][:, :], x[:, t, :], w["ipT"][:, :], start=True, stop=True).then_inc(s["in_ready"], 1)

            def turned(src, n_blocks, selected, count, signal, t):
                pe.wait_ge(s[selected], count)
                for k in range(n_blocks):
                    last = pe.transpose(turn[t % 2][:, P * k:P * k + P], src[:, t, P * k:P * k + P], R.c("ident"))
                last.then_inc(s[signal], 1)

            for t in range(QUAD):
                product_in(t, t)

            def quad(i, more):
                for pair in PAIRS:
                    for t in pair:
                        n = QUAD * i + t
                        turned(sel_in, 4, "in_selected", n + 1 + QUAD, "in_turned", t)
                    for t in pair:
                        n = QUAD * i + t
                        pe.wait_ge(s["in_evacuated"], n + 1)
                        for k in range(4):
                            last = pe.matmul(bank[t][:, 0:N_PROC], inT[:, t % 2, P * k:P * k + P], w["piT"][:, k, :],
                                             start=(k == 0), stop=(k == 3))
                        last.then_inc(s["proc_ready"], 1)
                for pair in PAIRS:
                    for t in pair:
                        n = QUAD * i + t
                        turned(sel_proc, 2, "proc_selected", n + 1, "proc_turned", t)
                    for t in pair:
                        n = QUAD * i + t
                        pe.wait_ge(s["proc_evacuated"], n + 1)
                        pe.wait_ge(s["done"], QUAD * i + (t % 2) + 1)
                        for k in range(2):
                            last = pe.matmul(small[t % 2][:, 0:P], w["pv"][:, k, :], procT[:, t % 2, P * k:P * k + P],
                                             start=(k == 0), stop=(k == 1))
                        last.then_inc(s["agg_ready"], 1)
                    for t in pair:
                        n = QUAD * i + t
                        pe.wait_ge(s["agg_evacuated"], n + 1)
                        pe.matmul(bank[t][:, :], aggT[:, t % 2, :], w["oiT"][:, :], start=True, stop=True).then_inc(
                            s["out_ready"], 1)
                if more:
                    for t in range(QUAD):
                        product_in(QUAD * i + QUAD + t, t)
                for pair in PAIRS:
                    for t in pair:
                        n = QUAD * i + t
                        turned(sel_out, 4, "out_selected", n + 1, "out_turned", t)
                    for t in pair:
                        n = QUAD * i + t
                        pe.wait_ge(s["out_evacuated"], n + 1)
                        pe.wait_ge(s["done"], n + 1)
                        for k in range(4):
                            last = pe.matmul(small[t % 2][:, P:2 * P], w["op"][:, k, :], outT[:, t % 2, P * k:P * k + P],
                                             start=(k == 0), stop=(k == 3))
                        last.then_inc(s["y_ready"], 1)

            with pe.Fori(0, TURNS - 1) as i:
                quad(i, True)
            quad(TURNS - 1, False)

        @block.scalar
        def _(act):
            act.sem_inc(s["out_acted"], QUAD)
            act.sem_inc(s["done"], 2)

            def gelu_in(n, t):
                act.wait_ge(s["in_ready"], n + 1 + QUAD)
                act.wait_ge(s["in_selected"], n + 1)
                act.activation(act_in[:, t, :], bank[t][:, :], ACT.Gelu).then_inc(s["in_acted"], 1)

            for t in range(QUAD):
                gelu_in(t, t)

            def quad(i, more):
                for pair in PAIRS:
                    for t in pair:
                        act.wait_ge(s["in_turned"], QUAD * i + t + 1)
                        act.copy(inT[:, t % 2, :], turn[t % 2][:, :]).then_inc(s["in_evacuated"], 1)
                    for t in pair:
                        act.wait_ge(s["proc_ready"], QUAD * i + t + 1)
                        act.activation(act_proc[:, t, :], bank[t][:, 0:N_PROC], ACT.Gelu).then_inc(s["proc_acted"], 1)
                for pair in PAIRS:
                    for t in pair:
                        act.wait_ge(s["peak_ready"], QUAD * i + t + 1)
                        act.activation(soft[:, t, :], act_proc[:, t, :], ACT.Exp, bias=peak[:, t, :]).then_inc(
                            s["soft_ready"], 1)
                    for t in pair:
                        act.wait_ge(s["proc_turned"], QUAD * i + t + 1)
                        act.copy(procT[:, t % 2, :], turn[t % 2][:, 0:N_PROC]).then_inc(s["proc_evacuated"], 1)
                    for t in pair:
                        act.wait_ge(s["agg_ready"], QUAD * i + t + 1)
                        act.copy(aggT[:, t % 2, :], small[t % 2][:, 0:P]).then_inc(s["agg_evacuated"], 1)
                    for t in pair:
                        act.wait_ge(s["out_ready"], QUAD * i + t + 1)
                        act.activation(act_out[:, t, :], bank[t][:, :], ACT.Gelu).then_inc(s["out_acted"], 1)
                if more:
                    for t in range(QUAD):
                        gelu_in(QUAD * i + QUAD + t, t)
                for pair in PAIRS:
                    for t in pair:
                        act.wait_ge(s["out_turned"], QUAD * i + t + 1)
                        act.copy(outT[:, t % 2, :], turn[t % 2][:, :]).then_inc(s["out_evacuated"], 1)
                    for t in pair:
                        act.wait_ge(s["y_ready"], QUAD * i + t + 1)
                        act.wait_ge(s["added"], QUAD * i + t + 1)
                        act.copy(y[:, t % 2, :], small[t % 2][:, P:2 * P]).then_inc(s["done"], 1)

            with act.Fori(0, TURNS - 1) as i:
                quad(i, True)
            quad(TURNS - 1, False)

        @block.vector
        def _(dve):
            dve.sem_inc(s["in_selected"], QUAD)
            chain = Chain(dve, s["order"])

            def select(src, marked, pair, k, peaks=False):
                for t in pair:
                    chain.late(dve.memset(top[:, t, :], 0.0))
                for r in range(k // 8):
                    a = src if r == 0 else marked
                    for t in pair:
                        chain.late(dve.max(top[:, t, :], a[:, t, :]))
                    if peaks and r == 0:
                        chain.catch_up()
                        for t in pair:
                            dve.tensor_scalar(peak[:, t, :], top[:, t, 0:1], -1.0, None, ALU.mult).then_inc(
                                s["peak_ready"], 1)
                    for t in pair:
                        chain.late(dve.match_replace(marked[:, t, :], top[:, t, :], a[:, t, :], NEVER))

            with dve.Fori(0, TURNS) as i:
                chain.restart()
                for src, marked, acted, before, k, signal in ((act_in, sel_in, "in_acted", 0, K_IN, "in_selected"),
                                                              (act_proc, sel_proc, "proc_acted", 0, K_PROC, None),
                                                              (act_out, sel_out, "out_acted", QUAD, K_OUT, "out_selected")):
                    for pair in PAIRS:
                        dve.wait_ge(s[acted], QUAD * i + pair[1] + 1 + before)
                        select(src, marked, pair, k, signal is None)
                        for t in pair:
                            if signal is not None:
                                dve.scalar_tensor_tensor(out=marked[:, t, :], in0=marked[:, t, :], scalar=NEVER,
                                                         in1=src[:, t, :], op0=ALU.is_equal, op1=ALU.mult).then_inc(
                                    s[signal], 1)
                                if t == pair[0]:
                                    chain.catch_up()
                                continue
                            dve.wait_ge(s["soft_ready"], QUAD * i + t + 1)
                            chain.late(dve.scalar_tensor_tensor(out=marked[:, t, :], in0=marked[:, t, :], scalar=NEVER,
                                                                in1=soft[:, t, :], op0=ALU.is_equal, op1=ALU.mult,
                                                                accum_out=total[:, t, :]))
                        if signal is None:
                            for t in pair:
                                chain.late(dve.reciprocal(total[:, t, :], total[:, t, :]))
                            chain.catch_up()
                            for t in pair:
                                dve.tensor_scalar(marked[:, t, :], marked[:, t, :], total[:, t, :], None,
                                                  ALU.mult).then_inc(s["proc_selected"], 1)


STAGES = {
    "tokens": tokens,
    "attention_0": attention_0,
    "feed_forward_0": feed_forward_0,
    "attention_1": attention_1,
    "feed_forward_1": feed_forward_1,
    "attention_2": attention_2,
    "feed_forward_2": feed_forward_2,
    "attention_3": attention_3,
    "feed_forward_3": feed_forward_3,
}


def program(nc, ins, out):
    with ExitStack() as ctx:
        R = Resident(nc, ctx, ins, out)
        R.eps = {e: ctx.enter_context(nc.sbuf_tensor(f"eps{k}", [P, 1], F32)) for k, e in enumerate((1e-5, 1e-3))}
        R.scratch = [nc.dram_tensor(f"scratch{n}", (P, N), F32, kind="Internal").ap() for n in range(5)]
        R.groups = nc.dram_tensor("lsh_groups", (P, N), BF16, kind="Internal").ap()
        R.self_value = ctx.enter_context(nc.sbuf_tensor("self_value", [P, 1], F32))
        with nc.Block() as block:
            @block.vector
            def _(dve):
                for e, t in R.eps.items():
                    dve.memset(t[:, :], e)
                dve.memset(R.self_value[:, :], -50000.0)
        set_up(nc, R)
        for stage in STAGES.values():
            stage(nc, R)


def kernel(**inputs):
    import concourse.bacc as bacc
    from concourse.bass_utils import run_bass_kernel_spmd

    nc = bacc.Bacc("TRN2", target_bir_lowering=False, num_devices=1)
    arrays, ins = {}, {}
    together = [name for name, _ in VECTORS + WEIGHTS]
    given = {name: a for name, a in inputs.items() if name not in together}
    for name, a in {**given, **packed(inputs), "consts": CONSTS}.items():
        a = np.ascontiguousarray(a)
        arrays[f"in_{name}_dram"] = a
        ins[name] = nc.dram_tensor(f"in_{name}_dram", a.shape, mybir.dt.from_np(a.dtype), kind="ExternalInput").ap()
    out = nc.dram_tensor("out_0_dram", (B, T, C), F32, kind="ExternalOutput").ap()
    program(nc, ins, out)
    r = run_bass_kernel_spmd(nc, [arrays], core_ids=[0])
    return r.results[0]["out_0_dram"]
```
